# Optimizing a Trainium2 kernel written in Bass

```python
import numpy as np
import jax
import jax.numpy as jnp

def _softmax(x, axis=-1):
    return jax.nn.softmax(x, axis=axis)

def _gelu(x):
    return jax.nn.gelu(x, approximate=True)

def _silu(x):
    return jax.nn.silu(x)

def _sigmoid(x):
    return jax.nn.sigmoid(x)

def _layernorm(x, axis=-1, eps=1e-05):
    m = jnp.mean(x, axis=axis, keepdims=True)
    v = jnp.var(x, axis=axis, keepdims=True)
    return (x - m) / jnp.sqrt(v + eps)

def _scatter_add(tgt, idx, src, axis=0):
    return tgt.at[idx].add(src)

def _segment_sum(src, seg, n):
    return jax.ops.segment_sum(src, seg, n)
kernel_name = 'mk_decoder_preln_d4_seqx_r8_4f65bf'

def setup_inputs(seed: int=0):
    np.random.seed(seed)
    _w = jnp.asarray

    def _rec_inputs():
        import jax
        import jax.numpy as jnp
        _rk = jax.random.key(seed)
        x = -0.0002928 + 1 * jax.random.normal(jax.random.fold_in(_rk, 1), (16, 64, 128), jnp.float32)
        _lenS = 64 - jax.random.randint(jax.random.fold_in(_rk, 7), (16,), 0, max(1, 64 // 4) + 1, jnp.int32)
        _lenS2 = 64 - jax.random.randint(jax.random.fold_in(_rk, 8), (16,), 0, max(1, 64 // 4) + 1, jnp.int32)
        _ctx_1024P = jax.random.normal(jax.random.fold_in(_rk, 11), (16, 16, 128), jnp.float32)
        _ctx_1024c = jax.random.dirichlet(jax.random.fold_in(_rk, 511), 0.3 * jnp.ones((16,), jnp.float32), (16, 64))
        _ctx_1024t = jnp.einsum('bsk,bkd->bsd', _ctx_1024c, _ctx_1024P)
        _ctx_1024t = _ctx_1024t * jax.lax.rsqrt(jnp.mean(jnp.square(_ctx_1024t)) + 1e-12) * 0.953939
        ctx_1024 = -1.39393e-06 + 0.999914 * (_ctx_1024t + 0.3 * jax.random.normal(jax.random.fold_in(_rk, 611), (16, 64, 128), jnp.float32))
        return (x, ctx_1024)
    x, ctx_1024 = _rec_inputs()

    def _L0_attn_setup():
        import jax, jax.numpy as jnp
        import numpy as np
        import math
        B, S, D = (4, 256, 128)
        H = 16
        HD = D // H
        DL = 32
        LAMBDA_DECAY = 0.01
        key = jax.random.key(seed)
        ks = jax.random.split(key, 8)
        sc = lambda fan_in: 1.0 / math.sqrt(fan_in)
        return {'x': jax.random.normal(ks[0], (B, S, D), dtype=jnp.float32), 'W_q': jax.random.normal(ks[1], (D, D), dtype=jnp.float32) * sc(D), 'W_k': jax.random.normal(ks[2], (D, D), dtype=jnp.float32) * sc(D), 'W_v': jax.random.normal(ks[3], (D, D), dtype=jnp.float32) * sc(D), 'W_o': jax.random.normal(ks[4], (D, D), dtype=jnp.float32) * sc(D), 'W_down_kv': jax.random.normal(ks[5], (D, DL), dtype=jnp.float32) * sc(D), 'W_up_k': jax.random.normal(ks[6], (DL, D), dtype=jnp.float32) * sc(DL), 'W_up_v': jax.random.normal(ks[7], (DL, D), dtype=jnp.float32) * sc(DL)}
    _L0_attn_all = _L0_attn_setup()
    _L0_attn_in = {k: v for k, v in _L0_attn_all.items() if k in ('W_q', 'W_k', 'W_v', 'W_o', 'W_down_kv', 'W_up_k', 'W_up_v')}
    del _L0_attn_all

    def _L0_xattn_setup():
        import jax, jax.numpy as jnp
        import numpy as np
        EMB = 128
        NH = 8
        HD = EMB // NH
        EPS = 1e-06

        def _mlstm_head(q, k, v, ig, fg):
            S, DH = q.shape
            log_fg = jax.nn.log_sigmoid(fg)
            cs = jnp.concatenate([jnp.zeros((1, 1), q.dtype), jnp.cumsum(log_fg, axis=0)], axis=0)
            fg_mat_full = cs - cs.T
            ltr = jnp.tril(jnp.ones((S, S), bool))
            log_fg_matrix = jnp.where(ltr, fg_mat_full[1:, 1:], -jnp.inf)
            log_D = log_fg_matrix + ig.T
            max_log_D = jnp.max(log_D, axis=-1, keepdims=True)
            D = jnp.exp(log_D - max_log_D)
            qk = q @ (k.T / jnp.sqrt(jnp.asarray(DH, q.dtype)))
            C = qk * D
            normalizer = jnp.maximum(jnp.abs(C.sum(-1, keepdims=True)), jnp.exp(-max_log_D))
            return C / (normalizer + EPS) @ v
        key = jax.random.key(seed)
        ks = jax.random.split(key, 6)
        B, S = (2, 256)
        q = jax.random.normal(ks[0], (B, S, EMB), jnp.float32)
        k = jax.random.normal(ks[1], (B, S, EMB), jnp.float32)
        v = jax.random.normal(ks[2], (B, S, EMB), jnp.float32)
        igate_kernel = jax.random.normal(ks[3], (3 * EMB, NH), jnp.float32) * 0.02
        igate_bias = jax.random.normal(ks[4], (NH,), jnp.float32) * 0.1
        fgate_kernel = jax.random.normal(ks[5], (3 * EMB, NH), jnp.float32) * 0.02
        fgate_bias = jnp.linspace(3.0, 6.0, NH).astype(jnp.float32)
        return dict(q=q, k=k, v=v, igate_kernel=igate_kernel, igate_bias=igate_bias, fgate_kernel=fgate_kernel, fgate_bias=fgate_bias)
    _L0_xattn_all = _L0_xattn_setup()
    _L0_xattn_in = {k: v for k, v in _L0_xattn_all.items() if k in ('igate_kernel', 'igate_bias', 'fgate_kernel', 'fgate_bias')}
    del _L0_xattn_all

    def _L0_ffn_setup():
        import jax, jax.numpy as jnp
        import numpy as np
        B, S, D, H, M, E, K = (4, 256, 128, 256, 64, 8, 2)

        def _layernorm(x, g, b, eps=1e-05):
            mu = x.mean(-1, keepdims=True)
            var = ((x - mu) ** 2).mean(-1, keepdims=True)
            return (x - mu) * jax.lax.rsqrt(var + eps) * g + b

        def _forward(inputs_embeds, enc_W, enc_b, s2c_W, s2c_b, rW1, rb1, rW2, rb2, We1, be1, We2, be2, c2s_W, c2s_b, dec_W, dec_b, ln_g, ln_b):
            b, s, _ = inputs_embeds.shape
            spikes_enc = jax.nn.sigmoid(inputs_embeds @ enc_W + enc_b)
            flat = spikes_enc.reshape(b * s, H)
            cont = flat @ s2c_W + s2c_b
            logits = jnp.tanh(cont @ rW1 + rb1) @ rW2 + rb2
            probs = jax.nn.softmax(logits, axis=-1)
            topw, topi = jax.lax.top_k(probs, K)
            w = topw / topw.sum(-1, keepdims=True)
            gates = (jax.nn.one_hot(topi, E, dtype=cont.dtype) * w[..., None]).sum(1)
            h = jax.nn.relu(jnp.einsum('nm,emh->enh', cont, We1) + be1[:, None, :])
            expert_out = jnp.einsum('enh,ehm->enm', h, We2) + be2[:, None, :]
            output_flat = jnp.einsum('enm,ne->nm', expert_out, gates)
            spikes_moe = jax.nn.sigmoid(output_flat @ c2s_W + c2s_b).reshape(b, s, H)
            decoded = jax.nn.sigmoid(spikes_moe @ dec_W + dec_b)
            return _layernorm(decoded, ln_g, ln_b)
        key = jax.random.key(seed)
        ks = jax.random.split(key, 10)
        r = lambda k, shape: jax.random.normal(k, shape, dtype=jnp.float32) * 0.02
        return {'inputs_embeds': jax.random.normal(ks[0], (B, S, D), dtype=jnp.float32), 'enc_W': r(ks[1], (D, H)), 'enc_b': jnp.zeros((H,), jnp.float32), 's2c_W': r(ks[2], (H, M)), 's2c_b': jnp.zeros((M,), jnp.float32), 'rW1': r(ks[3], (M, 64)), 'rb1': jnp.zeros((64,), jnp.float32), 'rW2': r(ks[4], (64, E)), 'rb2': jnp.zeros((E,), jnp.float32), 'We1': r(ks[5], (E, M, H // 2)), 'be1': jnp.zeros((E, H // 2), jnp.float32), 'We2': r(ks[6], (E, H // 2, M)), 'be2': jnp.zeros((E, M), jnp.float32), 'c2s_W': r(ks[7], (M, H)), 'c2s_b': jnp.zeros((H,), jnp.float32), 'dec_W': r(ks[8], (H, D)), 'dec_b': jnp.zeros((D,), jnp.float32), 'ln_g': jnp.ones((D,), jnp.float32), 'ln_b': jnp.zeros((D,), jnp.float32)}
    _L0_ffn_all = _L0_ffn_setup()
    _L0_ffn_in = {k: v for k, v in _L0_ffn_all.items() if k in ('enc_W', 'enc_b', 's2c_W', 's2c_b', 'rW1', 'rb1', 'rW2', 'rb2', 'We1', 'be1', 'We2', 'be2', 'c2s_W', 'c2s_b', 'dec_W', 'dec_b', 'ln_g', 'ln_b')}
    del _L0_ffn_all

    def _L1_attn_setup():
        import jax, jax.numpy as jnp
        import numpy as np
        B, N, D, H = (4, 512, 128, 16)
        GN_EPS = 0.00064
        key = jax.random.key(seed)
        ks = jax.random.split(key, 12)
        x = jax.random.normal(ks[0], (B, N, D), jnp.float32)
        ddd = jnp.linspace(0.0, 1.0, D).reshape(1, 1, D)
        s = 1.0 / np.sqrt(D)
        w = lambda k: jax.random.normal(k, (D, D), jnp.float32) * s
        return {'x': x, 'x_r': 1.0 - ddd ** 0.2, 'x_w': 1.0 - ddd ** 0.9, 'x_k': 1.0 - ddd ** 0.7, 'x_v': 1.0 - ddd ** 0.7, 'x_a': 1.0 - ddd ** 0.9, 'x_g': 1.0 - ddd ** 0.2, 'W_r': w(ks[1]), 'W_w': w(ks[2]), 'W_k': w(ks[3]), 'W_v': w(ks[4]), 'W_a': w(ks[5]), 'W_g': w(ks[6]), 'W_out': jax.random.normal(ks[7], (D, D), jnp.float32) * s, 'b_out': jax.random.normal(ks[8], (D,), jnp.float32) * 0.01, 'gn_w': 1.0 + 0.1 * jax.random.normal(ks[9], (D,), jnp.float32), 'gn_b': 0.1 * jax.random.normal(ks[10], (D,), jnp.float32)}
    _L1_attn_all = _L1_attn_setup()
    _L1_attn_in = {k: v for k, v in _L1_attn_all.items() if k in ('x_r', 'x_w', 'x_k', 'x_v', 'x_a', 'x_g', 'W_r', 'W_w', 'W_k', 'W_v', 'W_a', 'W_g', 'W_out', 'b_out', 'gn_w', 'gn_b')}
    del _L1_attn_all

    def _L1_xattn_setup():
        import jax, jax.numpy as jnp
        import numpy as np
        BETA = 128
        NUM_HEADS = 16
        NORM = (BETA // NUM_HEADS) ** (-0.5)
        key = jax.random.key(seed)
        ks = jax.random.split(key, 6)
        B, N = (4, 256)
        D_in_q = D_in_k = D_in_v = 128
        D_out_k = D_out_v = 128
        q = jax.random.normal(ks[0], (B, N, D_in_q), dtype=jnp.float32)
        k = jax.random.normal(ks[1], (B, N, D_in_k), dtype=jnp.float32)
        v = jax.random.normal(ks[2], (B, N, D_in_v), dtype=jnp.float32)
        Wq = jax.random.normal(ks[3], (D_out_k, D_in_q), dtype=jnp.float32) * D_in_q ** (-0.5)
        Wk = jax.random.normal(ks[4], (D_out_k, D_in_k), dtype=jnp.float32) * D_in_k ** (-0.5)
        Wv = jax.random.normal(ks[5], (D_out_v, D_in_v), dtype=jnp.float32) * D_in_v ** (-0.5)
        return {'q': q, 'k': k, 'v': v, 'Wq': Wq, 'Wk': Wk, 'Wv': Wv}
    _L1_xattn_all = _L1_xattn_setup()
    _L1_xattn_in = {k: v for k, v in _L1_xattn_all.items() if k in ('Wq', 'Wk', 'Wv')}
    del _L1_xattn_all

    def _L1_ffn_setup():
        import jax, jax.numpy as jnp
        import numpy as np
        import math
        BETA = 0.9
        THRESHOLD = 1.0
        NUM_STEPS = 5
        ALPHA = 2.0

        @jax.custom_vjp
        def spike_fn(u):
            return (u > 0).astype(u.dtype)

        def _spike_fwd(u):
            return (spike_fn(u), u)

        def _spike_bwd(u, g):
            s = jnp.pi / 2.0 * ALPHA * u
            return (g * (ALPHA / 2.0) / (1.0 + s * s),)
        spike_fn.defvjp(_spike_fwd, _spike_bwd)
        key = jax.random.key(seed)
        k1, k2, k3 = jax.random.split(key, 3)
        n_embd = 128
        x = jax.random.normal(k1, (4, 256, n_embd), dtype=jnp.float32)
        W_fc = jax.random.normal(k2, (4 * n_embd, n_embd), dtype=jnp.float32) / math.sqrt(n_embd)
        W_proj = jax.random.normal(k3, (n_embd, 4 * n_embd), dtype=jnp.float32) / math.sqrt(4 * n_embd)
        return {'x': x, 'W_fc': W_fc, 'W_proj': W_proj}
    _L1_ffn_all = _L1_ffn_setup()
    _L1_ffn_in = {k: v for k, v in _L1_ffn_all.items() if k in ('W_fc', 'W_proj')}
    del _L1_ffn_all

    def _L2_attn_setup():
        import math
        import jax, jax.numpy as jnp
        import numpy as np
        B, T, D, H = (4, 256, 128, 16)
        HD = D // H

        def apply_rope(x, base=10000.0):
            _, t, _, dh = x.shape
            half = dh // 2
            inv_freq = 1.0 / base ** (jnp.arange(half, dtype=jnp.float32) / float(half))
            pos = jnp.arange(t, dtype=jnp.float32)
            angles = pos[:, None] * inv_freq[None, :]
            sin = jnp.sin(angles)[None, :, None, :]
            cos = jnp.cos(angles)[None, :, None, :]
            x1 = x[..., :half]
            x2 = x[..., half:2 * half]
            rot1 = x1 * cos - x2 * sin
            rot2 = x1 * sin + x2 * cos
            return jnp.concatenate([rot1, rot2, x[..., 2 * half:]], axis=-1)
        key = jax.random.key(seed)
        k1, k2, k3 = jax.random.split(key, 3)
        x = jax.random.normal(k1, (B, T, D), dtype=jnp.float32)
        Wqkv = jax.random.normal(k2, (D, 3 * D), dtype=jnp.float32) / math.sqrt(D)
        Wo = jax.random.normal(k3, (D, D), dtype=jnp.float32) / math.sqrt(D)
        bo = jnp.zeros((D,), dtype=jnp.float32)
        return {'x': x, 'Wqkv': Wqkv, 'Wo': Wo, 'bo': bo}
    _L2_attn_all = _L2_attn_setup()
    _L2_attn_in = {k: v for k, v in _L2_attn_all.items() if k in ('Wqkv', 'Wo', 'bo')}
    del _L2_attn_all

    def _L2_xattn_setup():
        import jax, jax.numpy as jnp
        import numpy as np
        import math
        D_MODEL = 128
        N_HEADS = 16
        HEAD_DIM = D_MODEL // N_HEADS
        TOP_K = 32
        SCALE = math.sqrt(HEAD_DIM)

        def _split_heads(t, n):
            B, L, _ = t.shape
            return t.reshape(B, L, N_HEADS, HEAD_DIM).transpose(0, 2, 1, 3)
        key = jax.random.key(seed)
        ks = jax.random.split(key, 12)
        B, S, N = (2, 256, 256)
        std = 1.0 / math.sqrt(D_MODEL)
        inp = {'x': jax.random.normal(ks[0], (B, S, D_MODEL), dtype=jnp.float32), 'knowledge_embeddings': jax.random.normal(ks[1], (B, N, D_MODEL), dtype=jnp.float32), 'Wq': jax.random.normal(ks[2], (D_MODEL, D_MODEL), dtype=jnp.float32) * std, 'bq': jnp.zeros((D_MODEL,), dtype=jnp.float32), 'Wk': jax.random.normal(ks[3], (D_MODEL, D_MODEL), dtype=jnp.float32) * std, 'bk': jnp.zeros((D_MODEL,), dtype=jnp.float32), 'Wv': jax.random.normal(ks[4], (D_MODEL, D_MODEL), dtype=jnp.float32) * std, 'bv': jnp.zeros((D_MODEL,), dtype=jnp.float32), 'Wo': jax.random.normal(ks[5], (D_MODEL, D_MODEL), dtype=jnp.float32) * std, 'bo': jnp.zeros((D_MODEL,), dtype=jnp.float32)}
        return inp
    _L2_xattn_all = _L2_xattn_setup()
    _L2_xattn_in = {k: v for k, v in _L2_xattn_all.items() if k in ('Wq', 'bq', 'Wk', 'bk', 'Wv', 'bv', 'Wo', 'bo')}
    del _L2_xattn_all

    def _L2_ffn_setup():
        import jax, jax.numpy as jnp
        import numpy as np
        EPS = 1e-08

        def _ternary_linear(x, w):
            alpha = jnp.mean(jnp.abs(w))
            w_t = jnp.sign(w) * (jnp.abs(w) > 0.5 * alpha).astype(w.dtype)
            w_q = w + jax.lax.stop_gradient(w_t - w)
            d = x.shape[-1]
            rms = jnp.sqrt(jnp.sum(x * x, axis=-1, keepdims=True)) / jnp.sqrt(jnp.asarray(d, x.dtype))
            x_norm = x / (rms + EPS)
            return jnp.einsum('bsd,fd->bsf', x_norm, w_q)
        key = jax.random.key(seed)
        k1, k2, k3 = jax.random.split(key, 3)
        d_model, d_ff = (128, 512)
        B, S = (4, 512)
        x = jax.random.normal(k1, (B, S, d_model), dtype=jnp.float32)
        w_up = jax.random.normal(k2, (d_ff, d_model), dtype=jnp.float32) * 0.02
        w_down = jax.random.normal(k3, (d_model, d_ff), dtype=jnp.float32) * 0.02
        return {'x': x, 'w_up': w_up, 'w_down': w_down}
    _L2_ffn_all = _L2_ffn_setup()
    _L2_ffn_in = {k: v for k, v in _L2_ffn_all.items() if k in ('w_up', 'w_down')}
    del _L2_ffn_all

    def _L3_attn_setup():
        import jax, jax.numpy as jnp
        import numpy as np
        D_MODEL = 128
        N_HEADS = 16
        D_K = D_MODEL // N_HEADS
        MAX_LEN = 256
        B, T = (2, 256)
        key = jax.random.key(seed)
        ks = jax.random.split(key, 10)
        s = 1.0 / np.sqrt(D_MODEL)
        inp = {'x': jax.random.normal(ks[0], (B, T, D_MODEL), dtype=jnp.float32), 'WQ': jax.random.uniform(ks[1], (D_MODEL, D_MODEL), minval=-s, maxval=s, dtype=jnp.float32), 'bQ': jax.random.uniform(ks[2], (D_MODEL,), minval=-s, maxval=s, dtype=jnp.float32), 'WK': jax.random.uniform(ks[3], (D_MODEL, D_MODEL), minval=-s, maxval=s, dtype=jnp.float32), 'bK': jax.random.uniform(ks[4], (D_MODEL,), minval=-s, maxval=s, dtype=jnp.float32), 'WV': jax.random.uniform(ks[5], (D_MODEL, D_MODEL), minval=-s, maxval=s, dtype=jnp.float32), 'bV': jax.random.uniform(ks[6], (D_MODEL,), minval=-s, maxval=s, dtype=jnp.float32), 'WO': jax.random.uniform(ks[7], (D_MODEL, D_MODEL), minval=-s, maxval=s, dtype=jnp.float32), 'bO': jax.random.uniform(ks[8], (D_MODEL,), minval=-s, maxval=s, dtype=jnp.float32), 'rel_pos_table': jax.random.normal(ks[9], (2 * MAX_LEN - 1, N_HEADS), dtype=jnp.float32)}
        return inp
    _L3_attn_all = _L3_attn_setup()
    _L3_attn_in = {k: v for k, v in _L3_attn_all.items() if k in ('WQ', 'bQ', 'WK', 'bK', 'WV', 'bV', 'WO', 'bO', 'rel_pos_table')}
    del _L3_attn_all

    def _L3_xattn_setup():
        import jax, jax.numpy as jnp
        import numpy as np
        D_MODEL = 128
        NUM_HEADS = 16
        HEAD_DIM = D_MODEL // NUM_HEADS
        key = jax.random.key(seed)
        ks = jax.random.split(key, 11)
        B, S = (2, 256)
        scale = 1.0 / np.sqrt(D_MODEL)
        inp = {'query': jax.random.normal(ks[0], (B, S, D_MODEL), jnp.float32), 'key': jax.random.normal(ks[1], (B, S, D_MODEL), jnp.float32), 'value': jax.random.normal(ks[2], (B, S, D_MODEL), jnp.float32), 'Wq': jax.random.normal(ks[3], (D_MODEL, D_MODEL), jnp.float32) * scale, 'bq': jnp.zeros((D_MODEL,), jnp.float32), 'Wk': jax.random.normal(ks[4], (D_MODEL, D_MODEL), jnp.float32) * scale, 'bk': jnp.zeros((D_MODEL,), jnp.float32), 'Wv': jax.random.normal(ks[5], (D_MODEL, D_MODEL), jnp.float32) * scale, 'bv': jnp.zeros((D_MODEL,), jnp.float32), 'Wo': jax.random.normal(ks[6], (D_MODEL, D_MODEL), jnp.float32) * scale, 'bo': jnp.zeros((D_MODEL,), jnp.float32)}
        return inp
    _L3_xattn_all = _L3_xattn_setup()
    _L3_xattn_in = {k: v for k, v in _L3_xattn_all.items() if k in ('Wq', 'bq', 'Wk', 'bk', 'Wv', 'bv', 'Wo', 'bo')}
    del _L3_xattn_all

    def _L3_ffn_setup():
        import jax, jax.numpy as jnp
        import numpy as np
        DIM = 128
        DEPTH = 2
        HEADS = 8
        DIM_HEAD = 64
        WINDOW = 64
        INNER = HEADS * DIM_HEAD
        HID = int(DIM * 4 * 2 / 3)
        B, N = (2, 1024)
        QK_SCALE = 8.0

        def shift_token(t):
            t1, t2 = jnp.split(t, 2, axis=-1)
            t2 = jnp.pad(t2, ((0, 0), (1, 0), (0, 0)))[:, :-1]
            return jnp.concatenate([t1, t2], axis=-1)

        def l2norm(t):
            return t / jnp.clip(jnp.linalg.norm(t, axis=-1, keepdims=True), 1e-12)

        def rotate_half(x):
            x1, x2 = jnp.split(x, 2, axis=-1)
            return jnp.concatenate([-x2, x1], axis=-1)

        def rotary_xpos(q, k):
            n = q.shape[-2]
            half_idx = jnp.arange(0, DIM_HEAD, 2, dtype=jnp.float32)
            inv_freq = 1.0 / 10000.0 ** (half_idx / DIM_HEAD)
            t = jnp.arange(n, dtype=jnp.float32)
            freqs = t[:, None] * inv_freq[None, :]
            freqs = jnp.concatenate([freqs, freqs], axis=-1)
            base = (half_idx + 0.4 * DIM_HEAD) / (1.4 * DIM_HEAD)
            power = (t - n // 2) / float(WINDOW // 2)
            scale = base[None, :] ** power[:, None]
            scale = jnp.concatenate([scale, scale], axis=-1)
            cos, sin = (jnp.cos(freqs), jnp.sin(freqs))
            q = q * cos * scale + rotate_half(q) * sin * scale
            k = k * cos / scale + rotate_half(k) * sin / scale
            return (q, k)

        def local_attention(q, k, v):
            b, h, n, d = q.shape
            w = n // WINDOW
            bq = q.reshape(b, h, w, WINDOW, d) * QK_SCALE
            bk = k.reshape(b, h, w, WINDOW, d)
            bv = v.reshape(b, h, w, WINDOW, d)

            def look_around(t):
                p = jnp.pad(t, ((0, 0), (0, 0), (1, 0), (0, 0), (0, 0)))
                return jnp.concatenate([p[:, :, :w], p[:, :, 1:]], axis=3)
            bk, bv = (look_around(bk), look_around(bv))
            bt = jnp.arange(n).reshape(w, WINDOW)
            btp = jnp.pad(bt, ((1, 0), (0, 0)), constant_values=-1)
            btk = jnp.concatenate([btp[:w], btp[1:]], axis=1)
            sim = jnp.einsum('bhwid,bhwjd->bhwij', bq, bk)
            i = bt[:, :, None]
            j = btk[:, None, :]
            mask = (i < j) | (i > j + WINDOW) | (j == -1)
            sim = jnp.where(mask, -jnp.finfo(sim.dtype).max, sim)
            attn = jax.nn.softmax(sim, axis=-1)
            out = jnp.einsum('bhwij,bhwjd->bhwid', attn, bv)
            return out.reshape(b, h, n, d)

        def _layer(x, wqkv, qs, ksc, wo, lg, lb, w1, b1, w2, b2):
            b, n, _ = x.shape
            h = shift_token(x)
            qkv = h @ wqkv
            q, k, v = jnp.split(qkv, 3, axis=-1)
            to_heads = lambda t: t.reshape(b, n, HEADS, DIM_HEAD).transpose(0, 2, 1, 3)
            q, k, v = (to_heads(q), to_heads(k), to_heads(v))
            q = l2norm(q) * qs
            k = l2norm(k) * ksc
            q, k = rotary_xpos(q, k)
            o = local_attention(q, k, v)
            o = o.transpose(0, 2, 1, 3).reshape(b, n, INNER)
            x = x + o @ wo
            h = shift_token(x)
            mu = h.mean(-1, keepdims=True)
            var = h.var(-1, keepdims=True)
            h = (h - mu) / jnp.sqrt(var + 1e-05) * lg + lb
            h = h @ w1 + b1
            a, g = jnp.split(h, 2, axis=-1)
            h = a * jax.nn.gelu(g, approximate=False)
            x = x + h @ w2 + b2
            return x
        key = jax.random.key(seed)
        ks = jax.random.split(key, 6)
        return {'x': jax.random.normal(ks[0], (B, N, DIM), jnp.float32), 'wqkv': jax.random.normal(ks[1], (DEPTH, DIM, 3 * INNER), jnp.float32) * 0.02, 'q_scale': jnp.ones((DEPTH, DIM_HEAD), jnp.float32), 'k_scale': jnp.ones((DEPTH, DIM_HEAD), jnp.float32), 'wo': jax.random.normal(ks[2], (DEPTH, INNER, DIM), jnp.float32) * 0.02, 'ln_g': jnp.ones((DEPTH, DIM), jnp.float32), 'ln_b': jnp.zeros((DEPTH, DIM), jnp.float32), 'w1': jax.random.normal(ks[3], (DEPTH, DIM, 2 * HID), jnp.float32) * 0.02, 'b1': jnp.zeros((DEPTH, 2 * HID), jnp.float32), 'w2': jax.random.normal(ks[4], (DEPTH, HID, DIM), jnp.float32) * 0.02, 'b2': jnp.zeros((DEPTH, DIM), jnp.float32)}
    _L3_ffn_all = _L3_ffn_setup()
    _L3_ffn_in = {k: v for k, v in _L3_ffn_all.items() if k in ('wqkv', 'q_scale', 'k_scale', 'wo', 'ln_g', 'ln_b', 'w1', 'b1', 'w2', 'b2')}
    del _L3_ffn_all
    return {'x': x, 'ctx_1024': ctx_1024, 'L0_attn_W_q': _L0_attn_in['W_q'], 'L0_attn_W_k': _L0_attn_in['W_k'], 'L0_attn_W_v': _L0_attn_in['W_v'], 'L0_attn_W_o': _L0_attn_in['W_o'], 'L0_attn_W_down_kv': _L0_attn_in['W_down_kv'], 'L0_attn_W_up_k': _L0_attn_in['W_up_k'], 'L0_attn_W_up_v': _L0_attn_in['W_up_v'], 'L0_xattn_igate_kernel': _L0_xattn_in['igate_kernel'], 'L0_xattn_igate_bias': _L0_xattn_in['igate_bias'], 'L0_xattn_fgate_kernel': _L0_xattn_in['fgate_kernel'], 'L0_xattn_fgate_bias': _L0_xattn_in['fgate_bias'], 'L0_ffn_enc_W': _L0_ffn_in['enc_W'], 'L0_ffn_enc_b': _L0_ffn_in['enc_b'], 'L0_ffn_s2c_W': _L0_ffn_in['s2c_W'], 'L0_ffn_s2c_b': _L0_ffn_in['s2c_b'], 'L0_ffn_rW1': _L0_ffn_in['rW1'], 'L0_ffn_rb1': _L0_ffn_in['rb1'], 'L0_ffn_rW2': _L0_ffn_in['rW2'], 'L0_ffn_rb2': _L0_ffn_in['rb2'], 'L0_ffn_We1': _L0_ffn_in['We1'], 'L0_ffn_be1': _L0_ffn_in['be1'], 'L0_ffn_We2': _L0_ffn_in['We2'], 'L0_ffn_be2': _L0_ffn_in['be2'], 'L0_ffn_c2s_W': _L0_ffn_in['c2s_W'], 'L0_ffn_c2s_b': _L0_ffn_in['c2s_b'], 'L0_ffn_dec_W': _L0_ffn_in['dec_W'], 'L0_ffn_dec_b': _L0_ffn_in['dec_b'], 'L0_ffn_ln_g': _L0_ffn_in['ln_g'], 'L0_ffn_ln_b': _L0_ffn_in['ln_b'], 'L1_attn_x_r': _L1_attn_in['x_r'], 'L1_attn_x_w': _L1_attn_in['x_w'], 'L1_attn_x_k': _L1_attn_in['x_k'], 'L1_attn_x_v': _L1_attn_in['x_v'], 'L1_attn_x_a': _L1_attn_in['x_a'], 'L1_attn_x_g': _L1_attn_in['x_g'], 'L1_attn_W_r': _L1_attn_in['W_r'], 'L1_attn_W_w': _L1_attn_in['W_w'], 'L1_attn_W_k': _L1_attn_in['W_k'], 'L1_attn_W_v': _L1_attn_in['W_v'], 'L1_attn_W_a': _L1_attn_in['W_a'], 'L1_attn_W_g': _L1_attn_in['W_g'], 'L1_attn_W_out': _L1_attn_in['W_out'], 'L1_attn_b_out': _L1_attn_in['b_out'], 'L1_attn_gn_w': _L1_attn_in['gn_w'], 'L1_attn_gn_b': _L1_attn_in['gn_b'], 'L1_xattn_Wq': _L1_xattn_in['Wq'], 'L1_xattn_Wk': _L1_xattn_in['Wk'], 'L1_xattn_Wv': _L1_xattn_in['Wv'], 'L1_ffn_W_fc': _L1_ffn_in['W_fc'], 'L1_ffn_W_proj': _L1_ffn_in['W_proj'], 'L2_attn_Wqkv': _L2_attn_in['Wqkv'], 'L2_attn_Wo': _L2_attn_in['Wo'], 'L2_attn_bo': _L2_attn_in['bo'], 'L2_xattn_Wq': _L2_xattn_in['Wq'], 'L2_xattn_bq': _L2_xattn_in['bq'], 'L2_xattn_Wk': _L2_xattn_in['Wk'], 'L2_xattn_bk': _L2_xattn_in['bk'], 'L2_xattn_Wv': _L2_xattn_in['Wv'], 'L2_xattn_bv': _L2_xattn_in['bv'], 'L2_xattn_Wo': _L2_xattn_in['Wo'], 'L2_xattn_bo': _L2_xattn_in['bo'], 'L2_ffn_w_up': _L2_ffn_in['w_up'], 'L2_ffn_w_down': _L2_ffn_in['w_down'], 'L3_attn_WQ': _L3_attn_in['WQ'], 'L3_attn_bQ': _L3_attn_in['bQ'], 'L3_attn_WK': _L3_attn_in['WK'], 'L3_attn_bK': _L3_attn_in['bK'], 'L3_attn_WV': _L3_attn_in['WV'], 'L3_attn_bV': _L3_attn_in['bV'], 'L3_attn_WO': _L3_attn_in['WO'], 'L3_attn_bO': _L3_attn_in['bO'], 'L3_attn_rel_pos_table': _L3_attn_in['rel_pos_table'], 'L3_xattn_Wq': _L3_xattn_in['Wq'], 'L3_xattn_bq': _L3_xattn_in['bq'], 'L3_xattn_Wk': _L3_xattn_in['Wk'], 'L3_xattn_bk': _L3_xattn_in['bk'], 'L3_xattn_Wv': _L3_xattn_in['Wv'], 'L3_xattn_bv': _L3_xattn_in['bv'], 'L3_xattn_Wo': _L3_xattn_in['Wo'], 'L3_xattn_bo': _L3_xattn_in['bo'], 'L3_ffn_wqkv': _L3_ffn_in['wqkv'], 'L3_ffn_q_scale': _L3_ffn_in['q_scale'], 'L3_ffn_k_scale': _L3_ffn_in['k_scale'], 'L3_ffn_wo': _L3_ffn_in['wo'], 'L3_ffn_ln_g': _L3_ffn_in['ln_g'], 'L3_ffn_ln_b': _L3_ffn_in['ln_b'], 'L3_ffn_w1': _L3_ffn_in['w1'], 'L3_ffn_b1': _L3_ffn_in['b1'], 'L3_ffn_w2': _L3_ffn_in['w2'], 'L3_ffn_b2': _L3_ffn_in['b2']}

def reference(x, ctx_1024, L0_attn_W_q, L0_attn_W_k, L0_attn_W_v, L0_attn_W_o, L0_attn_W_down_kv, L0_attn_W_up_k, L0_attn_W_up_v, L0_xattn_igate_kernel, L0_xattn_igate_bias, L0_xattn_fgate_kernel, L0_xattn_fgate_bias, L0_ffn_enc_W, L0_ffn_enc_b, L0_ffn_s2c_W, L0_ffn_s2c_b, L0_ffn_rW1, L0_ffn_rb1, L0_ffn_rW2, L0_ffn_rb2, L0_ffn_We1, L0_ffn_be1, L0_ffn_We2, L0_ffn_be2, L0_ffn_c2s_W, L0_ffn_c2s_b, L0_ffn_dec_W, L0_ffn_dec_b, L0_ffn_ln_g, L0_ffn_ln_b, L1_attn_x_r, L1_attn_x_w, L1_attn_x_k, L1_attn_x_v, L1_attn_x_a, L1_attn_x_g, L1_attn_W_r, L1_attn_W_w, L1_attn_W_k, L1_attn_W_v, L1_attn_W_a, L1_attn_W_g, L1_attn_W_out, L1_attn_b_out, L1_attn_gn_w, L1_attn_gn_b, L1_xattn_Wq, L1_xattn_Wk, L1_xattn_Wv, L1_ffn_W_fc, L1_ffn_W_proj, L2_attn_Wqkv, L2_attn_Wo, L2_attn_bo, L2_xattn_Wq, L2_xattn_bq, L2_xattn_Wk, L2_xattn_bk, L2_xattn_Wv, L2_xattn_bv, L2_xattn_Wo, L2_xattn_bo, L2_ffn_w_up, L2_ffn_w_down, L3_attn_WQ, L3_attn_bQ, L3_attn_WK, L3_attn_bK, L3_attn_WV, L3_attn_bV, L3_attn_WO, L3_attn_bO, L3_attn_rel_pos_table, L3_xattn_Wq, L3_xattn_bq, L3_xattn_Wk, L3_xattn_bk, L3_xattn_Wv, L3_xattn_bv, L3_xattn_Wo, L3_xattn_bo, L3_ffn_wqkv, L3_ffn_q_scale, L3_ffn_k_scale, L3_ffn_wo, L3_ffn_ln_g, L3_ffn_ln_b, L3_ffn_w1, L3_ffn_b1, L3_ffn_w2, L3_ffn_b2):
    import jax
    import jax.numpy as jnp

    def _L0_attn_ref(x, W_q, W_k, W_v, W_o, W_down_kv, W_up_k, W_up_v):
        import jax, jax.numpy as jnp
        import numpy as np
        import math
        B, S, D = (4, 256, 128)
        H = 16
        HD = D // H
        DL = 32
        LAMBDA_DECAY = 0.01
        b, s, d = x.shape
        q = x @ W_q
        k = x @ W_k
        v = x @ W_v
        latent_kv = (k + v) @ W_down_kv
        k_rec = (latent_kv @ W_up_k).reshape(b, s, H, HD).transpose(0, 2, 1, 3)
        v_rec = (latent_kv @ W_up_v).reshape(b, s, H, HD).transpose(0, 2, 1, 3)
        qh = q.reshape(b, s, H, HD).transpose(0, 2, 1, 3)
        scores = jnp.einsum('bhqd,bhkd->bhqk', qh, k_rec) / math.sqrt(d)
        t = jnp.arange(s, dtype=jnp.float32)
        decay = jnp.exp(-LAMBDA_DECAY * jnp.abs(t[:, None] - t[None, :]))
        scores = scores * decay[None, None, :, :]
        attn = jax.nn.softmax(scores, axis=-1)
        out = jnp.einsum('bhqk,bhkd->bhqd', attn, v_rec)
        out = out.transpose(0, 2, 1, 3).reshape(b, s, d)
        return out @ W_o

    def _L0_xattn_ref(q, k, v, igate_kernel, igate_bias, fgate_kernel, fgate_bias):
        import jax, jax.numpy as jnp
        import numpy as np
        EMB = 128
        NH = 8
        HD = EMB // NH
        EPS = 1e-06

        def _mlstm_head(q, k, v, ig, fg):
            S, DH = q.shape
            log_fg = jax.nn.log_sigmoid(fg)
            cs = jnp.concatenate([jnp.zeros((1, 1), q.dtype), jnp.cumsum(log_fg, axis=0)], axis=0)
            fg_mat_full = cs - cs.T
            ltr = jnp.tril(jnp.ones((S, S), bool))
            log_fg_matrix = jnp.where(ltr, fg_mat_full[1:, 1:], -jnp.inf)
            log_D = log_fg_matrix + ig.T
            max_log_D = jnp.max(log_D, axis=-1, keepdims=True)
            D = jnp.exp(log_D - max_log_D)
            qk = q @ (k.T / jnp.sqrt(jnp.asarray(DH, q.dtype)))
            C = qk * D
            normalizer = jnp.maximum(jnp.abs(C.sum(-1, keepdims=True)), jnp.exp(-max_log_D))
            return C / (normalizer + EPS) @ v
        B, S, H = q.shape
        x = jnp.concatenate([q, k, v], axis=-1)
        ig = x @ igate_kernel + igate_bias
        fg = x @ fgate_kernel + fgate_bias
        qh = q.reshape(B, S, NH, HD).swapaxes(1, 2)
        kh = k.reshape(B, S, NH, HD).swapaxes(1, 2)
        vh = v.reshape(B, S, NH, HD).swapaxes(1, 2)
        igp = ig.swapaxes(1, 2)[..., None]
        fgp = fg.swapaxes(1, 2)[..., None]
        h = jax.vmap(jax.vmap(_mlstm_head))(qh, kh, vh, igp, fgp)
        hf = h.astype(jnp.float32)
        h = (hf * jax.lax.rsqrt(jnp.mean(jnp.square(hf), axis=-1, keepdims=True) + 1e-06)).astype(h.dtype)
        return h.swapaxes(1, 2).reshape(B, S, H)

    def _L0_ffn_ref(inputs_embeds, enc_W, enc_b, s2c_W, s2c_b, rW1, rb1, rW2, rb2, We1, be1, We2, be2, c2s_W, c2s_b, dec_W, dec_b, ln_g, ln_b):
        import jax, jax.numpy as jnp
        import numpy as np
        B, S, D, H, M, E, K = (4, 256, 128, 256, 64, 8, 2)

        def _layernorm(x, g, b, eps=1e-05):
            mu = x.mean(-1, keepdims=True)
            var = ((x - mu) ** 2).mean(-1, keepdims=True)
            return (x - mu) * jax.lax.rsqrt(var + eps) * g + b

        def _forward(inputs_embeds, enc_W, enc_b, s2c_W, s2c_b, rW1, rb1, rW2, rb2, We1, be1, We2, be2, c2s_W, c2s_b, dec_W, dec_b, ln_g, ln_b):
            b, s, _ = inputs_embeds.shape
            spikes_enc = jax.nn.sigmoid(inputs_embeds @ enc_W + enc_b)
            flat = spikes_enc.reshape(b * s, H)
            cont = flat @ s2c_W + s2c_b
            logits = jnp.tanh(cont @ rW1 + rb1) @ rW2 + rb2
            probs = jax.nn.softmax(logits, axis=-1)
            topw, topi = jax.lax.top_k(probs, K)
            w = topw / topw.sum(-1, keepdims=True)
            gates = (jax.nn.one_hot(topi, E, dtype=cont.dtype) * w[..., None]).sum(1)
            h = jax.nn.relu(jnp.einsum('nm,emh->enh', cont, We1) + be1[:, None, :])
            expert_out = jnp.einsum('enh,ehm->enm', h, We2) + be2[:, None, :]
            output_flat = jnp.einsum('enm,ne->nm', expert_out, gates)
            spikes_moe = jax.nn.sigmoid(output_flat @ c2s_W + c2s_b).reshape(b, s, H)
            decoded = jax.nn.sigmoid(spikes_moe @ dec_W + dec_b)
            return _layernorm(decoded, ln_g, ln_b)
        return _forward(inputs_embeds, enc_W, enc_b, s2c_W, s2c_b, rW1, rb1, rW2, rb2, We1, be1, We2, be2, c2s_W, c2s_b, dec_W, dec_b, ln_g, ln_b)

    def _L1_attn_ref(x, x_r, x_w, x_k, x_v, x_a, x_g, W_r, W_w, W_k, W_v, W_a, W_g, W_out, b_out, gn_w, gn_b):
        import jax, jax.numpy as jnp
        import numpy as np
        B, N, D, H = (4, 512, 128, 16)
        GN_EPS = 0.00064
        b, n, d = x.shape
        prev = jnp.concatenate([jnp.zeros_like(x[:, :1]), x[:, :-1]], axis=1)
        xx = prev - x
        lin = lambda mix, W: (x + xx * mix) @ W.T
        r = jax.nn.sigmoid(lin(x_r, W_r))
        decay = jnp.exp(-jax.nn.softplus(lin(x_w, W_w)))
        k = jnp.tanh(lin(x_k, W_k))
        v = lin(x_v, W_v)
        alpha = jax.nn.sigmoid(lin(x_a, W_a))
        g = jax.nn.sigmoid(lin(x_g, W_g))
        u = alpha * k * v

        def step(state, inp):
            d_t, u_t, r_t = inp
            state = state * d_t + u_t
            return (state, r_t * state)
        inputs_tm = (jnp.swapaxes(decay, 0, 1), jnp.swapaxes(u, 0, 1), jnp.swapaxes(r, 0, 1))
        state0 = jnp.zeros((b, d), x.dtype)
        _, mixed_tm = jax.lax.scan(step, state0, inputs_tm)
        mixed = jnp.swapaxes(mixed_tm, 0, 1)
        m = mixed.reshape(b * n, H, d // H)
        mu = m.mean(-1, keepdims=True)
        var = ((m - mu) ** 2).mean(-1, keepdims=True)
        mn = ((m - mu) / jnp.sqrt(var + GN_EPS)).reshape(b, n, d)
        mn = mn * gn_w + gn_b
        return mn * g @ W_out.T + b_out

    def _L1_xattn_ref(q, k, v, Wq, Wk, Wv):
        import jax, jax.numpy as jnp
        import numpy as np
        BETA = 128
        NUM_HEADS = 16
        NORM = (BETA // NUM_HEADS) ** (-0.5)
        qp = jax.nn.relu(jnp.einsum('bnd,od->bno', q, Wq))
        kp = jax.nn.relu(jnp.einsum('bnd,od->bno', k, Wk))
        vp = jax.nn.relu(jnp.einsum('bnd,od->bno', v, Wv))
        B, N, D = qp.shape
        dh = D // NUM_HEADS
        qh = qp.reshape(B, N, NUM_HEADS, dh)
        kh = kp.reshape(B, N, NUM_HEADS, dh)
        vh = vp.reshape(B, N, NUM_HEADS, vp.shape[-1] // NUM_HEADS)
        E = NORM * jnp.einsum('bqhd,bkhd->bhqk', qh, kh)
        A = jax.nn.softmax(E, axis=-1)
        out = jnp.einsum('bhqk,bkhd->bqhd', A, vh)
        return out.reshape(B, N, -1)

    def _L1_ffn_ref(x, W_fc, W_proj):
        import jax, jax.numpy as jnp
        import numpy as np
        import math
        BETA = 0.9
        THRESHOLD = 1.0
        NUM_STEPS = 5
        ALPHA = 2.0

        @jax.custom_vjp
        def spike_fn(u):
            return (u > 0).astype(u.dtype)

        def _spike_fwd(u):
            return (spike_fn(u), u)

        def _spike_bwd(u, g):
            s = jnp.pi / 2.0 * ALPHA * u
            return (g * (ALPHA / 2.0) / (1.0 + s * s),)
        spike_fn.defvjp(_spike_fwd, _spike_bwd)
        h = jnp.square(jax.nn.relu(jnp.einsum('bsd,fd->bsf', x, W_fc)))
        y = jnp.einsum('bsf,df->bsd', h, W_proj)

        def step(mem, _):
            reset = jax.lax.stop_gradient(spike_fn(mem - THRESHOLD))
            mem_new = BETA * mem + y - reset * THRESHOLD
            spk = spike_fn(mem_new - THRESHOLD)
            return (mem_new, spk)
        mem0 = jnp.zeros_like(y)
        _, spks = jax.lax.scan(step, mem0, None, length=NUM_STEPS)
        return jnp.sum(spks, axis=0) / NUM_STEPS

    def _L2_attn_ref(x, Wqkv, Wo, bo):
        import math
        import jax, jax.numpy as jnp
        import numpy as np
        B, T, D, H = (4, 256, 128, 16)
        HD = D // H

        def apply_rope(x, base=10000.0):
            _, t, _, dh = x.shape
            half = dh // 2
            inv_freq = 1.0 / base ** (jnp.arange(half, dtype=jnp.float32) / float(half))
            pos = jnp.arange(t, dtype=jnp.float32)
            angles = pos[:, None] * inv_freq[None, :]
            sin = jnp.sin(angles)[None, :, None, :]
            cos = jnp.cos(angles)[None, :, None, :]
            x1 = x[..., :half]
            x2 = x[..., half:2 * half]
            rot1 = x1 * cos - x2 * sin
            rot2 = x1 * sin + x2 * cos
            return jnp.concatenate([rot1, rot2, x[..., 2 * half:]], axis=-1)
        b, t, d = x.shape
        qkv = x @ Wqkv
        q, k, v = jnp.split(qkv, 3, axis=-1)
        q = q.reshape(b, t, H, HD)
        k = k.reshape(b, t, H, HD)
        v = v.reshape(b, t, H, HD)
        q = apply_rope(q)
        k = apply_rope(k)
        q = q / jnp.sqrt(jnp.sum(q * q, axis=-1, keepdims=True) + 1e-06)
        k = k / jnp.sqrt(jnp.sum(k * k, axis=-1, keepdims=True) + 1e-06)
        attn = jnp.einsum('bthd,bshd->bhts', q, k) / math.sqrt(HD)
        attn = jax.nn.softmax(attn, axis=-1)
        out = jnp.einsum('bhts,bshd->bthd', attn, v).reshape(b, t, d)
        return out @ Wo + bo

    def _L2_xattn_ref(x, knowledge_embeddings, Wq, bq, Wk, bk, Wv, bv, Wo, bo):
        import jax, jax.numpy as jnp
        import numpy as np
        import math
        D_MODEL = 128
        N_HEADS = 16
        HEAD_DIM = D_MODEL // N_HEADS
        TOP_K = 32
        SCALE = math.sqrt(HEAD_DIM)

        def _split_heads(t, n):
            B, L, _ = t.shape
            return t.reshape(B, L, N_HEADS, HEAD_DIM).transpose(0, 2, 1, 3)
        B, S, _ = x.shape
        N = knowledge_embeddings.shape[1]
        Q = _split_heads(x @ Wq.T + bq, N_HEADS)
        K = _split_heads(knowledge_embeddings @ Wk.T + bk, N_HEADS)
        V = _split_heads(knowledge_embeddings @ Wv.T + bv, N_HEADS)
        scores = jnp.einsum('bhsd,bhnd->bhsn', Q, K) / SCALE
        k = min(TOP_K, N)
        topk_scores, topk_indices = jax.lax.top_k(scores, k)
        sparse_weights = jax.nn.softmax(topk_scores, axis=-1)
        sel_V = jnp.take_along_axis(V[:, :, None, :, :], topk_indices[..., None], axis=3)
        context = jnp.einsum('bhsk,bhskd->bhsd', sparse_weights, sel_V)
        context = context.transpose(0, 2, 1, 3).reshape(B, S, D_MODEL)
        return context @ Wo.T + bo

    def _L2_ffn_ref(x, w_up, w_down):
        import jax, jax.numpy as jnp
        import numpy as np
        EPS = 1e-08

        def _ternary_linear(x, w):
            alpha = jnp.mean(jnp.abs(w))
            w_t = jnp.sign(w) * (jnp.abs(w) > 0.5 * alpha).astype(w.dtype)
            w_q = w + jax.lax.stop_gradient(w_t - w)
            d = x.shape[-1]
            rms = jnp.sqrt(jnp.sum(x * x, axis=-1, keepdims=True)) / jnp.sqrt(jnp.asarray(d, x.dtype))
            x_norm = x / (rms + EPS)
            return jnp.einsum('bsd,fd->bsf', x_norm, w_q)
        h = jax.nn.gelu(_ternary_linear(x, w_up), approximate=False)
        return _ternary_linear(h, w_down)

    def _L3_attn_ref(x, WQ, bQ, WK, bK, WV, bV, WO, bO, rel_pos_table):
        import jax, jax.numpy as jnp
        import numpy as np
        D_MODEL = 128
        N_HEADS = 16
        D_K = D_MODEL // N_HEADS
        MAX_LEN = 256
        B, T = (2, 256)
        b, t, d = x.shape
        q = (x @ WQ.T + bQ).reshape(b, t, N_HEADS, D_K).transpose(0, 2, 1, 3)
        k = (x @ WK.T + bK).reshape(b, t, N_HEADS, D_K).transpose(0, 2, 1, 3)
        v = (x @ WV.T + bV).reshape(b, t, N_HEADS, D_K).transpose(0, 2, 1, 3)
        scores = jnp.einsum('bhqd,bhkd->bhqk', q, k) / jnp.sqrt(jnp.float32(D_K))
        pos = jnp.arange(t)
        rel = pos[:, None] - pos[None, :] + (MAX_LEN - 1)
        rel = jnp.clip(rel, 0, 2 * MAX_LEN - 2)
        rel_bias = rel_pos_table[rel]
        scores = scores + rel_bias.transpose(2, 0, 1)[None]
        causal = pos[None, :] <= pos[:, None]
        scores = jnp.where(causal[None, None], scores, -jnp.inf)
        attn = jax.nn.softmax(scores, axis=-1)
        out = jnp.einsum('bhqk,bhkd->bhqd', attn, v)
        out = out.transpose(0, 2, 1, 3).reshape(b, t, d)
        return out @ WO.T + bO

    def _L3_xattn_ref(query, key, value, Wq, bq, Wk, bk, Wv, bv, Wo, bo):
        import jax, jax.numpy as jnp
        import numpy as np
        D_MODEL = 128
        NUM_HEADS = 16
        HEAD_DIM = D_MODEL // NUM_HEADS
        B, S, _ = query.shape
        q = query @ Wq + bq
        k = key @ Wk + bk
        v = value @ Wv + bv
        q = q.reshape(B, S, NUM_HEADS, HEAD_DIM).transpose(0, 2, 1, 3)
        k = k.reshape(B, -1, NUM_HEADS, HEAD_DIM).transpose(0, 2, 1, 3)
        v = v.reshape(B, -1, NUM_HEADS, HEAD_DIM).transpose(0, 2, 1, 3)
        scores = jnp.einsum('bhqd,bhkd->bhqk', q, k) / jnp.sqrt(jnp.asarray(HEAD_DIM, q.dtype))
        attn = jax.nn.softmax(scores, axis=-1)
        out = jnp.einsum('bhqk,bhkd->bhqd', attn, v)
        out = out.transpose(0, 2, 1, 3).reshape(B, S, D_MODEL)
        return out @ Wo + bo

    def _L3_ffn_ref(x, wqkv, q_scale, k_scale, wo, ln_g, ln_b, w1, b1, w2, b2):
        import jax, jax.numpy as jnp
        import numpy as np
        DIM = 128
        DEPTH = 2
        HEADS = 8
        DIM_HEAD = 64
        WINDOW = 64
        INNER = HEADS * DIM_HEAD
        HID = int(DIM * 4 * 2 / 3)
        B, N = (2, 1024)
        QK_SCALE = 8.0

        def shift_token(t):
            t1, t2 = jnp.split(t, 2, axis=-1)
            t2 = jnp.pad(t2, ((0, 0), (1, 0), (0, 0)))[:, :-1]
            return jnp.concatenate([t1, t2], axis=-1)

        def l2norm(t):
            return t / jnp.clip(jnp.linalg.norm(t, axis=-1, keepdims=True), 1e-12)

        def rotate_half(x):
            x1, x2 = jnp.split(x, 2, axis=-1)
            return jnp.concatenate([-x2, x1], axis=-1)

        def rotary_xpos(q, k):
            n = q.shape[-2]
            half_idx = jnp.arange(0, DIM_HEAD, 2, dtype=jnp.float32)
            inv_freq = 1.0 / 10000.0 ** (half_idx / DIM_HEAD)
            t = jnp.arange(n, dtype=jnp.float32)
            freqs = t[:, None] * inv_freq[None, :]
            freqs = jnp.concatenate([freqs, freqs], axis=-1)
            base = (half_idx + 0.4 * DIM_HEAD) / (1.4 * DIM_HEAD)
            power = (t - n // 2) / float(WINDOW // 2)
            scale = base[None, :] ** power[:, None]
            scale = jnp.concatenate([scale, scale], axis=-1)
            cos, sin = (jnp.cos(freqs), jnp.sin(freqs))
            q = q * cos * scale + rotate_half(q) * sin * scale
            k = k * cos / scale + rotate_half(k) * sin / scale
            return (q, k)

        def local_attention(q, k, v):
            b, h, n, d = q.shape
            w = n // WINDOW
            bq = q.reshape(b, h, w, WINDOW, d) * QK_SCALE
            bk = k.reshape(b, h, w, WINDOW, d)
            bv = v.reshape(b, h, w, WINDOW, d)

            def look_around(t):
                p = jnp.pad(t, ((0, 0), (0, 0), (1, 0), (0, 0), (0, 0)))
                return jnp.concatenate([p[:, :, :w], p[:, :, 1:]], axis=3)
            bk, bv = (look_around(bk), look_around(bv))
            bt = jnp.arange(n).reshape(w, WINDOW)
            btp = jnp.pad(bt, ((1, 0), (0, 0)), constant_values=-1)
            btk = jnp.concatenate([btp[:w], btp[1:]], axis=1)
            sim = jnp.einsum('bhwid,bhwjd->bhwij', bq, bk)
            i = bt[:, :, None]
            j = btk[:, None, :]
            mask = (i < j) | (i > j + WINDOW) | (j == -1)
            sim = jnp.where(mask, -jnp.finfo(sim.dtype).max, sim)
            attn = jax.nn.softmax(sim, axis=-1)
            out = jnp.einsum('bhwij,bhwjd->bhwid', attn, bv)
            return out.reshape(b, h, n, d)

        def _layer(x, wqkv, qs, ksc, wo, lg, lb, w1, b1, w2, b2):
            b, n, _ = x.shape
            h = shift_token(x)
            qkv = h @ wqkv
            q, k, v = jnp.split(qkv, 3, axis=-1)
            to_heads = lambda t: t.reshape(b, n, HEADS, DIM_HEAD).transpose(0, 2, 1, 3)
            q, k, v = (to_heads(q), to_heads(k), to_heads(v))
            q = l2norm(q) * qs
            k = l2norm(k) * ksc
            q, k = rotary_xpos(q, k)
            o = local_attention(q, k, v)
            o = o.transpose(0, 2, 1, 3).reshape(b, n, INNER)
            x = x + o @ wo
            h = shift_token(x)
            mu = h.mean(-1, keepdims=True)
            var = h.var(-1, keepdims=True)
            h = (h - mu) / jnp.sqrt(var + 1e-05) * lg + lb
            h = h @ w1 + b1
            a, g = jnp.split(h, 2, axis=-1)
            h = a * jax.nn.gelu(g, approximate=False)
            x = x + h @ w2 + b2
            return x
        for l in range(DEPTH):
            x = _layer(x, wqkv[l], q_scale[l], k_scale[l], wo[l], ln_g[l], ln_b[l], w1[l], b1[l], w2[l], b2[l])
        return x
    x = x + _L0_attn_ref(_layernorm(x, axis=-1), L0_attn_W_q, L0_attn_W_k, L0_attn_W_v, L0_attn_W_o, L0_attn_W_down_kv, L0_attn_W_up_k, L0_attn_W_up_v)
    x = x + _L0_xattn_ref(_layernorm(x, axis=-1), ctx_1024, ctx_1024, L0_xattn_igate_kernel, L0_xattn_igate_bias, L0_xattn_fgate_kernel, L0_xattn_fgate_bias)
    x = x + _L0_ffn_ref(_layernorm(x, axis=-1), L0_ffn_enc_W, L0_ffn_enc_b, L0_ffn_s2c_W, L0_ffn_s2c_b, L0_ffn_rW1, L0_ffn_rb1, L0_ffn_rW2, L0_ffn_rb2, L0_ffn_We1, L0_ffn_be1, L0_ffn_We2, L0_ffn_be2, L0_ffn_c2s_W, L0_ffn_c2s_b, L0_ffn_dec_W, L0_ffn_dec_b, L0_ffn_ln_g, L0_ffn_ln_b)
    x = x + _L1_attn_ref(_layernorm(x, axis=-1), L1_attn_x_r, L1_attn_x_w, L1_attn_x_k, L1_attn_x_v, L1_attn_x_a, L1_attn_x_g, L1_attn_W_r, L1_attn_W_w, L1_attn_W_k, L1_attn_W_v, L1_attn_W_a, L1_attn_W_g, L1_attn_W_out, L1_attn_b_out, L1_attn_gn_w, L1_attn_gn_b)
    x = x + _L1_xattn_ref(_layernorm(x, axis=-1), ctx_1024, ctx_1024, L1_xattn_Wq, L1_xattn_Wk, L1_xattn_Wv)
    x = x + _L1_ffn_ref(_layernorm(x, axis=-1), L1_ffn_W_fc, L1_ffn_W_proj)
    x = x + _L2_attn_ref(_layernorm(x, axis=-1), L2_attn_Wqkv, L2_attn_Wo, L2_attn_bo)
    x = x + _L2_xattn_ref(_layernorm(x, axis=-1), ctx_1024, L2_xattn_Wq, L2_xattn_bq, L2_xattn_Wk, L2_xattn_bk, L2_xattn_Wv, L2_xattn_bv, L2_xattn_Wo, L2_xattn_bo)
    x = x + _L2_ffn_ref(_layernorm(x, axis=-1), L2_ffn_w_up, L2_ffn_w_down)
    x = x + _L3_attn_ref(_layernorm(x, axis=-1), L3_attn_WQ, L3_attn_bQ, L3_attn_WK, L3_attn_bK, L3_attn_WV, L3_attn_bV, L3_attn_WO, L3_attn_bO, L3_attn_rel_pos_table)
    x = x + _L3_xattn_ref(_layernorm(x, axis=-1), ctx_1024, ctx_1024, L3_xattn_Wq, L3_xattn_bq, L3_xattn_Wk, L3_xattn_bk, L3_xattn_Wv, L3_xattn_bv, L3_xattn_Wo, L3_xattn_bo)
    x = x + _L3_ffn_ref(_layernorm(x, axis=-1), L3_ffn_wqkv, L3_ffn_q_scale, L3_ffn_k_scale, L3_ffn_wo, L3_ffn_ln_g, L3_ffn_ln_b, L3_ffn_w1, L3_ffn_b1, L3_ffn_w2, L3_ffn_b2)
    return x

_drawn_inputs = setup_inputs


def setup_inputs(seed=0):
    import zlib

    import numpy as np

    out = dict(_drawn_inputs(seed))
    spreads = {'L0_ffn_enc_b': (0.0, 0.8),
     'L0_ffn_s2c_b': (0.0, 0.8),
     'L0_ffn_rb1': (0.0, 0.8),
     'L0_ffn_rb2': (0.0, 0.8),
     'L0_ffn_be1': (0.0, 0.8),
     'L0_ffn_be2': (0.0, 0.8),
     'L0_ffn_c2s_b': (0.0, 0.304),
     'L0_ffn_dec_b': (0.0, 0.1),
     'L0_ffn_ln_g': (1.0, 0.2),
     'L0_ffn_ln_b': (0.0, 0.1),
     'L2_attn_bo': (0.0, 0.1),
     'L2_xattn_bq': (0.0, 0.528),
     'L2_xattn_bk': (0.0, 2.0),
     'L2_xattn_bv': (0.0, 0.1),
     'L2_xattn_bo': (0.0, 0.1),
     'L3_xattn_bq': (0.0, 2.0),
     'L3_xattn_bk': (0.0, 2.0),
     'L3_xattn_bv': (0.0, 0.8),
     'L3_xattn_bo': (0.0, 0.8),
     'L3_ffn_q_scale': (1.0, 0.6),
     'L3_ffn_k_scale': (1.0, 0.6),
     'L3_ffn_ln_g': (1.0, 0.6),
     'L3_ffn_ln_b': (0.0, 0.8),
     'L3_ffn_b1': (0.0, 0.8),
     'L3_ffn_b2': (0.0, 0.8)}
    factors = {'L0_xattn_igate_bias': 64.0,
     'L0_xattn_fgate_kernel': 6.364,
     'L0_ffn_enc_W': 8.0,
     'L0_ffn_s2c_W': 8.0,
     'L0_ffn_rW1': 8.0,
     'L0_ffn_rW2': 8.0,
     'L0_ffn_We1': 8.0,
     'L0_ffn_We2': 8.0,
     'L0_ffn_c2s_W': 8.0,
     'L1_attn_x_r': 3.125,
     'L1_attn_x_w': 2.706,
     'L1_attn_x_g': 2.754,
     'L1_attn_b_out': 7.459,
     'L3_attn_WQ': 8.0,
     'L3_attn_bQ': 8.0,
     'L3_attn_WK': 8.0,
     'L3_attn_bK': 64.0,
     'L3_attn_WV': 4.284,
     'L3_attn_bV': 8.0,
     'L3_attn_WO': 4.069,
     'L3_attn_bO': 8.0,
     'L3_attn_rel_pos_table': 8.0,
     'L3_xattn_Wq': 4.875,
     'L3_xattn_Wk': 4.809,
     'L3_ffn_wqkv': 8.0,
     'L3_ffn_wo': 8.0,
     'L3_ffn_w1': 8.0,
     'L3_ffn_w2': 8.0}
    for name, (base, spread) in spreads.items():
        noise = np.random.default_rng([zlib.crc32(name.encode()), seed]).standard_normal(out[name].shape)
        drawn = base * np.exp(spread * noise) if base else spread * noise
        out[name] = jnp.asarray(drawn.astype(out[name].dtype))
    for name, factor in factors.items():
        out[name] = (out[name] * factor).astype(out[name].dtype)
    return out
```

```python
from contextlib import ExitStack

import concourse.bass as bass
from concourse import mybir

F32 = mybir.dt.float32
ALU = mybir.AluOpType
ACT = mybir.ActivationFunctionType
AX = mybir.AxisListType.X

P = 128
NSEQ, SEQ, D = 16, 64, 128
TOK = NSEQ * SEQ
T = TOK // P
LN_EPS = 1e-5
MASKED = -1e30


STAGES = ("l0a", "l0x", "l0f", "l1a", "l1x", "l1f", "l2a", "l2x", "l2f", "l3a", "l3x", "l3f", "l3g", "l3h")


EARLY = ("0a", "0x", "0f", "1")


def per_stage(**counts):
    return [counts.get(n, counts.get("rest", 0)) for n in STAGES]


SIGNALS = {
    "stats": per_stage(l0f=2 * T, rest=T),
    "moments": per_stage(l0f=2 * T, rest=T),
    "var": per_stage(rest=1),
    "rstd": per_stage(rest=1),
    "xn": per_stage(l0f=2 * T, rest=T),
    "keys_pool": per_stage(l0a=T, l0x=T, l1x=T, l2a=T, l2x=T, l3a=T, l3x=T),
    "keys_dve": per_stage(l0a=T, l0x=T, l1x=T, l2a=T, l2x=T, l3a=T, l3x=T),
    "top": per_stage(l0a=T, l1x=T, l2x=T, l3a=T, l3x=T, l3g=T, l3h=T),
    "rden": per_stage(l0a=T, l1x=T, l2a=T, l2x=T, l3a=T, l3x=T, l3g=T, l3h=T),
    "less": per_stage(l0a=T, l0x=T, l0f=1, l2x=T, l3a=T, l3g=T, l3h=T),
    "exp": per_stage(l0a=T, l0f=1, l1x=T, l2x=T, l3a=T, l3x=T, l3g=T, l3h=T),
    "b_out": per_stage(l1a=1, l2a=1, l2x=1, l3a=1, l3x=1),
}


class PsumBook:

    def __init__(self, rings):
        self.rings = rings
        self.turn = {r: 0 for r in rings}
        self.full = {}
        self.read = {}
        self.record = {}

    def place(self, name, ring, fulls, reads):
        slots = self.rings[ring]
        slot = slots[self.turn[ring] % len(slots)]
        self.turn[ring] += 1
        before, base = self.read.get(slot, 0), self.full.get(slot, 0)
        self.read[slot], self.full[slot] = before + reads, base + fulls
        assert name not in self.record, name
        self.record[name] = (slot, base, fulls, before + reads)
        return slot, before

    def whole(self, name, part=None):
        slot, base, fulls, _ = self.record[name]
        return slot, base + (fulls if part is None else part + 1)

    def done(self, name):
        slot, _, _, read = self.record[name]
        return slot, read


def build(nc, dram, where, out):
    with ExitStack() as ctx:
        def sb(name, shape):
            return ctx.enter_context(nc.sbuf_tensor(name, shape, F32))

        class Sems(dict):
            def __missing__(self, name):
                self[name] = ctx.enter_context(nc.semaphore(name.replace(".", "_")))
                return self[name]

        sem = Sems()

        def at(n, part, value):
            counts = SIGNALS[part]
            return sum(counts[:STAGES.index(n)]) + value

        psum = ctx.enter_context(nc.psum_tensor("psum", [P, 8, 512], F32))
        slots = {"a0": psum[:, 0:2, :], "a1": psum[:, 2:4, :], "a2": psum[:, 4:6, :],
                 "b0": psum[:, 6:7, :], "b1": psum[:, 7:8, :]}
        flat = {k: v.rearrange("p a b -> p (a b)") for k, v in slots.items()}
        book = PsumBook({"A": ["a0", "a1", "a2"], "B": ["b0", "b1"]})

        packs = list(dict.fromkeys(w[0] for w in where.values()))
        width = {g: dram[g].shape[1] for g in packs}
        packed = {g: sb("w_" + g, [P, width[g]]) for g in ("c", "2", "3")}
        early = sb("w_early", [P, max(sum(width[g] for g in EARLY), width["4"])])
        for i, g in enumerate(EARLY):
            start = sum(width[h] for h in EARLY[:i])
            packed[g] = early[:, start:start + width[g]]
        packed["4"] = early[:, 0:width["4"]]

        def W(name):
            g, c, rows, cols = where[name]
            return packed[g][0:rows, c:c + cols]

        def Wk(name, k):
            return W(name).rearrange("p (k n) -> p k n", k=k)

        def weights(eng, g):
            eng.wait_ge(sem["pack." + g], 16)

        def fill(pe, name, ring="A", fulls=1, reads=1):
            slot, before = book.place(name, ring, fulls, reads)
            if before:
                pe.wait_ge(sem["read." + slot], before)
            return flat[slot]

        def full(name):
            return sem["full." + book.record[name][0]]

        def read(name):
            return sem["read." + book.record[name][0]]

        def wait_full(eng, name, part=None):
            slot, value = book.whole(name, part)
            eng.wait_ge(sem["full." + slot], value)
            return flat[slot]

        def wait_read(eng, name):
            slot, value = book.done(name)
            eng.wait_ge(sem["read." + slot], value)

        x_res = sb("x_res", [P, T, D])
        xn = sb("xn", [P, T, D])
        xnT = sb("xnT", [P, TOK])
        ctxT = sb("ctxT", [P, TOK])
        qT = sb("qT", [P, TOK])
        kT = sb("kT", [P, TOK])
        kcT = sb("kcT", [P, TOK])
        keys = [sb(f"keys{i}", [P, 16, P]) for i in range(2)]
        prob = [sb(f"prob{i}", [P, 1024]) for i in range(2)]
        probT = [sb(f"probT{i}", [P, 1024]) for i in range(2)]
        v_self = sb("v_self", [P, NSEQ, 8, 18])
        v_ctx = sb("v_ctx", [P, NSEQ, 8, 18])
        heads_out = [sb(f"heads_out{i}", [P, D]) for i in range(2)]
        attnT = [sb(f"attnT{i}", [P, D]) for i in range(2)]
        bn = sb("bn", [P, T, 6])
        mv = sb("mv", [P, T, 2])
        var_eps = sb("var_eps", [P, T])
        rstd = sb("rstd", [P, T])
        minus_half = sb("minus_half", [P, T])
        top = [sb(f"top{i}", [P, 16]) for i in range(2)]
        rden = [sb(f"rden{i}", [P, 16]) for i in range(2)]

        def halves(mem):
            return [mem[:, 0:512], mem[:, 512:1024]]


        def ln_vector(dve, n, before, src=x_res, dst=xn):
            for t in range(T):
                before(dve, t)
                nc.vector.bn_stats(bn[:, t, :], src[:, t, :]).then_inc(sem["stats"], 1)
            for t in range(T):
                dve.wait_ge(sem["stats"], at(n, "stats", t + 1))
                nc.vector.bn_aggr(mv[:, t, :], bn[:, t, :]).then_inc(sem["moments"], 1)
            dve.wait_ge(sem["rstd"], at(n, "rstd", 1))
            dve.wait_ge(sem["moments"], at(n, "moments", T))
            for t in range(T):
                nc.vector.tensor_scalar(dst[:, t, :], src[:, t, :], mv[:, t, 0:1], rstd[:, t:t + 1],
                                        ALU.subtract, ALU.mult).then_inc(sem["xn"], 1)

        def ln_pool(pool, n):
            pool.wait_ge(sem["moments"], at(n, "moments", T))
            nc.gpsimd.tensor_scalar(var_eps[:, :], mv[:, :, 1], LN_EPS, None, ALU.add).then_inc(sem["var"], 1)
            pool.wait_ge(sem["var"], at(n, "var", 1))
            nc.gpsimd.tensor_tensor(rstd[:, :], var_eps[:, :], minus_half[:, :], ALU.pow).then_inc(sem["rstd"], 1)

        def tiles_T_tensor(pe, name, src, ready, before=0):
            mem = fill(pe, name, fulls=2, reads=2)
            for t in range(T):
                pe.wait_ge(sem[ready], before + t + 1)
                mm = nc.tensor.transpose(mem[:, t * P:(t + 1) * P], src[:, t, :], W("ident"))
                if t % 4 == 3:
                    mm.then_inc(full(name), 1)

        def copy_half_scalar(act, name, dst):
            mem = wait_full(act, name, 0)
            nc.scalar.copy(dst[:, 0:512], mem[:, 0:512]).then_inc(read(name), 1)

        def copy_half_vector(dve, name, dst):
            mem = wait_full(dve, name, 1)
            nc.vector.tensor_copy(dst[:, 512:1024], mem[:, 512:1024]).then_inc(read(name), 1)


        def project_tensor(pe, name, terms, rows=P, reads=2):
            mem = fill(pe, name, fulls=2, reads=reads)
            for half in range(2):
                for i, (w, src) in enumerate(terms):
                    mm = nc.tensor.matmul(mem[0:rows, 512 * half:512 * half + 512], w, src[:, 512 * half:512 * half + 512],
                                          start=i == 0, stop=i == len(terms) - 1)
                mm.then_inc(full(name), 1)

        def values_tensor(pe, name, w, srcT):
            mem = fill(pe, name, fulls=1, reads=2)
            wp = w.rearrange("p (a h f) -> p h a f", h=2, f=8)
            for b in range(NSEQ):
                for h in range(2):
                    mm = nc.tensor.matmul(mem[64 * h:64 * h + 64, 64 * b:64 * b + 64], srcT[:, 64 * b:64 * b + 64],
                                          wp[:, h], start=True, stop=True)
            mm.then_inc(full(name), 1)

        def values_copy(eng, name, dst, h, relu=False):
            mem = wait_full(eng, name)
            src = mem[64 * h:64 * h + 64, :].rearrange("p (b a f) -> p b a f", b=NSEQ, f=8)
            to = dst[64 * h:64 * h + 64, :, :, 8 * h:8 * h + 8]
            if h == 0:
                nc.scalar.activation(to, src, ACT.Relu if relu else ACT.Copy).then_inc(read(name), 1)
            elif relu:
                nc.vector.tensor_scalar(to, src, 0.0, None, ALU.max).then_inc(read(name), 1)
            else:
                nc.vector.tensor_copy(to, src).then_inc(read(name), 1)


        POOL_HEADS = 10

        def spread(eng, ops, a, t, lo, hi, who):
            n, H = a["n"], a["heads"]
            lo, hi = lo * H // 16, hi * H // 16
            if t == 0:
                a["k_ready"](eng)
            if t >= 2:
                wait_full(eng, f"{n}.s{t - 2}")
            elif "before_keys" in a:
                a["before_keys"](eng, t)
            kt = a["k"][:, t * P:(t + 1) * P].rearrange("p (o k) -> p o k", o=1).broadcast_to([P, hi - lo, P])
            mask = W("head_mask" if H == 16 else "head_mask8")[:, lo:hi].rearrange("p (h o) -> p h o", o=1)
            ops.tensor_tensor(keys[t % 2][:, lo:hi, :], kt, mask.broadcast_to([P, hi - lo, P]), ALU.mult)\
               .then_inc(sem["keys_" + who], 1)

        def scores_tensor(pe, a, t):
            n, H = a["n"], a["heads"]
            if t == 0:
                a["q_ready"](pe)
            pe.wait_ge(sem["keys_pool"], at(n, "keys_pool", t + 1))
            pe.wait_ge(sem["keys_dve"], at(n, "keys_dve", t + 1))
            mem = fill(pe, f"{n}.s{t}")
            for g in range(H // 8):
                for b in range(2):
                    mm = nc.tensor.matmul(mem[64 * b:64 * b + 64, 512 * g:512 * g + 512],
                                          a["q"][:, t * P + 64 * b:t * P + 64 * b + 64],
                                          keys[t % 2][:, 8 * g:8 * g + 8, 64 * b:64 * b + 64], start=True, stop=True)
            mm.then_inc(full(f"{n}.s{t}"), 1)

        def transposes_tensor(pe, a, t):
            n, pairs = a["n"], a["heads"] // 2
            a["prob_ready"](pe, t)
            parts = a["heads"] // 8
            mem = fill(pe, f"{n}.t{t}", a.get("t_ring", "A"), fulls=parts, reads=parts)
            for p in range(pairs):
                mm = nc.tensor.transpose(mem[:, p * P:(p + 1) * P], prob[t % 2][:, p * P:(p + 1) * P], W("ident"))
                if p % 4 == 3:
                    mm.then_inc(full(f"{n}.t{t}"), 1)

        def outputs_tensor(pe, a, t):
            n, pairs = a["n"], a["heads"] // 2
            if t == 0:
                a["v_ready"](pe)
            wait_read(pe, f"{n}.t{t}")
            w = a["v"].shape[3]
            mem = fill(pe, f"{n}.o{t}", "B")
            for p in range(pairs):
                for b in range(2):
                    mm = nc.tensor.matmul(mem[64 * b:64 * b + 64, w * p:w * p + w],
                                          probT[t % 2][:, p * P + 64 * b:p * P + 64 * b + 64],
                                          a["v"][:, 2 * t + b, p, :], start=True, stop=True)
            mm.then_inc(full(f"{n}.o{t}"), 1)

        def heads_T_tensor(pe, a, t):
            n = a["n"]
            wait_read(pe, f"{n}.o{t}")
            mem = fill(pe, f"{n}.ot{t}", "B")
            nc.tensor.transpose(mem[:, 0:P], heads_out[t % 2][:, :], W("ident")).then_inc(full(f"{n}.ot{t}"), 1)

        def out_tensor(pe, a, t):
            n = a["n"]
            wait_read(pe, f"{n}.ot{t}")
            mem = fill(pe, f"{n}.y{t}", "B")
            nc.tensor.matmul(mem[:, 0:P], attnT[t % 2][:, :], W(a["wo"]), start=True, stop=True)\
              .then_inc(full(f"{n}.y{t}"), 1)

        def attention_tensor(pe, a):
            scores_tensor(pe, a, 0)
            for t in range(T + 3):
                if t + 1 < T:
                    scores_tensor(pe, a, t + 1)
                if 1 <= t <= T:
                    outputs_tensor(pe, a, t - 1)
                if t < T:
                    transposes_tensor(pe, a, t)
                if a.get("wo"):
                    if 2 <= t <= T + 1:
                        heads_T_tensor(pe, a, t - 2)
                    if t >= 3:
                        out_tensor(pe, a, t - 3)

        def max_vector(dve, src, a, t):
            n, H = a["n"], a["heads"]
            if t >= 2:
                wait_read_or(dve, a, t - 2)
            nc.vector.tensor_reduce(top[t % 2][:, 0:H], src.rearrange("p (h k) -> p h k", k=SEQ), AX, ALU.max)\
              .then_inc(sem["top"], 1)
            dve.wait_ge(sem["top"], at(n, "top", t + 1))

        def wait_read_or(eng, a, t):
            a["less_done"](eng, t)

        def softmax_vector(dve, a, t):
            n, H, kind = a["n"], a["heads"], a["kind"]
            s = f"{n}.s{t}"
            mem = wait_full(dve, s)
            if t >= 2:
                wait_full(dve, f"{n}.t{t - 2}")
            three = lambda x: x.rearrange("p (h k) -> p h k", k=SEQ)
            pr = three(prob[t % 2][:, :])
            if kind == "decay":
                d = W("decay").rearrange("p (o k) -> p o k", o=1).broadcast_to([P, H, SEQ])
                nc.vector.tensor_tensor(pr, three(mem), d, ALU.mult).then_inc(read(s), 1)
                wait_read(dve, s)
                src = prob[t % 2][:, :]
            elif kind == "bias":
                nc.vector.scalar_tensor_tensor(out=prob[t % 2][:, :], in0=mem, scalar=a["scale"],
                                               in1=rel_bias[:, :], op0=ALU.mult, op1=ALU.add).then_inc(read(s), 1)
                wait_read(dve, s)
                src = prob[t % 2][:, :]
            else:
                src = mem
            max_vector(dve, src, a, t)
            tb = top[t % 2][:, 0:H].rearrange("p (h o) -> p h o", o=1).broadcast_to([P, H, SEQ])
            nc.vector.tensor_tensor(pr, three(src), tb, ALU.subtract)\
              .then_inc(read(s) if kind == "plain" else sem["less"], 1)

        def normalise_vector(dve, a, t):
            n, pairs = a["n"], a["heads"] // 2
            o = f"{n}.o{t}"
            mem = wait_full(dve, o)
            v = mem[:, 0:18 * pairs].rearrange("p (a w) -> p a w", w=18)
            rd = rden[t % 2][:, :].rearrange("p (a h) -> p a h", h=2)
            if t >= 2:
                wait_read(dve, f"{n}.o{t - 2}")
                if a.get("wo"):
                    wait_full(dve, f"{n}.ot{t - 2}")
            nc.vector.reciprocal(rd, v[:, :, 16:18]).then_inc(sem["rden"], 1)
            dve.wait_ge(sem["rden"], at(n, "rden", t + 1))
            ho = heads_out[t % 2][:, :].rearrange("p (a h f) -> p a h f", h=2, f=8)
            num = v[:, :, 0:16].rearrange("p a (h f) -> p a h f", h=2)
            rb = rd.rearrange("p a (h o) -> p a h o", o=1).broadcast_to([P, pairs, 2, 8])
            nc.vector.tensor_tensor(ho, num, rb, ALU.mult).then_inc(read(o), 1)
            if not a.get("wo"):
                wait_read(dve, o)
                nc.vector.tensor_tensor(x_res[:, t, :], x_res[:, t, :], heads_out[t % 2][:, :], ALU.add)\
                  .then_inc(sem[n + ".x"], 1)
                dve.wait_ge(sem[n + ".x"], t + 1)

        def residual_vector(dve, a, t):
            y = f"{a['n']}.y{t}"
            mem = wait_full(dve, y)
            if a.get("bo") and t == 0:
                dve.wait_ge(sem["b_out"], at(a["n"], "b_out", 1))
            nc.vector.tensor_tensor(x_res[:, t, :], mem[:, 0:P], x_res[:, t, :], ALU.add).then_inc(read(y), 1)

        def attention_vector(dve, a):
            spread(dve, nc.vector, a, 0, POOL_HEADS, 16, "dve")
            spread(dve, nc.vector, a, 1, POOL_HEADS, 16, "dve")
            for t in range(T + 4):
                if t < T:
                    a.get("softmax", softmax_vector)(dve, a, t)
                if t + 2 < T:
                    spread(dve, nc.vector, a, t + 2, POOL_HEADS, 16, "dve")
                if 2 <= t <= T + 1:
                    a.get("normalise", normalise_vector)(dve, a, t - 2)
                if a.get("wo") and t >= 4:
                    residual_vector(dve, a, t - 4)

        def attention_scalar(act, a):
            n = a["n"]
            for t in range(T + 3):
                if a.get("copy") and t == 0:
                    a["copy"](act, a, 0)
                if a.get("copy") and t + 1 < T:
                    a["copy"](act, a, t + 1)
                if t < T:
                    a["less_done"](act, t)
                    w = 64 * a["heads"]
                    if a["kind"] == "unit":
                        if t >= 2:
                            wait_full(act, f"{n}.t{t - 2}")
                        mem = wait_full(act, f"{n}.s{t}")
                        nc.scalar.activation(prob[t % 2][:, 0:w], mem[:, 0:w], ACT.Exp, scale=a["scale"])\
                          .then_inc(read(f"{n}.s{t}"), 1)
                    else:
                        nc.scalar.activation(prob[t % 2][:, 0:w], prob[t % 2][:, 0:w], ACT.Exp,
                                             scale=1.0 if a["kind"] in ("decay", "bias", "mlstm") else a["scale"])\
                          .then_inc(sem["exp"], 1)
                if 1 <= t <= T:
                    u = t - 1
                    if u >= 2:
                        wait_full(act, f"{n}.o{u - 2}")
                    w = 32 * a["heads"]
                    for half in range(2):
                        mem = wait_full(act, f"{n}.t{u}", half)
                        nc.scalar.copy(probT[u % 2][:, w * half:w * half + w], mem[:, w * half:w * half + w])\
                          .then_inc(read(f"{n}.t{u}"), 1)
                if a.get("wo") and t >= 3:
                    u = t - 3
                    if u >= 2:
                        wait_full(act, f"{n}.y{u - 2}")
                    mem = wait_full(act, f"{n}.ot{u}")
                    if a.get("bv"):
                        nc.scalar.activation(attnT[u % 2][:, :], mem[:, 0:P], ACT.Identity, bias=W(a["bv"]))\
                          .then_inc(read(f"{n}.ot{u}"), 1)
                    else:
                        nc.scalar.copy(attnT[u % 2][:, :], mem[:, 0:P]).then_inc(read(f"{n}.ot{u}"), 1)

        def attention_pool(pool, a):
            for t in range(T):
                spread(pool, nc.gpsimd, a, t, 0, POOL_HEADS, "pool")

        def residual_ready(a):
            if a.get("wo"):
                return lambda eng, t: wait_read(eng, f"{a['n']}.y{t}")
            return lambda eng, t: eng.wait_ge(sem[a["n"] + ".x"], t + 1)

        def attention(n, kind, scale=1.0, heads=16, **more):
            a = dict(n=n, kind=kind, scale=scale, heads=heads, **more)
            if kind == "plain":
                a["less_done"] = lambda eng, t: wait_read(eng, f"{n}.s{t}")
            elif kind == "unit":
                a["less_done"] = lambda eng, t: None
            else:
                a["less_done"] = lambda eng, t: eng.wait_ge(sem["less"], at(n, "less", t + 1))
            if kind == "unit":
                a["prob_ready"] = lambda eng, t: wait_read(eng, f"{n}.s{t}")
            else:
                a["prob_ready"] = lambda eng, t: eng.wait_ge(sem["exp"], at(n, "exp", t + 1))
            return a


        VALUES_SET = 12
        L0A = attention("l0a", "decay", wo="L0_attn_W_o", q=qT, k=kT, v=v_self,
                        before_keys=lambda eng, t: eng.wait_ge(sem["lstm_values"], 2),
                        q_ready=lambda eng: wait_read(eng, "l0a.q"), k_ready=lambda eng: wait_read(eng, "l0a.k"),
                        v_ready=lambda eng: wait_read(eng, "l0a.v"))
        scr = sb("scratch", [P, 12, 1024])
        kvT, latT = scr[:, 0, :], scr[0:32, 8, :]

        def l0a_tensor(pe):
            n = "l0a"
            tiles_T_tensor(pe, n + ".T", xn, "xn", at(n, "xn", 0))
            wait_read(pe, n + ".T")
            project_tensor(pe, n + ".kv", [(W("L0_attn_W_k"), xnT), (W("L0_attn_W_v"), xnT)])
            project_tensor(pe, n + ".q", [(W("L0_attn_W_q"), xnT)])
            wait_read(pe, n + ".kv")
            project_tensor(pe, n + ".lat", [(W("L0_attn_W_down_kv"), kvT)], rows=32)
            wait_read(pe, n + ".lat")
            project_tensor(pe, n + ".k", [(W("L0_attn_W_up_k"), latT)])
            values_tensor(pe, n + ".v", W("L0_attn_W_up_v"), latT)
            attention_tensor(pe, L0A)

        def l0a_vector(dve):
            n = "l0a"
            dve.wait_ge(sem["x_loaded"], 16)
            ln_vector(dve, n, lambda eng, t: None)
            copy_half_vector(dve, n + ".T", xnT)
            copy_half_vector(dve, n + ".kv", kvT)
            copy_half_vector(dve, n + ".q", qT)
            mem = wait_full(dve, n + ".lat", 1)
            nc.vector.tensor_copy(latT[:, 512:], mem[0:32, 512:]).then_inc(read(n + ".lat"), 1)
            copy_half_vector(dve, n + ".k", kT)
            dve.wait_ge(sem["values_set"], VALUES_SET)
            values_copy(dve, n + ".v", v_self, 1)
            attention_vector(dve, L0A)

        def l0a_scalar(act):
            n = "l0a"
            copy_half_scalar(act, n + ".T", xnT)
            copy_half_scalar(act, n + ".kv", kvT)
            copy_half_scalar(act, n + ".q", qT)
            mem = wait_full(act, n + ".lat", 0)
            nc.scalar.copy(latT[:, 0:512], mem[0:32, 0:512]).then_inc(read(n + ".lat"), 1)
            copy_half_scalar(act, n + ".k", kT)
            act.wait_ge(sem["values_set"], VALUES_SET)
            values_copy(act, n + ".v", v_self, 0)
            attention_scalar(act, L0A)

        def l0a_pool(pool):
            ln_pool(pool, "l0a")
            attention_pool(pool, L0A)



        links = {}

        def link(eng, name, ins):
            links[name] = links.get(name, 0) + 1
            ins.then_inc(sem[name], 1)
            eng.wait_ge(sem[name], links[name])

        newton_t = sb("newton_t", [P, 256])
        newton_u = sb("newton_u", [P, 256])

        def rsqrt_vector(dve, n, x, y, w):
            t, u = newton_t[:, 0:w], newton_u[:, 0:w]
            U32, I32 = mybir.dt.uint32, mybir.dt.int32
            link(dve, n, nc.vector.tensor_scalar(t.bitcast(U32), x.bitcast(U32), 1, None, ALU.logical_shift_right))
            link(dve, n, nc.vector.tensor_scalar(y.bitcast(I32), t.bitcast(I32), -1.0, float(0x5F3759DF), ALU.mult, ALU.add))
            for _ in range(3):
                link(dve, n, nc.vector.tensor_tensor(t, y, y, ALU.mult))
                link(dve, n, nc.vector.scalar_tensor_tensor(out=u, in0=t, scalar=-0.5, in1=x, op0=ALU.mult, op1=ALU.mult))
                link(dve, n, nc.vector.scalar_tensor_tensor(out=y, in0=u, scalar=1.5, in1=y, op0=ALU.add, op1=ALU.mult))


        ctx_tok = scr[:, 11, :].rearrange("p (t d) -> p t d", t=T)
        ctx_keys = keys[0]
        v_lstm = sb("v_lstm", [P, NSEQ, 4, 34])

        def context_tensor(pe):
            pe.wait_ge(sem["ctx_loaded"], 16)
            mem = fill(pe, "ctx.T", fulls=2, reads=2)
            for t in range(T):
                mm = nc.tensor.transpose(mem[:, t * P:(t + 1) * P], ctx_tok[:, t, :], W("ident"))
                if t % 4 == 3:
                    mm.then_inc(full("ctx.T"), 1)

        def context_vector(dve):
            copy_half_vector(dve, "ctx.T", ctxT)

        def context_scalar(act):
            copy_half_scalar(act, "ctx.T", ctxT)
            act.wait_ge(sem["ctx_keys_loaded"], 32)
            act.wait_ge(sem["lstm_values_set"], 6)
            for h in range(2):
                rows = slice(64 * h, 64 * h + 64)
                src = ctx_keys[rows, :, :].rearrange("p b (a h f) -> p b a h f", h=2, f=16)[:, :, :, h]
                nc.scalar.copy(v_lstm[rows, :, :, 16 * h:16 * h + 16], src).then_inc(sem["lstm_values"], 1)

        def context_pool(pool):
            pass


        gate = scr[0:40, 5, :]
        lstm = scr[0:40, 1:5, :]
        spread_b = [scr[0:8, 6 + i, :].rearrange("p (h k) -> p h k", h=8) for i in range(2)]
        tok_gate = sb("tok_gate", [P, T, 40])
        least = sb("least", [P, T, 8])
        lstm_out = xn
        ms = sb("ms", [P, 64])
        rms = sb("rms", [P, 64])
        L0X = attention("l0x", "mlstm", heads=8, t_ring="B", q=xnT, k=ctxT, v=v_lstm,
                        q_ready=lambda eng: wait_read(eng, "l0x.T"), k_ready=lambda eng: wait_read(eng, "ctx.T"),
                        v_ready=lambda eng: eng.wait_ge(sem["lstm_values"], 2),
                        before_keys=lambda eng, t: wait_full(eng, f"l0a.s{6 + t}"))

        L0X["prob_ready"] = lambda eng, t: wait_read(eng, f"l0x.s{t}")

        def l0x_tensor(pe):
            n = "l0x"
            tiles_T_tensor(pe, n + ".T", xn, "xn", at(n, "xn", 0))
            wait_read(pe, n + ".T")
            project_tensor(pe, n + ".gate", [(W("l0x.gate_q"), xnT), (W("l0x.gate_k"), ctxT), (W("l0x.gate_v"), ctxT)],
                           rows=40, reads=1)
            mem = fill(pe, n + ".gateT")
            pe.wait_ge(sem[n + ".gates"], 1)
            for t in range(T):
                mm = nc.tensor.transpose(mem[:, 40 * t:40 * t + 40], lstm[:, 3, t * P:(t + 1) * P], W("ident")[0:40, 0:40])
            mm.then_inc(full(n + ".gateT"), 1)

            def scores(t):
                pe.wait_ge(sem["keys_pool"], at(n, "keys_pool", t + 1))
                pe.wait_ge(sem["keys_dve"], at(n, "keys_dve", t + 1))
                pe.wait_ge(sem[n + ".spread_b"], t + 1)
                mem = fill(pe, f"{n}.s{t}")
                for b in range(2):
                    nc.tensor.matmul(mem[64 * b:64 * b + 64, 0:512], xnT[:, t * P + 64 * b:t * P + 64 * b + 64],
                                     keys[t % 2][:, 0:8, 64 * b:64 * b + 64], start=True, stop=True)
                for b in range(2):
                    mm = nc.tensor.matmul(mem[64 * b:64 * b + 64, 512:1024], W("ones8"),
                                          spread_b[t % 2][:, :, 64 * b:64 * b + 64], start=True, stop=True)
                mm.then_inc(full(f"{n}.s{t}"), 1)

            scores(0)
            for t in range(T + 2):
                if t + 1 < T:
                    scores(t + 1)
                if t >= 2:
                    outputs_tensor(pe, L0X, t - 2)
                if 1 <= t <= T:
                    transposes_tensor(pe, L0X, t - 1)

        def l0x_vector(dve):
            n = "l0x"
            lf, cs, gb, M = (lstm[0:8, i, :] for i in range(4))
            ln_vector(dve, n, residual_ready(L0A))
            copy_half_vector(dve, n + ".T", xnT)
            dve.wait_ge(sem[n + ".softplus"], 3)
            link(dve, "vector_chain", nc.vector.scalar_tensor_tensor(out=lf, in0=gate[32:40, :], scalar=0.0, in1=lstm[32:40, 1, :],
                                                               op0=ALU.min, op1=ALU.subtract))
            link(dve, "vector_chain", nc.vector.tensor_tensor_scan(cs, W("keep"), lf, 0.0, ALU.mult, ALU.add))
            link(dve, "vector_chain", nc.vector.tensor_tensor(gb, gate[0:8, :], cs, ALU.subtract))
            dve.sem_inc(sem[n + ".gb"], 1)
            link(dve, "vector_chain", nc.vector.tensor_tensor_scan(M, W("restart"), gb, MASKED, ALU.add, ALU.max))
            dve.wait_ge(sem["lstm_values_set"], 7)
            nc.vector.tensor_tensor(lstm[32:40, 3, :], M, cs, ALU.add).then_inc(sem[n + ".gates"], 1)
            mem = wait_full(dve, n + ".gateT")
            nc.vector.tensor_copy(tok_gate[:, :, :], mem[:, 0:320].rearrange("p (t g) -> p t g", t=T)).then_inc(read(n + ".gateT"), 1)
            wait_read(dve, n + ".gateT")

            three = lambda x: x.rearrange("p (h k) -> p h k", k=SEQ)

            def weigh(t):
                mem = wait_full(dve, f"{n}.s{t}")
                if t >= 2:
                    wait_read(dve, f"{n}.s{t - 2}")
                    wait_full(dve, f"{n}.t{t - 2}")
                d = three(prob[t % 2][:, 512:1024])
                m = tok_gate[:, t, 0:8].rearrange("p (h o) -> p h o", o=1).broadcast_to([P, 8, SEQ])
                link(dve, "vector_chain", nc.vector.tensor_tensor(d, three(mem[:, 512:1024]), m, ALU.subtract))
                c = W("causal").rearrange("p (o k) -> p o k", o=1).broadcast_to([P, 8, SEQ])
                nc.vector.tensor_tensor(d, d, c, ALU.add).then_inc(sem["less"], 1)

            def combine(t):
                dve.wait_ge(sem[n + ".weight"], t + 1)
                mem = flat[book.record[f"{n}.s{t}"][0]]
                nc.vector.scalar_tensor_tensor(out=prob[t % 2][:, 0:512], in0=mem[:, 0:512], scalar=0.25,
                                               in1=prob[t % 2][:, 512:1024], op0=ALU.mult, op1=ALU.mult)\
                  .then_inc(read(f"{n}.s{t}"), 1)

            def normalise(t):
                mem = wait_full(dve, f"{n}.o{t}")
                v = mem[:, 0:136].rearrange("p (a w) -> p a w", w=34)
                rd = rden[t % 2][:, 0:8].rearrange("p (a h) -> p a h", h=2)
                lt = least[:, t, :].rearrange("p (a h) -> p a h", h=2)
                if t == 0:
                    dve.wait_ge(sem[n + ".least"], 1)
                link(dve, "vector_chain", nc.vector.tensor_scalar(rd, v[:, :, 32:34], -1.0, None, ALU.mult))
                link(dve, "vector_chain", nc.vector.tensor_tensor(rd, rd, v[:, :, 32:34], ALU.max))
                link(dve, "vector_chain", nc.vector.tensor_tensor(rd, rd, lt, ALU.max))
                link(dve, "vector_chain", nc.vector.tensor_scalar(rd, rd, 1e-6, None, ALU.add))
                link(dve, "vector_chain", nc.vector.reciprocal(rd, rd))
                ho = lstm_out[:, t, :].rearrange("p (a h f) -> p a h f", h=2, f=16)
                num = v[:, :, 0:32].rearrange("p a (h f) -> p a h f", h=2)
                rb = rd.rearrange("p a (h o) -> p a h o", o=1).broadcast_to([P, 4, 2, 16])
                nc.vector.tensor_tensor(ho, num, rb, ALU.mult).then_inc(read(f"{n}.o{t}"), 1)

            spread(dve, nc.vector, L0X, 0, POOL_HEADS, 16, "dve")
            spread(dve, nc.vector, L0X, 1, POOL_HEADS, 16, "dve")
            for t in range(T + 4):
                if t < T:
                    weigh(t)
                if 1 <= t <= T:
                    combine(t - 1)
                if t + 2 < T:
                    spread(dve, nc.vector, L0X, t + 2, POOL_HEADS, 16, "dve")
                if 3 <= t <= T + 2:
                    normalise(t - 3)
            dve.wait_ge(sem[n + ".square"], 1)
            sq = scr[:, 0, :].rearrange("p (g f) -> p g f", f=16)
            link(dve, "vector_chain", nc.vector.tensor_reduce(ms[:, :], sq, AX, ALU.add))
            link(dve, "vector_chain", nc.vector.tensor_scalar(ms[:, :], ms[:, :], 1.0 / 16, 1e-6, ALU.mult, ALU.add))
            rsqrt_vector(dve, "vector_chain", ms[:, :], rms[:, :], 64)
            lo = lstm_out[:, :, :].rearrange("p t (h f) -> p (t h) f", f=16)
            rb = rms[:, :].rearrange("p (g o) -> p g o", o=1).broadcast_to([P, 64, 16])
            link(dve, "vector_chain", nc.vector.tensor_tensor(lo, lo, rb, ALU.mult))
            for t in range(T):
                nc.vector.tensor_tensor(x_res[:, t, :], x_res[:, t, :], lstm_out[:, t, :], ALU.add).then_inc(sem[n + ".x"], 1)

        def l0x_scalar(act):
            n = "l0x"
            copy_half_scalar(act, n + ".T", xnT)
            mem = wait_full(act, n + ".gate")
            nc.scalar.activation(gate[:, :], mem[0:40, :], ACT.Identity, bias=W("l0x.gate_bias")).then_inc(read(n + ".gate"), 1)
            wait_read(act, n + ".gate")
            for i, (to, src, f, more) in enumerate(((0, gate[32:40, :], ACT.Abs, {}),
                                                    (0, lstm[32:40, 0, :], ACT.Exp, dict(scale=-1.0)),
                                                    (1, lstm[32:40, 0, :], ACT.Ln, dict(bias=1.0)))):
                nc.scalar.activation(lstm[32:40, to, :], src, f, **more).then_inc(sem[n + ".softplus"], 1)
                act.wait_ge(sem[n + ".softplus"], i + 1)
            wait_read(act, n + ".gateT")
            nc.scalar.activation(least[:, :, :], tok_gate[:, :, 32:40], ACT.Exp, scale=-1.0).then_inc(sem[n + ".least"], 1)
            for t in range(T + 2):
                if t < T:
                    act.wait_ge(sem["less"], at(n, "less", t + 1))
                    nc.scalar.activation(prob[t % 2][:, 512:1024], prob[t % 2][:, 512:1024], ACT.Exp)\
                       .then_inc(sem[n + ".weight"], 1)
                if t >= 2:
                    u = t - 2
                    if u >= 2:
                        wait_full(act, f"{n}.o{u - 2}")
                    mem = wait_full(act, f"{n}.t{u}")
                    nc.scalar.copy(probT[u % 2][:, 0:512], mem[:, 0:512]).then_inc(read(f"{n}.t{u}"), 1)
            wait_read(act, f"{n}.o{T - 1}")
            wait_read(act, f"{n}.o{T - 2}")
            nc.scalar.activation(scr[:, 0, :], lstm_out[:, :, :].rearrange("p t d -> p (t d)"), ACT.Square)\
              .then_inc(sem[n + ".square"], 1)

        def l0x_pool(pool):
            n = "l0x"
            ln_pool(pool, n)
            for t in range(T):
                spread(pool, nc.gpsimd, L0X, t, 0, POOL_HEADS, "pool")
                if t == 0:
                    pool.wait_ge(sem[n + ".gb"], 1)
                if t >= 2:
                    wait_full(pool, f"{n}.s{t - 2}")
                b = lstm[0:8, 2, t * P:(t + 1) * P].rearrange("p (o k) -> p o k", o=1).broadcast_to([8, 8, P])
                e = W("ident")[0:8, 0:8].rearrange("p (h o) -> p h o", o=1).broadcast_to([8, 8, P])
                nc.gpsimd.tensor_tensor(spread_b[t % 2][:, :, :], b, e, ALU.mult).then_inc(sem[n + ".spread_b"], 1)



        NE, M = 8, 64
        contT, r1T = scr[0:M, 0, :], scr[0:M, 1, :]
        spike = [scr[:, 2, :], scr[:, 3, :]]
        hidden = [scr[:, 4, :], scr[:, 5, :]]
        gate_rep = [scr[:, 6, :], scr[:, 7, :]]
        gated, moe = scr[:, 8, :], scr[:, 9, :]
        gT = scr[0:NE, 10, :]
        logit = sb("logit", [P, T, NE])
        pick = sb("pick", [P, T, NE])
        best = sb("best", [P, T, 1])
        tie = prob[0][:, :].rearrange("p (w t e f) -> p w t e f", w=2, t=T, e=NE)

        def tok_bias(name, tiles=T):
            return W(name).rearrange("p (o d) -> p o d", o=1).broadcast_to([P, tiles, W(name).shape[1]])

        def l0f_tensor(pe):
            n = "l0f"
            tiles_T_tensor(pe, n + ".T", xn, "xn", at(n, "xn", 0))
            wait_read(pe, n + ".T")
            for c in range(2):
                project_tensor(pe, f"{n}.enc{c}", [(W("L0_ffn_enc_W")[:, 128 * c:128 * c + 128], xnT)])
            wait_read(pe, n + ".enc0")
            wait_read(pe, n + ".enc1")
            project_tensor(pe, n + ".cont", [(W(f"l0f.s2c{c}"), spike[c]) for c in range(2)], rows=M)
            wait_read(pe, n + ".cont")
            project_tensor(pe, n + ".r1", [(W("L0_ffn_rW1"), contT)], rows=M)
            for e in range(2):
                project_tensor(pe, f"{n}.h{e}", [(W(f"l0f.We1_{e}"), contT)])
            wait_read(pe, n + ".r1")
            mem = fill(pe, n + ".logit")
            for t in range(T):
                mm = nc.tensor.matmul(mem[:, NE * t:NE * t + NE], r1T[:, t * P:(t + 1) * P], W("L0_ffn_rW2"),
                                      start=True, stop=True)
            mm.then_inc(full(n + ".logit"), 1)
            for p in range(NE // 2):
                if p:
                    for e in (2 * p, 2 * p + 1):
                        project_tensor(pe, f"{n}.h{e}", [(W(f"l0f.We1_{e}"), contT)])
                wait_read(pe, f"{n}.h{2 * p}")
                wait_read(pe, f"{n}.h{2 * p + 1}")
                if p == 0:
                    pe.wait_ge(sem[n + ".gates"], 1)
                    mem = fill(pe, n + ".gT")
                    for t in range(T):
                        mm = nc.tensor.transpose(mem[0:NE, t * P:(t + 1) * P], pick[:, t, :], W("ident"))
                    mm.then_inc(full(n + ".gT"), 1)
                mem = fill(pe, f"{n}.eo{p}")
                for half in range(2):
                    for e in range(2):
                        mm = nc.tensor.matmul(mem[64 * e:64 * e + 64, 512 * half:512 * half + 512], W(f"l0f.We2_{2 * p + e}"),
                                              hidden[e][:, 512 * half:512 * half + 512], start=True, stop=True)
                mm.then_inc(full(f"{n}.eo{p}"), 1)
                if p == 0:
                    wait_read(pe, n + ".gT")
                project_tensor(pe, f"{n}.rep{p}", [(W(f"l0f.pair{p}"), gT)])
            pe.wait_ge(sem[n + ".moe"], 4)
            for c in range(2):
                project_tensor(pe, f"{n}.c2s{c}", [(W("l0f.c2s2")[:, 128 * c:128 * c + 128], moe)])
            wait_read(pe, n + ".c2s0")
            wait_read(pe, n + ".c2s1")
            mem = fill(pe, n + ".dec")
            for t in range(T):
                for c in range(2):
                    mm = nc.tensor.matmul(mem[:, t * P:(t + 1) * P], spike[c][:, t * P:(t + 1) * P], W(f"l0f.dec{c}"),
                                          start=c == 0, stop=c == 1)
            mm.then_inc(full(n + ".dec"), 1)

        def l0f_scalar(act):
            n = "l0f"
            copy_half_scalar(act, n + ".T", xnT)
            for c in range(2):
                for half in range(2):
                    mem = wait_full(act, f"{n}.enc{c}", half)
                    s = slice(512 * half, 512 * half + 512)
                    nc.scalar.activation(spike[c][:, s], mem[:, s], ACT.Sigmoid, bias=W("l0f.enc_b")[:, c:c + 1])\
                      .then_inc(read(f"{n}.enc{c}"), 1)
            mem = wait_full(act, n + ".cont", 0)
            nc.scalar.activation(contT[:, 0:512], mem[0:M, 0:512], ACT.Identity, bias=W("l0f.s2c_b")).then_inc(read(n + ".cont"), 1)
            for half in range(2):
                mem = wait_full(act, n + ".r1", half)
                s = slice(512 * half, 512 * half + 512)
                nc.scalar.activation(r1T[:, s], mem[0:M, s], ACT.Tanh, bias=W("l0f.rb1")).then_inc(read(n + ".r1"), 1)

            def hidden_relu(e):
                mem = wait_full(act, f"{n}.h{e}", 0)
                if e >= 2:
                    wait_full(act, f"{n}.eo{e // 2 - 1}")
                nc.scalar.activation(hidden[e % 2][:, 0:512], mem[:, 0:512], ACT.Relu, bias=W("l0f.be1")[:, e:e + 1])\
                  .then_inc(read(f"{n}.h{e}"), 1)

            hidden_relu(0)
            hidden_relu(1)
            act.wait_ge(sem["less"], at(n, "less", 1))
            nc.scalar.activation(logit[:, :, :], logit[:, :, :], ACT.Exp).then_inc(sem["exp"], 1)
            for p in range(NE // 2):
                if p:
                    hidden_relu(2 * p)
                    hidden_relu(2 * p + 1)
                if p == 0:
                    mem = wait_full(act, n + ".gT")
                    nc.scalar.copy(gT, mem[0:NE, :]).then_inc(read(n + ".gT"), 1)
                if p >= 2:
                    wait_read(act, f"{n}.eo{p - 2}")
                for half in range(2):
                    mem = wait_full(act, f"{n}.rep{p}", half)
                    s = slice(512 * half, 512 * half + 512)
                    nc.scalar.copy(gate_rep[p % 2][:, s], mem[:, s]).then_inc(read(f"{n}.rep{p}"), 1)
            for c in range(2):
                for half in range(2):
                    mem = wait_full(act, f"{n}.c2s{c}", half)
                    s = slice(512 * half, 512 * half + 512)
                    nc.scalar.activation(spike[c][:, s], mem[:, s], ACT.Sigmoid, bias=W("l0f.c2s_b")[:, c:c + 1])\
                      .then_inc(read(f"{n}.c2s{c}"), 1)
            wait_read(act, n + ".dec")
            nc.scalar.activation(xn[:, :, :], xn[:, :, :], ACT.Sigmoid).then_inc(sem[n + ".decoded"], 1)

        def l0f_vector(dve):
            n = "l0f"
            ch = "vector_chain"
            ln_vector(dve, n, residual_ready(L0X))
            copy_half_vector(dve, n + ".T", xnT)
            mem = wait_full(dve, n + ".cont", 1)
            nc.vector.tensor_scalar(contT[:, 512:], mem[0:M, 512:], W("l0f.s2c_b"), None, ALU.add).then_inc(read(n + ".cont"), 1)

            def hidden_relu(e):
                mem = wait_full(dve, f"{n}.h{e}", 1)
                if e >= 2:
                    wait_full(dve, f"{n}.eo{e // 2 - 1}")
                nc.vector.tensor_scalar(hidden[e % 2][:, 512:], mem[:, 512:], W("l0f.be1")[:, e:e + 1], 0.0, ALU.add, ALU.max)\
                  .then_inc(read(f"{n}.h{e}"), 1)

            hidden_relu(0)
            hidden_relu(1)
            mem = wait_full(dve, n + ".logit")
            nc.vector.tensor_tensor(logit[:, :, :], mem[:, 0:T * NE].rearrange("p (t e) -> p t e", e=NE), tok_bias("l0f.rb2"),
                                    ALU.add).then_inc(read(n + ".logit"), 1)
            wait_read(dve, n + ".logit")
            mine = logit[:, :, :].rearrange("p t (e o) -> p t e o", o=1).broadcast_to([P, T, NE, NE])
            other = logit[:, :, :].rearrange("p t (o e) -> p t o e", o=1).broadcast_to([P, T, NE, NE])
            link(dve, ch, nc.vector.tensor_tensor(tie[:, 0], other, mine, ALU.is_gt))
            link(dve, ch, nc.vector.tensor_tensor(tie[:, 1], other, mine, ALU.is_equal))
            first = W("before").rearrange("p (o e f) -> p o e f", o=1, e=NE).broadcast_to([P, T, NE, NE])
            link(dve, ch, nc.vector.tensor_tensor(tie[:, 1], tie[:, 1], first, ALU.mult))
            link(dve, ch, nc.vector.tensor_tensor(tie[:, 0], tie[:, 0], tie[:, 1], ALU.add))
            link(dve, ch, nc.vector.tensor_reduce(pick[:, :, :], tie[:, 0], AX, ALU.add))
            link(dve, ch, nc.vector.tensor_reduce(best[:, :, 0], logit[:, :, :], AX, ALU.max))
            nc.vector.tensor_tensor(logit[:, :, :], logit[:, :, :], best[:, :, :].broadcast_to([P, T, NE]), ALU.subtract)\
              .then_inc(sem["less"], 1)
            dve.wait_ge(sem["exp"], at(n, "exp", 1))
            link(dve, ch, nc.vector.scalar_tensor_tensor(out=pick[:, :, :], in0=pick[:, :, :], scalar=2.0, in1=logit[:, :, :],
                                                         op0=ALU.is_lt, op1=ALU.mult))
            link(dve, ch, nc.vector.tensor_reduce(best[:, :, 0], pick[:, :, :], AX, ALU.add))
            link(dve, ch, nc.vector.reciprocal(best[:, :, :], best[:, :, :]))
            nc.vector.tensor_tensor(pick[:, :, :], pick[:, :, :], best[:, :, :].broadcast_to([P, T, NE]), ALU.mult)\
              .then_inc(sem[n + ".gates"], 1)
            for p in range(NE // 2):
                if p:
                    hidden_relu(2 * p)
                    hidden_relu(2 * p + 1)
                mem = wait_full(dve, f"{n}.eo{p}")
                wait_read(dve, f"{n}.rep{p}")
                if p >= 2:
                    dve.wait_ge(sem[n + ".moe"], p)
                to = moe if p == 0 else gated
                if p:
                    dve.wait_ge(sem[n + ".moe"], p)
                nc.vector.scalar_tensor_tensor(out=to, in0=mem, scalar=W("l0f.be2")[:, p:p + 1], in1=gate_rep[p % 2],
                                               op0=ALU.add, op1=ALU.mult).then_inc(read(f"{n}.eo{p}"), 1)
                wait_read(dve, f"{n}.eo{p}")
                if p:
                    nc.vector.tensor_tensor(moe, moe, gated, ALU.add).then_inc(sem[n + ".moe"], 1)
                else:
                    dve.sem_inc(sem[n + ".moe"], 1)
            mem = wait_full(dve, n + ".dec")
            nc.vector.tensor_tensor(xn[:, :, :], mem.rearrange("p (t d) -> p t d", t=T), tok_bias("l0f.dec_b"), ALU.add)\
              .then_inc(read(n + ".dec"), 1)
            dve.wait_ge(sem[n + ".decoded"], 1)
            for t in range(T):
                nc.vector.bn_stats(bn[:, t, :], xn[:, t, :]).then_inc(sem["stats"], 1)
            for t in range(T):
                dve.wait_ge(sem["stats"], at(n, "stats", T + t + 1))
                nc.vector.bn_aggr(mv[:, t, :], bn[:, t, :]).then_inc(sem["moments"], 1)
            dve.wait_ge(sem["moments"], at(n, "moments", 2 * T))
            link(dve, ch, nc.vector.tensor_scalar(var_eps[:, :], mv[:, :, 1], LN_EPS, None, ALU.add))
            rsqrt_vector(dve, ch, var_eps[:, :], rstd[:, :], T)
            for t in range(T):
                nc.vector.tensor_scalar(xn[:, t, :], xn[:, t, :], mv[:, t, 0:1], rstd[:, t:t + 1], ALU.subtract, ALU.mult)\
                  .then_inc(sem["xn"], 1)
            dve.wait_ge(sem["xn"], at(n, "xn", 2 * T))
            link(dve, ch, nc.vector.tensor_tensor(xn[:, :, :], xn[:, :, :], tok_bias("l0f.ln_g"), ALU.mult))
            link(dve, ch, nc.vector.tensor_tensor(xn[:, :, :], xn[:, :, :], tok_bias("l0f.ln_b"), ALU.add))
            for t in range(T):
                nc.vector.tensor_tensor(x_res[:, t, :], x_res[:, t, :], xn[:, t, :], ALU.add).then_inc(sem[n + ".x"], 1)

        def l0f_pool(pool):
            ln_pool(pool, "l0f")

        L0F_READY = lambda eng, t: eng.wait_ge(sem["l0f.x"], t + 1)


        mixes = ("w", "a", "k", "v", "r", "g")
        diff = scr[:, 0, :]
        mixed = [scr[:, 1, :], scr[:, 2, :]]
        lin = {m: scr[:, 3 + i, :] for i, m in enumerate(("w", "a", "k", "r", "g"))}
        upd, state = scr[:, 8, :], scr[:, 9, :]
        group = sb("group", [P, 2, 128])

        def l1a_tensor(pe):
            n = "l1a"
            tiles_T_tensor(pe, n + ".T", xn, "xn", at(n, "xn", 0))
            for i, m in enumerate(mixes):
                pe.wait_ge(sem[n + ".mix"], i + 1)
                project_tensor(pe, f"{n}.{m}", [(W("L1_attn_W_" + m), mixed[i % 2])])
            pe.wait_ge(sem[n + ".mixed"], 1)
            mem = fill(pe, n + ".mT")
            for t in range(T):
                mm = nc.tensor.transpose(mem[:, t * P:(t + 1) * P], state[:, t * P:(t + 1) * P], W("ident"))
            mm.then_inc(full(n + ".mT"), 1)
            mem = fill(pe, n + ".nT", fulls=1, reads=1)
            pe.wait_ge(sem[n + ".normed"], 1)
            for t in range(T):
                mm = nc.tensor.transpose(mem[:, t * P:(t + 1) * P], xn[:, t, :], W("ident"))
            mm.then_inc(full(n + ".nT"), 1)
            mem = fill(pe, n + ".y", reads=T)
            pe.wait_ge(sem[n + ".gated"], 1)
            for t in range(T):
                mm = nc.tensor.matmul(mem[:, t * P:(t + 1) * P], upd[:, t * P:(t + 1) * P], W("L1_attn_W_out"), start=True, stop=True)
            mm.then_inc(full(n + ".y"), 1)

        def l1a_scalar(act):
            n = "l1a"
            copy_half_scalar(act, n + ".T", xnT)
            for i, m in enumerate(mixes):
                if m == "v":
                    continue
                for half in range(2):
                    mem = wait_full(act, f"{n}.{m}", half)
                    s = slice(512 * half, 512 * half + 512)
                    nc.scalar.activation(lin[m][:, s], mem[:, s], ACT.Tanh if m == "k" else ACT.Sigmoid,
                                         scale=-1.0 if m == "w" else 1.0).then_inc(read(f"{n}.{m}"), 1)
            act.wait_ge(sem[n + ".centred"], 1)
            nc.scalar.activation(scr[:, 1, :], xn[:, :, :].rearrange("p t d -> p (t d)"), ACT.Square).then_inc(sem[n + ".square"], 1)

        def l1a_vector(dve):
            n = "l1a"
            ch = "vector_chain"
            ln_vector(dve, n, L0F_READY)
            copy_half_vector(dve, n + ".T", xnT)
            wait_read(dve, n + ".T")
            seq = lambda x: x.rearrange("p (b s) -> p b s", s=SEQ)
            nc.vector.tensor_tensor(seq(diff)[:, :, 1:], seq(xnT[:, :])[:, :, :SEQ - 1], seq(xnT[:, :])[:, :, 1:], ALU.subtract)\
              .then_inc(sem[n + ".diff"], 1)
            nc.vector.tensor_scalar(seq(diff)[:, :, 0:1], seq(xnT[:, :])[:, :, 0:1], -1.0, None, ALU.mult).then_inc(sem[n + ".diff"], 1)
            dve.wait_ge(sem[n + ".diff"], 2)

            def mix(i):
                if i >= 2:
                    wait_full(dve, f"{n}.{mixes[i - 2]}")
                nc.vector.scalar_tensor_tensor(out=mixed[i % 2], in0=diff, scalar=W("l1a.x_" + mixes[i]), in1=xnT[:, :],
                                               op0=ALU.mult, op1=ALU.add).then_inc(sem[n + ".mix"], 1)

            for i in range(6):
                mix(i)
                if i == 5:
                    wait_read(dve, n + ".w")
                    link(dve, ch, nc.vector.memset(seq(lin["w"])[:, :, 0:1], 0.0))
                    wait_read(dve, n + ".a")
                    wait_read(dve, n + ".k")
                    link(dve, ch, nc.vector.tensor_tensor(upd, lin["a"], lin["k"], ALU.mult))
                    mem = wait_full(dve, n + ".v")
                    nc.vector.tensor_tensor(upd, mem, upd, ALU.mult).then_inc(read(n + ".v"), 2)
            wait_read(dve, n + ".v")
            link(dve, ch, nc.vector.tensor_tensor_scan(state, lin["w"], upd, 0.0, ALU.mult, ALU.add))
            wait_read(dve, n + ".r")
            nc.vector.tensor_tensor(state, state, lin["r"], ALU.mult).then_inc(sem[n + ".mixed"], 1)
            mem = wait_full(dve, n + ".mT")
            groups = lambda x: x.rearrange("p (g f) -> p g f", f=8)
            flat_xn = xn[:, :, :].rearrange("p t d -> p (t d)")
            link(dve, ch, nc.vector.tensor_reduce(group[:, 0, :], groups(mem), AX, ALU.add))
            link(dve, ch, nc.vector.tensor_scalar(group[:, 0, :], group[:, 0, :], 1 / 8, None, ALU.mult))
            gb = lambda x: x.rearrange("p (g o) -> p g o", o=1).broadcast_to([P, 128, 8])
            nc.vector.tensor_tensor(groups(flat_xn), groups(mem), gb(group[:, 0, :]), ALU.subtract).then_inc(read(n + ".mT"), 1)
            wait_read(dve, n + ".mT")
            dve.sem_inc(sem[n + ".centred"], 1)
            dve.wait_ge(sem[n + ".square"], 1)
            link(dve, ch, nc.vector.tensor_reduce(group[:, 1, :], groups(scr[:, 1, :]), AX, ALU.add))
            link(dve, ch, nc.vector.tensor_scalar(group[:, 1, :], group[:, 1, :], 1 / 8, 0.00064, ALU.mult, ALU.add))
            rsqrt_vector(dve, ch, group[:, 1, :], group[:, 0, :], 128)
            nc.vector.tensor_tensor(groups(flat_xn), groups(flat_xn), gb(group[:, 0, :]), ALU.mult).then_inc(sem[n + ".normed"], 1)
            mem = wait_full(dve, n + ".nT")
            nc.vector.tensor_scalar(upd, mem, W("l1a.gn_w"), W("l1a.gn_b"), ALU.mult, ALU.add).then_inc(read(n + ".nT"), 1)
            wait_read(dve, n + ".nT")
            wait_read(dve, n + ".g")
            nc.vector.tensor_tensor(upd, upd, lin["g"], ALU.mult).then_inc(sem[n + ".gated"], 1)
            dve.wait_ge(sem["b_out"], at(n, "b_out", 1))
            mem = wait_full(dve, n + ".y")
            for t in range(T):
                nc.vector.tensor_tensor(x_res[:, t, :], mem[:, t * P:(t + 1) * P], x_res[:, t, :], ALU.add).then_inc(read(n + ".y"), 1)

        def add_bias_pool(pool, n, name):
            pool.wait_ge(sem["xn"], at(n, "xn", T))
            nc.gpsimd.tensor_tensor(x_res[:, :, :], x_res[:, :, :], tok_bias(name), ALU.add).then_inc(sem["b_out"], 1)

        def l1a_pool(pool):
            ln_pool(pool, "l1a")
            add_bias_pool(pool, "l1a", "l1a.b_out")

        def product_ready(name):
            return lambda eng, t: eng.wait_ge(sem["read." + book.record[name][0]], book.record[name][3] - T + t + 1)


        L1X = attention("l1x", "plain", scale=8 ** -0.5, q=qT, k=kcT, v=v_ctx,
                        q_ready=lambda eng: wait_read(eng, "l1x.q"), k_ready=lambda eng: wait_read(eng, "l1x.k"),
                        v_ready=lambda eng: wait_read(eng, "l1x.v"), before_keys=lambda eng, t: wait_full(eng, f"l0x.s{6 + t}"))

        def l1x_tensor(pe):
            n = "l1x"
            project_tensor(pe, n + ".k", [(W("L1_xattn_Wk"), ctxT)])
            values_tensor(pe, n + ".v", W("L1_xattn_Wv"), ctxT)
            tiles_T_tensor(pe, n + ".T", xn, "xn", at(n, "xn", 0))
            wait_read(pe, n + ".T")
            project_tensor(pe, n + ".q", [(W("L1_xattn_Wq"), xnT)])
            attention_tensor(pe, L1X)

        def relu_half(eng, name, dst, half):
            mem = wait_full(eng, name, half)
            s = slice(512 * half, 512 * half + 512)
            if half == 0:
                nc.scalar.activation(dst[:, s], mem[:, s], ACT.Relu).then_inc(read(name), 1)
            else:
                nc.vector.tensor_scalar(dst[:, s], mem[:, s], 0.0, None, ALU.max).then_inc(read(name), 1)

        def l1x_vector(dve):
            n = "l1x"
            relu_half(dve, n + ".k", kcT, 1)
            dve.wait_ge(sem["values_set"], VALUES_SET)
            values_copy(dve, n + ".v", v_ctx, 1, relu=True)
            ln_vector(dve, n, product_ready("l1a.y"))
            copy_half_vector(dve, n + ".T", xnT)
            relu_half(dve, n + ".q", qT, 1)
            attention_vector(dve, L1X)

        def l1x_scalar(act):
            n = "l1x"
            relu_half(act, n + ".k", kcT, 0)
            values_copy(act, n + ".v", v_ctx, 0, relu=True)
            copy_half_scalar(act, n + ".T", xnT)
            relu_half(act, n + ".q", qT, 0)
            attention_scalar(act, L1X)

        def l1x_pool(pool):
            ln_pool(pool, "l1x")
            attention_pool(pool, L1X)


        wide = [scr[:, i, :] for i in range(4)]
        mem_v, cur, spikes = scr[:, 4, :], scr[:, 5, :], scr[:, 6, :]
        lif_a = scr[:, 7, :]

        def l1f_tensor(pe):
            n = "l1f"
            tiles_T_tensor(pe, n + ".T", xn, "xn", at(n, "xn", 0))
            wait_read(pe, n + ".T")
            for c in range(4):
                project_tensor(pe, f"{n}.h{c}", [(W("L1_ffn_W_fc")[:, 128 * c:128 * c + 128], xnT)])
            mem = fill(pe, n + ".y", fulls=2, reads=2)
            for t in range(T):
                for c in range(4):
                    if t % 4 == 0:
                        pe.wait_ge(sem[n + ".square"], 4 * (t // 4) + c + 1)
                    mm = nc.tensor.matmul(mem[:, t * P:(t + 1) * P], wide[c][:, t * P:(t + 1) * P], W(f"l1f.proj{c}"),
                                          start=c == 0, stop=c == 3)
                if t % 4 == 3:
                    mm.then_inc(full(n + ".y"), 1)

        def l1f_scalar(act):
            n = "l1f"
            copy_half_scalar(act, n + ".T", xnT)
            for c in range(4):
                for half in range(2):
                    mem = wait_full(act, f"{n}.h{c}", half)
                    s = slice(512 * half, 512 * half + 512)
                    nc.scalar.activation(wide[c][:, s], mem[:, s], ACT.Relu).then_inc(read(f"{n}.h{c}"), 1)

        def l1f_vector(dve):
            n = "l1f"
            ch = "vector_chain"
            ln_vector(dve, n, residual_ready(L1X))
            copy_half_vector(dve, n + ".T", xnT)
            for half in range(2):
                for c in range(4):
                    s = slice(512 * half, 512 * half + 512)
                    wait_read(dve, f"{n}.h{c}")
                    nc.vector.tensor_tensor(wide[c][:, s], wide[c][:, s], wide[c][:, s], ALU.mult).then_inc(sem[n + ".square"], 1)
            for half in range(2):
                mem = wait_full(dve, n + ".y", half)
                s = slice(512 * half, 512 * half + 512)
                nc.vector.tensor_copy(cur[:, s], mem[:, s]).then_inc(read(n + ".y"), 1)
            wait_read(dve, n + ".y")
            link(dve, ch, nc.vector.tensor_scalar(spikes, cur, 1.0, None, ALU.is_gt))
            v = cur
            for step in range(4):
                link(dve, ch, nc.vector.scalar_tensor_tensor(out=lif_a, in0=v, scalar=0.9, in1=cur, op0=ALU.mult, op1=ALU.add))
                link(dve, ch, nc.vector.scalar_tensor_tensor(out=mem_v, in0=v, scalar=1.0, in1=lif_a, op0=ALU.is_gt,
                                                             op1=ALU.subtract, reverse1=True))
                v = mem_v
                link(dve, ch, nc.vector.scalar_tensor_tensor(out=spikes, in0=v, scalar=1.0, in1=spikes, op0=ALU.is_gt, op1=ALU.add))
            sp = spikes.rearrange("p (t d) -> p t d", t=T)
            for t in range(T):
                nc.vector.scalar_tensor_tensor(out=x_res[:, t, :], in0=sp[:, t, :], scalar=0.2, in1=x_res[:, t, :],
                                               op0=ALU.mult, op1=ALU.add).then_inc(sem[n + ".x"], 1)

        def l1f_pool(pool):
            ln_pool(pool, "l1f")

        L1F_READY = lambda eng, t: eng.wait_ge(sem["l1f.x"], t + 1)



        def bias_half(eng, name, dst, half, bias):
            mem = wait_full(eng, name, half)
            s = slice(512 * half, 512 * half + 512)
            if half == 0:
                nc.scalar.activation(dst[:, s], mem[:, s], ACT.Identity, bias=W(bias)).then_inc(read(name), 1)
            else:
                nc.vector.tensor_scalar(dst[:, s], mem[:, s], W(bias), None, ALU.add).then_inc(read(name), 1)

        rope_qk = scr[:, 0:2, :].rearrange("p a (b c) -> p (a b) c", c=256)
        rope_tmp = scr[:, 2:4, :].rearrange("p a (b c) -> p (a b) c", c=256)
        rope_sq = scr[:, 4:6, :].rearrange("p a b -> p (a b)")
        norm_qk = sb("norm_qk", [P, 2, 256])
        L2A = attention("l2a", "unit", bo=True, scale=8 ** -0.5, q=qT, k=kT, v=v_self, wo="L2_attn_Wo",
                        q_ready=lambda eng: wait_read(eng, "l2a.q"), k_ready=lambda eng: wait_read(eng, "l2a.k"),
                        v_ready=lambda eng: wait_read(eng, "l2a.v"), before_keys=lambda eng, t: wait_full(eng, f"l1x.s{6 + t}"))
        L2A["softmax"] = lambda dve, a, t: None

        def l2a_tensor(pe):
            n = "l2a"
            tiles_T_tensor(pe, n + ".T", xn, "xn", at(n, "xn", 0))
            wait_read(pe, n + ".T")
            for pair in range(T // 2):
                mem = fill(pe, f"{n}.qk{pair}", reads=1)
                for i in range(2):
                    t = 2 * pair + i
                    mm = nc.tensor.matmul(mem[:, 512 * i:512 * i + 512], xnT[:, t * P:(t + 1) * P], W("l2a.qk_rot"), start=True, stop=True)
                mm.then_inc(full(f"{n}.qk{pair}"), 1)
            values_tensor(pe, n + ".v", W("l2a.Wv"), xnT)
            for part, c in (("k", 1), ("q", 0)):
                pe.wait_ge(sem[n + ".unit"], 1)
                mem = fill(pe, f"{n}.{part}", fulls=2, reads=2)
                for t in range(T):
                    mm = nc.tensor.transpose(mem[:, t * P:(t + 1) * P], rope_qk[:, t, 128 * c:128 * c + 128], W("ident"))
                    if t % 4 == 3:
                        mm.then_inc(full(f"{n}.{part}"), 1)
            attention_tensor(pe, L2A)

        def l2a_vector(dve):
            n = "l2a"
            ch = "vector_chain"
            ln_vector(dve, n, L1F_READY)
            copy_half_vector(dve, n + ".T", xnT)
            table = lambda name: W(name).rearrange("p (a o f) -> p a o f", a=1, o=1).broadcast_to([P, 2, 32, 8])
            heads = lambda x: x.rearrange("p t (h f) -> p t h f", f=8)
            for pair in range(T // 2):
                mem = wait_full(dve, f"{n}.qk{pair}").rearrange("p (t c) -> p t c", t=2)
                s = slice(2 * pair, 2 * pair + 2)
                nc.vector.tensor_tensor(heads(rope_qk[:, s, :]), heads(mem[:, :, 0:256]), table("cos8"), ALU.mult)\
                  .then_inc(sem[n + ".cos"], 1)
                nc.vector.tensor_tensor(heads(rope_tmp[:, s, :]), heads(mem[:, :, 256:512]), table("sin8"), ALU.mult)\
                  .then_inc(read(f"{n}.qk{pair}"), 1)
            values_copy(dve, n + ".v", v_self, 1)
            dve.wait_ge(sem[n + ".rotated"], 4)
            dve.wait_ge(sem[n + ".square"], 1)
            link(dve, ch, nc.vector.tensor_reduce(norm_qk[:, 0, :], rope_sq.rearrange("p (g f) -> p g f", f=8), AX, ALU.add))
            link(dve, ch, nc.vector.tensor_scalar(norm_qk[:, 0, :], norm_qk[:, 0, :], 1e-6, None, ALU.add))
            rsqrt_vector(dve, ch, norm_qk[:, 0, :], norm_qk[:, 1, :], 256)
            qk = scr[:, 0:2, :].rearrange("p a (g f) -> p (a g) f", f=8)
            rb = norm_qk[:, 1, :].rearrange("p (g o) -> p g o", o=1).broadcast_to([P, 256, 8])
            nc.vector.tensor_tensor(qk, qk, rb, ALU.mult).then_inc(sem[n + ".unit"], 1)
            copy_half_vector(dve, n + ".k", kT)
            copy_half_vector(dve, n + ".q", qT)
            attention_vector(dve, L2A)

        def l2a_scalar(act):
            n = "l2a"
            copy_half_scalar(act, n + ".T", xnT)
            values_copy(act, n + ".v", v_self, 0)
            act.wait_ge(sem[n + ".rotated"], 4)
            nc.scalar.activation(rope_sq, scr[:, 0:2, :].rearrange("p a b -> p (a b)"), ACT.Square).then_inc(sem[n + ".square"], 1)
            copy_half_scalar(act, n + ".k", kT)
            copy_half_scalar(act, n + ".q", qT)
            attention_scalar(act, L2A)

        def l2a_pool(pool):
            n = "l2a"
            ln_pool(pool, n)
            for pair in range(T // 2):
                pool.wait_ge(sem[n + ".cos"], pair + 1)
                wait_read(pool, f"{n}.qk{pair}")
                s = slice(2 * pair, 2 * pair + 2)
                nc.gpsimd.tensor_tensor(rope_qk[:, s, :], rope_qk[:, s, :], rope_tmp[:, s, :], ALU.add).then_inc(sem[n + ".rotated"], 1)
            add_bias_pool(pool, n, "l2a.bo")
            attention_pool(pool, L2A)


        def biased_tensor(pe, a, src, wq, wk, wv):
            n = a["n"]
            if src is ctxT:
                project_tensor(pe, n + ".k", [(W(wk), src)])
                values_tensor(pe, n + ".v", W(wv), src)
            tiles_T_tensor(pe, n + ".T", xn, "xn", at(n, "xn", 0))
            wait_read(pe, n + ".T")
            if src is not ctxT:
                project_tensor(pe, n + ".k", [(W(wk), src)])
            project_tensor(pe, n + ".q", [(W(wq), xnT)])
            if src is not ctxT:
                values_tensor(pe, n + ".v", W(wv), src)
            attention_tensor(pe, a)

        def biased_vector(dve, a, src, bq, bk, before):
            n = a["n"]
            if src is ctxT:
                bias_half(dve, n + ".k", a["k"], 1, bk)
                values_copy(dve, n + ".v", a["v"], 1)
            ln_vector(dve, n, before)
            copy_half_vector(dve, n + ".T", xnT)
            if src is not ctxT:
                bias_half(dve, n + ".k", a["k"], 1, bk)
            bias_half(dve, n + ".q", qT, 1, bq)
            if src is not ctxT:
                values_copy(dve, n + ".v", a["v"], 1)
            attention_vector(dve, a)

        def biased_scalar(act, a, src, bq, bk):
            n = a["n"]
            if src is ctxT:
                bias_half(act, n + ".k", a["k"], 0, bk)
                values_copy(act, n + ".v", a["v"], 0)
            copy_half_scalar(act, n + ".T", xnT)
            if src is not ctxT:
                bias_half(act, n + ".k", a["k"], 0, bk)
            bias_half(act, n + ".q", qT, 0, bq)
            if src is not ctxT:
                values_copy(act, n + ".v", a["v"], 0)
            attention_scalar(act, a)

        def biased_pool(pool, a, bo):
            ln_pool(pool, a["n"])
            add_bias_pool(pool, a["n"], bo)
            attention_pool(pool, a)

        def biased_attention(n, kind, cross, last, pre, wo, bv):
            return attention(n, kind, scale=8 ** -0.5, q=qT, k=kcT if cross else kT, v=v_ctx if cross else v_self, wo=wo, bv=bv,
                             bo=True, q_ready=lambda eng: wait_read(eng, n + ".q"), k_ready=lambda eng: wait_read(eng, n + ".k"),
                             v_ready=lambda eng: wait_read(eng, n + ".v"),
                             before_keys=lambda eng, t: wait_full(eng, f"{last}.s{6 + t}"))


        L2X = biased_attention("l2x", "topk", True, "l2a", "L2_xattn", "l2x.Wo", "l2x.bv")
        L2X["prob_ready"] = lambda eng, t: eng.wait_ge(sem["l2x.chosen"], t + 1)
        FOUND = -3.0e38
        rest = [scr[:, 8, :], scr[:, 9, :]]
        best8 = [sb(f"best8_{i}", [P, 16, 8]) for i in range(2)]
        ROUNDS = 4

        def topk_vector(dve, a, t):
            n = a["n"]
            wait_read(dve, f"{n}.s{t}")
            pr = prob[t % 2][:, :].rearrange("p (h k) -> p h k", k=SEQ)
            left = rest[t % 2].rearrange("p (h k) -> p h k", k=SEQ)
            for r in range(ROUNDS):
                src = left if r else pr
                b8 = best8[r % 2]
                if r:
                    dve.wait_ge(sem[n + ".struck"], 16 * (ROUNDS * t + r))
                for h in range(16):
                    nc.vector.max(b8[:, h, :], src[:, h, :]).then_inc(sem[n + ".best"], 1)
                dve.wait_ge(sem[n + ".best"], 16 * (ROUNDS * t + r + 1))
                if r == 0:
                    nc.vector.tensor_copy(top[t % 2][:, :], b8[:, :, 0]).then_inc(sem["top"], 1)
                for h in range(16):
                    nc.vector.match_replace(out=left[:, h, :], in_to_replace=b8[:, h, :], in_values=src[:, h, :], imm_value=FOUND)\
                      .then_inc(sem[n + ".struck"], 1)
                if r == 0 and t:
                    choose(dve, a, t - 1)
            dve.wait_ge(sem[n + ".struck"], 16 * ROUNDS * (t + 1))
            dve.wait_ge(sem["top"], at(n, "top", t + 1))
            tb = top[t % 2][:, :].rearrange("p (h o) -> p h o", o=1).broadcast_to([P, 16, SEQ])
            nc.vector.tensor_tensor(pr, pr, tb, ALU.subtract).then_inc(sem["less"], 1)
            if t == T - 1:
                choose(dve, a, t)

        def choose(dve, a, t):
            n = a["n"]
            dve.wait_ge(sem["exp"], at(n, "exp", t + 1))
            nc.vector.scalar_tensor_tensor(out=prob[t % 2][:, :], in0=rest[t % 2], scalar=-2.0e38, in1=prob[t % 2][:, :],
                                           op0=ALU.is_le, op1=ALU.mult).then_inc(sem[n + ".chosen"], 1)

        L2X["softmax"] = topk_vector

        def topk_copy_scalar(act, a, t):
            n = a["n"]
            if t >= 2:
                wait_full(act, f"{n}.t{t - 2}")
            mem = wait_full(act, f"{n}.s{t}")
            nc.scalar.copy(prob[t % 2][:, :], mem).then_inc(read(f"{n}.s{t}"), 1)

        L2X["copy"] = topk_copy_scalar


        share = sb("share", [P, 2])
        thresh = sb("thresh", [P, 2, 2])
        tern = scr[:, 10, 0:512]
        tern2 = scr[:, 10, 512:1024]
        TERNARY = ("l2f.up", "l2f.down")

        def ternary_scalar(act):
            for i, w in enumerate(TERNARY):
                if i:
                    act.wait_ge(sem["tern.sum"], 1)
                nc.scalar.activation(tern, W(w), ACT.Abs, accum_out=share[:, i:i + 1]).then_inc(sem["tern.sum"], 1)

        def ternary_tensor(pe):
            pe.wait_ge(sem["tern.sum"], 2)
            mem = fill(pe, "tern.mean", "B")
            nc.tensor.matmul(mem[:, 0:2], W("ones128"), share[:, :], start=True, stop=True).then_inc(full("tern.mean"), 1)

        def ternary_vector(dve):
            mem = wait_full(dve, "tern.mean")
            half_mean = 0.5 / (512 * 128)
            link(dve, "vector_chain", nc.vector.tensor_scalar(thresh[:, :, 0], mem[:, 0:2], half_mean, None, ALU.mult))
            nc.vector.tensor_scalar(thresh[:, :, 1], mem[:, 0:2], -half_mean, None, ALU.mult).then_inc(read("tern.mean"), 1)

        def ternary_pool(pool):
            wait_read(pool, "tern.mean")
            pool.wait_ge(sem["tern.sum"], 2)
            for i, name in enumerate(TERNARY):
                w = W(name)
                link(pool, "pool_chain", nc.gpsimd.tensor_scalar(tern, w, thresh[:, i, 0:1], None, ALU.is_gt))
                link(pool, "pool_chain", nc.gpsimd.tensor_scalar(tern2, w, thresh[:, i, 1:2], None, ALU.is_lt))
                link(pool, "pool_chain", nc.gpsimd.tensor_tensor(tern, tern, tern2, ALU.subtract))
                link(pool, "pool_chain", nc.gpsimd.tensor_tensor(tern, tern, w, ALU.subtract))
                link(pool, "pool_chain", nc.gpsimd.tensor_tensor(w, w, tern, ALU.add))

        def l2x_tensor(pe):
            ternary_tensor(pe)
            biased_tensor(pe, L2X, ctxT, "l2x.Wq", "l2x.Wk", "l2x.Wv")

        def l2x_vector(dve):
            ternary_vector(dve)
            biased_vector(dve, L2X, ctxT, "l2x.bq", "l2x.bk", residual_ready(L2A))

        def l2x_scalar(act):
            ternary_scalar(act)
            biased_scalar(act, L2X, ctxT, "l2x.bq", "l2x.bk")

        def l2x_pool(pool):
            ln_pool(pool, "l2x")
            add_bias_pool(pool, "l2x", "l2x.bo")
            spread(pool, nc.gpsimd, L2X, 0, 0, POOL_HEADS, "pool")
            spread(pool, nc.gpsimd, L2X, 1, 0, POOL_HEADS, "pool")
            ternary_pool(pool)
            for t in range(2, T):
                spread(pool, nc.gpsimd, L2X, t, 0, POOL_HEADS, "pool")


        hid = scr[:, 0:4, :].rearrange("p a (b c) -> p (a b) c", c=512)
        hidT = scr[:, 4:8, :].rearrange("p a b -> p (a b)").rearrange("p (t c k) -> p t c k", t=T, c=4)
        junk = scr[:, 8, 0:512]
        row = sb("row", [P, 4, T])

        def l2f_tensor(pe):
            n = "l2f"
            tiles_T_tensor(pe, n + ".T", xn, n + ".scaled")
            wait_read(pe, n + ".T")
            for pair in range(T // 2):
                mem = fill(pe, f"{n}.up{pair}")
                for i in range(2):
                    t = 2 * pair + i
                    mm = nc.tensor.matmul(mem[:, 512 * i:512 * i + 512], xnT[:, t * P:(t + 1) * P], W("l2f.up"), start=True, stop=True)
                mm.then_inc(full(f"{n}.up{pair}"), 1)
            for pair in range(T // 2):
                wait_read(pe, f"{n}.up{pair}")
                mem = fill(pe, f"{n}.hT{pair}", fulls=2, reads=2)
                for i in range(2):
                    for c in range(4):
                        at = 512 * i + 128 * c
                        mm = nc.tensor.transpose(mem[:, at:at + 128], hid[:, 2 * pair + i, 128 * c:128 * c + 128], W("ident"))
                    mm.then_inc(full(f"{n}.hT{pair}"), 1)
            for half in range(2):
                for pair in (2 * half, 2 * half + 1):
                    wait_read(pe, f"{n}.hT{pair}")
                mem = fill(pe, f"{n}.y{half}", "B", reads=4)
                for t in range(4 * half, 4 * half + 4):
                    for c in range(4):
                        mm = nc.tensor.matmul(mem[:, (t % 4) * P:(t % 4 + 1) * P], hidT[:, t, c, :], W("l2f.down")[:, 128 * c:128 * c + 128],
                                              start=c == 0, stop=c == 3)
                mm.then_inc(full(f"{n}.y{half}"), 1)

        def l2f_scalar(act):
            n = "l2f"
            act.wait_ge(sem["xn"], at(n, "xn", T))
            nc.scalar.activation(scr[:, 9, :], xn[:, :, :].rearrange("p t d -> p (t d)"), ACT.Square).then_inc(sem[n + ".square"], 1)
            copy_half_scalar(act, n + ".T", xnT)
            for pair in range(T // 2):
                mem = wait_full(act, f"{n}.up{pair}")
                nc.scalar.activation(hid[:, 2 * pair:2 * pair + 2, :].rearrange("p a b -> p (a b)"), mem, ACT.Gelu)\
                  .then_inc(read(f"{n}.up{pair}"), 1)
            for t in range(T):
                wait_read(act, f"{n}.up{t // 2}")
                if t:
                    act.wait_ge(sem[n + ".ss"], t)
                nc.scalar.activation(junk, hid[:, t, :], ACT.Square, accum_out=row[:, 2, t:t + 1]).then_inc(sem[n + ".ss"], 1)
                if t % 2:
                    pair = t // 2
                    mem = wait_full(act, f"{n}.hT{pair}", 0)
                    nc.scalar.copy(hidT[:, 2 * pair, :, :].rearrange("p c k -> p (c k)"), mem[:, 0:512]).then_inc(read(f"{n}.hT{pair}"), 1)

        def rms_vector(dve, ch, ss, out_col, width, scale_width):
            rsqrt_vector(dve, ch, ss, out_col, scale_width)
            link(dve, ch, nc.vector.tensor_tensor(out_col, out_col, ss, ALU.mult))
            link(dve, ch, nc.vector.tensor_scalar(out_col, out_col, width ** -0.5, 1e-8, ALU.mult, ALU.add))
            link(dve, ch, nc.vector.reciprocal(out_col, out_col))

        def l2f_vector(dve):
            n = "l2f"
            ch = "vector_chain"
            ln_vector(dve, n, residual_ready(L2X))
            dve.wait_ge(sem[n + ".square"], 1)
            dve.wait_ge(sem["xn"], at(n, "xn", T))
            link(dve, ch, nc.vector.tensor_reduce(row[:, 0, :], scr[:, 9, :].rearrange("p (t d) -> p t d", t=T), AX, ALU.add))
            rms_vector(dve, ch, row[:, 0, :], row[:, 1, :], D, T)
            for t in range(T):
                nc.vector.tensor_scalar(xn[:, t, :], xn[:, t, :], row[:, 1, t:t + 1], None, ALU.mult).then_inc(sem[n + ".scaled"], 1)
            copy_half_vector(dve, n + ".T", xnT)
            for pair in range(T // 2):
                mem = wait_full(dve, f"{n}.hT{pair}", 1)
                nc.vector.tensor_copy(hidT[:, 2 * pair + 1, :, :].rearrange("p c k -> p (c k)"), mem[:, 512:1024])\
                  .then_inc(read(f"{n}.hT{pair}"), 1)
            dve.wait_ge(sem[n + ".ss"], T)
            rms_vector(dve, ch, row[:, 2, :], row[:, 3, :], 512, T)
            for t in range(T):
                mem = wait_full(dve, f"{n}.y{t // 4}")
                nc.vector.scalar_tensor_tensor(out=x_res[:, t, :], in0=mem[:, (t % 4) * P:(t % 4 + 1) * P], scalar=row[:, 3, t:t + 1],
                                               in1=x_res[:, t, :], op0=ALU.mult, op1=ALU.add).then_inc(read(f"{n}.y{t // 4}"), 1)

        def l2f_pool(pool):
            ln_pool(pool, "l2f")

        L2F_READY = lambda eng, t: wait_read(eng, f"l2f.y{t // 4}")


        L3A = biased_attention("l3a", "bias", False, "l2x", "L3_attn", "l3a.WO", "l3a.bV")
        L3X = biased_attention("l3x", "plain", True, "l3a", "L3_xattn", "l3x.Wo", "l3x.bv")
        rel_bias = scr[:, 11, :]

        def l3a_tensor(pe):
            biased_tensor(pe, L3A, xnT, "l3a.WQ", "l3a.WK", "l3a.WV")

        def l3a_vector(dve):
            c = W("causal").rearrange("p (o k) -> p o k", o=1).broadcast_to([P, 16, SEQ])
            link(dve, "vector_chain", nc.vector.tensor_tensor(rel_bias.rearrange("p (h k) -> p h k", k=SEQ),
                                                            W("l3a.rel").rearrange("p (h k) -> p h k", k=SEQ), c, ALU.add))
            biased_vector(dve, L3A, xnT, "l3a.bQ", "l3a.bK", L2F_READY)

        def l3a_scalar(act):
            biased_scalar(act, L3A, xnT, "l3a.bQ", "l3a.bK")

        def l3a_pool(pool):
            biased_pool(pool, L3A, "l3a.bO")

        def l3x_tensor(pe):
            biased_tensor(pe, L3X, ctxT, "l3x.Wq", "l3x.Wk", "l3x.Wv")

        def l3x_vector(dve):
            biased_vector(dve, L3X, ctxT, "l3x.bq", "l3x.bk", residual_ready(L3A))

        def l3x_scalar(act):
            biased_scalar(act, L3X, ctxT, "l3x.bq", "l3x.bk")

        def l3x_pool(pool):
            biased_pool(pool, L3X, "l3x.bo")


        z = xn
        half_shifted = kcT[:, :].rearrange("p (t d) -> p t d", t=T)
        turned = [scr[:, j, :] for j in (0, 1)]
        square4 = [scr[:, j, :] for j in (2, 3)]
        crossed = [scr[:, j, :] for j in (4, 5)]
        keys4 = [scr[:, j, :].rearrange("p (a b h k) -> p a b h k", a=4, b=2, h=2) for j in (6, 7)]
        qT4 = [scr[:, 8, 512 * j:512 * j + 512].rearrange("p (a k) -> p a k", a=4) for j in (0, 1)]
        out4 = [scr[:, 9, 512 * j:512 * j + 512] for j in (0, 1)]
        outT4 = [scr[:, 10, 512 * j:512 * j + 512] for j in (0, 1)]
        v4 = [v.rearrange("p b a w -> p (b a w)")[:, 0:1040].rearrange("p (b a w) -> p b a w", b=2, a=4) for v in (v_self, v_ctx)]
        gelu4, mlp4 = scr[:, 0:3, :], scr[:, 3:6, :]
        len_sq = sb("len_sq", [P, T, 16])
        len_inv = sb("len_inv", [P, T, 16])
        HIDDEN_ROWS = (128, 128, 85)
        LAYERS = ("l3g", "l3h")

        def z_ready(m):
            if m == "l3g":
                return lambda eng, t: eng.wait_ge(sem["xn"], at("l3f", "xn", t + 1))
            return lambda eng, t: wait_product_read(eng, f"l3g.mlp{t // 4}", t % 4)

        def wait_product_read(eng, name, tile):
            slot, _, _, done = book.record[name]
            eng.wait_ge(sem["read." + slot], done - 3 + tile)

        def steps(stages):
            for u in range(T + 7):
                for lag, piece in stages:
                    if 0 <= u - lag < T:
                        yield piece, u - lag

        def inner_attention_tensor(pe, m, i):
            mem = fill(pe, m + ".T", fulls=2, reads=2)
            for t in range(T):
                z_ready(m)(pe, t)
                nc.tensor.transpose(mem[0:64, t * P:(t + 1) * P], z[:, t, 0:64], W("ident"))
                mm = nc.tensor.matmul(mem[64:128, t * P:(t + 1) * P], z[:, t, 64:128], W("l3f.shift"), start=True, stop=True)
                if t % 4 == 3:
                    mm.then_inc(full(m + ".T"), 1)
            wait_read(pe, m + ".T")
            wqkv = W(f"l3f.wqkv{i}")

            def queries_keys(t):
                mem = fill(pe, f"{m}.qk{t}")
                for c in range(2):
                    mm = nc.tensor.matmul(mem[:, 512 * c:512 * c + 512], xnT[:, t * P:(t + 1) * P],
                                          wqkv[:, 512 * c:512 * c + 512], start=True, stop=True)
                mm.then_inc(full(f"{m}.qk{t}"), 1)

            def turned_T(t):
                pe.wait_ge(sem[m + ".unit"], t + 1)
                mem = fill(pe, f"{m}.qkT{t}", fulls=2, reads=3)
                for c in range(8):
                    mm = nc.tensor.transpose(mem[:, c * P:(c + 1) * P], turned[t % 2][:, c * P:(c + 1) * P], W("ident"))
                    if c % 4 == 3:
                        mm.then_inc(full(f"{m}.qkT{t}"), 1)

            def scores(t):
                wait_read(pe, f"{m}.qkT{t}")
                mem = fill(pe, f"{m}.s{t}", "B")
                for p in range(4):
                    for b in range(2):
                        mm = nc.tensor.matmul(mem[64 * b:64 * b + 64, p * P:(p + 1) * P], qT4[t % 2][:, p, 64 * b:64 * b + 64],
                                              keys4[t % 2][:, p, b, :, :], start=True, stop=True)
                mm.then_inc(full(f"{m}.s{t}"), 1)

            def values(t):
                mem = fill(pe, f"{m}.v{t}", "B", reads=2)
                wv = wqkv[:, 1024:1536].rearrange("p (a h f) -> p h a f", h=2, f=64)
                for b in range(2):
                    for h in range(2):
                        mm = nc.tensor.matmul(mem[64 * h:64 * h + 64, 256 * b:256 * b + 256],
                                              xnT[:, t * P + 64 * b:t * P + 64 * b + 64], wv[:, h], start=True, stop=True)
                mm.then_inc(full(f"{m}.v{t}"), 1)

            def prob_T(t):
                pe.wait_ge(sem["exp"], at(m, "exp", t + 1))
                mem = fill(pe, f"{m}.t{t}", "B")
                for p in range(4):
                    mm = nc.tensor.transpose(mem[:, p * P:(p + 1) * P], prob[t % 2][:, p * P:(p + 1) * P], W("ident"))
                mm.then_inc(full(f"{m}.t{t}"), 1)

            def outputs(t):
                wait_read(pe, f"{m}.t{t}")
                wait_read(pe, f"{m}.v{t}")
                mem = fill(pe, f"{m}.o{t}", reads=2)
                for p in range(4):
                    for b in range(2):
                        at_col = 512 * (p // 2) + 130 * (p % 2)
                        mm = nc.tensor.matmul(mem[64 * b:64 * b + 64, at_col:at_col + 130],
                                              probT[t % 2][:, p * P + 64 * b:p * P + 64 * b + 64], v4[t % 2][:, b, p, :],
                                              start=True, stop=True)
                mm.then_inc(full(f"{m}.o{t}"), 1)

            def outputs_T(t):
                wait_read(pe, f"{m}.o{t}")
                mem = fill(pe, f"{m}.ot{t}", "B")
                for c in range(4):
                    mm = nc.tensor.transpose(mem[:, c * P:(c + 1) * P], out4[t % 2][:, c * P:(c + 1) * P], W("ident"))
                mm.then_inc(full(f"{m}.ot{t}"), 1)

            def project(t):
                wait_read(pe, f"{m}.ot{t}")
                mem = fill(pe, f"{m}.y{t}", "B")
                for c in range(4):
                    mm = nc.tensor.matmul(mem[:, 0:P], outT4[t % 2][:, c * P:(c + 1) * P], W(f"l3f.wo{i}")[:, c * P:(c + 1) * P],
                                          start=c == 0, stop=c == 3)
                mm.then_inc(full(f"{m}.y{t}"), 1)

            for piece, t in steps([(6, project), (5, outputs_T), (4, outputs), (3, prob_T), (2, scores), (3, values),
                                   (1, turned_T), (0, queries_keys)]):
                piece(t)

        def inner_attention_vector(dve, m, i):
            mem = wait_full(dve, m + ".T", 1)
            nc.vector.tensor_copy(xnT[:, 512:], mem[:, 512:]).then_inc(read(m + ".T"), 1)

            def rotate(t):
                mem = wait_full(dve, f"{m}.qk{t}")
                dve.wait_ge(sem[m + ".square"], t + 1)
                nc.vector.tensor_reduce(len_sq[:, t, :], square4[t % 2].rearrange("p (g f) -> p g f", f=64), AX, ALU.add)\
                  .then_inc(sem[m + ".len"], 1)
                if t >= 2:
                    wait_full(dve, f"{m}.qkT{t - 2}", 1)
                    dve.wait_ge(sem[m + ".unit"], t - 1)
                elif i:
                    wait_full(dve, "l3g.mlp1")
                tab = W(f"l3f.scale{i}").rearrange("p (c a o f) -> p c a o f", c=2, a=2, o=1)
                qk = mem.rearrange("p (a h f) -> p a h f", a=2, f=64)
                c4 = crossed[t % 2].rearrange("p (a h f) -> p a h f", a=2, f=64)
                nc.vector.tensor_tensor(turned[t % 2].rearrange("p (a h f) -> p a h f", a=2, f=64), qk,
                                        tab[:, 0].broadcast_to([P, 2, 8, 64]), ALU.mult).then_inc(sem[m + ".turn"], 1)
                for lo, hi in ((0, 32), (32, 0)):
                    nc.vector.tensor_tensor(c4[:, :, :, lo:lo + 32], qk[:, :, :, hi:hi + 32],
                                            tab[:, 1, :, :, lo:lo + 32].broadcast_to([P, 2, 8, 32]), ALU.mult)\
                      .then_inc(read(f"{m}.qk{t}") if lo else sem[m + ".turn"], 1)

            def softmax(t):
                mem = wait_full(dve, f"{m}.s{t}")
                if t >= 2:
                    wait_full(dve, f"{m}.t{t - 2}")
                    dve.wait_ge(sem["less"], at(m, "less", t - 1))
                pr = prob[t % 2][:, 0:512].rearrange("p (h k) -> p h k", k=SEQ)
                c = W("causal").rearrange("p (o k) -> p o k", o=1).broadcast_to([P, 8, SEQ])
                nc.vector.scalar_tensor_tensor(out=pr, in0=mem.rearrange("p (h k) -> p h k", k=SEQ), scalar=8.0, in1=c,
                                               op0=ALU.mult, op1=ALU.add).then_inc(read(f"{m}.s{t}"), 1)
                wait_read(dve, f"{m}.s{t}")
                nc.vector.tensor_reduce(top[t % 2][:, 0:8], pr, AX, ALU.max).then_inc(sem["top"], 1)
                dve.wait_ge(sem["top"], at(m, "top", t + 1))
                tb = top[t % 2][:, 0:8].rearrange("p (h o) -> p h o", o=1).broadcast_to([P, 8, SEQ])
                nc.vector.tensor_tensor(pr, pr, tb, ALU.subtract).then_inc(sem["less"], 1)

            def normalise(t):
                mem = wait_full(dve, f"{m}.o{t}")
                if t >= 2:
                    wait_full(dve, f"{m}.ot{t - 2}")
                v = mem.rearrange("p (g w) -> p g w", g=2)[:, :, 0:260].rearrange("p g (a w) -> p g a w", w=130)
                rd = rden[t % 2][:, 0:8].rearrange("p (g a h) -> p g a h", g=2, a=2)
                nc.vector.reciprocal(rd, v[:, :, :, 128:130]).then_inc(sem["rden"], 1)
                dve.wait_ge(sem["rden"], at(m, "rden", t + 1))
                for g in range(2):
                    to = out4[t % 2][:, 256 * g:256 * g + 256].rearrange("p (a h f) -> p a h f", h=2, f=64)
                    rb = rd[:, g].rearrange("p a (h o) -> p a h o", o=1).broadcast_to([P, 2, 2, 64])
                    nc.vector.tensor_tensor(to, v[:, g, :, 0:128].rearrange("p a (h f) -> p a h f", h=2), rb, ALU.mult)\
                      .then_inc(read(f"{m}.o{t}"), 1)

            def residual(t):
                mem = wait_full(dve, f"{m}.y{t}")
                nc.vector.tensor_tensor(z[:, t, :], z[:, t, :], mem[:, 0:P], ALU.add).then_inc(read(f"{m}.y{t}"), 1)

            for piece, t in steps([(6, residual), (4, normalise), (2, softmax), (3, lambda t: values4_copy(dve, m, t, 1)),
                                   (0, rotate)]):
                piece(t)

        def values4_copy(eng, m, t, h):
            mem = wait_full(eng, f"{m}.v{t}")
            if t >= 2:
                wait_full(eng, f"{m}.o{t - 2}")
            elif h == 0:
                eng.wait_ge(sem["v4_set"], 6)
            src = mem[64 * h:64 * h + 64, 0:512].rearrange("p (b a f) -> p b a f", b=2, f=64)
            to = v4[t % 2][64 * h:64 * h + 64, :, :, 64 * h:64 * h + 64]
            (nc.vector.tensor_copy if h else nc.scalar.copy)(to, src).then_inc(read(f"{m}.v{t}"), 1)

        def inner_attention_scalar(act, m, i):
            copy_half_scalar(act, m + ".T", xnT)

            def squares(t):
                mem = wait_full(act, f"{m}.qk{t}")
                if t >= 2:
                    act.wait_ge(sem[m + ".len"], t - 1)
                elif i:
                    wait_full(act, "l3g.mlp1")
                nc.scalar.activation(square4[t % 2], mem, ACT.Square).then_inc(sem[m + ".square"], 1)

            def turned_copy(t):
                if t >= 2:
                    wait_full(act, f"{m}.s{t - 2}")
                elif i == 0:
                    act.wait_ge(sem["v4_set"], 6)
                mem = wait_full(act, f"{m}.qkT{t}", 0)
                nc.scalar.copy(qT4[t % 2][:, :, :].rearrange("p a k -> p (a k)"), mem[:, 0:512]).then_inc(read(f"{m}.qkT{t}"), 1)
                wait_full(act, f"{m}.qkT{t}", 1)
                for h in range(2):
                    rows = slice(64 * h, 64 * h + 64)
                    nc.scalar.copy(keys4[t % 2][rows, :, :, h, :], mem[rows, 512:1024].rearrange("p (a b k) -> p a b k", a=4, b=2))\
                      .then_inc(read(f"{m}.qkT{t}"), 1)

            def exponential(t):
                act.wait_ge(sem["less"], at(m, "less", t + 1))
                nc.scalar.activation(prob[t % 2][:, 0:512], prob[t % 2][:, 0:512], ACT.Exp).then_inc(sem["exp"], 1)

            def prob_copy(t):
                if t >= 2:
                    wait_full(act, f"{m}.o{t - 2}")
                mem = wait_full(act, f"{m}.t{t}")
                nc.scalar.copy(probT[t % 2][:, 0:512], mem[:, 0:512]).then_inc(read(f"{m}.t{t}"), 1)

            def outputs_copy(t):
                if t >= 2:
                    wait_full(act, f"{m}.y{t - 2}")
                mem = wait_full(act, f"{m}.ot{t}")
                nc.scalar.copy(outT4[t % 2], mem[:, 0:512]).then_inc(read(f"{m}.ot{t}"), 1)

            for piece, t in steps([(5, outputs_copy), (3, prob_copy), (3, lambda t: values4_copy(act, m, t, 0)),
                                   (2, exponential), (1, turned_copy), (0, squares)]):
                piece(t)

        def inner_attention_pool(pool, m, i):
            for t in range(T):
                pool.wait_ge(sem[m + ".len"], t + 1)
                link(pool, "pool_chain", nc.gpsimd.tensor_scalar(len_inv[:, t, :], len_sq[:, t, :], 1e-24, None, ALU.max))
                half = minus_half[:, 0:1].broadcast_to([P, 16])
                link(pool, "pool_chain", nc.gpsimd.tensor_tensor(len_inv[:, t, :], len_inv[:, t, :], half, ALU.pow))
                pool.wait_ge(sem[m + ".turn"], 2 * t + 2)
                wait_product(pool, f"{m}.qk{t}")
                link(pool, "pool_chain", nc.gpsimd.tensor_tensor(turned[t % 2], turned[t % 2], crossed[t % 2], ALU.add))
                r = len_inv[:, t, :].rearrange("p (g o) -> p g o", o=1).broadcast_to([P, 16, 64])
                t3 = turned[t % 2].rearrange("p (g f) -> p g f", f=64)
                nc.gpsimd.tensor_tensor(t3, t3, r, ALU.mult).then_inc(sem[m + ".unit"], 1)

        def wait_product(eng, name):
            wait_read(eng, name)


        def inner_mlp_tensor(pe, m, i):
            for t in range(T):
                wait_read(pe, f"{m}.y{t}")
            mem = fill(pe, m + ".shift", "B")
            nc.tensor.matmul(mem, W("l3f.shift"), z[:, :, 64:128], start=True, stop=True).then_inc(full(m + ".shift"), 1)
            tiles_T_tensor(pe, m + ".hT", half_shifted, "xn", at(m, "xn", 0))
            wait_read(pe, m + ".hT")
            for c, rows in enumerate(HIDDEN_ROWS):
                for part in ("g", "a"):
                    mem = fill(pe, f"{m}.{part}{c}")
                    lo = P * c + (341 if part == "g" else 0)
                    for half in range(2):
                        s = slice(512 * half, 512 * half + 512)
                        mm = nc.tensor.matmul(mem[0:rows, s], W(f"l3f.w1_{i}")[:, lo:lo + rows], xnT[:, s], start=True, stop=True)
                    mm.then_inc(full(f"{m}.{part}{c}"), 1)
            for c in range(3):
                wait_read(pe, f"{m}.a{c}")
            for half in range(2):
                mem = fill(pe, f"{m}.mlp{half}", "B", reads=4)
                for t in range(4 * half, 4 * half + 4):
                    for c, rows in enumerate(HIDDEN_ROWS):
                        mm = nc.tensor.matmul(mem[:, (t % 4) * P:(t % 4 + 1) * P], mlp4[0:rows, c, t * P:(t + 1) * P],
                                              W(f"l3f.w2_{i}")[0:rows, c * P:(c + 1) * P], start=c == 0, stop=c == 2)
                mm.then_inc(full(f"{m}.mlp{half}"), 1)

        def inner_mlp_vector(dve, m, i):
            def ready(eng, t):
                eng.wait_ge(sem[m + ".first_half"], 1)
                wait_read(eng, m + ".shift")

            ln_vector(dve, m, ready, half_shifted, half_shifted)
            mem = wait_full(dve, m + ".hT", 1)
            nc.vector.tensor_scalar(xnT[:, 512:], mem[:, 512:], W(f"l3f.ln_g{i}"), W(f"l3f.ln_b{i}"), ALU.mult, ALU.add)\
              .then_inc(read(m + ".hT"), 1)
            for c, rows in enumerate(HIDDEN_ROWS):
                mem = wait_full(dve, f"{m}.a{c}")
                wait_read(dve, f"{m}.g{c}")
                nc.vector.scalar_tensor_tensor(out=mlp4[0:rows, c, :], in0=mem[0:rows, :], scalar=W(f"l3f.b1a{i}")[0:rows, c:c + 1],
                                               in1=gelu4[0:rows, c, :], op0=ALU.add, op1=ALU.mult).then_inc(read(f"{m}.a{c}"), 1)
            dve.wait_ge(sem[m + ".b2"], 1)
            for t in range(T):
                mem = wait_full(dve, f"{m}.mlp{t // 4}")
                nc.vector.tensor_tensor(z[:, t, :], z[:, t, :], mem[:, (t % 4) * P:(t % 4 + 1) * P], ALU.add)\
                  .then_inc(read(f"{m}.mlp{t // 4}"), 1)

        def inner_mlp_scalar(act, m, i):
            mem = wait_full(act, m + ".shift")
            nc.scalar.copy(half_shifted[:, :, 64:128], mem.rearrange("p (t d) -> p t d", t=T)).then_inc(read(m + ".shift"), 1)
            mem = wait_full(act, m + ".hT", 0)
            nc.scalar.activation(xnT[:, 0:512], mem[:, 0:512], ACT.Identity, scale=W(f"l3f.ln_g{i}"), bias=W(f"l3f.ln_b{i}"))\
              .then_inc(read(m + ".hT"), 1)
            for c, rows in enumerate(HIDDEN_ROWS):
                mem = wait_full(act, f"{m}.g{c}")
                nc.scalar.activation(gelu4[0:rows, c, :], mem[0:rows, :], ACT.Gelu, bias=W(f"l3f.b1g{i}")[0:rows, c:c + 1])\
                  .then_inc(read(f"{m}.g{c}"), 1)

        def inner_mlp_pool(pool, m, i):
            for t in range(T):
                wait_read(pool, f"{m}.y{t}")
            nc.gpsimd.tensor_copy(half_shifted[:, :, 0:64], z[:, :, 0:64]).then_inc(sem[m + ".first_half"], 1)
            pool.wait_ge(sem[m + ".first_half"], 1)
            ln_pool(pool, m)
            wait_full(pool, m + ".shift")
            nc.gpsimd.tensor_tensor(z[:, :, :], z[:, :, :], tok_bias(f"l3f.b2_{i}"), ALU.add).then_inc(sem[m + ".b2"], 1)

        def l3f_tensor(pe):
            pe.wait_ge(sem["v4_set"], 6)
            for i, m in enumerate(LAYERS):
                inner_attention_tensor(pe, m, i)
                inner_mlp_tensor(pe, m, i)

        def l3f_vector(dve):
            ln_vector(dve, "l3f", residual_ready(L3X))
            for t in (T - 2, T - 1):
                wait_full(dve, f"l3x.o{t}")
            for j in range(2):
                link(dve, "vector_chain", nc.vector.memset(v4[j][:, :, :, :], 0.0))
                for h in range(2):
                    nc.vector.memset(v4[j][64 * h:64 * h + 64, :, :, 128 + h:129 + h], 1.0).then_inc(sem["v4_set"], 1)
                nc.vector.memset(keys4[j][:, :, :, :, :], 0.0).then_inc(sem["v4_set"], 1)
            dve.wait_ge(sem["v4_set"], 6)
            dve.wait_ge(sem["rope_table"], 2)
            for i, m in enumerate(LAYERS):
                inner_attention_vector(dve, m, i)
                inner_mlp_vector(dve, m, i)
            for t in range(T):
                z_ready_last(dve, t)
                nc.vector.tensor_tensor(x_res[:, t, :], x_res[:, t, :], z[:, t, :], ALU.add).then_inc(sem["l3f.x"], 1)

        def z_ready_last(eng, t):
            wait_product_read(eng, f"l3h.mlp{t // 4}", t % 4)

        def l3f_scalar(act):
            for i, m in enumerate(LAYERS):
                inner_attention_scalar(act, m, i)
                inner_mlp_scalar(act, m, i)

        def l3f_pool(pool):
            ln_pool(pool, "l3f")
            for i in range(2):
                nc.gpsimd.tensor_tensor(W(f"l3f.scale{i}"), W(f"l3f.scale{i}"), W("l3f.rope"), ALU.mult)\
                  .then_inc(sem["rope_table"], 1)
            for i, m in enumerate(LAYERS):
                inner_attention_pool(pool, m, i)
                inner_mlp_pool(pool, m, i)

        def setup_vector(dve):
            nc.vector.memset(minus_half[:, :], -0.5).then_inc(sem["minus_half"], 1)
            for p0, lo, hi, value in ((0, 16, 32, 0.0), (0, 32, 33, 1.0), (0, 33, 34, 0.0),
                                      (64, 0, 16, 0.0), (64, 32, 33, 0.0), (64, 33, 34, 1.0)):
                nc.vector.memset(v_lstm[p0:p0 + 64, :, :, lo:hi], value).then_inc(sem["lstm_values_set"], 1)
            nc.vector.memset(lstm[:, 3, :], 0.0).then_inc(sem["lstm_values_set"], 1)
            for v in (v_self, v_ctx):
                for p0, lo, hi, value in ((0, 8, 16, 0.0), (0, 16, 17, 1.0), (0, 17, 18, 0.0),
                                          (64, 0, 8, 0.0), (64, 16, 17, 0.0), (64, 17, 18, 1.0)):
                    nc.vector.memset(v[p0:p0 + 64, :, :, lo:hi], value).then_inc(sem["values_set"], 1)

        stages = [
            ("0a", l0a_tensor, l0a_vector, l0a_scalar, l0a_pool, residual_ready(L0A)),
            ("0x", l0x_tensor, l0x_vector, l0x_scalar, l0x_pool, residual_ready(L0X)),
            ("0f", l0f_tensor, l0f_vector, l0f_scalar, l0f_pool, L0F_READY),
            ("1", l1a_tensor, l1a_vector, l1a_scalar, l1a_pool, product_ready("l1a.y")),
            ("1", l1x_tensor, l1x_vector, l1x_scalar, l1x_pool, residual_ready(L1X)),
            ("1", l1f_tensor, l1f_vector, l1f_scalar, l1f_pool, L1F_READY),
            ("2", l2a_tensor, l2a_vector, l2a_scalar, l2a_pool, residual_ready(L2A)),
            ("2", l2x_tensor, l2x_vector, l2x_scalar, l2x_pool, residual_ready(L2X)),
            ("2", l2f_tensor, l2f_vector, l2f_scalar, l2f_pool, L2F_READY),
            ("3", l3a_tensor, l3a_vector, l3a_scalar, l3a_pool, residual_ready(L3A)),
            ("3", l3x_tensor, l3x_vector, l3x_scalar, l3x_pool, residual_ready(L3X)),
            ("4", l3f_tensor, l3f_vector, l3f_scalar, l3f_pool, lambda eng, t: eng.wait_ge(sem["l3f.x"], t + 1)),
        ]

        block = ctx.enter_context(nc.Block())

        @block.tensor
        def _(pe):
            weights(pe, "c")
            context_tensor(pe)
            for s in stages:
                weights(pe, s[0])
                s[1](pe)

        @block.vector
        def _(dve):
            setup_vector(dve)
            weights(dve, "c")
            context_vector(dve)
            for s in stages:
                weights(dve, s[0])
                s[2](dve)

        @block.scalar
        def _(act):
            weights(act, "c")
            context_scalar(act)
            for s in stages:
                weights(act, s[0])
                s[3](act)

        @block.gpsimd
        def _(pool):
            weights(pool, "c")
            pool.wait_ge(sem["minus_half"], 1)
            for s in stages:
                weights(pool, s[0])
                s[4](pool)

        @block.sync
        def _(sp):
            sp.dma_start(x_res[:, :, :], dram["x"].rearrange("t p d -> p t d")).then_inc(sem["x_loaded"], 16)
            sp.dma_start(packed["c"][:, :], dram["c"]).then_inc(sem["pack.c"], 16)
            sp.dma_start(ctx_tok, dram["ctx"].rearrange("t p d -> p t d")).then_inc(sem["ctx_loaded"], 16)
            sp.dma_start(packed["0a"][:, :], dram["0a"]).then_inc(sem["pack.0a"], 16)
            for h in range(2):
                sp.dma_start(ctx_keys[64 * h:64 * h + 64, :, :],
                             dram["ctx"].rearrange("t (b k) d -> k (t b) d", b=2)).then_inc(sem["ctx_keys_loaded"], 16)
            for g in packs[2:]:
                if g == "4":
                    for t in range(T):
                        L1F_READY(sp, t)
                sp.dma_start(packed[g][:, :], dram[g]).then_inc(sem["pack." + g], 16)
            for t in range(T):
                stages[-1][5](sp, t)
            sp.dma_start(out.rearrange("t p d -> p t d"), x_res[:, :, :]).then_inc(sem["stored"], 16)
            sp.wait_ge(sem["stored"], 16)



def arrange(inputs):
    import numpy as np

    i = {k: np.asarray(v) for k, v in inputs.items()}
    packs = {}
    where = {}

    def put(pack, name, a):
        a = np.asarray(a)
        assert a.dtype == np.float32, (name, a.dtype)
        cols = packs.setdefault(pack, [])
        at = sum(c.shape[1] for c in cols)
        where[name] = (pack, at, a.shape[0], a.shape[1])
        if a.shape[0] < P:
            a = np.concatenate([a, np.zeros((P - a.shape[0], a.shape[1]), np.float32)], 0)
        cols.append(a)

    pos = np.arange(SEQ)
    feature = np.arange(P)
    put("c", "ident", np.eye(P, dtype=np.float32))
    put("c", "head_mask", (feature[:, None] // 8 == np.arange(16)[None]).astype(np.float32))
    put("c", "head_mask8", (feature[:, None] // 16 == np.arange(8)[None]).astype(np.float32))
    decay = np.exp(-0.01 * np.abs(pos[:, None] - pos[None]).astype(np.float32)) / np.float32(np.sqrt(128))
    put("c", "decay", np.tile(decay.astype(np.float32), (2, 1)))
    put("c", "causal", np.tile(np.where(pos[None] <= pos[:, None], 0, MASKED).astype(np.float32), (2, 1)))
    for w in ("W_k", "W_v", "W_q", "W_down_kv", "W_up_k", "W_up_v", "W_o"):
        put("0a", "L0_attn_" + w, i["L0_attn_" + w])
    for part, rows in (("q", slice(0, 128)), ("k", slice(128, 256)), ("v", slice(256, 384))):
        g = np.zeros((P, 40), np.float32)
        g[:, 0:8] = i["L0_xattn_igate_kernel"][rows]
        g[:, 32:40] = i["L0_xattn_fgate_kernel"][rows]
        put("0x", "l0x.gate_" + part, g)
    g = np.zeros((40, 1), np.float32)
    g[0:8, 0], g[32:40, 0] = i["L0_xattn_igate_bias"], i["L0_xattn_fgate_bias"]
    put("0x", "l0x.gate_bias", g)
    put("0x", "ones8", np.ones((8, 64), np.float32))
    start = np.arange(TOK)[None] % SEQ == 0
    put("0x", "keep", np.tile(np.where(start, 0, 1).astype(np.float32), (8, 1)))
    put("0x", "restart", np.tile(np.where(start, 2 * MASKED, 0).astype(np.float32), (8, 1)))

    def column(v):
        return v.reshape(-1, 1)

    def chunks(v):
        return np.ascontiguousarray(v.reshape(-1, P).T)

    def rows(v):
        return np.broadcast_to(v.reshape(1, -1), (P, v.size))

    f = "L0_ffn_"
    put("0f", f + "enc_W", i[f + "enc_W"])
    put("0f", "l0f.enc_b", chunks(i[f + "enc_b"]))
    for c in range(2):
        put("0f", f"l0f.s2c{c}", i[f + "s2c_W"][128 * c:128 * c + 128])
    put("0f", "l0f.s2c_b", column(i[f + "s2c_b"]))
    put("0f", f + "rW1", i[f + "rW1"])
    put("0f", "l0f.rb1", column(i[f + "rb1"]))
    put("0f", f + "rW2", i[f + "rW2"])
    put("0f", "l0f.rb2", rows(i[f + "rb2"]))
    for e in range(8):
        put("0f", f"l0f.We1_{e}", i[f + "We1"][e])
        put("0f", f"l0f.We2_{e}", i[f + "We2"][e])
    put("0f", "l0f.be1", i[f + "be1"].T)
    put("0f", "l0f.be2", i[f + "be2"].reshape(4, P).T)
    for p in range(4):
        put("0f", f"l0f.pair{p}", (np.arange(8)[:, None] == 2 * p + np.arange(P)[None] // 64).astype(np.float32))
    put("0f", "before", rows((np.arange(8)[None] < np.arange(8)[:, None]).astype(np.float32)))
    put("0f", "l0f.c2s2", np.concatenate([i[f + "c2s_W"]] * 2, 0))
    put("0f", "l0f.c2s_b", chunks(i[f + "c2s_b"]))
    for c in range(2):
        put("0f", f"l0f.dec{c}", i[f + "dec_W"][128 * c:128 * c + 128])
    for b in ("dec_b", "ln_g", "ln_b"):
        put("0f", "l0f." + b, rows(i[f + b]))

    for m in ("r", "w", "k", "v", "a", "g", "out"):
        put("1", "L1_attn_W_" + m, i["L1_attn_W_" + m].T)
    for m in ("r", "w", "k", "v", "a", "g"):
        put("1", "l1a.x_" + m, column(i["L1_attn_x_" + m]))
    put("1", "l1a.gn_w", column(i["L1_attn_gn_w"]))
    put("1", "l1a.gn_b", column(i["L1_attn_gn_b"]))
    put("1", "l1a.b_out", rows(i["L1_attn_b_out"]))
    for m in ("Wq", "Wk", "Wv"):
        put("1", "L1_xattn_" + m, i["L1_xattn_" + m].T)
    put("1", "L1_ffn_W_fc", i["L1_ffn_W_fc"].T)
    for c in range(4):
        put("1", f"l1f.proj{c}", i["L1_ffn_W_proj"].T[128 * c:128 * c + 128])

    angle = pos[:, None].astype(np.float32) * (1.0 / 10000.0 ** (np.arange(4, dtype=np.float32) / 4))[None]
    put("2", "cos8", np.tile(np.cos(angle).astype(np.float32), (2, 2)))
    put("2", "sin8", np.tile(np.concatenate([-np.sin(angle), np.sin(angle)], 1).astype(np.float32), (2, 1)))
    w = i["L2_attn_Wqkv"]
    swapped = np.arange(256).reshape(32, 2, 4)[:, ::-1].reshape(-1)
    put("2", "l2a.qk_rot", np.concatenate([w[:, 0:256], w[:, swapped]], 1))
    put("2", "l2a.Wv", w[:, 256:384])
    put("2", "L2_attn_Wo", i["L2_attn_Wo"])
    put("2", "l2a.bo", rows(i["L2_attn_bo"]))
    for m in ("Wq", "Wk", "Wv", "Wo"):
        put("2", "l2x." + m, i["L2_xattn_" + m].T)
    for m in ("bq", "bk", "bv"):
        put("2", "l2x." + m, column(i["L2_xattn_" + m]))
    put("2", "l2x.bo", rows(i["L2_xattn_bo"]))
    put("2", "l2f.up", i["L2_ffn_w_up"].T)
    put("2", "l2f.down", np.concatenate([i["L2_ffn_w_down"].T[128 * c:128 * c + 128] for c in range(4)], 1))
    put("2", "ones128", np.ones((P, P), np.float32))

    for m in ("WQ", "WK", "WV", "WO"):
        put("3", "l3a." + m, i["L3_attn_" + m].T)
    for m in ("bQ", "bK", "bV"):
        put("3", "l3a." + m, column(i["L3_attn_" + m]))
    put("3", "l3a.bO", rows(i["L3_attn_bO"]))
    rel = i["L3_attn_rel_pos_table"][pos[:, None] - pos[None] + 255]
    rel = rel.transpose(0, 2, 1).reshape(SEQ, -1)
    put("3", "l3a.rel", np.concatenate([rel, rel], 0))
    for m in ("Wq", "Wk", "Wv", "Wo"):
        put("3", "l3x." + m, i["L3_xattn_" + m])
    for m in ("bq", "bk", "bv"):
        put("3", "l3x." + m, column(i["L3_xattn_" + m]))
    put("3", "l3x.bo", rows(i["L3_xattn_bo"]))

    put("4", "l3f.shift", ((feature[:, None] == feature[None] - 1) & (feature[None] % SEQ != 0)).astype(np.float32))
    f = "L3_ffn_"
    half = np.arange(0, 64, 2, dtype=np.float32)
    at = np.arange(SEQ, dtype=np.float32)
    angle = at[:, None] * (1.0 / 10000.0 ** (half / 64))[None]
    power = (at - SEQ // 2) / 32.0
    grow = ((half + 0.4 * 64) / (1.4 * 64))[None] ** power[:, None]
    twice = lambda a: np.concatenate([a, a], 1)
    cos, grow, sin = twice(np.cos(angle)), twice(grow), np.concatenate([-np.sin(angle), np.sin(angle)], 1)
    rope = np.concatenate([cos * grow, cos / grow, sin * grow, sin / grow], 1).astype(np.float32)
    put("4", "l3f.rope", np.tile(rope, (2, 1)))
    other = (np.arange(64) + 32) % 64
    for l in range(2):
        qs, ks = i[f + "q_scale"][l].reshape(-1), i[f + "k_scale"][l].reshape(-1)
        put("4", f"l3f.scale{l}", np.broadcast_to(np.concatenate([qs, ks, qs[other], ks[other]])[None], (P, 256)))
        put("4", f"l3f.wqkv{l}", i[f + "wqkv"][l])
        put("4", f"l3f.wo{l}", np.concatenate([i[f + "wo"][l][128 * c:128 * c + 128] for c in range(4)], 1))
        put("4", f"l3f.ln_g{l}", column(i[f + "ln_g"][l]))
        put("4", f"l3f.ln_b{l}", column(i[f + "ln_b"][l]))
        put("4", f"l3f.w1_{l}", i[f + "w1"][l])

        def padded(v):
            v = v.reshape(341, -1)
            v = np.concatenate([v, np.zeros((384 - 341, v.shape[1]), np.float32)], 0)
            return np.concatenate([v[128 * c:128 * c + 128] for c in range(3)], 1)

        put("4", f"l3f.b1a{l}", padded(i[f + "b1"][l][:341]))
        put("4", f"l3f.b1g{l}", padded(i[f + "b1"][l][341:]))
        put("4", f"l3f.w2_{l}", padded(i[f + "w2"][l]))
        put("4", f"l3f.b2_{l}", rows(i[f + "b2"][l]))
    arrays = {g: np.concatenate(c, 1) for g, c in packs.items()}
    arrays["x"] = i["x"].reshape(T, P, D)
    arrays["ctx"] = i["ctx_1024"].reshape(T, P, D)
    return arrays, where


def kernel(**inputs):
    import numpy as np
    import concourse.bacc as bacc
    from concourse.bass_utils import run_bass_kernel_spmd

    arrays, where = arrange(inputs)
    nc = bacc.Bacc("TRN2", target_bir_lowering=False, num_devices=1)
    dram = {g: nc.dram_tensor("in_" + g, a.shape, F32, kind="ExternalInput").ap() for g, a in arrays.items()}
    out = nc.dram_tensor("out", (T, P, D), F32, kind="ExternalOutput").ap()
    build(nc, dram, where, out)
    r = run_bass_kernel_spmd(nc, [{"in_" + g: a for g, a in arrays.items()}], core_ids=[0])
    return np.asarray(r.results[0]["out"]).reshape(NSEQ, SEQ, D)
```

```python
from contextlib import ExitStack

import concourse.bass as bass
from concourse import mybir

F32 = mybir.dt.float32
ALU = mybir.AluOpType
ACT = mybir.ActivationFunctionType
AX = mybir.AxisListType.X

P = 128
NSEQ, SEQ, D = 16, 64, 128
TOK = NSEQ * SEQ
T = TOK // P
LN_EPS = 1e-5
MASKED = -1e30


STAGES = ("l0a", "l0x", "l0f", "l1a", "l1x", "l1f", "l2a", "l2x", "l2f", "l3a", "l3x", "l3f", "l3g", "l3h")


EARLY = ("0a", "0x", "0f", "1")


def per_stage(**counts):
    return [counts.get(n, counts.get("rest", 0)) for n in STAGES]


SIGNALS = {
    "stats": per_stage(l0f=2 * T, rest=T),
    "moments": per_stage(l0f=2 * T, rest=T),
    "var": per_stage(l0f=T, rest=T // 2),
    "rstd": per_stage(l0f=T, rest=T // 2),
    "xn": per_stage(rest=T),
    "keys_pool": per_stage(l0a=T, l0x=T, l1x=T, l2a=T, l2x=T, l3a=T, l3x=T),
    "keys_dve": per_stage(l0a=T, l0x=T, l1x=T, l2a=T, l3a=T, l3x=T),
    "top": per_stage(l0a=2 * T, l1x=2 * T, l2x=T, l3a=2 * T, l3x=2 * T, l3g=T, l3h=T),
    "rden": per_stage(l0a=T, l1x=T, l2a=T, l2x=T, l3a=T, l3x=T, l3g=T, l3h=T),
    "less": per_stage(l0a=2 * T, l0x=T, l0f=1, l2x=T, l3a=2 * T, l3g=T, l3h=T),
    "exp": per_stage(l0a=2 * T, l0f=1, l1x=2 * T, l2x=T, l3a=2 * T, l3x=2 * T, l3g=T, l3h=T),
    "b_out": per_stage(l0f=1, l1a=1, l2a=1, l2x=1, l3a=1, l3x=1),
}


class PsumBook:

    def __init__(self, rings):
        self.rings = rings
        self.turn = {r: 0 for r in rings}
        self.full = {}
        self.read = {}
        self.record = {}
        self.reads = {}

    def place(self, name, ring, fulls, reads):
        slots = self.rings[ring]
        slot = slots[self.turn[ring] % len(slots)]
        self.turn[ring] += 1
        before, base = self.read.get(slot, 0), self.full.get(slot, 0)
        self.read[slot], self.full[slot] = before + reads, base + fulls
        assert name not in self.record, name
        self.record[name] = (slot, base, fulls, before + reads)
        self.reads[name] = reads
        return slot, before

    def whole(self, name, part=None):
        slot, base, fulls, _ = self.record[name]
        return slot, base + (fulls if part is None else part + 1)

    def done(self, name, part=None):
        slot, _, _, read = self.record[name]
        return slot, read if part is None else read - self.reads[name] + part + 1


def build(nc, dram, where, out):
    with ExitStack() as ctx:
        def sb(name, shape):
            return ctx.enter_context(nc.sbuf_tensor(name, shape, F32))

        class Sems(dict):
            def __missing__(self, name):
                self[name] = ctx.enter_context(nc.semaphore(name.replace(".", "_")))
                return self[name]

        sem = Sems()

        def at(n, part, value):
            counts = SIGNALS[part]
            return sum(counts[:STAGES.index(n)]) + value

        psum = ctx.enter_context(nc.psum_tensor("psum", [P, 8, 512], F32))
        slots = {"a0": psum[:, 0:2, :], "a1": psum[:, 2:4, :], "a2": psum[:, 4:6, :],
                 "b0": psum[:, 6:7, :], "b1": psum[:, 7:8, :]}
        flat = {k: v.rearrange("p a b -> p (a b)") for k, v in slots.items()}
        book = PsumBook({"A": ["a0", "a1", "a2"], "B": ["b0", "b1"]})

        packs = list(dict.fromkeys(w[0] for w in where.values()))
        width = {g: dram[g].shape[1] for g in packs}
        packed = {g: sb("w_" + g, [P, width[g]]) for g in ("c", "2", "3")}
        early = sb("w_early", [P, max(sum(width[g] for g in EARLY), width["4"])])
        for i, g in enumerate(EARLY):
            start = sum(width[h] for h in EARLY[:i])
            packed[g] = early[:, start:start + width[g]]
        packed["4"] = early[:, 0:width["4"]]

        def W(name):
            g, c, rows, cols = where[name]
            return packed[g][0:rows, c:c + cols]

        def W_padded(name):
            g, c, rows, cols = where[name]
            return packed[g][:, c:c + cols]

        def Wk(name, k):
            return W(name).rearrange("p (k n) -> p k n", k=k)

        def weights(eng, g):
            eng.wait_ge(sem["pack." + g], 16)

        def fill(pe, name, ring="A", fulls=1, reads=1):
            slot, before = book.place(name, ring, fulls, reads)
            if before:
                pe.wait_ge(sem["read." + slot], before)
            return flat[slot]

        def full(name):
            return sem["full." + book.record[name][0]]

        def read(name):
            return sem["read." + book.record[name][0]]

        def wait_full(eng, name, part=None):
            slot, value = book.whole(name, part)
            eng.wait_ge(sem["full." + slot], value)
            return flat[slot]

        def memory(name):
            return flat[book.record[name][0]]

        def wait_read(eng, name, part=None):
            slot, value = book.done(name, part)
            eng.wait_ge(sem["read." + slot], value)

        x_res = sb("x_res", [P, T, D])
        xn = sb("xn", [P, T, D])
        xnT = sb("xnT", [P, TOK])
        ctxT = sb("ctxT", [P, TOK])
        qT = sb("qT", [P, TOK])
        kT = sb("kT", [P, TOK])
        kcT = sb("kcT", [P, TOK])
        keys = [sb(f"keys{i}", [P, 16, P]) for i in range(2)]
        prob = [sb(f"prob{i}", [P, 1024]) for i in range(2)]
        probT = [sb(f"probT{i}", [P, 1024]) for i in range(2)]
        v_self = sb("v_self", [P, NSEQ, 8, 18])
        v_ctx = sb("v_ctx", [P, NSEQ, 8, 18])
        heads_out = [sb(f"heads_out{i}", [P, D]) for i in range(2)]
        attnT = [sb(f"attnT{i}", [P, D]) for i in range(2)]
        bn = sb("bn", [P, T, 6])
        mv = sb("mv", [P, T, 2])
        var_eps = sb("var_eps", [P, T])
        rstd = sb("rstd", [P, T])
        minus_half = sb("minus_half", [P, T])
        top = [sb(f"top{i}", [P, 16]) for i in range(2)]
        rden = [sb(f"rden{i}", [P, 16]) for i in range(2)]

        def halves(mem):
            return [mem[:, 0:512], mem[:, 512:1024]]


        def ln_stats(dve, n, t, src=x_res, before=0):
            nc.vector.bn_stats(bn[:, t, :], src[:, t, :]).then_inc(sem["stats"], 1)
            dve.wait_ge(sem["stats"], at(n, "stats", before + t + 1))
            nc.vector.bn_aggr(mv[:, t, :], bn[:, t, :]).then_inc(sem["moments"], 1)

        def ln_apply(dve, n, t, src=x_res, dst=xn):
            dve.wait_ge(sem["moments"], at(n, "moments", t + 1))
            dve.wait_ge(sem["rstd"], at(n, "rstd", t // 2 + 1))
            nc.vector.tensor_scalar(dst[:, t, :], src[:, t, :], mv[:, t, 0:1], rstd[:, t:t + 1],
                                    ALU.subtract, ALU.mult).then_inc(sem["xn"], 1)

        def ln_vector(dve, n, before, src=x_res, dst=xn):
            for t in range(T + 3):
                if t < T:
                    before(dve, t)
                    ln_stats(dve, n, t, src)
                if t >= 3:
                    ln_apply(dve, n, t - 3, src, dst)

        def ln_pool(pool, n, before=0):
            for t in range(0, T, 2):
                two, pair = slice(t, t + 2), (before + t) // 2
                pool.wait_ge(sem["moments"], at(n, "moments", before + t + 2))
                nc.gpsimd.tensor_scalar(var_eps[:, two], mv[:, two, 1], LN_EPS, None, ALU.add).then_inc(sem["var"], 1)
                pool.wait_ge(sem["var"], at(n, "var", pair + 1))
                nc.gpsimd.tensor_tensor(rstd[:, two], var_eps[:, two], minus_half[:, 0:2], ALU.pow).then_inc(sem["rstd"], 1)

        def tiles_T_tensor(pe, name, src, ready, before=0, halves=(0, 1)):
            for half in halves:
                mem = memory(name) if half else fill(pe, name, fulls=2, reads=2)
                for t in range(4 * half, 4 * half + 4):
                    pe.wait_ge(sem[ready], before + t + 1)
                    mm = nc.tensor.transpose(mem[:, t * P:(t + 1) * P], src[:, t, :], W("ident"))
                mm.then_inc(full(name), 1)

        def copy_half_scalar(act, name, dst):
            mem = wait_full(act, name, 0)
            nc.scalar.copy(dst[:, 0:512], mem[:, 0:512]).then_inc(read(name), 1)

        def copy_half_vector(dve, name, dst):
            mem = wait_full(dve, name, 1)
            wait_read(dve, name, 0)
            nc.vector.tensor_copy(dst[:, 512:1024], mem[:, 512:1024]).then_inc(read(name), 1)


        def project_tensor(pe, name, terms, rows=P, reads=2, after=(), halves=(0, 1)):
            for half in halves:
                mem = memory(name) if half else fill(pe, name, fulls=2, reads=reads)
                for product in after:
                    wait_read(pe, product, half)
                for i, (w, src) in enumerate(terms):
                    mm = nc.tensor.matmul(mem[0:rows, 512 * half:512 * half + 512], w, src[:, 512 * half:512 * half + 512],
                                          start=i == 0, stop=i == len(terms) - 1)
                mm.then_inc(full(name), 1)

        def values_tensor(pe, name, w, srcT):
            mem = fill(pe, name, fulls=1, reads=2)
            wp = w.rearrange("p (a h f) -> p h a f", h=2, f=8)
            for b in range(NSEQ):
                for h in range(2):
                    mm = nc.tensor.matmul(mem[64 * h:64 * h + 64, 64 * b:64 * b + 64], srcT[:, 64 * b:64 * b + 64],
                                          wp[:, h], start=True, stop=True)
            mm.then_inc(full(name), 1)

        def values_copy(eng, name, dst, h, relu=False):
            mem = wait_full(eng, name)
            src = mem[64 * h:64 * h + 64, :].rearrange("p (b a f) -> p b a f", b=NSEQ, f=8)
            to = dst[64 * h:64 * h + 64, :, :, 8 * h:8 * h + 8]
            if h == 0:
                nc.scalar.activation(to, src, ACT.Relu if relu else ACT.Copy).then_inc(read(name), 1)
            elif relu:
                nc.vector.tensor_scalar(to, src, 0.0, None, ALU.max).then_inc(read(name), 1)
            else:
                nc.vector.tensor_copy(to, src).then_inc(read(name), 1)


        POOL_HEADS = 10

        def spread(eng, ops, a, t, lo, hi, who):
            n, H = a["n"], a["heads"]
            if a["kind"] == "topk":
                lo, hi = (0, 16) if who == "pool" else (0, 0)
                if who == "dve":
                    return
            lo, hi = lo * H // 16, hi * H // 16
            if t % 4 == 0:
                a["k_ready"](eng, t // 4)
            if t >= 2:
                wait_full(eng, f"{n}.s{t - 2}")
            elif "before_keys" in a:
                a["before_keys"](eng, t)
            kt = a["k"][:, t * P:(t + 1) * P].rearrange("p (o k) -> p o k", o=1).broadcast_to([P, hi - lo, P])
            mask = W("head_mask" if H == 16 else "head_mask8")[:, lo:hi].rearrange("p (h o) -> p h o", o=1)
            ops.tensor_tensor(keys[t % 2][:, lo:hi, :], kt, mask.broadcast_to([P, hi - lo, P]), ALU.mult)\
               .then_inc(sem["keys_" + who], 1)

        def scores_tensor(pe, a, t, g):
            n = a["n"]
            if t % 4 == 0 and g == 0:
                a["q_ready"](pe, t // 4)
            if g == 0:
                pe.wait_ge(sem["keys_pool"], at(n, "keys_pool", t + 1))
                fill(pe, f"{n}.s{t}", fulls=2, reads=a["parts"])
            if g == 1 and a["kind"] != "topk":
                pe.wait_ge(sem["keys_dve"], at(n, "keys_dve", t + 1))
            mem = memory(f"{n}.s{t}")
            for b in range(2):
                mm = nc.tensor.matmul(mem[64 * b:64 * b + 64, 512 * g:512 * g + 512],
                                      a["q"][:, t * P + 64 * b:t * P + 64 * b + 64],
                                      keys[t % 2][:, 8 * g:8 * g + 8, 64 * b:64 * b + 64], start=True, stop=True)
            mm.then_inc(full(f"{n}.s{t}"), 1)

        def transposes_tensor(pe, a, t, g):
            n = a["n"]
            a["prob_ready"](pe, t, g)
            if g == 0:
                parts = a["heads"] // 8
                fill(pe, f"{n}.t{t}", a.get("t_ring", "A"), fulls=parts, reads=parts)
            mem = memory(f"{n}.t{t}")
            for p in range(4 * g, 4 * g + 4):
                mm = nc.tensor.transpose(mem[:, p * P:(p + 1) * P], prob[t % 2][:, p * P:(p + 1) * P], W("ident"))
            mm.then_inc(full(f"{n}.t{t}"), 1)

        def outputs_tensor(pe, a, t):
            n, pairs = a["n"], a["heads"] // 2
            if t == 0:
                wait_read(pe, n + ".v") if "wv" in a else a["v_ready"](pe)
            wait_read(pe, f"{n}.t{t}")
            w = a["v"].shape[3]
            mem = fill(pe, f"{n}.o{t}", "B")
            for p in range(pairs):
                for b in range(2):
                    mm = nc.tensor.matmul(mem[64 * b:64 * b + 64, w * p:w * p + w],
                                          probT[t % 2][:, p * P + 64 * b:p * P + 64 * b + 64],
                                          a["v"][:, 2 * t + b, p, :], start=True, stop=True)
            mm.then_inc(full(f"{n}.o{t}"), 1)

        def heads_T_tensor(pe, a, t):
            n = a["n"]
            wait_read(pe, f"{n}.o{t}")
            mem = fill(pe, f"{n}.ot{t}", "B")
            nc.tensor.transpose(mem[:, 0:P], heads_out[t % 2][:, :], W("ident")).then_inc(full(f"{n}.ot{t}"), 1)

        def out_tensor(pe, a, t):
            n = a["n"]
            wait_read(pe, f"{n}.ot{t}")
            mem = fill(pe, f"{n}.y{t}", "B")
            nc.tensor.matmul(mem[:, 0:P], attnT[t % 2][:, :], W(a["wo"]), start=True, stop=True)\
              .then_inc(full(f"{n}.y{t}"), 1)

        leads = {}

        def lead(n, engine, step, eng):
            for piece in leads.get((n, engine, step), ()):
                piece(eng)

        def half_ready(name):
            return lambda eng, half: wait_read(eng, name, half)

        def attention_tensor(pe, a):
            for g in range(2):
                scores_tensor(pe, a, 0, g)
            if "wv" in a:
                values_tensor(pe, a["n"] + ".v", a["wv"], xnT)
            whole = a["parts"] == 1
            for t in range(T + 3):
                if t + 1 < T:
                    scores_tensor(pe, a, t + 1, 0)
                    if whole:
                        scores_tensor(pe, a, t + 1, 1)
                if a.get("wo") and t >= 3:
                    out_tensor(pe, a, t - 3)
                if 1 <= t <= T:
                    outputs_tensor(pe, a, t - 1)
                if t < T:
                    transposes_tensor(pe, a, t, 0)
                if t + 1 < T and not whole:
                    scores_tensor(pe, a, t + 1, 1)
                if t < T:
                    transposes_tensor(pe, a, t, 1)
                if a.get("wo") and 2 <= t <= T + 1:
                    heads_T_tensor(pe, a, t - 2)
                lead(a["next"], "tensor", t - T, pe)
                lead(a["n"], "tensor", ("step", t), pe)

        def softmax_vector(dve, a, t):
            n, kind = a["n"], a["kind"]
            s = f"{n}.s{t}"
            three = lambda x: x.rearrange("p (h k) -> p h k", k=SEQ)
            for g in range(2):
                cols, hs = slice(512 * g, 512 * g + 512), slice(8 * g, 8 * g + 8)
                mem = wait_full(dve, s, g)
                if t >= 2:
                    wait_full(dve, f"{n}.t{t - 2}", g)
                pr = prob[t % 2][:, cols]
                if kind == "decay":
                    d = W("decay").rearrange("p (o k) -> p o k", o=1).broadcast_to([P, 8, SEQ])
                    nc.vector.tensor_tensor(three(pr), three(mem[:, cols]), d, ALU.mult).then_inc(read(s), 1)
                    wait_read(dve, s, g)
                    src = pr
                elif kind == "bias":
                    nc.vector.scalar_tensor_tensor(out=pr, in0=mem[:, cols], scalar=a["scale"],
                                                   in1=rel_bias[:, cols], op0=ALU.mult, op1=ALU.add).then_inc(read(s), 1)
                    wait_read(dve, s, g)
                    src = pr
                else:
                    src = mem[:, cols]
                if t >= 2 and g == 0:
                    a["less_done"](dve, t - 2, 1)
                nc.vector.tensor_reduce(top[t % 2][:, hs], three(src), AX, ALU.max).then_inc(sem["top"], 1)
                dve.wait_ge(sem["top"], at(n, "top", 2 * t + g + 1))
                if kind == "plain":
                    tb = top[t % 2][:, hs].rearrange("p (h o) -> p h o", o=1).broadcast_to([P, 8, SEQ])
                    nc.vector.tensor_tensor(three(pr), three(src), tb, ALU.subtract).then_inc(read(s), 1)

        def less_pool(pool, a, t):
            n = a["n"]
            for g in range(2):
                cols, hs = slice(512 * g, 512 * g + 512), slice(8 * g, 8 * g + 8)
                pool.wait_ge(sem["top"], at(n, "top", 2 * t + g + 1))
                pr = prob[t % 2][:, cols].rearrange("p (h k) -> p h k", k=SEQ)
                tb = top[t % 2][:, hs].rearrange("p (h o) -> p h o", o=1).broadcast_to([P, 8, SEQ])
                nc.gpsimd.tensor_tensor(pr, pr, tb, ALU.subtract).then_inc(sem["less"], 1)

        def normalise_vector(dve, a, t):
            n, pairs = a["n"], a["heads"] // 2
            o = f"{n}.o{t}"
            mem = wait_full(dve, o)
            v = mem[:, 0:18 * pairs].rearrange("p (a w) -> p a w", w=18)
            rd = rden[t % 2][:, :].rearrange("p (a h) -> p a h", h=2)
            if t >= 2:
                wait_read(dve, f"{n}.o{t - 2}")
                if a.get("wo"):
                    wait_full(dve, f"{n}.ot{t - 2}")
            nc.vector.reciprocal(rd, v[:, :, 16:18]).then_inc(sem["rden"], 1)
            dve.wait_ge(sem["rden"], at(n, "rden", t + 1))
            ho = heads_out[t % 2][:, :].rearrange("p (a h f) -> p a h f", h=2, f=8)
            num = v[:, :, 0:16].rearrange("p a (h f) -> p a h f", h=2)
            rb = rd.rearrange("p a (h o) -> p a h o", o=1).broadcast_to([P, pairs, 2, 8])
            nc.vector.tensor_tensor(ho, num, rb, ALU.mult).then_inc(read(o), 1)
            if not a.get("wo"):
                wait_read(dve, o)
                nc.vector.tensor_tensor(x_res[:, t, :], x_res[:, t, :], heads_out[t % 2][:, :], ALU.add)\
                  .then_inc(sem[n + ".x"], 1)
                dve.wait_ge(sem[n + ".x"], t + 1)

        def residual_vector(dve, a, t):
            y = f"{a['n']}.y{t}"
            mem = wait_full(dve, y)
            if a.get("bo") and t == 0:
                dve.wait_ge(sem["b_out"], at(a["n"], "b_out", 1))
            nc.vector.tensor_tensor(x_res[:, t, :], mem[:, 0:P], x_res[:, t, :], ALU.add).then_inc(read(y), 1)

        def attention_vector(dve, a):
            nxt = a["next"]
            lag = 3 if a.get("wo") else 1
            spread(dve, nc.vector, a, 0, POOL_HEADS, 16, "dve")
            spread(dve, nc.vector, a, 1, POOL_HEADS, 16, "dve")
            for t in range(T + 3):
                if t < T:
                    a.get("softmax", softmax_vector)(dve, a, t)
                if t == 0 and "wv" in a:
                    values_copy(dve, a["n"] + ".v", a["v"], 1)
                if 1 <= t <= T:
                    a.get("normalise", normalise_vector)(dve, a, t - 1)
                if a.get("wo") and t >= 3:
                    residual_vector(dve, a, t - 3)
                if lag <= t < T + lag:
                    residual_ready(a)(dve, t - lag)
                    ln_stats(dve, nxt, t - lag)
                first = T - 2 if a["kind"] in ("plain", "unit") else T
                if t >= first:
                    for u in range(0 if t == first else t - lag - 1, min(t - lag, T)):
                        ln_apply(dve, nxt, u)
                if t + 2 < T:
                    spread(dve, nc.vector, a, t + 2, POOL_HEADS, 16, "dve")
                lead(nxt, "vector", t - T, dve)
                lead(a["n"], "vector", ("step", t), dve)
            for u in range(T + 2 - lag, T):
                ln_apply(dve, nxt, u)

        def exp_scalar(act, a, t, g):
            n = a["n"]
            w = 1024 // a["parts"]
            cols = slice(w * g, w * g + w)
            a["less_done"](act, t, g)
            if a["kind"] == "unit":
                if t >= 2:
                    wait_full(act, f"{n}.t{t - 2}", g)
                mem = wait_full(act, f"{n}.s{t}", g)
                nc.scalar.activation(prob[t % 2][:, cols], mem[:, cols], ACT.Exp, scale=a["scale"]).then_inc(read(f"{n}.s{t}"), 1)
            else:
                nc.scalar.activation(prob[t % 2][:, cols], prob[t % 2][:, cols], ACT.Exp,
                                     scale=1.0 if a["kind"] in ("decay", "bias") else a["scale"]).then_inc(sem["exp"], 1)

        def attention_scalar(act, a):
            n = a["n"]
            for t in range(T + 3):
                if a.get("copy") and t == 0:
                    a["copy"](act, a, 0)
                if a.get("copy") and t + 1 < T:
                    a["copy"](act, a, t + 1)
                if t < T:
                    for g in range(a["parts"]):
                        exp_scalar(act, a, t, g)
                    if t == 0 and "wv" in a:
                        values_copy(act, a["n"] + ".v", a["v"], 0)
                    if t >= 2:
                        wait_full(act, f"{n}.o{t - 2}")
                    for g in range(2):
                        mem = wait_full(act, f"{n}.t{t}", g)
                        nc.scalar.copy(probT[t % 2][:, 512 * g:512 * g + 512], mem[:, 512 * g:512 * g + 512])\
                          .then_inc(read(f"{n}.t{t}"), 1)
                if a.get("wo") and 2 <= t <= T + 1:
                    u = t - 2
                    if u >= 2:
                        wait_full(act, f"{n}.y{u - 2}")
                    mem = wait_full(act, f"{n}.ot{u}")
                    if a.get("bv"):
                        nc.scalar.activation(attnT[u % 2][:, :], mem[:, 0:P], ACT.Identity, bias=W(a["bv"]))\
                          .then_inc(read(f"{n}.ot{u}"), 1)
                    else:
                        nc.scalar.copy(attnT[u % 2][:, :], mem[:, 0:P]).then_inc(read(f"{n}.ot{u}"), 1)
                lead(a["next"], "scalar", t - T, act)
                lead(a["n"], "scalar", ("step", t), act)

        def attention_pool(pool, a):
            for t in range(-2, T):
                if t >= 0 and a["kind"] in ("decay", "bias"):
                    less_pool(pool, a, t)
                if t + 2 < T:
                    spread(pool, nc.gpsimd, a, t + 2, 0, POOL_HEADS, "pool")
                if t == -1 and a.get("bo"):
                    add_bias_pool(pool, a["n"], a["bo"])

        def residual_ready(a):
            if a.get("wo"):
                return lambda eng, t: wait_read(eng, f"{a['n']}.y{t}")
            return lambda eng, t: eng.wait_ge(sem[a["n"] + ".x"], t + 1)

        def attention(n, kind, scale=1.0, heads=16, **more):
            a = dict(n=n, kind=kind, scale=scale, heads=heads, parts=2, next=STAGES[STAGES.index(n) + 1], **more)
            if kind == "plain":
                a["less_done"] = lambda eng, t, g: wait_read(eng, f"{n}.s{t}", g)
            elif kind == "unit":
                a["less_done"] = lambda eng, t, g: None
            elif kind == "topk":
                a["parts"] = 1
                a["less_done"] = lambda eng, t, g: eng.wait_ge(sem["less"], at(n, "less", t + 1))
            else:
                a["less_done"] = lambda eng, t, g: eng.wait_ge(sem["less"], at(n, "less", 2 * t + g + 1))
            if kind == "unit":
                a["prob_ready"] = lambda eng, t, g: wait_read(eng, f"{n}.s{t}", g)
            else:
                a["prob_ready"] = lambda eng, t, g: eng.wait_ge(sem["exp"], at(n, "exp", 2 * t + g + 1))
            return a


        VALUES_SET = 12
        L0A = attention("l0a", "decay", wo="L0_attn_W_o", q=qT, k=kT, v=v_self,
                        before_keys=lambda eng, t: eng.wait_ge(sem["lstm_values"], 2),
                        q_ready=half_ready("l0a.q"), k_ready=half_ready("l0a.k"),
                        v_ready=lambda eng: wait_read(eng, "l0a.v"))
        scr = sb("scratch", [P, 12, 1024])
        kvT, lat_all = scr[:, 0, :], scr[:, 8, :]
        latT = lat_all[0:32]

        def l0a_tensor(pe):
            n = "l0a"
            tiles_T_tensor(pe, n + ".T", xn, "xn", at(n, "xn", 0))
            project_tensor(pe, n + ".kv", [(W("L0_attn_W_k"), xnT), (W("L0_attn_W_v"), xnT)], after=[n + ".T"])
            project_tensor(pe, n + ".q", [(W("L0_attn_W_q"), xnT)])
            project_tensor(pe, n + ".lat", [(W("L0_attn_W_down_kv"), kvT)], rows=32, after=[n + ".kv"])
            pe.wait_ge(sem["latent_padded"], 1)
            project_tensor(pe, n + ".k", [(W_padded("L0_attn_W_up_k"), lat_all)], after=[n + ".lat"])
            values_tensor(pe, n + ".v", W_padded("L0_attn_W_up_v"), lat_all)
            attention_tensor(pe, L0A)

        def l0a_vector(dve):
            n = "l0a"
            dve.wait_ge(sem["x_loaded"], 16)
            ln_vector(dve, n, lambda eng, t: None)
            copy_half_vector(dve, n + ".T", xnT)
            copy_half_vector(dve, n + ".kv", kvT)
            copy_half_vector(dve, n + ".q", qT)
            mem = wait_full(dve, n + ".lat", 1)
            dve.wait_ge(sem["latent_padded"], 1)
            wait_read(dve, n + ".lat", 0)
            nc.vector.tensor_copy(latT[:, 512:], mem[0:32, 512:]).then_inc(read(n + ".lat"), 1)
            copy_half_vector(dve, n + ".k", kT)
            dve.wait_ge(sem["values_set"], VALUES_SET)
            values_copy(dve, n + ".v", v_self, 1)
            attention_vector(dve, L0A)

        def l0a_scalar(act):
            n = "l0a"
            copy_half_scalar(act, n + ".T", xnT)
            copy_half_scalar(act, n + ".kv", kvT)
            copy_half_scalar(act, n + ".q", qT)
            mem = wait_full(act, n + ".lat", 0)
            act.wait_ge(sem["latent_padded"], 1)
            nc.scalar.copy(latT[:, 0:512], mem[0:32, 0:512]).then_inc(read(n + ".lat"), 1)
            copy_half_scalar(act, n + ".k", kT)
            act.wait_ge(sem["values_set"], VALUES_SET)
            values_copy(act, n + ".v", v_self, 0)
            attention_scalar(act, L0A)

        def l0a_pool(pool):
            nc.gpsimd.memset(lat_all, 0.0).then_inc(sem["latent_padded"], 1)
            nc.gpsimd.memset(scr[:, 6:8, :], 0.0).then_inc(sem["gates_padded"], 1)
            ln_pool(pool, "l0a")
            attention_pool(pool, L0A)



        links = {}

        def link(eng, name, ins):
            links[name] = links.get(name, 0) + 1
            ins.then_inc(sem[name], 1)
            eng.wait_ge(sem[name], links[name])

        newton_t = sb("newton_t", [P, 256])
        newton_u = sb("newton_u", [P, 256])

        def rsqrt_vector(dve, n, x, y, w):
            t, u = newton_t[:, 0:w], newton_u[:, 0:w]
            U32, I32 = mybir.dt.uint32, mybir.dt.int32
            link(dve, n, nc.vector.tensor_scalar(t.bitcast(U32), x.bitcast(U32), 1, None, ALU.logical_shift_right))
            link(dve, n, nc.vector.tensor_scalar(y.bitcast(I32), t.bitcast(I32), -1.0, float(0x5F3759DF), ALU.mult, ALU.add))
            for _ in range(3):
                link(dve, n, nc.vector.tensor_tensor(t, y, y, ALU.mult))
                link(dve, n, nc.vector.scalar_tensor_tensor(out=u, in0=t, scalar=-0.5, in1=x, op0=ALU.mult, op1=ALU.mult))
                link(dve, n, nc.vector.scalar_tensor_tensor(out=y, in0=u, scalar=1.5, in1=y, op0=ALU.add, op1=ALU.mult))


        ctx_tok = scr[:, 11, :].rearrange("p (t d) -> p t d", t=T)
        ctx_keys = keys[0]
        v_lstm = sb("v_lstm", [P, NSEQ, 4, 34])

        def context_tensor(pe):
            pe.wait_ge(sem["ctx_loaded"], 16)
            mem = fill(pe, "ctx.T", fulls=2, reads=2)
            for t in range(T):
                mm = nc.tensor.transpose(mem[:, t * P:(t + 1) * P], ctx_tok[:, t, :], W("ident"))
                if t % 4 == 3:
                    mm.then_inc(full("ctx.T"), 1)

        def context_vector(dve):
            copy_half_vector(dve, "ctx.T", ctxT)

        def context_scalar(act):
            copy_half_scalar(act, "ctx.T", ctxT)
            act.wait_ge(sem["ctx_keys_loaded"], 32)
            act.wait_ge(sem["lstm_values_set"], 6)
            for h in range(2):
                rows = slice(64 * h, 64 * h + 64)
                src = ctx_keys[rows, :, :].rearrange("p b (a h f) -> p b a h f", h=2, f=16)[:, :, :, h]
                nc.scalar.copy(v_lstm[rows, :, :, 16 * h:16 * h + 16], src).then_inc(sem["lstm_values"], 1)

        def context_pool(pool):
            pass


        gate = scr[0:40, 5, :]
        lstm = scr[0:40, 1:5, :]
        spread_all = [scr[:, 6 + i, :].rearrange("p (h k) -> p h k", h=8) for i in range(2)]
        spread_b = [s[0:8] for s in spread_all]
        tok_gate = sb("tok_gate", [P, T, 40])
        least = sb("least", [P, T, 8])
        lstm_out = xn
        ms = sb("ms", [P, 64])
        rms = sb("rms", [P, 64])
        L0X = attention("l0x", "mlstm", heads=8, t_ring="B", q=xnT, k=ctxT, v=v_lstm,
                        q_ready=half_ready("l0x.T"), k_ready=half_ready("ctx.T"),
                        v_ready=lambda eng: eng.wait_ge(sem["lstm_values"], 2),
                        before_keys=lambda eng, t: wait_full(eng, f"l0a.s{6 + t}"))

        L0X["prob_ready"] = lambda eng, t, g: wait_read(eng, f"l0x.s{t}")

        def first_half_T(n):
            leads[n, "tensor", 0] = [lambda pe: tiles_T_tensor(pe, n + ".T", xn, "xn", at(n, "xn", 0), halves=(0,))]
            leads[n, "scalar", 0] = [lambda act: copy_half_scalar(act, n + ".T", xnT)]

        def second_half_T(pe, n):
            tiles_T_tensor(pe, n + ".T", xn, "xn", at(n, "xn", 0), halves=(1,))

        first_half_T("l0x")

        def l0x_tensor(pe):
            n = "l0x"
            mem = fill(pe, n + ".gate", fulls=2, reads=1)
            parts = ((W("l0x.gate_k"), ctxT), (W("l0x.gate_v"), ctxT), (W("l0x.gate_q"), xnT))
            for i, (w, src) in enumerate(parts):
                if i == 2:
                    second_half_T(pe, n)
                for half in range(2):
                    if i == 2:
                        wait_read(pe, n + ".T", half)
                    s = slice(512 * half, 512 * half + 512)
                    mm = nc.tensor.matmul(mem[0:40, s], w, src[:, s], start=i == 0, stop=i == 2)
                    if i == 2:
                        mm.then_inc(full(n + ".gate"), 1)
            mem = fill(pe, n + ".gateT")
            pe.wait_ge(sem[n + ".gates"], 1)
            for t in range(T):
                mm = nc.tensor.transpose(mem[:, 40 * t:40 * t + 40], lstm[:, 3, t * P:(t + 1) * P], W("ident")[0:40, 0:40])
            mm.then_inc(full(n + ".gateT"), 1)

            def scores(t):
                pe.wait_ge(sem["keys_pool"], at(n, "keys_pool", t + 1))
                pe.wait_ge(sem["keys_dve"], at(n, "keys_dve", t + 1))
                pe.wait_ge(sem[n + ".spread_b"], t + 1)
                pe.wait_ge(sem["gates_padded"], 1)
                mem = fill(pe, f"{n}.s{t}")
                for b in range(2):
                    nc.tensor.matmul(mem[64 * b:64 * b + 64, 0:512], xnT[:, t * P + 64 * b:t * P + 64 * b + 64],
                                     keys[t % 2][:, 0:8, 64 * b:64 * b + 64], start=True, stop=True)
                for b in range(2):
                    mm = nc.tensor.matmul(mem[64 * b:64 * b + 64, 512:1024], W_padded("ones8"),
                                          spread_all[t % 2][:, :, 64 * b:64 * b + 64], start=True, stop=True)
                mm.then_inc(full(f"{n}.s{t}"), 1)

            scores(0)
            for t in range(T + 2):
                if t + 1 < T:
                    scores(t + 1)
                if t >= 2:
                    outputs_tensor(pe, L0X, t - 2)
                if 1 <= t <= T:
                    transposes_tensor(pe, L0X, t - 1, 0)

        def l0x_vector(dve):
            n = "l0x"
            lf, cs, gb, M = (lstm[0:8, i, :] for i in range(4))
            copy_half_vector(dve, n + ".T", xnT)
            dve.wait_ge(sem[n + ".softplus"], 3)
            link(dve, "vector_chain", nc.vector.scalar_tensor_tensor(out=lf, in0=gate[32:40, :], scalar=0.0, in1=lstm[32:40, 1, :],
                                                               op0=ALU.min, op1=ALU.subtract))
            link(dve, "vector_chain", nc.vector.tensor_tensor_scan(cs, W("keep"), lf, 0.0, ALU.mult, ALU.add))
            link(dve, "vector_chain", nc.vector.tensor_tensor(gb, gate[0:8, :], cs, ALU.subtract))
            dve.sem_inc(sem[n + ".gb"], 1)
            link(dve, "vector_chain", nc.vector.tensor_tensor_scan(M, W("restart"), gb, MASKED, ALU.add, ALU.max))
            dve.wait_ge(sem["lstm_values_set"], 7)
            nc.vector.tensor_tensor(lstm[32:40, 3, :], M, cs, ALU.add).then_inc(sem[n + ".gates"], 1)
            mem = wait_full(dve, n + ".gateT")
            nc.vector.tensor_copy(tok_gate[:, :, :], mem[:, 0:320].rearrange("p (t g) -> p t g", t=T)).then_inc(read(n + ".gateT"), 1)
            wait_read(dve, n + ".gateT")

            three = lambda x: x.rearrange("p (h k) -> p h k", k=SEQ)

            def weigh(t):
                mem = wait_full(dve, f"{n}.s{t}")
                if t >= 2:
                    wait_read(dve, f"{n}.s{t - 2}")
                    wait_full(dve, f"{n}.t{t - 2}")
                d = three(prob[t % 2][:, 512:1024])
                m = tok_gate[:, t, 0:8].rearrange("p (h o) -> p h o", o=1).broadcast_to([P, 8, SEQ])
                link(dve, "vector_chain", nc.vector.tensor_tensor(d, three(mem[:, 512:1024]), m, ALU.subtract))
                c = W("causal").rearrange("p (o k) -> p o k", o=1).broadcast_to([P, 8, SEQ])
                nc.vector.tensor_tensor(d, d, c, ALU.add).then_inc(sem["less"], 1)

            def combine(t):
                dve.wait_ge(sem[n + ".weight"], t + 1)
                mem = flat[book.record[f"{n}.s{t}"][0]]
                nc.vector.scalar_tensor_tensor(out=prob[t % 2][:, 0:512], in0=mem[:, 0:512], scalar=0.25,
                                               in1=prob[t % 2][:, 512:1024], op0=ALU.mult, op1=ALU.mult)\
                  .then_inc(read(f"{n}.s{t}"), 1)

            def normalise(t):
                mem = wait_full(dve, f"{n}.o{t}")
                v = mem[:, 0:136].rearrange("p (a w) -> p a w", w=34)
                rd = rden[t % 2][:, 0:8].rearrange("p (a h) -> p a h", h=2)
                lt = least[:, t, :].rearrange("p (a h) -> p a h", h=2)
                if t == 0:
                    dve.wait_ge(sem[n + ".least"], 1)
                link(dve, "vector_chain", nc.vector.tensor_scalar(rd, v[:, :, 32:34], -1.0, None, ALU.mult))
                link(dve, "vector_chain", nc.vector.tensor_tensor(rd, rd, v[:, :, 32:34], ALU.max))
                link(dve, "vector_chain", nc.vector.tensor_tensor(rd, rd, lt, ALU.max))
                link(dve, "vector_chain", nc.vector.tensor_scalar(rd, rd, 1e-6, None, ALU.add))
                link(dve, "vector_chain", nc.vector.reciprocal(rd, rd))
                ho = lstm_out[:, t, :].rearrange("p (a h f) -> p a h f", h=2, f=16)
                num = v[:, :, 0:32].rearrange("p a (h f) -> p a h f", h=2)
                rb = rd.rearrange("p a (h o) -> p a h o", o=1).broadcast_to([P, 4, 2, 16])
                nc.vector.tensor_tensor(ho, num, rb, ALU.mult).then_inc(read(f"{n}.o{t}"), 1)

            spread(dve, nc.vector, L0X, 0, POOL_HEADS, 16, "dve")
            spread(dve, nc.vector, L0X, 1, POOL_HEADS, 16, "dve")
            for t in range(T + 4):
                if 1 <= t <= T:
                    combine(t - 1)
                if 3 <= t <= T + 2:
                    normalise(t - 3)
                if t < T:
                    weigh(t)
                if t + 2 < T:
                    spread(dve, nc.vector, L0X, t + 2, POOL_HEADS, 16, "dve")
            dve.wait_ge(sem[n + ".square"], 1)
            sq = scr[:, 0, :].rearrange("p (g f) -> p g f", f=16)
            link(dve, "vector_chain", nc.vector.tensor_reduce(ms[:, :], sq, AX, ALU.add))
            link(dve, "vector_chain", nc.vector.tensor_scalar(ms[:, :], ms[:, :], 1.0 / 16, 1e-6, ALU.mult, ALU.add))
            rsqrt_vector(dve, "vector_chain", ms[:, :], rms[:, :], 64)
            lo = lstm_out[:, :, :].rearrange("p t (h f) -> p (t h) f", f=16)
            rb = rms[:, :].rearrange("p (g o) -> p g o", o=1).broadcast_to([P, 64, 16])
            link(dve, "vector_chain", nc.vector.tensor_tensor(lo, lo, rb, ALU.mult))
            for t in range(T):
                nc.vector.tensor_tensor(x_res[:, t, :], x_res[:, t, :], lstm_out[:, t, :], ALU.add).then_inc(sem[n + ".x"], 1)

        def l0x_scalar(act):
            n = "l0x"
            mem = wait_full(act, n + ".gate")
            nc.scalar.activation(gate[:, :], mem[0:40, :], ACT.Identity, bias=W("l0x.gate_bias")).then_inc(read(n + ".gate"), 1)
            wait_read(act, n + ".gate")
            for i, (to, src, f, more) in enumerate(((0, gate[32:40, :], ACT.Abs, {}),
                                                    (0, lstm[32:40, 0, :], ACT.Exp, dict(scale=-1.0)),
                                                    (1, lstm[32:40, 0, :], ACT.Ln, dict(bias=1.0)))):
                nc.scalar.activation(lstm[32:40, to, :], src, f, **more).then_inc(sem[n + ".softplus"], 1)
                act.wait_ge(sem[n + ".softplus"], i + 1)
            wait_read(act, n + ".gateT")
            nc.scalar.activation(least[:, :, :], tok_gate[:, :, 32:40], ACT.Exp, scale=-1.0).then_inc(sem[n + ".least"], 1)
            for t in range(T + 2):
                if t < T:
                    act.wait_ge(sem["less"], at(n, "less", t + 1))
                    nc.scalar.activation(prob[t % 2][:, 512:1024], prob[t % 2][:, 512:1024], ACT.Exp)\
                       .then_inc(sem[n + ".weight"], 1)
                if t >= 2:
                    u = t - 2
                    if u >= 2:
                        wait_full(act, f"{n}.o{u - 2}")
                    mem = wait_full(act, f"{n}.t{u}")
                    nc.scalar.copy(probT[u % 2][:, 0:512], mem[:, 0:512]).then_inc(read(f"{n}.t{u}"), 1)
            wait_read(act, f"{n}.o{T - 1}")
            wait_read(act, f"{n}.o{T - 2}")
            nc.scalar.activation(scr[:, 0, :], lstm_out[:, :, :].rearrange("p t d -> p (t d)"), ACT.Square)\
              .then_inc(sem[n + ".square"], 1)

        def l0x_pool(pool):
            n = "l0x"
            ln_pool(pool, n)
            for t in range(T):
                spread(pool, nc.gpsimd, L0X, t, 0, POOL_HEADS, "pool")
                if t == 0:
                    pool.wait_ge(sem[n + ".gb"], 1)
                    pool.wait_ge(sem["gates_padded"], 1)
                if t >= 2:
                    wait_full(pool, f"{n}.s{t - 2}")
                b = lstm[0:8, 2, t * P:(t + 1) * P].rearrange("p (o k) -> p o k", o=1).broadcast_to([8, 8, P])
                e = W("ident")[0:8, 0:8].rearrange("p (h o) -> p h o", o=1).broadcast_to([8, 8, P])
                nc.gpsimd.tensor_tensor(spread_b[t % 2][:, :, :], b, e, ALU.mult).then_inc(sem[n + ".spread_b"], 1)



        NE, M = 8, 64
        contT, r1T = scr[0:M, 0, :], scr[0:M, 1, :]
        spike = [scr[:, 2, :], scr[:, 3, :]]
        hidden = [scr[:, 4, :], scr[:, 5, :]]
        gate_rep = [scr[:, 6, :], scr[:, 7, :]]
        gated, moe = scr[:, 8, :], scr[:, 9, :]
        gT = scr[0:NE, 10, :]
        cont_all, r1_all, g_all = scr[:, 0, :], scr[:, 1, :], scr[:, 10, :]
        logit = sb("logit", [P, T, NE])
        pick = sb("pick", [P, T, NE])
        best = sb("best", [P, T, 1])
        tie = prob[0][:, :].rearrange("p (w t e f) -> p w t e f", w=2, t=T, e=NE)

        def tok_bias(name, tiles=T):
            return W(name).rearrange("p (o d) -> p o d", o=1).broadcast_to([P, tiles, W(name).shape[1]])

        def l0f_tensor(pe):
            n = "l0f"
            tiles_T_tensor(pe, n + ".T", xn, "xn", at(n, "xn", 0))
            wait_read(pe, n + ".T")
            for c in range(2):
                project_tensor(pe, f"{n}.enc{c}", [(W("L0_ffn_enc_W")[:, 128 * c:128 * c + 128], xnT)])
            wait_read(pe, n + ".enc0")
            wait_read(pe, n + ".enc1")
            project_tensor(pe, n + ".cont", [(W(f"l0f.s2c{c}"), spike[c]) for c in range(2)], rows=M)
            wait_read(pe, n + ".cont")
            pe.wait_ge(sem[n + ".padded"], 3)
            project_tensor(pe, n + ".r1", [(W_padded("L0_ffn_rW1"), cont_all)], rows=M)
            for e in range(2):
                project_tensor(pe, f"{n}.h{e}", [(W_padded(f"l0f.We1_{e}"), cont_all)])
            wait_read(pe, n + ".r1")
            mem = fill(pe, n + ".logit")
            for t in range(T):
                mm = nc.tensor.matmul(mem[:, NE * t:NE * t + NE], r1_all[:, t * P:(t + 1) * P], W_padded("L0_ffn_rW2"),
                                      start=True, stop=True)
            mm.then_inc(full(n + ".logit"), 1)

            def outputs(p):
                mem = fill(pe, f"{n}.eo{p}")
                for half in range(2):
                    for e in range(2):
                        mm = nc.tensor.matmul(mem[64 * e:64 * e + 64, 512 * half:512 * half + 512], W(f"l0f.We2_{2 * p + e}"),
                                              hidden[e][:, 512 * half:512 * half + 512], start=True, stop=True)
                mm.then_inc(full(f"{n}.eo{p}"), 1)

            for p in range(NE // 2):
                if p:
                    for e in (2 * p, 2 * p + 1):
                        project_tensor(pe, f"{n}.h{e}", [(W_padded(f"l0f.We1_{e}"), cont_all)])
                if p == 0:
                    wait_read(pe, n + ".h0")
                    wait_read(pe, n + ".h1")
                    pe.wait_ge(sem[n + ".gates"], 1)
                    mem = fill(pe, n + ".gT")
                    for t in range(T):
                        mm = nc.tensor.transpose(mem[0:NE, t * P:(t + 1) * P], pick[:, t, :], W("ident"))
                    mm.then_inc(full(n + ".gT"), 1)
                    outputs(p)
                    wait_read(pe, n + ".gT")
                project_tensor(pe, f"{n}.rep{p}", [(W_padded(f"l0f.pair{p}"), g_all)])
                if p:
                    wait_read(pe, f"{n}.h{2 * p}")
                    wait_read(pe, f"{n}.h{2 * p + 1}")
                    outputs(p)
            pe.wait_ge(sem[n + ".moe"], 4)
            for c in range(2):
                project_tensor(pe, f"{n}.c2s{c}", [(W("l0f.c2s2")[:, 128 * c:128 * c + 128], moe)])
            wait_read(pe, n + ".c2s0")
            wait_read(pe, n + ".c2s1")
            mem = fill(pe, n + ".dec", fulls=2, reads=2)
            for t in range(T):
                for c in range(2):
                    mm = nc.tensor.matmul(mem[:, t * P:(t + 1) * P], spike[c][:, t * P:(t + 1) * P], W(f"l0f.dec{c}"),
                                          start=c == 0, stop=c == 1)
                if t % 4 == 3:
                    mm.then_inc(full(n + ".dec"), 1)

        def l0f_scalar(act):
            n = "l0f"
            copy_half_scalar(act, n + ".T", xnT)
            act.wait_ge(sem[n + ".padded"], 3)
            for c in range(2):
                for half in range(2):
                    mem = wait_full(act, f"{n}.enc{c}", half)
                    s = slice(512 * half, 512 * half + 512)
                    nc.scalar.activation(spike[c][:, s], mem[:, s], ACT.Sigmoid, bias=W("l0f.enc_b")[:, c:c + 1])\
                      .then_inc(read(f"{n}.enc{c}"), 1)
            mem = wait_full(act, n + ".cont", 0)
            nc.scalar.activation(contT[:, 0:512], mem[0:M, 0:512], ACT.Identity, bias=W("l0f.s2c_b")).then_inc(read(n + ".cont"), 1)
            for half in range(2):
                mem = wait_full(act, n + ".r1", half)
                s = slice(512 * half, 512 * half + 512)
                nc.scalar.activation(r1T[:, s], mem[0:M, s], ACT.Tanh, bias=W("l0f.rb1")).then_inc(read(n + ".r1"), 1)

            def hidden_relu(e):
                mem = wait_full(act, f"{n}.h{e}", 0)
                if e >= 2:
                    wait_full(act, f"{n}.eo{e // 2 - 1}")
                nc.scalar.activation(hidden[e % 2][:, 0:512], mem[:, 0:512], ACT.Relu, bias=W("l0f.be1")[:, e:e + 1])\
                  .then_inc(read(f"{n}.h{e}"), 1)

            hidden_relu(0)
            hidden_relu(1)
            act.wait_ge(sem["less"], at(n, "less", 1))
            nc.scalar.activation(logit[:, :, :], logit[:, :, :], ACT.Exp).then_inc(sem["exp"], 1)
            for p in range(NE // 2):
                if p:
                    hidden_relu(2 * p)
                    hidden_relu(2 * p + 1)
                if p == 0:
                    mem = wait_full(act, n + ".gT")
                    nc.scalar.copy(gT, mem[0:NE, :]).then_inc(read(n + ".gT"), 1)
                if p >= 2:
                    wait_read(act, f"{n}.eo{p - 2}")
                for half in range(2):
                    mem = wait_full(act, f"{n}.rep{p}", half)
                    s = slice(512 * half, 512 * half + 512)
                    nc.scalar.copy(gate_rep[p % 2][:, s], mem[:, s]).then_inc(read(f"{n}.rep{p}"), 1)
            for c in range(2):
                for half in range(2):
                    mem = wait_full(act, f"{n}.c2s{c}", half)
                    s = slice(512 * half, 512 * half + 512)
                    nc.scalar.activation(spike[c][:, s], mem[:, s], ACT.Sigmoid, bias=W("l0f.c2s_b")[:, c:c + 1])\
                      .then_inc(read(f"{n}.c2s{c}"), 1)
            for half in range(2):
                wait_read(act, n + ".dec", half)
                s = slice(4 * half, 4 * half + 4)
                nc.scalar.activation(xn[:, s, :], xn[:, s, :], ACT.Sigmoid).then_inc(sem[n + ".decoded"], 1)

        def l0f_vector(dve):
            n = "l0f"
            ch = "vector_chain"
            ln_vector(dve, n, residual_ready(L0X))
            copy_half_vector(dve, n + ".T", xnT)
            dve.wait_ge(sem[n + ".padded"], 3)
            mem = wait_full(dve, n + ".cont", 1)
            nc.vector.tensor_scalar(contT[:, 512:], mem[0:M, 512:], W("l0f.s2c_b"), None, ALU.add).then_inc(read(n + ".cont"), 1)

            def hidden_relu(e):
                mem = wait_full(dve, f"{n}.h{e}", 1)
                if e >= 2:
                    wait_full(dve, f"{n}.eo{e // 2 - 1}")
                nc.vector.tensor_scalar(hidden[e % 2][:, 512:], mem[:, 512:], W("l0f.be1")[:, e:e + 1], 0.0, ALU.add, ALU.max)\
                  .then_inc(read(f"{n}.h{e}"), 1)

            hidden_relu(0)
            hidden_relu(1)
            mem = wait_full(dve, n + ".logit")
            nc.vector.tensor_tensor(logit[:, :, :], mem[:, 0:T * NE].rearrange("p (t e) -> p t e", e=NE), tok_bias("l0f.rb2"),
                                    ALU.add).then_inc(read(n + ".logit"), 1)
            wait_read(dve, n + ".logit")
            mine = logit[:, :, :].rearrange("p t (e o) -> p t e o", o=1).broadcast_to([P, T, NE, NE])
            other = logit[:, :, :].rearrange("p t (o e) -> p t o e", o=1).broadcast_to([P, T, NE, NE])
            link(dve, ch, nc.vector.tensor_tensor(tie[:, 0], other, mine, ALU.is_gt))
            link(dve, ch, nc.vector.tensor_tensor(tie[:, 1], other, mine, ALU.is_equal))
            first = W("before").rearrange("p (o e f) -> p o e f", o=1, e=NE).broadcast_to([P, T, NE, NE])
            link(dve, ch, nc.vector.tensor_tensor(tie[:, 1], tie[:, 1], first, ALU.mult))
            link(dve, ch, nc.vector.tensor_tensor(tie[:, 0], tie[:, 0], tie[:, 1], ALU.add))
            link(dve, ch, nc.vector.tensor_reduce(pick[:, :, :], tie[:, 0], AX, ALU.add))
            link(dve, ch, nc.vector.tensor_reduce(best[:, :, 0], logit[:, :, :], AX, ALU.max))
            nc.vector.tensor_tensor(logit[:, :, :], logit[:, :, :], best[:, :, :].broadcast_to([P, T, NE]), ALU.subtract)\
              .then_inc(sem["less"], 1)
            dve.wait_ge(sem["exp"], at(n, "exp", 1))
            link(dve, ch, nc.vector.scalar_tensor_tensor(out=pick[:, :, :], in0=pick[:, :, :], scalar=2.0, in1=logit[:, :, :],
                                                         op0=ALU.is_lt, op1=ALU.mult))
            link(dve, ch, nc.vector.tensor_reduce(best[:, :, 0], pick[:, :, :], AX, ALU.add))
            link(dve, ch, nc.vector.reciprocal(best[:, :, :], best[:, :, :]))
            nc.vector.tensor_tensor(pick[:, :, :], pick[:, :, :], best[:, :, :].broadcast_to([P, T, NE]), ALU.mult)\
              .then_inc(sem[n + ".gates"], 1)
            for p in range(NE // 2):
                if p:
                    hidden_relu(2 * p)
                    hidden_relu(2 * p + 1)
                mem = wait_full(dve, f"{n}.eo{p}")
                wait_read(dve, f"{n}.rep{p}")
                if p >= 2:
                    dve.wait_ge(sem[n + ".moe"], p)
                to = moe if p == 0 else gated
                if p:
                    dve.wait_ge(sem[n + ".moe"], p)
                nc.vector.scalar_tensor_tensor(out=to, in0=mem, scalar=W("l0f.be2")[:, p:p + 1], in1=gate_rep[p % 2],
                                               op0=ALU.add, op1=ALU.mult).then_inc(read(f"{n}.eo{p}"), 1)
                wait_read(dve, f"{n}.eo{p}")
                if p:
                    nc.vector.tensor_tensor(moe, moe, gated, ALU.add).then_inc(sem[n + ".moe"], 1)
                else:
                    dve.sem_inc(sem[n + ".moe"], 1)
            for half in range(2):
                mem = wait_full(dve, n + ".dec", half)
                nc.vector.tensor_tensor(xn[:, 4 * half:4 * half + 4, :],
                                        mem[:, 512 * half:512 * half + 512].rearrange("p (t d) -> p t d", d=D),
                                        tok_bias("l0f.dec_b", 4), ALU.add).then_inc(read(n + ".dec"), 1)
            gain = W("l0f.ln_g")
            for t in range(T + 2):
                if t < T:
                    dve.wait_ge(sem[n + ".decoded"], t // 4 + 1)
                    ln_stats(dve, n, t, xn, T)
                    dve.wait_ge(sem["moments"], at(n, "moments", T + t + 1))
                    nc.vector.scalar_tensor_tensor(out=xn[:, t, :], in0=xn[:, t, :], scalar=mv[:, t, 0:1], in1=gain,
                                                   op0=ALU.subtract, op1=ALU.mult).then_inc(sem[n + ".centred"], 1)
                if t >= 2:
                    u = t - 2
                    dve.wait_ge(sem[n + ".centred"], u + 1)
                    dve.wait_ge(sem["rstd"], at(n, "rstd", (T + u) // 2 + 1))
                    if u == 0:
                        dve.wait_ge(sem["b_out"], at(n, "b_out", 1))
                    nc.vector.scalar_tensor_tensor(out=x_res[:, u, :], in0=xn[:, u, :], scalar=rstd[:, u:u + 1],
                                                   in1=x_res[:, u, :], op0=ALU.mult, op1=ALU.add).then_inc(sem[n + ".x"], 1)

        def l0f_pool(pool):
            for t in range(T):
                pool.wait_ge(sem["l0x.x"], t + 1)
            for i, rows in enumerate((cont_all, r1_all, g_all)):
                nc.gpsimd.memset(rows, 0.0).then_inc(sem["l0f.padded"], 1)
            ln_pool(pool, "l0f")
            add_bias_pool(pool, "l0f", "l0f.ln_b")
            ln_pool(pool, "l0f", T)

        L0F_READY = lambda eng, t: eng.wait_ge(sem["l0f.x"], t + 1)


        mixes = ("w", "a", "k", "v", "r", "g")
        diff = scr[:, 0, :]
        mixed = [scr[:, 1, :], scr[:, 2, :]]
        lin = {m: scr[:, 3 + i, :] for i, m in enumerate(("w", "a", "k", "r", "g"))}
        upd, state = scr[:, 8, :], scr[:, 9, :]
        group = sb("group", [P, 2, 128])

        def l1a_tensor(pe):
            n = "l1a"
            tiles_T_tensor(pe, n + ".T", xn, "xn", at(n, "xn", 0))
            for i, m in enumerate(mixes):
                pe.wait_ge(sem[n + ".mix"], i + 1)
                project_tensor(pe, f"{n}.{m}", [(W("L1_attn_W_" + m), mixed[i % 2])])
            project_tensor(pe, "l1x.k", [(W("L1_xattn_Wk"), ctxT)])
            values_tensor(pe, "l1x.v", W("L1_xattn_Wv"), ctxT)
            pe.wait_ge(sem[n + ".mixed"], 1)
            mem = fill(pe, n + ".mT")
            for t in range(T):
                mm = nc.tensor.transpose(mem[:, t * P:(t + 1) * P], state[:, t * P:(t + 1) * P], W("ident"))
            mm.then_inc(full(n + ".mT"), 1)
            mem = fill(pe, n + ".nT", fulls=1, reads=1)
            pe.wait_ge(sem[n + ".normed"], 1)
            for t in range(T):
                mm = nc.tensor.transpose(mem[:, t * P:(t + 1) * P], xn[:, t, :], W("ident"))
            mm.then_inc(full(n + ".nT"), 1)
            mem = fill(pe, n + ".y", reads=T)
            pe.wait_ge(sem[n + ".gated"], 1)
            for t in range(T):
                mm = nc.tensor.matmul(mem[:, t * P:(t + 1) * P], upd[:, t * P:(t + 1) * P], W("L1_attn_W_out"), start=True, stop=True)
            mm.then_inc(full(n + ".y"), 1)

        def l1a_scalar(act):
            n = "l1a"
            copy_half_scalar(act, n + ".T", xnT)
            for i, m in enumerate(mixes):
                if m == "v":
                    continue
                for half in range(2):
                    mem = wait_full(act, f"{n}.{m}", half)
                    s = slice(512 * half, 512 * half + 512)
                    nc.scalar.activation(lin[m][:, s], mem[:, s], ACT.Tanh if m == "k" else ACT.Sigmoid,
                                         scale=-1.0 if m == "w" else 1.0).then_inc(read(f"{n}.{m}"), 1)
            relu_half(act, "l1x.k", kcT, 0)
            act.wait_ge(sem["values_set"], VALUES_SET)
            values_copy(act, "l1x.v", v_ctx, 0, relu=True)
            act.wait_ge(sem[n + ".centred"], 1)
            nc.scalar.activation(scr[:, 1, :], xn[:, :, :].rearrange("p t d -> p (t d)"), ACT.Square).then_inc(sem[n + ".square"], 1)

        def l1a_vector(dve):
            n = "l1a"
            ch = "vector_chain"
            ln_vector(dve, n, L0F_READY)
            copy_half_vector(dve, n + ".T", xnT)
            wait_read(dve, n + ".T")
            seq = lambda x: x.rearrange("p (b s) -> p b s", s=SEQ)
            nc.vector.tensor_tensor(seq(diff)[:, :, 1:], seq(xnT[:, :])[:, :, :SEQ - 1], seq(xnT[:, :])[:, :, 1:], ALU.subtract)\
              .then_inc(sem[n + ".diff"], 1)
            nc.vector.tensor_scalar(seq(diff)[:, :, 0:1], seq(xnT[:, :])[:, :, 0:1], -1.0, None, ALU.mult).then_inc(sem[n + ".diff"], 1)
            dve.wait_ge(sem[n + ".diff"], 2)

            def mix(i):
                if i >= 2:
                    wait_full(dve, f"{n}.{mixes[i - 2]}")
                nc.vector.scalar_tensor_tensor(out=mixed[i % 2], in0=diff, scalar=W("l1a.x_" + mixes[i]), in1=xnT[:, :],
                                               op0=ALU.mult, op1=ALU.add).then_inc(sem[n + ".mix"], 1)

            for i in range(6):
                mix(i)
                if i == 5:
                    wait_read(dve, n + ".w")
                    link(dve, ch, nc.vector.memset(seq(lin["w"])[:, :, 0:1], 0.0))
                    wait_read(dve, n + ".a")
                    wait_read(dve, n + ".k")
                    link(dve, ch, nc.vector.tensor_tensor(upd, lin["a"], lin["k"], ALU.mult))
                    mem = wait_full(dve, n + ".v")
                    nc.vector.tensor_tensor(upd, mem, upd, ALU.mult).then_inc(read(n + ".v"), 2)
            wait_read(dve, n + ".v")
            link(dve, ch, nc.vector.tensor_tensor_scan(state, lin["w"], upd, 0.0, ALU.mult, ALU.add))
            wait_read(dve, n + ".r")
            nc.vector.tensor_tensor(state, state, lin["r"], ALU.mult).then_inc(sem[n + ".mixed"], 1)
            relu_half(dve, "l1x.k", kcT, 1)
            dve.wait_ge(sem["values_set"], VALUES_SET)
            values_copy(dve, "l1x.v", v_ctx, 1, relu=True)
            mem = wait_full(dve, n + ".mT")
            groups = lambda x: x.rearrange("p (g f) -> p g f", f=8)
            flat_xn = xn[:, :, :].rearrange("p t d -> p (t d)")
            link(dve, ch, nc.vector.tensor_reduce(group[:, 0, :], groups(mem), AX, ALU.add))
            link(dve, ch, nc.vector.tensor_scalar(group[:, 0, :], group[:, 0, :], 1 / 8, None, ALU.mult))
            gb = lambda x: x.rearrange("p (g o) -> p g o", o=1).broadcast_to([P, 128, 8])
            nc.vector.tensor_tensor(groups(flat_xn), groups(mem), gb(group[:, 0, :]), ALU.subtract).then_inc(read(n + ".mT"), 1)
            wait_read(dve, n + ".mT")
            dve.sem_inc(sem[n + ".centred"], 1)
            dve.wait_ge(sem[n + ".square"], 1)
            link(dve, ch, nc.vector.tensor_reduce(group[:, 1, :], groups(scr[:, 1, :]), AX, ALU.add))
            link(dve, ch, nc.vector.tensor_scalar(group[:, 1, :], group[:, 1, :], 1 / 8, 0.00064, ALU.mult, ALU.add))
            rsqrt_vector(dve, ch, group[:, 1, :], group[:, 0, :], 128)
            nc.vector.tensor_tensor(groups(flat_xn), groups(flat_xn), gb(group[:, 0, :]), ALU.mult).then_inc(sem[n + ".normed"], 1)
            mem = wait_full(dve, n + ".nT")
            nc.vector.tensor_scalar(upd, mem, W("l1a.gn_w"), W("l1a.gn_b"), ALU.mult, ALU.add).then_inc(read(n + ".nT"), 1)
            wait_read(dve, n + ".nT")
            wait_read(dve, n + ".g")
            nc.vector.tensor_tensor(upd, upd, lin["g"], ALU.mult).then_inc(sem[n + ".gated"], 1)
            dve.wait_ge(sem["b_out"], at(n, "b_out", 1))
            mem = wait_full(dve, n + ".y")
            for t in range(T):
                nc.vector.tensor_tensor(x_res[:, t, :], mem[:, t * P:(t + 1) * P], x_res[:, t, :], ALU.add).then_inc(read(n + ".y"), 1)

        def add_bias_pool(pool, n, name):
            pool.wait_ge(sem["xn"], at(n, "xn", T))
            nc.gpsimd.tensor_tensor(x_res[:, :, :], x_res[:, :, :], tok_bias(name), ALU.add).then_inc(sem["b_out"], 1)

        def l1a_pool(pool):
            ln_pool(pool, "l1a")
            add_bias_pool(pool, "l1a", "l1a.b_out")

        def product_ready(name):
            return lambda eng, t: eng.wait_ge(sem["read." + book.record[name][0]], book.record[name][3] - T + t + 1)


        L1X = attention("l1x", "plain", scale=8 ** -0.5, q=qT, k=kcT, v=v_ctx,
                        q_ready=half_ready("l1x.q"), k_ready=half_ready("l1x.k"),
                        v_ready=lambda eng: wait_read(eng, "l1x.v"), before_keys=lambda eng, t: wait_full(eng, f"l0x.s{6 + t}"))

        def l1x_tensor(pe):
            n = "l1x"
            tiles_T_tensor(pe, n + ".T", xn, "xn", at(n, "xn", 0))
            project_tensor(pe, n + ".q", [(W("L1_xattn_Wq"), xnT)], after=[n + ".T"])
            attention_tensor(pe, L1X)

        def relu_half(eng, name, dst, half):
            mem = wait_full(eng, name, half)
            s = slice(512 * half, 512 * half + 512)
            if half == 0:
                nc.scalar.activation(dst[:, s], mem[:, s], ACT.Relu).then_inc(read(name), 1)
            else:
                wait_read(eng, name, 0)
                nc.vector.tensor_scalar(dst[:, s], mem[:, s], 0.0, None, ALU.max).then_inc(read(name), 1)

        def l1x_vector(dve):
            n = "l1x"
            ln_vector(dve, n, product_ready("l1a.y"))
            copy_half_vector(dve, n + ".T", xnT)
            relu_half(dve, n + ".q", qT, 1)
            attention_vector(dve, L1X)

        def l1x_scalar(act):
            n = "l1x"
            copy_half_scalar(act, n + ".T", xnT)
            relu_half(act, n + ".q", qT, 0)
            attention_scalar(act, L1X)

        def l1x_pool(pool):
            ln_pool(pool, "l1x")
            attention_pool(pool, L1X)


        wide = [scr[:, i, :] for i in range(4)]
        mem_v, cur, spikes = scr[:, 4, :], scr[:, 5, :], scr[:, 6, :]
        lif_a = scr[:, 7, :]

        first_half_T("l1f")

        def l1f_tensor(pe):
            n = "l1f"
            second_half_T(pe, n)
            wait_read(pe, n + ".T")
            for c in range(4):
                project_tensor(pe, f"{n}.h{c}", [(W("L1_ffn_W_fc")[:, 128 * c:128 * c + 128], xnT)])
            mem = fill(pe, n + ".y", fulls=2, reads=2)
            for t in range(T):
                for c in range(4):
                    if t % 4 == 0:
                        pe.wait_ge(sem[n + ".square"], 4 * (t // 4) + c + 1)
                    mm = nc.tensor.matmul(mem[:, t * P:(t + 1) * P], wide[c][:, t * P:(t + 1) * P], W(f"l1f.proj{c}"),
                                          start=c == 0, stop=c == 3)
                if t % 4 == 3:
                    mm.then_inc(full(n + ".y"), 1)

        def l1f_scalar(act):
            n = "l1f"
            for c in range(4):
                for half in range(2):
                    mem = wait_full(act, f"{n}.h{c}", half)
                    s = slice(512 * half, 512 * half + 512)
                    nc.scalar.activation(wide[c][:, s], mem[:, s], ACT.Relu).then_inc(read(f"{n}.h{c}"), 1)

        def l1f_vector(dve):
            n = "l1f"
            ch = "vector_chain"
            copy_half_vector(dve, n + ".T", xnT)
            for half in range(2):
                for c in range(4):
                    s = slice(512 * half, 512 * half + 512)
                    wait_read(dve, f"{n}.h{c}")
                    nc.vector.tensor_tensor(wide[c][:, s], wide[c][:, s], wide[c][:, s], ALU.mult).then_inc(sem[n + ".square"], 1)
            for half in range(2):
                mem = wait_full(dve, n + ".y", half)
                s = slice(512 * half, 512 * half + 512)
                nc.vector.tensor_copy(cur[:, s], mem[:, s]).then_inc(read(n + ".y"), 1)
            wait_read(dve, n + ".y")
            link(dve, ch, nc.vector.tensor_scalar(spikes, cur, 1.0, None, ALU.is_gt))
            v = cur
            for step in range(4):
                link(dve, ch, nc.vector.scalar_tensor_tensor(out=lif_a, in0=v, scalar=0.9, in1=cur, op0=ALU.mult, op1=ALU.add))
                link(dve, ch, nc.vector.scalar_tensor_tensor(out=mem_v, in0=v, scalar=1.0, in1=lif_a, op0=ALU.is_gt,
                                                             op1=ALU.subtract, reverse1=True))
                v = mem_v
                link(dve, ch, nc.vector.scalar_tensor_tensor(out=spikes, in0=v, scalar=1.0, in1=spikes, op0=ALU.is_gt, op1=ALU.add))
            sp = spikes.rearrange("p (t d) -> p t d", t=T)
            for t in range(T):
                nc.vector.scalar_tensor_tensor(out=x_res[:, t, :], in0=sp[:, t, :], scalar=0.2, in1=x_res[:, t, :],
                                               op0=ALU.mult, op1=ALU.add).then_inc(sem[n + ".x"], 1)

        def l1f_pool(pool):
            ln_pool(pool, "l1f")

        L1F_READY = lambda eng, t: eng.wait_ge(sem["l1f.x"], t + 1)



        def bias_half(eng, name, dst, half, bias):
            mem = wait_full(eng, name, half)
            s = slice(512 * half, 512 * half + 512)
            if half == 0:
                nc.scalar.activation(dst[:, s], mem[:, s], ACT.Identity, bias=W(bias)).then_inc(read(name), 1)
            else:
                wait_read(eng, name, 0)
                nc.vector.tensor_scalar(dst[:, s], mem[:, s], W(bias), None, ALU.add).then_inc(read(name), 1)

        rope_qk = scr[:, 0:2, :].rearrange("p a (b c) -> p (a b) c", c=256)
        rope_tmp = scr[:, 2:4, :].rearrange("p a (b c) -> p (a b) c", c=256)
        rope_sq = scr[:, 4:6, :].rearrange("p a b -> p (a b)")
        norm_qk = sb("norm_qk", [P, 2, 256])
        L2A = attention("l2a", "unit", bo=True, scale=8 ** -0.5, q=qT, k=kT, v=v_self, wo="L2_attn_Wo",
                        q_ready=lambda eng, half: wait_read(eng, f"l2a.q{half}"), k_ready=lambda eng, half: wait_read(eng, f"l2a.k{half}"),
                        v_ready=lambda eng: wait_read(eng, "l2a.v"), before_keys=lambda eng, t: wait_full(eng, f"l1x.s{6 + t}"))
        L2A["softmax"] = lambda dve, a, t: None

        raw_qk = scr[:, 6:8, :].rearrange("p a (b c) -> p (a b) c", c=512)
        rope_heads = lambda x: x.rearrange("p t (h f) -> p t h f", f=8)
        rope_table = lambda name: W(name).rearrange("p (a o f) -> p a o f", a=1, o=1).broadcast_to([P, 2, 32, 8])

        def unit_T_tensor(pe, half):
            pe.wait_ge(sem["l2a.unit"], half + 1)
            for part, c in (("k", 1), ("q", 0)):
                mem = fill(pe, f"l2a.{part}{half}", "B")
                for t in range(4):
                    mm = nc.tensor.transpose(mem[:, t * P:(t + 1) * P], rope_qk[:, 4 * half + t, 128 * c:128 * c + 128], W("ident"))
                mm.then_inc(full(f"l2a.{part}{half}"), 1)

        def unit_copy_scalar(act, half):
            mem = wait_full(act, f"l2a.k{half}")
            nc.scalar.copy(kT[:, 512 * half:512 * half + 512], mem).then_inc(read(f"l2a.k{half}"), 1)

        def unit_copy_vector(dve, half):
            mem = wait_full(dve, f"l2a.q{half}")
            nc.vector.tensor_copy(qT[:, 512 * half:512 * half + 512], mem).then_inc(read(f"l2a.q{half}"), 1)

        def unit_vector(dve, half):
            ch = "vector_chain"
            g, rows = slice(128 * half, 128 * half + 128), slice(4 * half, 4 * half + 4)
            dve.wait_ge(sem["l2a.square"], 2 * half + 2)
            sq = rope_sq[:, 1024 * half:1024 * half + 1024].rearrange("p (g f) -> p g f", f=8)
            link(dve, ch, nc.vector.tensor_reduce(norm_qk[:, 0, g], sq, AX, ALU.add))
            link(dve, ch, nc.vector.tensor_scalar(norm_qk[:, 0, g], norm_qk[:, 0, g], 1e-6, None, ALU.add))
            rsqrt_vector(dve, ch, norm_qk[:, 0, g], norm_qk[:, 1, g], 128)
            dve.wait_ge(sem["l2a.rotated"], 2 * half + 2)
            qk = rope_qk[:, rows, :].rearrange("p t (h f) -> p (t h) f", f=8)
            rb = norm_qk[:, 1, g].rearrange("p (g o) -> p g o", o=1).broadcast_to([P, 128, 8])
            nc.vector.tensor_tensor(qk, qk, rb, ALU.mult).then_inc(sem["l2a.unit"], 1)

        leads["l2a", "vector", ("step", 0)] = [lambda dve: unit_vector(dve, 1)]
        leads["l2a", "tensor", ("step", 1)] = [lambda pe: unit_T_tensor(pe, 1)]
        leads["l2a", "scalar", ("step", 1)] = [lambda act: unit_copy_scalar(act, 1)]
        leads["l2a", "vector", ("step", 1)] = [lambda dve: unit_copy_vector(dve, 1)]

        def l2a_tensor(pe):
            n = "l2a"
            tiles_T_tensor(pe, n + ".T", xn, "xn", at(n, "xn", 0))
            for pair in range(T // 2):
                wait_read(pe, n + ".T", pair // 2)
                mem = fill(pe, f"{n}.qk{pair}", reads=1 if pair < 2 else 2)
                for i in range(2):
                    t = 2 * pair + i
                    mm = nc.tensor.matmul(mem[:, 512 * i:512 * i + 512], xnT[:, t * P:(t + 1) * P], W("l2a.qk_rot"), start=True, stop=True)
                mm.then_inc(full(f"{n}.qk{pair}"), 1)
            values_tensor(pe, n + ".v", W("l2a.Wv"), xnT)
            unit_T_tensor(pe, 0)
            attention_tensor(pe, L2A)

        def l2a_vector(dve):
            n = "l2a"
            ln_vector(dve, n, L1F_READY)
            copy_half_vector(dve, n + ".T", xnT)
            for pair in range(2):
                mem = wait_full(dve, f"{n}.qk{pair}").rearrange("p (t c) -> p t c", t=2)
                dve.wait_ge(sem[n + ".square"], pair + 1)
                s = slice(2 * pair, 2 * pair + 2)
                nc.vector.tensor_tensor(rope_heads(rope_qk[:, s, :]), rope_heads(mem[:, :, 0:256]), rope_table("cos8"), ALU.mult)\
                  .then_inc(sem[n + ".cos"], 1)
                nc.vector.tensor_tensor(rope_heads(rope_tmp[:, s, :]), rope_heads(mem[:, :, 256:512]), rope_table("sin8"), ALU.mult)\
                  .then_inc(read(f"{n}.qk{pair}"), 1)
            unit_vector(dve, 0)
            unit_copy_vector(dve, 0)
            values_copy(dve, n + ".v", v_self, 1)
            attention_vector(dve, L2A)

        def l2a_scalar(act):
            n = "l2a"
            copy_half_scalar(act, n + ".T", xnT)
            for pair in range(T // 2):
                mem = wait_full(act, f"{n}.qk{pair}").rearrange("p (t c) -> p t c", t=2)
                sq = rope_sq[:, 512 * pair:512 * pair + 512].rearrange("p (t c) -> p t c", t=2)
                nc.scalar.activation(sq, mem[:, :, 0:256], ACT.Square).then_inc(sem[n + ".square"], 1)
                if pair >= 2:
                    for i in range(2):
                        nc.scalar.copy(raw_qk[:, 2 * (pair - 2) + i, :], mem[:, i, :]).then_inc(read(f"{n}.qk{pair}"), 1)
            values_copy(act, n + ".v", v_self, 0)
            unit_copy_scalar(act, 0)
            attention_scalar(act, L2A)

        def l2a_pool(pool):
            n = "l2a"
            ln_pool(pool, n)
            for pair in range(T // 2):
                s = slice(2 * pair, 2 * pair + 2)
                wait_read(pool, f"{n}.qk{pair}")
                if pair < 2:
                    pool.wait_ge(sem[n + ".cos"], pair + 1)
                else:
                    raw = raw_qk[:, 2 * (pair - 2):2 * (pair - 2) + 2, :]
                    link(pool, "pool_chain", nc.gpsimd.tensor_tensor(rope_heads(rope_qk[:, s, :]), rope_heads(raw[:, :, 0:256]),
                                                                     rope_table("cos8"), ALU.mult))
                    link(pool, "pool_chain", nc.gpsimd.tensor_tensor(rope_heads(rope_tmp[:, s, :]), rope_heads(raw[:, :, 256:512]),
                                                                     rope_table("sin8"), ALU.mult))
                nc.gpsimd.tensor_tensor(rope_qk[:, s, :], rope_qk[:, s, :], rope_tmp[:, s, :], ALU.add).then_inc(sem[n + ".rotated"], 1)
                if pair == 2:
                    spread(pool, nc.gpsimd, L2A, 0, 0, POOL_HEADS, "pool")
                    spread(pool, nc.gpsimd, L2A, 1, 0, POOL_HEADS, "pool")
            for t in range(2, T):
                spread(pool, nc.gpsimd, L2A, t, 0, POOL_HEADS, "pool")
                if t == 3:
                    add_bias_pool(pool, n, "l2a.bo")


        def context_lead(a, wq, wk, wv, bq, bk):
            n = a["n"]
            first_half_T(n)
            leads[n, "tensor", 0].insert(0, lambda pe: project_tensor(pe, n + ".k", [(W(wk), ctxT)]))
            leads[n, "scalar", 0].insert(0, lambda act: bias_half(act, n + ".k", a["k"], 0, bk))
            leads[n, "vector", 0] = [lambda dve: bias_half(dve, n + ".k", a["k"], 1, bk)]
            leads[n, "tensor", 1] = [lambda pe: values_tensor(pe, n + ".v", W(wv), ctxT)]
            leads[n, "scalar", 1] = [lambda act: values_copy(act, n + ".v", a["v"], 0)]
            leads[n, "vector", 1] = [lambda dve: values_copy(dve, n + ".v", a["v"], 1)]
            leads[n, "tensor", 2] = [lambda pe: project_tensor(pe, n + ".q", [(W(wq), xnT)], after=[n + ".T"], halves=(0,))]
            leads[n, "scalar", 2] = [lambda act: bias_half(act, n + ".q", qT, 0, bq)]

        def context_tensor_rest(pe, a, wq):
            n = a["n"]
            second_half_T(pe, n)
            project_tensor(pe, n + ".q", [(W(wq), xnT)], after=[n + ".T"], halves=(1,))
            attention_tensor(pe, a)

        def context_vector_rest(dve, a, bq):
            n = a["n"]
            copy_half_vector(dve, n + ".T", xnT)
            bias_half(dve, n + ".q", qT, 1, bq)
            attention_vector(dve, a)

        def biased_pool(pool, a, bo):
            ln_pool(pool, a["n"])
            a["bo"] = bo
            attention_pool(pool, a)

        def biased_attention(n, kind, cross, last, pre, wo, bv):
            return attention(n, kind, scale=8 ** -0.5, q=qT, k=kcT if cross else kT, v=v_ctx if cross else v_self, wo=wo, bv=bv,
                             bo=True, q_ready=half_ready(n + ".q"), k_ready=half_ready(n + ".k"),
                             v_ready=lambda eng: wait_read(eng, n + ".v"),
                             before_keys=lambda eng, t: wait_full(eng, f"{last}.s{6 + t}"))


        L2X = biased_attention("l2x", "topk", True, "l2a", "L2_xattn", "l2x.Wo", "l2x.bv")
        L2X["prob_ready"] = lambda eng, t, g: eng.wait_ge(sem["l2x.chosen"], t + 1)
        FOUND = -3.0e38
        rest = [scr[:, 8, :], scr[:, 9, :]]
        best8 = [sb(f"best8_{i}", [P, 16, 8]) for i in range(2)]
        ROUNDS = 4

        def topk_vector(dve, a, t):
            n = a["n"]
            wait_read(dve, f"{n}.s{t}")
            pr = prob[t % 2][:, :].rearrange("p (h k) -> p h k", k=SEQ)
            left = rest[t % 2].rearrange("p (h k) -> p h k", k=SEQ)
            for r in range(ROUNDS):
                src = left if r else pr
                b8 = best8[r % 2]
                if r:
                    dve.wait_ge(sem[n + ".struck"], 16 * (ROUNDS * t + r))
                for h in range(16):
                    nc.vector.max(b8[:, h, :], src[:, h, :]).then_inc(sem[n + ".best"], 1)
                dve.wait_ge(sem[n + ".best"], 16 * (ROUNDS * t + r + 1))
                if r == 0 and t >= 2:
                    dve.wait_ge(sem["less"], at(n, "less", t - 1))
                    dve.wait_ge(sem[n + ".chosen"], t - 1)
                if r == 0:
                    nc.vector.tensor_copy(top[t % 2][:, :], b8[:, :, 0]).then_inc(sem["top"], 1)
                for h in range(16):
                    nc.vector.match_replace(out=left[:, h, :], in_to_replace=b8[:, h, :], in_values=src[:, h, :], imm_value=FOUND)\
                      .then_inc(sem[n + ".struck"], 1)
            if t == T - 1:
                weigh(dve, nc.vector, a, t)

        def weigh(eng, ops, a, t):
            n, chain = a["n"], "vector_chain" if t == T - 1 else "pool_chain"
            eng.wait_ge(sem[n + ".struck"], 16 * ROUNDS * (t + 1))
            eng.wait_ge(sem["top"], at(n, "top", t + 1))
            if t == T - 1:
                eng.wait_ge(sem["less"], at(n, "less", t))
                eng.wait_ge(sem[n + ".chosen"], t)
            pr = prob[t % 2][:, :].rearrange("p (h k) -> p h k", k=SEQ)
            tb = top[t % 2][:, :].rearrange("p (h o) -> p h o", o=1).broadcast_to([P, 16, SEQ])
            ops.tensor_tensor(pr, pr, tb, ALU.subtract).then_inc(sem["less"], 1)
            link(eng, chain, ops.tensor_scalar(rest[t % 2], rest[t % 2], -2.0e38, None, ALU.is_le))
            eng.wait_ge(sem["exp"], at(n, "exp", t + 1))
            ops.tensor_tensor(prob[t % 2][:, :], rest[t % 2], prob[t % 2][:, :], ALU.mult).then_inc(sem[n + ".chosen"], 1)

        L2X["softmax"] = topk_vector

        def topk_copy_scalar(act, a, t):
            n = a["n"]
            if t >= 2:
                wait_full(act, f"{n}.t{t - 2}")
            mem = wait_full(act, f"{n}.s{t}")
            nc.scalar.copy(prob[t % 2][:, :], mem).then_inc(read(f"{n}.s{t}"), 1)

        L2X["copy"] = topk_copy_scalar


        share = sb("share", [P, 2])
        thresh = sb("thresh", [P, 2, 2])
        tern = scr[:, 10, 0:512]
        tern2 = scr[:, 10, 512:1024]
        TERNARY = ("l2f.up", "l2f.down")

        def ternary_scalar(act):
            for i, w in enumerate(TERNARY):
                if i:
                    act.wait_ge(sem["tern.sum"], 1)
                nc.scalar.activation(tern, W(w), ACT.Abs, accum_out=share[:, i:i + 1]).then_inc(sem["tern.sum"], 1)

        def ternary_tensor(pe):
            pe.wait_ge(sem["tern.sum"], 2)
            mem = fill(pe, "tern.mean", "B")
            nc.tensor.matmul(mem[:, 0:2], W("ones128"), share[:, :], start=True, stop=True).then_inc(full("tern.mean"), 1)

        def ternary_vector(dve):
            mem = wait_full(dve, "tern.mean")
            half_mean = 0.5 / (512 * 128)
            link(dve, "vector_chain", nc.vector.tensor_scalar(thresh[:, :, 0], mem[:, 0:2], half_mean, None, ALU.mult))
            nc.vector.tensor_scalar(thresh[:, :, 1], mem[:, 0:2], -half_mean, None, ALU.mult).then_inc(read("tern.mean"), 1)

        def ternary_pool(pool):
            wait_read(pool, "tern.mean")
            pool.wait_ge(sem["tern.sum"], 2)
            for i, name in enumerate(TERNARY):
                w = W(name)
                link(pool, "pool_chain", nc.gpsimd.tensor_scalar(tern, w, thresh[:, i, 0:1], None, ALU.is_gt))
                link(pool, "pool_chain", nc.gpsimd.tensor_scalar(tern2, w, thresh[:, i, 1:2], None, ALU.is_lt))
                link(pool, "pool_chain", nc.gpsimd.tensor_tensor(tern, tern, tern2, ALU.subtract))
                link(pool, "pool_chain", nc.gpsimd.tensor_tensor(tern, tern, w, ALU.subtract))
                link(pool, "pool_chain", nc.gpsimd.tensor_tensor(w, w, tern, ALU.add))

        context_lead(L2X, "l2x.Wq", "l2x.Wk", "l2x.Wv", "l2x.bq", "l2x.bk")

        def l2x_tensor(pe):
            ternary_tensor(pe)
            context_tensor_rest(pe, L2X, "l2x.Wq")

        def l2x_vector(dve):
            ternary_vector(dve)
            context_vector_rest(dve, L2X, "l2x.bq")

        def l2x_scalar(act):
            ternary_scalar(act)
            attention_scalar(act, L2X)

        def l2x_pool(pool):
            ln_pool(pool, "l2x")
            spread(pool, nc.gpsimd, L2X, 0, 0, POOL_HEADS, "pool")
            spread(pool, nc.gpsimd, L2X, 1, 0, POOL_HEADS, "pool")
            add_bias_pool(pool, "l2x", "l2x.bo")
            ternary_pool(pool)
            for t in range(T - 1):
                weigh(pool, nc.gpsimd, L2X, t)
                if t + 2 < T:
                    spread(pool, nc.gpsimd, L2X, t + 2, 0, POOL_HEADS, "pool")


        hid = scr[:, 0:4, :].rearrange("p a (b c) -> p (a b) c", c=512)
        hidT = scr[:, 4:8, :].rearrange("p a b -> p (a b)").rearrange("p (t c k) -> p t c k", t=T, c=4)
        junk = scr[:, 8, 0:512]
        row = sb("row", [P, 4, T])

        def l2f_tensor(pe):
            n = "l2f"
            tiles_T_tensor(pe, n + ".T", xn, n + ".scaled")
            wait_read(pe, n + ".T")
            for pair in range(T // 2):
                mem = fill(pe, f"{n}.up{pair}")
                for i in range(2):
                    t = 2 * pair + i
                    mm = nc.tensor.matmul(mem[:, 512 * i:512 * i + 512], xnT[:, t * P:(t + 1) * P], W("l2f.up"), start=True, stop=True)
                mm.then_inc(full(f"{n}.up{pair}"), 1)
            for pair in range(T // 2):
                wait_read(pe, f"{n}.up{pair}")
                mem = fill(pe, f"{n}.hT{pair}", fulls=2, reads=2)
                for i in range(2):
                    for c in range(4):
                        at = 512 * i + 128 * c
                        mm = nc.tensor.transpose(mem[:, at:at + 128], hid[:, 2 * pair + i, 128 * c:128 * c + 128], W("ident"))
                    mm.then_inc(full(f"{n}.hT{pair}"), 1)
            for half in range(2):
                for pair in (2 * half, 2 * half + 1):
                    wait_read(pe, f"{n}.hT{pair}")
                mem = fill(pe, f"{n}.y{half}", "B", reads=4)
                for t in range(4 * half, 4 * half + 4):
                    for c in range(4):
                        mm = nc.tensor.matmul(mem[:, (t % 4) * P:(t % 4 + 1) * P], hidT[:, t, c, :], W("l2f.down")[:, 128 * c:128 * c + 128],
                                              start=c == 0, stop=c == 3)
                mm.then_inc(full(f"{n}.y{half}"), 1)

        def l2f_scalar(act):
            n = "l2f"
            act.wait_ge(sem["xn"], at(n, "xn", T))
            nc.scalar.activation(scr[:, 9, :], xn[:, :, :].rearrange("p t d -> p (t d)"), ACT.Square).then_inc(sem[n + ".square"], 1)
            copy_half_scalar(act, n + ".T", xnT)
            for pair in range(T // 2):
                mem = wait_full(act, f"{n}.up{pair}")
                nc.scalar.activation(hid[:, 2 * pair:2 * pair + 2, :].rearrange("p a b -> p (a b)"), mem, ACT.Gelu)\
                  .then_inc(read(f"{n}.up{pair}"), 1)
            for t in range(T):
                wait_read(act, f"{n}.up{t // 2}")
                if t:
                    act.wait_ge(sem[n + ".ss"], t)
                nc.scalar.activation(junk, hid[:, t, :], ACT.Square, accum_out=row[:, 2, t:t + 1]).then_inc(sem[n + ".ss"], 1)
                if t % 2:
                    pair = t // 2
                    mem = wait_full(act, f"{n}.hT{pair}", 0)
                    nc.scalar.copy(hidT[:, 2 * pair, :, :].rearrange("p c k -> p (c k)"), mem[:, 0:512]).then_inc(read(f"{n}.hT{pair}"), 1)

        def rms_vector(dve, ch, ss, out_col, width, scale_width):
            rsqrt_vector(dve, ch, ss, out_col, scale_width)
            link(dve, ch, nc.vector.tensor_tensor(out_col, out_col, ss, ALU.mult))
            link(dve, ch, nc.vector.tensor_scalar(out_col, out_col, width ** -0.5, 1e-8, ALU.mult, ALU.add))
            link(dve, ch, nc.vector.reciprocal(out_col, out_col))

        def l2f_vector(dve):
            n = "l2f"
            ch = "vector_chain"
            dve.wait_ge(sem[n + ".square"], 1)
            dve.wait_ge(sem["xn"], at(n, "xn", T))
            link(dve, ch, nc.vector.tensor_reduce(row[:, 0, :], scr[:, 9, :].rearrange("p (t d) -> p t d", t=T), AX, ALU.add))
            rms_vector(dve, ch, row[:, 0, :], row[:, 1, :], D, T)
            for t in range(T):
                nc.vector.tensor_scalar(xn[:, t, :], xn[:, t, :], row[:, 1, t:t + 1], None, ALU.mult).then_inc(sem[n + ".scaled"], 1)
            copy_half_vector(dve, n + ".T", xnT)
            for pair in range(T // 2):
                mem = wait_full(dve, f"{n}.hT{pair}", 1)
                nc.vector.tensor_copy(hidT[:, 2 * pair + 1, :, :].rearrange("p c k -> p (c k)"), mem[:, 512:1024])\
                  .then_inc(read(f"{n}.hT{pair}"), 1)
            dve.wait_ge(sem[n + ".ss"], T)
            rms_vector(dve, ch, row[:, 2, :], row[:, 3, :], 512, T)
            for t in range(T):
                mem = wait_full(dve, f"{n}.y{t // 4}")
                nc.vector.scalar_tensor_tensor(out=x_res[:, t, :], in0=mem[:, (t % 4) * P:(t % 4 + 1) * P], scalar=row[:, 3, t:t + 1],
                                               in1=x_res[:, t, :], op0=ALU.mult, op1=ALU.add).then_inc(read(f"{n}.y{t // 4}"), 1)

        def l2f_pool(pool):
            ln_pool(pool, "l2f")

        L2F_READY = lambda eng, t: wait_read(eng, f"l2f.y{t // 4}")


        L3A = biased_attention("l3a", "bias", False, "l2x", "L3_attn", "l3a.WO", "l3a.bV")
        L3X = biased_attention("l3x", "plain", True, "l3a", "L3_xattn", "l3x.Wo", "l3x.bv")
        L3A["wv"] = W("l3a.WV")
        rel_bias = scr[:, 11, :]

        def l3a_tensor(pe):
            tiles_T_tensor(pe, "l3a.T", xn, "xn", at("l3a", "xn", 0))
            project_tensor(pe, "l3a.k", [(W("l3a.WK"), xnT)], after=["l3a.T"])
            project_tensor(pe, "l3a.q", [(W("l3a.WQ"), xnT)])
            attention_tensor(pe, L3A)

        def l3a_vector(dve):
            c = W("causal").rearrange("p (o k) -> p o k", o=1).broadcast_to([P, 16, SEQ])
            link(dve, "vector_chain", nc.vector.tensor_tensor(rel_bias.rearrange("p (h k) -> p h k", k=SEQ),
                                                            W("l3a.rel").rearrange("p (h k) -> p h k", k=SEQ), c, ALU.add))
            ln_vector(dve, "l3a", L2F_READY)
            copy_half_vector(dve, "l3a.T", xnT)
            bias_half(dve, "l3a.k", kT, 1, "l3a.bK")
            bias_half(dve, "l3a.q", qT, 1, "l3a.bQ")
            attention_vector(dve, L3A)

        def l3a_scalar(act):
            copy_half_scalar(act, "l3a.T", xnT)
            bias_half(act, "l3a.k", kT, 0, "l3a.bK")
            bias_half(act, "l3a.q", qT, 0, "l3a.bQ")
            attention_scalar(act, L3A)

        def l3a_pool(pool):
            biased_pool(pool, L3A, "l3a.bO")

        context_lead(L3X, "l3x.Wq", "l3x.Wk", "l3x.Wv", "l3x.bq", "l3x.bk")

        def l3x_tensor(pe):
            context_tensor_rest(pe, L3X, "l3x.Wq")

        def l3x_vector(dve):
            context_vector_rest(dve, L3X, "l3x.bq")

        def l3x_scalar(act):
            attention_scalar(act, L3X)

        def l3x_pool(pool):
            biased_pool(pool, L3X, "l3x.bo")
            for j in range(2):
                nc.gpsimd.memset(keys4[j][:, :, :, :, :], 0.0).then_inc(sem["zeros_set"], 1)
            nc.gpsimd.memset(v4[0][:, :, :, :], 0.0).then_inc(sem["zeros_set"], 1)


        z = xn
        half_shifted = kcT[:, :].rearrange("p (t d) -> p t d", t=T)
        turned = [scr[:, j, :] for j in (0, 1, 11)]
        square4 = [scr[:, j, :] for j in (2, 3)]
        crossed = [scr[:, j, :] for j in (4, 5)]
        keys4 = [scr[:, j, :].rearrange("p (a b h k) -> p a b h k", a=4, b=2, h=2) for j in (6, 7)]
        qT4 = [scr[:, 8, 512 * j:512 * j + 512].rearrange("p (a k) -> p a k", a=4) for j in (0, 1)]
        out4 = [scr[:, 9, 512 * j:512 * j + 512] for j in (0, 1)]
        outT4 = [scr[:, 10, 512 * j:512 * j + 512] for j in (0, 1)]
        v4 = [v.rearrange("p b a w -> p (b a w)")[:, 0:1040].rearrange("p (b a w) -> p b a w", b=2, a=4) for v in (v_self, v_ctx)]
        gelu4, mlp4 = scr[:, 0:3, :], scr[:, 3:6, :]
        len_sq = sb("len_sq", [P, T, 16])
        len_inv = sb("len_inv", [P, T, 16])
        HIDDEN_ROWS = (128, 128, 85)
        LAYERS = ("l3g", "l3h")

        def z_ready(m):
            if m == "l3g":
                return lambda eng, t: eng.wait_ge(sem["xn"], at("l3f", "xn", t + 1))
            return lambda eng, t: wait_product_read(eng, f"l3g.mlp{t // 4}", t % 4)

        def wait_product_read(eng, name, tile):
            slot, _, _, done = book.record[name]
            eng.wait_ge(sem["read." + slot], done - 3 + tile)

        def steps(stages):
            for u in range(T + 8):
                for lag, piece in stages:
                    if 0 <= u - lag < T:
                        yield piece, u - lag

        def inner_attention_tensor(pe, m, i):
            mem = fill(pe, m + ".T", fulls=2, reads=2)
            for t in range(T):
                z_ready(m)(pe, t)
                nc.tensor.transpose(mem[0:64, t * P:(t + 1) * P], z[:, t, 0:64], W("ident"))
                mm = nc.tensor.matmul(mem[64:128, t * P:(t + 1) * P], z[:, t, 64:128], W("l3f.shift"), start=True, stop=True)
                if t % 4 == 3:
                    mm.then_inc(full(m + ".T"), 1)
            wait_read(pe, m + ".T")
            wqkv = W(f"l3f.wqkv{i}")

            def queries_keys(t):
                mem = fill(pe, f"{m}.qk{t}")
                for c in range(2):
                    mm = nc.tensor.matmul(mem[:, 512 * c:512 * c + 512], xnT[:, t * P:(t + 1) * P],
                                          wqkv[:, 512 * c:512 * c + 512], start=True, stop=True)
                mm.then_inc(full(f"{m}.qk{t}"), 1)

            def turned_T(t):
                pe.wait_ge(sem[m + ".unit"], t + 1)
                mem = fill(pe, f"{m}.qkT{t}", fulls=2, reads=3)
                for c in range(8):
                    mm = nc.tensor.transpose(mem[:, c * P:(c + 1) * P], turned[t % 3][:, c * P:(c + 1) * P], W("ident"))
                    if c % 4 == 3:
                        mm.then_inc(full(f"{m}.qkT{t}"), 1)

            def scores(t):
                wait_read(pe, f"{m}.qkT{t}")
                mem = fill(pe, f"{m}.s{t}", "B")
                for p in range(4):
                    for b in range(2):
                        mm = nc.tensor.matmul(mem[64 * b:64 * b + 64, p * P:(p + 1) * P], qT4[t % 2][:, p, 64 * b:64 * b + 64],
                                              keys4[t % 2][:, p, b, :, :], start=True, stop=True)
                mm.then_inc(full(f"{m}.s{t}"), 1)

            def values(t):
                mem = fill(pe, f"{m}.v{t}", "B", reads=2)
                wv = wqkv[:, 1024:1536].rearrange("p (a h f) -> p h a f", h=2, f=64)
                for b in range(2):
                    for h in range(2):
                        mm = nc.tensor.matmul(mem[64 * h:64 * h + 64, 256 * b:256 * b + 256],
                                              xnT[:, t * P + 64 * b:t * P + 64 * b + 64], wv[:, h], start=True, stop=True)
                mm.then_inc(full(f"{m}.v{t}"), 1)

            def prob_T(t):
                pe.wait_ge(sem["exp"], at(m, "exp", t + 1))
                mem = fill(pe, f"{m}.t{t}", "B")
                for p in range(4):
                    mm = nc.tensor.transpose(mem[:, p * P:(p + 1) * P], prob[t % 2][:, p * P:(p + 1) * P], W("ident"))
                mm.then_inc(full(f"{m}.t{t}"), 1)

            def outputs(t):
                wait_read(pe, f"{m}.t{t}")
                wait_read(pe, f"{m}.v{t}")
                mem = fill(pe, f"{m}.o{t}", reads=2)
                for p in range(4):
                    for b in range(2):
                        at_col = 512 * (p // 2) + 130 * (p % 2)
                        mm = nc.tensor.matmul(mem[64 * b:64 * b + 64, at_col:at_col + 130],
                                              probT[t % 2][:, p * P + 64 * b:p * P + 64 * b + 64], v4[t % 2][:, b, p, :],
                                              start=True, stop=True)
                mm.then_inc(full(f"{m}.o{t}"), 1)

            def outputs_T(t):
                wait_read(pe, f"{m}.o{t}")
                mem = fill(pe, f"{m}.ot{t}", "B")
                for c in range(4):
                    mm = nc.tensor.transpose(mem[:, c * P:(c + 1) * P], out4[t % 2][:, c * P:(c + 1) * P], W("ident"))
                mm.then_inc(full(f"{m}.ot{t}"), 1)

            def project(t):
                wait_read(pe, f"{m}.ot{t}")
                mem = fill(pe, f"{m}.y{t}", "B")
                for c in range(4):
                    mm = nc.tensor.matmul(mem[:, 0:P], outT4[t % 2][:, c * P:(c + 1) * P], W(f"l3f.wo{i}")[:, c * P:(c + 1) * P],
                                          start=c == 0, stop=c == 3)
                mm.then_inc(full(f"{m}.y{t}"), 1)

            for piece, t in steps([(0, queries_keys), (7, project), (6, outputs_T), (5, outputs), (4, prob_T),
                                   (3, scores), (4, values), (2, turned_T)]):
                piece(t)

        def inner_attention_vector(dve, m, i):
            mem = wait_full(dve, m + ".T", 1)
            nc.vector.tensor_copy(xnT[:, 512:], mem[:, 512:]).then_inc(read(m + ".T"), 1)

            def rotate(t):
                mem = wait_full(dve, f"{m}.qk{t}")
                dve.wait_ge(sem[m + ".square"], t + 1)
                nc.vector.tensor_reduce(len_sq[:, t, :], square4[t % 2].rearrange("p (g f) -> p g f", f=64), AX, ALU.add)\
                  .then_inc(sem[m + ".len"], 1)
                if t >= 3:
                    wait_full(dve, f"{m}.qkT{t - 3}", 1)
                if t >= 2:
                    dve.wait_ge(sem[m + ".unit"], t - 1)
                elif i:
                    wait_full(dve, "l3g.mlp1")
                tab = W(f"l3f.scale{i}").rearrange("p (c a o f) -> p c a o f", c=2, a=2, o=1)
                qk = mem.rearrange("p (a h f) -> p a h f", a=2, f=64)
                c4 = crossed[t % 2].rearrange("p (a h f) -> p a h f", a=2, f=64)
                nc.vector.tensor_tensor(turned[t % 3].rearrange("p (a h f) -> p a h f", a=2, f=64), qk,
                                        tab[:, 0].broadcast_to([P, 2, 8, 64]), ALU.mult).then_inc(sem[m + ".turn"], 1)
                for lo, hi in ((0, 32), (32, 0)):
                    nc.vector.tensor_tensor(c4[:, :, :, lo:lo + 32], qk[:, :, :, hi:hi + 32],
                                            tab[:, 1, :, :, lo:lo + 32].broadcast_to([P, 2, 8, 32]), ALU.mult)\
                      .then_inc(read(f"{m}.qk{t}") if lo else sem[m + ".turn"], 1)

            def softmax(t):
                mem = wait_full(dve, f"{m}.s{t}")
                if t >= 2:
                    wait_full(dve, f"{m}.t{t - 2}")
                    dve.wait_ge(sem["less"], at(m, "less", t - 1))
                pr = prob[t % 2][:, 0:512].rearrange("p (h k) -> p h k", k=SEQ)
                c = W("causal").rearrange("p (o k) -> p o k", o=1).broadcast_to([P, 8, SEQ])
                nc.vector.scalar_tensor_tensor(out=pr, in0=mem.rearrange("p (h k) -> p h k", k=SEQ), scalar=8.0, in1=c,
                                               op0=ALU.mult, op1=ALU.add).then_inc(read(f"{m}.s{t}"), 1)
                wait_read(dve, f"{m}.s{t}")
                nc.vector.tensor_reduce(top[t % 2][:, 0:8], pr, AX, ALU.max).then_inc(sem["top"], 1)
                dve.wait_ge(sem["top"], at(m, "top", t + 1))
                tb = top[t % 2][:, 0:8].rearrange("p (h o) -> p h o", o=1).broadcast_to([P, 8, SEQ])
                nc.vector.tensor_tensor(pr, pr, tb, ALU.subtract).then_inc(sem["less"], 1)

            def normalise(t):
                mem = wait_full(dve, f"{m}.o{t}")
                if t >= 2:
                    wait_full(dve, f"{m}.ot{t - 2}")
                v = mem.rearrange("p (g w) -> p g w", g=2)[:, :, 0:260].rearrange("p g (a w) -> p g a w", w=130)
                rd = rden[t % 2][:, 0:8].rearrange("p (g a h) -> p g a h", g=2, a=2)
                nc.vector.reciprocal(rd, v[:, :, :, 128:130]).then_inc(sem["rden"], 1)
                dve.wait_ge(sem["rden"], at(m, "rden", t + 1))
                for g in range(2):
                    to = out4[t % 2][:, 256 * g:256 * g + 256].rearrange("p (a h f) -> p a h f", h=2, f=64)
                    rb = rd[:, g].rearrange("p a (h o) -> p a h o", o=1).broadcast_to([P, 2, 2, 64])
                    nc.vector.tensor_tensor(to, v[:, g, :, 0:128].rearrange("p a (h f) -> p a h f", h=2), rb, ALU.mult)\
                      .then_inc(read(f"{m}.o{t}"), 1)

            def residual(t):
                mem = wait_full(dve, f"{m}.y{t}")
                nc.vector.tensor_tensor(z[:, t, :], z[:, t, :], mem[:, 0:P], ALU.add).then_inc(read(f"{m}.y{t}"), 1)

            for piece, t in steps([(7, residual), (0, rotate), (5, normalise), (3, softmax)]):
                piece(t)

        def values4_copy(act, m, t):
            mem = wait_full(act, f"{m}.v{t}")
            if t >= 2:
                wait_full(act, f"{m}.o{t - 2}")
            for h in range(2):
                src = mem[64 * h:64 * h + 64, 0:512].rearrange("p (b a f) -> p b a f", b=2, f=64)
                nc.scalar.copy(v4[t % 2][64 * h:64 * h + 64, :, :, 64 * h:64 * h + 64], src).then_inc(read(f"{m}.v{t}"), 1)

        def inner_attention_scalar(act, m, i):
            copy_half_scalar(act, m + ".T", xnT)

            def squares(t):
                mem = wait_full(act, f"{m}.qk{t}")
                if t >= 2:
                    act.wait_ge(sem[m + ".len"], t - 1)
                elif i:
                    wait_full(act, "l3g.mlp1")
                nc.scalar.activation(square4[t % 2], mem, ACT.Square).then_inc(sem[m + ".square"], 1)

            def turned_copy(t):
                if t >= 2:
                    wait_full(act, f"{m}.s{t - 2}")
                elif i == 0:
                    act.wait_ge(sem["v4_set"], 4)
                mem = wait_full(act, f"{m}.qkT{t}", 0)
                nc.scalar.copy(qT4[t % 2][:, :, :].rearrange("p a k -> p (a k)"), mem[:, 0:512]).then_inc(read(f"{m}.qkT{t}"), 1)
                wait_full(act, f"{m}.qkT{t}", 1)
                for h in range(2):
                    rows = slice(64 * h, 64 * h + 64)
                    nc.scalar.copy(keys4[t % 2][rows, :, :, h, :], mem[rows, 512:1024].rearrange("p (a b k) -> p a b k", a=4, b=2))\
                      .then_inc(read(f"{m}.qkT{t}"), 1)

            def exponential(t):
                act.wait_ge(sem["less"], at(m, "less", t + 1))
                nc.scalar.activation(prob[t % 2][:, 0:512], prob[t % 2][:, 0:512], ACT.Exp).then_inc(sem["exp"], 1)

            def prob_copy(t):
                if t >= 2:
                    wait_full(act, f"{m}.o{t - 2}")
                mem = wait_full(act, f"{m}.t{t}")
                nc.scalar.copy(probT[t % 2][:, 0:512], mem[:, 0:512]).then_inc(read(f"{m}.t{t}"), 1)

            def outputs_copy(t):
                if t >= 2:
                    wait_full(act, f"{m}.y{t - 2}")
                mem = wait_full(act, f"{m}.ot{t}")
                nc.scalar.copy(outT4[t % 2], mem[:, 0:512]).then_inc(read(f"{m}.ot{t}"), 1)

            for piece, t in steps([(0, squares), (6, outputs_copy), (4, prob_copy), (4, lambda t: values4_copy(act, m, t)),
                                   (3, exponential), (2, turned_copy)]):
                piece(t)

        def inner_attention_pool(pool, m, i):
            for t in range(T):
                pool.wait_ge(sem[m + ".len"], t + 1)
                link(pool, "pool_chain", nc.gpsimd.tensor_scalar(len_inv[:, t, :], len_sq[:, t, :], 1e-24, None, ALU.max))
                half = minus_half[:, 0:1].broadcast_to([P, 16])
                link(pool, "pool_chain", nc.gpsimd.tensor_tensor(len_inv[:, t, :], len_inv[:, t, :], half, ALU.pow))
                pool.wait_ge(sem[m + ".turn"], 2 * t + 2)
                wait_product(pool, f"{m}.qk{t}")
                link(pool, "pool_chain", nc.gpsimd.tensor_tensor(turned[t % 3], turned[t % 3], crossed[t % 2], ALU.add))
                r = len_inv[:, t, :].rearrange("p (g o) -> p g o", o=1).broadcast_to([P, 16, 64])
                t3 = turned[t % 3].rearrange("p (g f) -> p g f", f=64)
                nc.gpsimd.tensor_tensor(t3, t3, r, ALU.mult).then_inc(sem[m + ".unit"], 1)

        def wait_product(eng, name):
            wait_read(eng, name)


        def inner_mlp_tensor(pe, m, i):
            for t in range(T):
                wait_read(pe, f"{m}.y{t}")
            mem = fill(pe, m + ".shift", "B")
            nc.tensor.matmul(mem, W("l3f.shift"), z[:, :, 64:128], start=True, stop=True).then_inc(full(m + ".shift"), 1)
            tiles_T_tensor(pe, m + ".hT", half_shifted, "xn", at(m, "xn", 0))
            wait_read(pe, m + ".hT")
            for c, rows in enumerate(HIDDEN_ROWS):
                for part in ("g", "a"):
                    mem = fill(pe, f"{m}.{part}{c}")
                    lo = P * c + (341 if part == "g" else 0)
                    for half in range(2):
                        s = slice(512 * half, 512 * half + 512)
                        mm = nc.tensor.matmul(mem[0:rows, s], W(f"l3f.w1_{i}")[:, lo:lo + rows], xnT[:, s], start=True, stop=True)
                    mm.then_inc(full(f"{m}.{part}{c}"), 1)
            for c in range(3):
                wait_read(pe, f"{m}.a{c}")
            for half in range(2):
                mem = fill(pe, f"{m}.mlp{half}", "B", reads=4)
                for t in range(4 * half, 4 * half + 4):
                    for c, rows in enumerate(HIDDEN_ROWS):
                        mm = nc.tensor.matmul(mem[:, (t % 4) * P:(t % 4 + 1) * P], mlp4[0:rows, c, t * P:(t + 1) * P],
                                              W(f"l3f.w2_{i}")[0:rows, c * P:(c + 1) * P], start=c == 0, stop=c == 2)
                mm.then_inc(full(f"{m}.mlp{half}"), 1)

        def inner_mlp_vector(dve, m, i):
            def ready(eng, t):
                eng.wait_ge(sem[m + ".first_half"], 1)
                wait_read(eng, m + ".shift")

            ln_vector(dve, m, ready, half_shifted, half_shifted)
            mem = wait_full(dve, m + ".hT", 1)
            nc.vector.tensor_scalar(xnT[:, 512:], mem[:, 512:], W(f"l3f.ln_g{i}"), W(f"l3f.ln_b{i}"), ALU.mult, ALU.add)\
              .then_inc(read(m + ".hT"), 1)
            for c, rows in enumerate(HIDDEN_ROWS):
                mem = wait_full(dve, f"{m}.a{c}")
                wait_read(dve, f"{m}.g{c}")
                nc.vector.scalar_tensor_tensor(out=mlp4[0:rows, c, :], in0=mem[0:rows, :], scalar=W(f"l3f.b1a{i}")[0:rows, c:c + 1],
                                               in1=gelu4[0:rows, c, :], op0=ALU.add, op1=ALU.mult).then_inc(read(f"{m}.a{c}"), 1)
            dve.wait_ge(sem[m + ".b2"], 1)
            for t in range(T):
                mem = wait_full(dve, f"{m}.mlp{t // 4}")
                nc.vector.tensor_tensor(z[:, t, :], z[:, t, :], mem[:, (t % 4) * P:(t % 4 + 1) * P], ALU.add)\
                  .then_inc(read(f"{m}.mlp{t // 4}"), 1)

        def inner_mlp_scalar(act, m, i):
            mem = wait_full(act, m + ".shift")
            nc.scalar.copy(half_shifted[:, :, 64:128], mem.rearrange("p (t d) -> p t d", t=T)).then_inc(read(m + ".shift"), 1)
            mem = wait_full(act, m + ".hT", 0)
            nc.scalar.activation(xnT[:, 0:512], mem[:, 0:512], ACT.Identity, scale=W(f"l3f.ln_g{i}"), bias=W(f"l3f.ln_b{i}"))\
              .then_inc(read(m + ".hT"), 1)
            for c, rows in enumerate(HIDDEN_ROWS):
                mem = wait_full(act, f"{m}.g{c}")
                nc.scalar.activation(gelu4[0:rows, c, :], mem[0:rows, :], ACT.Gelu, bias=W(f"l3f.b1g{i}")[0:rows, c:c + 1])\
                  .then_inc(read(f"{m}.g{c}"), 1)

        def inner_mlp_pool(pool, m, i):
            for t in range(T):
                wait_read(pool, f"{m}.y{t}")
            nc.gpsimd.tensor_copy(half_shifted[:, :, 0:64], z[:, :, 0:64]).then_inc(sem[m + ".first_half"], 1)
            pool.wait_ge(sem[m + ".first_half"], 1)
            ln_pool(pool, m)
            wait_full(pool, m + ".shift")
            nc.gpsimd.tensor_tensor(z[:, :, :], z[:, :, :], tok_bias(f"l3f.b2_{i}"), ALU.add).then_inc(sem[m + ".b2"], 1)

        def l3f_tensor(pe):
            pe.wait_ge(sem["v4_set"], 4)
            for i, m in enumerate(LAYERS):
                inner_attention_tensor(pe, m, i)
                inner_mlp_tensor(pe, m, i)

        def l3f_vector(dve):
            dve.wait_ge(sem["zeros_set"], 4)
            for j in range(2):
                for h in range(2):
                    nc.vector.memset(v4[j][64 * h:64 * h + 64, :, :, 128 + h:129 + h], 1.0).then_inc(sem["v4_set"], 1)
            dve.wait_ge(sem["v4_set"], 4)
            dve.wait_ge(sem["rope_table"], 2)
            for i, m in enumerate(LAYERS):
                inner_attention_vector(dve, m, i)
                inner_mlp_vector(dve, m, i)
            for t in range(T):
                z_ready_last(dve, t)
                nc.vector.tensor_tensor(x_res[:, t, :], x_res[:, t, :], z[:, t, :], ALU.add).then_inc(sem["l3f.x"], 1)

        def z_ready_last(eng, t):
            wait_product_read(eng, f"l3h.mlp{t // 4}", t % 4)

        def l3f_scalar(act):
            for i, m in enumerate(LAYERS):
                inner_attention_scalar(act, m, i)
                inner_mlp_scalar(act, m, i)

        def l3f_pool(pool):
            ln_pool(pool, "l3f")
            wait_full(pool, f"l3x.o{T - 1}")
            nc.gpsimd.memset(v4[1][:, :, :, :], 0.0).then_inc(sem["zeros_set"], 1)
            for i in range(2):
                nc.gpsimd.tensor_tensor(W(f"l3f.scale{i}"), W(f"l3f.scale{i}"), W("l3f.rope"), ALU.mult)\
                  .then_inc(sem["rope_table"], 1)
            for i, m in enumerate(LAYERS):
                inner_attention_pool(pool, m, i)
                inner_mlp_pool(pool, m, i)

        def setup_vector(dve):
            nc.vector.memset(minus_half[:, :], -0.5).then_inc(sem["minus_half"], 1)
            for p0, lo, hi, value in ((0, 16, 32, 0.0), (0, 32, 33, 1.0), (0, 33, 34, 0.0),
                                      (64, 0, 16, 0.0), (64, 32, 33, 0.0), (64, 33, 34, 1.0)):
                nc.vector.memset(v_lstm[p0:p0 + 64, :, :, lo:hi], value).then_inc(sem["lstm_values_set"], 1)
            nc.vector.memset(lstm[:, 3, :], 0.0).then_inc(sem["lstm_values_set"], 1)
            for v in (v_self, v_ctx):
                for p0, lo, hi, value in ((0, 8, 16, 0.0), (0, 16, 17, 1.0), (0, 17, 18, 0.0),
                                          (64, 0, 8, 0.0), (64, 16, 17, 0.0), (64, 17, 18, 1.0)):
                    nc.vector.memset(v[p0:p0 + 64, :, :, lo:hi], value).then_inc(sem["values_set"], 1)

        stages = [
            ("0a", l0a_tensor, l0a_vector, l0a_scalar, l0a_pool, residual_ready(L0A)),
            ("0x", l0x_tensor, l0x_vector, l0x_scalar, l0x_pool, residual_ready(L0X)),
            ("0f", l0f_tensor, l0f_vector, l0f_scalar, l0f_pool, L0F_READY),
            ("1", l1a_tensor, l1a_vector, l1a_scalar, l1a_pool, product_ready("l1a.y")),
            ("1", l1x_tensor, l1x_vector, l1x_scalar, l1x_pool, residual_ready(L1X)),
            ("1", l1f_tensor, l1f_vector, l1f_scalar, l1f_pool, L1F_READY),
            ("2", l2a_tensor, l2a_vector, l2a_scalar, l2a_pool, residual_ready(L2A)),
            ("2", l2x_tensor, l2x_vector, l2x_scalar, l2x_pool, residual_ready(L2X)),
            ("2", l2f_tensor, l2f_vector, l2f_scalar, l2f_pool, L2F_READY),
            ("3", l3a_tensor, l3a_vector, l3a_scalar, l3a_pool, residual_ready(L3A)),
            ("3", l3x_tensor, l3x_vector, l3x_scalar, l3x_pool, residual_ready(L3X)),
            ("4", l3f_tensor, l3f_vector, l3f_scalar, l3f_pool, lambda eng, t: eng.wait_ge(sem["l3f.x"], t + 1)),
        ]

        block = ctx.enter_context(nc.Block())

        @block.tensor
        def _(pe):
            weights(pe, "c")
            context_tensor(pe)
            for s in stages:
                weights(pe, s[0])
                s[1](pe)

        @block.vector
        def _(dve):
            setup_vector(dve)
            weights(dve, "c")
            context_vector(dve)
            for s in stages:
                weights(dve, s[0])
                s[2](dve)

        @block.scalar
        def _(act):
            weights(act, "c")
            context_scalar(act)
            for s in stages:
                weights(act, s[0])
                s[3](act)

        @block.gpsimd
        def _(pool):
            weights(pool, "c")
            pool.wait_ge(sem["minus_half"], 1)
            for s in stages:
                weights(pool, s[0])
                s[4](pool)

        @block.sync
        def _(sp):
            sp.dma_start(x_res[:, :, :], dram["x"].rearrange("t p d -> p t d")).then_inc(sem["x_loaded"], 16)
            sp.dma_start(packed["c"][:, :], dram["c"]).then_inc(sem["pack.c"], 16)
            sp.dma_start(ctx_tok, dram["ctx"].rearrange("t p d -> p t d")).then_inc(sem["ctx_loaded"], 16)
            sp.dma_start(packed["0a"][:, :], dram["0a"]).then_inc(sem["pack.0a"], 16)
            for h in range(2):
                sp.dma_start(ctx_keys[64 * h:64 * h + 64, :, :],
                             dram["ctx"].rearrange("t (b k) d -> k (t b) d", b=2)).then_inc(sem["ctx_keys_loaded"], 16)
            for g in packs[2:]:
                if g == "4":
                    for t in range(T):
                        L1F_READY(sp, t)
                sp.dma_start(packed[g][:, :], dram[g]).then_inc(sem["pack." + g], 16)
            for t in range(T):
                stages[-1][5](sp, t)
            sp.dma_start(out.rearrange("t p d -> p t d"), x_res[:, :, :]).then_inc(sem["stored"], 16)
            sp.wait_ge(sem["stored"], 16)



def arrange(inputs):
    import numpy as np

    i = {k: np.asarray(v) for k, v in inputs.items()}
    packs = {}
    where = {}

    def put(pack, name, a):
        a = np.asarray(a)
        assert a.dtype == np.float32, (name, a.dtype)
        cols = packs.setdefault(pack, [])
        at = sum(c.shape[1] for c in cols)
        where[name] = (pack, at, a.shape[0], a.shape[1])
        if a.shape[0] < P:
            a = np.concatenate([a, np.zeros((P - a.shape[0], a.shape[1]), np.float32)], 0)
        cols.append(a)

    pos = np.arange(SEQ)
    feature = np.arange(P)
    put("c", "ident", np.eye(P, dtype=np.float32))
    put("c", "head_mask", (feature[:, None] // 8 == np.arange(16)[None]).astype(np.float32))
    put("c", "head_mask8", (feature[:, None] // 16 == np.arange(8)[None]).astype(np.float32))
    decay = np.exp(-0.01 * np.abs(pos[:, None] - pos[None]).astype(np.float32)) / np.float32(np.sqrt(128))
    put("c", "decay", np.tile(decay.astype(np.float32), (2, 1)))
    put("c", "causal", np.tile(np.where(pos[None] <= pos[:, None], 0, MASKED).astype(np.float32), (2, 1)))
    for w in ("W_k", "W_v", "W_q", "W_down_kv", "W_up_k", "W_up_v", "W_o"):
        put("0a", "L0_attn_" + w, i["L0_attn_" + w])
    for part, rows in (("q", slice(0, 128)), ("k", slice(128, 256)), ("v", slice(256, 384))):
        g = np.zeros((P, 40), np.float32)
        g[:, 0:8] = i["L0_xattn_igate_kernel"][rows]
        g[:, 32:40] = i["L0_xattn_fgate_kernel"][rows]
        put("0x", "l0x.gate_" + part, g)
    g = np.zeros((40, 1), np.float32)
    g[0:8, 0], g[32:40, 0] = i["L0_xattn_igate_bias"], i["L0_xattn_fgate_bias"]
    put("0x", "l0x.gate_bias", g)
    put("0x", "ones8", np.ones((8, 64), np.float32))
    start = np.arange(TOK)[None] % SEQ == 0
    put("0x", "keep", np.tile(np.where(start, 0, 1).astype(np.float32), (8, 1)))
    put("0x", "restart", np.tile(np.where(start, 2 * MASKED, 0).astype(np.float32), (8, 1)))

    def column(v):
        return v.reshape(-1, 1)

    def chunks(v):
        return np.ascontiguousarray(v.reshape(-1, P).T)

    def rows(v):
        return np.broadcast_to(v.reshape(1, -1), (P, v.size))

    f = "L0_ffn_"
    put("0f", f + "enc_W", i[f + "enc_W"])
    put("0f", "l0f.enc_b", chunks(i[f + "enc_b"]))
    for c in range(2):
        put("0f", f"l0f.s2c{c}", i[f + "s2c_W"][128 * c:128 * c + 128])
    put("0f", "l0f.s2c_b", column(i[f + "s2c_b"]))
    put("0f", f + "rW1", i[f + "rW1"])
    put("0f", "l0f.rb1", column(i[f + "rb1"]))
    put("0f", f + "rW2", i[f + "rW2"])
    put("0f", "l0f.rb2", rows(i[f + "rb2"]))
    for e in range(8):
        put("0f", f"l0f.We1_{e}", i[f + "We1"][e])
        put("0f", f"l0f.We2_{e}", i[f + "We2"][e])
    put("0f", "l0f.be1", i[f + "be1"].T)
    put("0f", "l0f.be2", i[f + "be2"].reshape(4, P).T)
    for p in range(4):
        put("0f", f"l0f.pair{p}", (np.arange(8)[:, None] == 2 * p + np.arange(P)[None] // 64).astype(np.float32))
    put("0f", "before", rows((np.arange(8)[None] < np.arange(8)[:, None]).astype(np.float32)))
    put("0f", "l0f.c2s2", np.concatenate([i[f + "c2s_W"]] * 2, 0))
    put("0f", "l0f.c2s_b", chunks(i[f + "c2s_b"]))
    for c in range(2):
        put("0f", f"l0f.dec{c}", i[f + "dec_W"][128 * c:128 * c + 128])
    for b in ("dec_b", "ln_g", "ln_b"):
        put("0f", "l0f." + b, rows(i[f + b]))

    for m in ("r", "w", "k", "v", "a", "g", "out"):
        put("1", "L1_attn_W_" + m, i["L1_attn_W_" + m].T)
    for m in ("r", "w", "k", "v", "a", "g"):
        put("1", "l1a.x_" + m, column(i["L1_attn_x_" + m]))
    put("1", "l1a.gn_w", column(i["L1_attn_gn_w"]))
    put("1", "l1a.gn_b", column(i["L1_attn_gn_b"]))
    put("1", "l1a.b_out", rows(i["L1_attn_b_out"]))
    for m in ("Wq", "Wk", "Wv"):
        put("1", "L1_xattn_" + m, i["L1_xattn_" + m].T)
    put("1", "L1_ffn_W_fc", i["L1_ffn_W_fc"].T)
    for c in range(4):
        put("1", f"l1f.proj{c}", i["L1_ffn_W_proj"].T[128 * c:128 * c + 128])

    angle = pos[:, None].astype(np.float32) * (1.0 / 10000.0 ** (np.arange(4, dtype=np.float32) / 4))[None]
    put("2", "cos8", np.tile(np.cos(angle).astype(np.float32), (2, 2)))
    put("2", "sin8", np.tile(np.concatenate([-np.sin(angle), np.sin(angle)], 1).astype(np.float32), (2, 1)))
    w = i["L2_attn_Wqkv"]
    swapped = np.arange(256).reshape(32, 2, 4)[:, ::-1].reshape(-1)
    put("2", "l2a.qk_rot", np.concatenate([w[:, 0:256], w[:, swapped]], 1))
    put("2", "l2a.Wv", w[:, 256:384])
    put("2", "L2_attn_Wo", i["L2_attn_Wo"])
    put("2", "l2a.bo", rows(i["L2_attn_bo"]))
    for m in ("Wq", "Wk", "Wv", "Wo"):
        put("2", "l2x." + m, i["L2_xattn_" + m].T)
    for m in ("bq", "bk", "bv"):
        put("2", "l2x." + m, column(i["L2_xattn_" + m]))
    put("2", "l2x.bo", rows(i["L2_xattn_bo"]))
    put("2", "l2f.up", i["L2_ffn_w_up"].T)
    put("2", "l2f.down", np.concatenate([i["L2_ffn_w_down"].T[128 * c:128 * c + 128] for c in range(4)], 1))
    put("2", "ones128", np.ones((P, P), np.float32))

    for m in ("WQ", "WK", "WV", "WO"):
        put("3", "l3a." + m, i["L3_attn_" + m].T)
    for m in ("bQ", "bK", "bV"):
        put("3", "l3a." + m, column(i["L3_attn_" + m]))
    put("3", "l3a.bO", rows(i["L3_attn_bO"]))
    rel = i["L3_attn_rel_pos_table"][pos[:, None] - pos[None] + 255]
    rel = rel.transpose(0, 2, 1).reshape(SEQ, -1)
    put("3", "l3a.rel", np.concatenate([rel, rel], 0))
    for m in ("Wq", "Wk", "Wv", "Wo"):
        put("3", "l3x." + m, i["L3_xattn_" + m])
    for m in ("bq", "bk", "bv"):
        put("3", "l3x." + m, column(i["L3_xattn_" + m]))
    put("3", "l3x.bo", rows(i["L3_xattn_bo"]))

    put("4", "l3f.shift", ((feature[:, None] == feature[None] - 1) & (feature[None] % SEQ != 0)).astype(np.float32))
    f = "L3_ffn_"
    half = np.arange(0, 64, 2, dtype=np.float32)
    at = np.arange(SEQ, dtype=np.float32)
    angle = at[:, None] * (1.0 / 10000.0 ** (half / 64))[None]
    power = (at - SEQ // 2) / 32.0
    grow = ((half + 0.4 * 64) / (1.4 * 64))[None] ** power[:, None]
    twice = lambda a: np.concatenate([a, a], 1)
    cos, grow, sin = twice(np.cos(angle)), twice(grow), np.concatenate([-np.sin(angle), np.sin(angle)], 1)
    rope = np.concatenate([cos * grow, cos / grow, sin * grow, sin / grow], 1).astype(np.float32)
    put("4", "l3f.rope", np.tile(rope, (2, 1)))
    other = (np.arange(64) + 32) % 64
    for l in range(2):
        qs, ks = i[f + "q_scale"][l].reshape(-1), i[f + "k_scale"][l].reshape(-1)
        put("4", f"l3f.scale{l}", np.broadcast_to(np.concatenate([qs, ks, qs[other], ks[other]])[None], (P, 256)))
        put("4", f"l3f.wqkv{l}", i[f + "wqkv"][l])
        put("4", f"l3f.wo{l}", np.concatenate([i[f + "wo"][l][128 * c:128 * c + 128] for c in range(4)], 1))
        put("4", f"l3f.ln_g{l}", column(i[f + "ln_g"][l]))
        put("4", f"l3f.ln_b{l}", column(i[f + "ln_b"][l]))
        put("4", f"l3f.w1_{l}", i[f + "w1"][l])

        def padded(v):
            v = v.reshape(341, -1)
            v = np.concatenate([v, np.zeros((384 - 341, v.shape[1]), np.float32)], 0)
            return np.concatenate([v[128 * c:128 * c + 128] for c in range(3)], 1)

        put("4", f"l3f.b1a{l}", padded(i[f + "b1"][l][:341]))
        put("4", f"l3f.b1g{l}", padded(i[f + "b1"][l][341:]))
        put("4", f"l3f.w2_{l}", padded(i[f + "w2"][l]))
        put("4", f"l3f.b2_{l}", rows(i[f + "b2"][l]))
    arrays = {g: np.concatenate(c, 1) for g, c in packs.items()}
    arrays["x"] = i["x"].reshape(T, P, D)
    arrays["ctx"] = i["ctx_1024"].reshape(T, P, D)
    return arrays, where


def kernel(**inputs):
    import numpy as np
    import concourse.bacc as bacc
    from concourse.bass_utils import run_bass_kernel_spmd

    arrays, where = arrange(inputs)
    nc = bacc.Bacc("TRN2", target_bir_lowering=False, num_devices=1)
    dram = {g: nc.dram_tensor("in_" + g, a.shape, F32, kind="ExternalInput").ap() for g, a in arrays.items()}
    out = nc.dram_tensor("out", (T, P, D), F32, kind="ExternalOutput").ap()
    build(nc, dram, where, out)
    r = run_bass_kernel_spmd(nc, [{"in_" + g: a for g, a in arrays.items()}], core_ids=[0])
    return np.asarray(r.results[0]["out"]).reshape(NSEQ, SEQ, D)
```

```python
from contextlib import ExitStack

import concourse.bass as bass
from concourse import mybir

F32 = mybir.dt.float32
ALU = mybir.AluOpType
ACT = mybir.ActivationFunctionType
AX = mybir.AxisListType.X

P = 128
NSEQ, SEQ, D = 16, 64, 128
TOK = NSEQ * SEQ
T = TOK // P
LN_EPS = 1e-5
MASKED = -1e30


STAGES = ("l0a", "l0x", "l0f", "l1a", "l1x", "l1f", "l2a", "l2x", "l2f", "l3a", "l3x", "l3f", "l3g", "l3h")


EARLY = ("0a", "0x", "0f", "1")


def per_stage(**counts):
    return [counts.get(n, counts.get("rest", 0)) for n in STAGES]


SIGNALS = {
    "stats": per_stage(l0f=2 * T, rest=T),
    "moments": per_stage(l0f=2 * T, rest=T),
    "var": per_stage(l0f=T, rest=T // 2),
    "rstd": per_stage(l0f=T, rest=T // 2),
    "xn": per_stage(rest=T),
    "keys_pool": per_stage(l0a=T, l0x=T, l1x=T, l2a=T, l2x=T, l3a=T, l3x=T),
    "keys_dve": per_stage(l0a=T, l0x=T, l1x=T, l2a=T, l3a=T, l3x=T),
    "top": per_stage(l0a=2 * T, l1x=2 * T, l2x=T, l3a=2 * T, l3x=2 * T, l3g=T, l3h=T),
    "rden": per_stage(l0a=T, l1x=T, l2a=T, l2x=T, l3a=T, l3x=T, l3g=T, l3h=T),
    "less": per_stage(l0a=2 * T, l0x=T, l0f=1, l2x=T, l3a=2 * T, l3g=T, l3h=T),
    "exp": per_stage(l0a=2 * T, l0f=1, l1x=2 * T, l2x=T, l3a=2 * T, l3x=2 * T, l3g=T, l3h=T),
    "b_out": per_stage(l0f=1, l1a=1, l2a=1, l2x=1, l3a=1, l3x=1),
}


class PsumBook:

    def __init__(self, rings):
        self.rings = rings
        self.turn = {r: 0 for r in rings}
        self.full = {}
        self.read = {}
        self.record = {}
        self.reads = {}

    def place(self, name, ring, fulls, reads):
        slots = self.rings[ring]
        slot = slots[self.turn[ring] % len(slots)]
        self.turn[ring] += 1
        before, base = self.read.get(slot, 0), self.full.get(slot, 0)
        self.read[slot], self.full[slot] = before + reads, base + fulls
        assert name not in self.record, name
        self.record[name] = (slot, base, fulls, before + reads)
        self.reads[name] = reads
        return slot, before

    def whole(self, name, part=None):
        slot, base, fulls, _ = self.record[name]
        return slot, base + (fulls if part is None else part + 1)

    def done(self, name, part=None):
        slot, _, _, read = self.record[name]
        return slot, read if part is None else read - self.reads[name] + part + 1


def build(nc, dram, where, out):
    with ExitStack() as ctx:
        def sb(name, shape):
            return ctx.enter_context(nc.sbuf_tensor(name, shape, F32))

        class Sems(dict):
            def __missing__(self, name):
                self[name] = ctx.enter_context(nc.semaphore(name.replace(".", "_")))
                return self[name]

        sem = Sems()

        def at(n, part, value):
            counts = SIGNALS[part]
            return sum(counts[:STAGES.index(n)]) + value

        psum = ctx.enter_context(nc.psum_tensor("psum", [P, 8, 512], F32))
        slots = {"a0": psum[:, 0:2, :], "a1": psum[:, 2:4, :], "a2": psum[:, 4:6, :],
                 "b0": psum[:, 6:7, :], "b1": psum[:, 7:8, :]}
        flat = {k: v.rearrange("p a b -> p (a b)") for k, v in slots.items()}
        book = PsumBook({"A": ["a0", "a1", "a2"], "B": ["b0", "b1"]})

        packs = list(dict.fromkeys(w[0] for w in where.values()))
        width = {g: dram[g].shape[1] for g in packs}
        packed = {g: sb("w_" + g, [P, width[g]]) for g in ("c", "2", "3")}
        early = sb("w_early", [P, max(sum(width[g] for g in EARLY), width["4"])])
        for i, g in enumerate(EARLY):
            start = sum(width[h] for h in EARLY[:i])
            packed[g] = early[:, start:start + width[g]]
        packed["4"] = early[:, 0:width["4"]]

        def W(name):
            g, c, rows, cols = where[name]
            return packed[g][0:rows, c:c + cols]

        def W_padded(name):
            g, c, rows, cols = where[name]
            return packed[g][:, c:c + cols]

        def weights(eng, g):
            eng.wait_ge(sem["pack." + g], 16)

        def fill(pe, name, ring="A", fulls=1, reads=1):
            slot, before = book.place(name, ring, fulls, reads)
            if before:
                pe.wait_ge(sem["read." + slot], before)
            return flat[slot]

        def full(name):
            return sem["full." + book.record[name][0]]

        def read(name):
            return sem["read." + book.record[name][0]]

        def wait_full(eng, name, part=None):
            slot, value = book.whole(name, part)
            eng.wait_ge(sem["full." + slot], value)
            return flat[slot]

        def memory(name):
            return flat[book.record[name][0]]

        def wait_read(eng, name, part=None):
            slot, value = book.done(name, part)
            eng.wait_ge(sem["read." + slot], value)

        x_res = sb("x_res", [P, T, D])
        xn = sb("xn", [P, T, D])
        xnT = sb("xnT", [P, TOK])
        ctxT = sb("ctxT", [P, TOK])
        qT = sb("qT", [P, TOK])
        kT = sb("kT", [P, TOK])
        kcT = sb("kcT", [P, TOK])
        keys = [sb(f"keys{i}", [P, 16, P]) for i in range(2)]
        prob = [sb(f"prob{i}", [P, 1024]) for i in range(2)]
        probT = [sb(f"probT{i}", [P, 1024]) for i in range(2)]
        v_self = sb("v_self", [P, NSEQ, 8, 18])
        v_ctx = sb("v_ctx", [P, NSEQ, 8, 18])
        heads_out = [sb(f"heads_out{i}", [P, D]) for i in range(2)]
        attnT = [sb(f"attnT{i}", [P, D]) for i in range(2)]
        bn = sb("bn", [P, T, 6])
        mv = sb("mv", [P, T, 2])
        var_eps = sb("var_eps", [P, T])
        rstd = sb("rstd", [P, T])
        minus_half = sb("minus_half", [P, T])
        plus_half = sb("plus_half", [P, 1])
        top = [sb(f"top{i}", [P, 16]) for i in range(2)]
        rden = [sb(f"rden{i}", [P, 16]) for i in range(2)]

        def halves(mem):
            return [mem[:, 0:512], mem[:, 512:1024]]


        def ln_stats(dve, n, t, src=x_res, before=0):
            nc.vector.bn_stats(bn[:, t, :], src[:, t, :]).then_inc(sem["stats"], 1)
            dve.wait_ge(sem["stats"], at(n, "stats", before + t + 1))
            nc.vector.bn_aggr(mv[:, t, :], bn[:, t, :]).then_inc(sem["moments"], 1)

        def ln_apply(dve, n, t, src=x_res, dst=xn):
            dve.wait_ge(sem["moments"], at(n, "moments", t + 1))
            dve.wait_ge(sem["rstd"], at(n, "rstd", t // 2 + 1))
            nc.vector.tensor_scalar(dst[:, t, :], src[:, t, :], mv[:, t, 0:1], rstd[:, t:t + 1],
                                    ALU.subtract, ALU.mult).then_inc(sem["xn"], 1)

        def ln_vector(dve, n, before, src=x_res, dst=xn):
            for t in range(T + 3):
                if t < T:
                    before(dve, t)
                    ln_stats(dve, n, t, src)
                if t >= 3:
                    ln_apply(dve, n, t - 3, src, dst)

        def ln_pool(pool, n, before=0, tiles=(0, T)):
            for t in range(*tiles, 2):
                two, pair = slice(t, t + 2), (before + t) // 2
                pool.wait_ge(sem["moments"], at(n, "moments", before + t + 2))
                nc.gpsimd.tensor_scalar(var_eps[:, two], mv[:, two, 1], LN_EPS, None, ALU.add).then_inc(sem["var"], 1)
                pool.wait_ge(sem["var"], at(n, "var", pair + 1))
                nc.gpsimd.tensor_tensor(rstd[:, two], var_eps[:, two], minus_half[:, 0:2], ALU.pow).then_inc(sem["rstd"], 1)

        def tiles_T_tensor(pe, name, src, ready, before=0, halves=(0, 1)):
            for half in halves:
                mem = memory(name) if half else fill(pe, name, fulls=2, reads=2)
                for t in range(4 * half, 4 * half + 4):
                    pe.wait_ge(sem[ready], before + t + 1)
                    mm = nc.tensor.transpose(mem[:, t * P:(t + 1) * P], src[:, t, :], W("ident"))
                mm.then_inc(full(name), 1)

        def copy_half_scalar(act, name, dst):
            mem = wait_full(act, name, 0)
            nc.scalar.copy(dst[:, 0:512], mem[:, 0:512]).then_inc(read(name), 1)

        def copy_half_vector(dve, name, dst):
            mem = wait_full(dve, name, 1)
            wait_read(dve, name, 0)
            nc.vector.tensor_copy(dst[:, 512:1024], mem[:, 512:1024]).then_inc(read(name), 1)


        def project_tensor(pe, name, terms, rows=P, reads=2, after=(), halves=(0, 1)):
            for half in halves:
                mem = memory(name) if half else fill(pe, name, fulls=2, reads=reads)
                for product in after:
                    wait_read(pe, product, half)
                for i, (w, src) in enumerate(terms):
                    mm = nc.tensor.matmul(mem[0:rows, 512 * half:512 * half + 512], w, src[:, 512 * half:512 * half + 512],
                                          start=i == 0, stop=i == len(terms) - 1)
                mm.then_inc(full(name), 1)

        def values_tensor(pe, name, w, srcT):
            mem = fill(pe, name, fulls=1, reads=2)
            wp = w.rearrange("p (a h f) -> p h a f", h=2, f=8)
            for b in range(NSEQ):
                for h in range(2):
                    mm = nc.tensor.matmul(mem[64 * h:64 * h + 64, 64 * b:64 * b + 64], srcT[:, 64 * b:64 * b + 64],
                                          wp[:, h], start=True, stop=True)
            mm.then_inc(full(name), 1)

        def values_copy(eng, name, dst, h, relu=False):
            mem = wait_full(eng, name)
            src = mem[64 * h:64 * h + 64, :].rearrange("p (b a f) -> p b a f", b=NSEQ, f=8)
            to = dst[64 * h:64 * h + 64, :, :, 8 * h:8 * h + 8]
            if h == 0:
                nc.scalar.activation(to, src, ACT.Relu if relu else ACT.Copy).then_inc(read(name), 1)
            elif relu:
                nc.vector.tensor_scalar(to, src, 0.0, None, ALU.max).then_inc(read(name), 1)
            else:
                nc.vector.tensor_copy(to, src).then_inc(read(name), 1)


        POOL_HEADS = 10
        MORE_POOL_HEADS = {"plain": 14}

        def spread(eng, ops, a, t, lo, hi, who):
            n, H = a["n"], a["heads"]
            if a["kind"] == "topk":
                lo, hi = (0, 16) if who == "pool" else (0, 0)
                if who == "dve":
                    return
            if a["kind"] in MORE_POOL_HEADS:
                share = MORE_POOL_HEADS[a["kind"]]
                lo, hi = (0, share) if who == "pool" else (share, 16)
            lo, hi = lo * H // 16, hi * H // 16
            if t % 4 == 0:
                a["k_ready"](eng, t // 4)
            if t >= 2:
                wait_full(eng, f"{n}.s{t - 2}")
            elif "before_keys" in a:
                a["before_keys"](eng, t)
            kt = a["k"][:, t * P:(t + 1) * P].rearrange("p (o k) -> p o k", o=1).broadcast_to([P, hi - lo, P])
            mask = W("head_mask" if H == 16 else "head_mask8")[:, lo:hi].rearrange("p (h o) -> p h o", o=1)
            ops.tensor_tensor(keys[t % 2][:, lo:hi, :], kt, mask.broadcast_to([P, hi - lo, P]), ALU.mult)\
               .then_inc(sem["keys_" + who], 1)

        def scores_tensor(pe, a, t, g):
            n = a["n"]
            if t % 4 == 0 and g == 0:
                a["q_ready"](pe, t // 4)
            if g == 0:
                pe.wait_ge(sem["keys_pool"], at(n, "keys_pool", t + 1))
                fill(pe, f"{n}.s{t}", fulls=2, reads=a["parts"])
            if g == 1 and a["kind"] != "topk":
                pe.wait_ge(sem["keys_dve"], at(n, "keys_dve", t + 1))
            mem = memory(f"{n}.s{t}")
            for b in range(2):
                mm = nc.tensor.matmul(mem[64 * b:64 * b + 64, 512 * g:512 * g + 512],
                                      a["q"][:, t * P + 64 * b:t * P + 64 * b + 64],
                                      keys[t % 2][:, 8 * g:8 * g + 8, 64 * b:64 * b + 64], start=True, stop=True)
            mm.then_inc(full(f"{n}.s{t}"), 1)

        def transposes_tensor(pe, a, t, g):
            n = a["n"]
            a["prob_ready"](pe, t, g)
            if g == 0:
                parts = a["heads"] // 8
                fill(pe, f"{n}.t{t}", a.get("t_ring", "A"), fulls=parts, reads=parts)
            mem = memory(f"{n}.t{t}")
            for p in range(4 * g, 4 * g + 4):
                mm = nc.tensor.transpose(mem[:, p * P:(p + 1) * P], prob[t % 2][:, p * P:(p + 1) * P], W("ident"))
            mm.then_inc(full(f"{n}.t{t}"), 1)

        def outputs_tensor(pe, a, t):
            n, pairs = a["n"], a["heads"] // 2
            if t == 0:
                wait_read(pe, n + ".v") if "wv" in a else a["v_ready"](pe)
            wait_read(pe, f"{n}.t{t}")
            w = a["v"].shape[3]
            mem = fill(pe, f"{n}.o{t}", "B")
            for p in range(pairs):
                for b in range(2):
                    mm = nc.tensor.matmul(mem[64 * b:64 * b + 64, w * p:w * p + w],
                                          probT[t % 2][:, p * P + 64 * b:p * P + 64 * b + 64],
                                          a["v"][:, 2 * t + b, p, :], start=True, stop=True)
            mm.then_inc(full(f"{n}.o{t}"), 1)

        def heads_T_tensor(pe, a, t):
            n = a["n"]
            wait_read(pe, f"{n}.o{t}")
            mem = fill(pe, f"{n}.ot{t}", "B")
            nc.tensor.transpose(mem[:, 0:P], heads_out[t % 2][:, :], W("ident")).then_inc(full(f"{n}.ot{t}"), 1)

        def out_tensor(pe, a, t):
            n = a["n"]
            wait_read(pe, f"{n}.ot{t}")
            mem = fill(pe, f"{n}.y{t}", "B")
            nc.tensor.matmul(mem[:, 0:P], attnT[t % 2][:, :], W(a["wo"]), start=True, stop=True)\
              .then_inc(full(f"{n}.y{t}"), 1)

        leads = {}

        def lead(n, engine, step, eng):
            for piece in leads.get((n, engine, step), ()):
                piece(eng)

        def half_ready(name):
            return lambda eng, half: wait_read(eng, name, half)

        def attention_tensor(pe, a):
            for g in range(2):
                scores_tensor(pe, a, 0, g)
            if "wv" in a:
                values_tensor(pe, a["n"] + ".v", a["wv"], xnT)
            whole = a["parts"] == 1
            for t in range(T + 3):
                if t + 1 < T:
                    scores_tensor(pe, a, t + 1, 0)
                    if whole:
                        scores_tensor(pe, a, t + 1, 1)
                if a.get("wo") and t >= 3:
                    out_tensor(pe, a, t - 3)
                if 1 <= t <= T:
                    outputs_tensor(pe, a, t - 1)
                if t < T:
                    transposes_tensor(pe, a, t, 0)
                if t + 1 < T and not whole:
                    scores_tensor(pe, a, t + 1, 1)
                if t < T:
                    transposes_tensor(pe, a, t, 1)
                if a.get("wo") and 2 <= t <= T + 1:
                    heads_T_tensor(pe, a, t - 2)
                lead(a["next"], "tensor", t - T, pe)
                lead(a["n"], "tensor", ("step", t), pe)

        def softmax_vector(dve, a, t):
            n, kind = a["n"], a["kind"]
            s = f"{n}.s{t}"
            three = lambda x: x.rearrange("p (h k) -> p h k", k=SEQ)
            parts = [(g, slice(512 * g, 512 * g + 512), slice(8 * g, 8 * g + 8)) for g in range(2)]
            src = {}
            for g, cols, hs in parts:
                mem = wait_full(dve, s, g)
                if t >= 2:
                    wait_full(dve, f"{n}.t{t - 2}", g)
                pr = prob[t % 2][:, cols]
                src[g] = pr
                if kind == "decay":
                    d = W("decay").rearrange("p (o k) -> p o k", o=1).broadcast_to([P, 8, SEQ])
                    nc.vector.tensor_tensor(three(pr), three(mem[:, cols]), d, ALU.mult).then_inc(read(s), 1)
                elif kind == "bias":
                    nc.vector.scalar_tensor_tensor(out=pr, in0=mem[:, cols], scalar=a["scale"],
                                                   in1=rel_bias[:, cols], op0=ALU.mult, op1=ALU.add).then_inc(read(s), 1)
                else:
                    src[g] = mem[:, cols]
            if t >= 2:
                a["less_done"](dve, t - 2, 1)
            for g, cols, hs in parts:
                if kind != "plain":
                    wait_read(dve, s, g)
                nc.vector.tensor_reduce(top[t % 2][:, hs], three(src[g]), AX, ALU.max).then_inc(sem["top"], 1)
            if kind == "plain":
                for g, cols, hs in parts:
                    dve.wait_ge(sem["top"], at(n, "top", 2 * t + g + 1))
                    tb = top[t % 2][:, hs].rearrange("p (h o) -> p h o", o=1).broadcast_to([P, 8, SEQ])
                    nc.vector.tensor_tensor(three(prob[t % 2][:, cols]), three(src[g]), tb, ALU.subtract).then_inc(read(s), 1)

        def less_pool(pool, a, t):
            n = a["n"]
            for g in range(2):
                cols, hs = slice(512 * g, 512 * g + 512), slice(8 * g, 8 * g + 8)
                pool.wait_ge(sem["top"], at(n, "top", 2 * t + g + 1))
                pr = prob[t % 2][:, cols].rearrange("p (h k) -> p h k", k=SEQ)
                tb = top[t % 2][:, hs].rearrange("p (h o) -> p h o", o=1).broadcast_to([P, 8, SEQ])
                nc.gpsimd.tensor_tensor(pr, pr, tb, ALU.subtract).then_inc(sem["less"], 1)

        def normalise_vector(dve, a, t):
            n, pairs = a["n"], a["heads"] // 2
            o = f"{n}.o{t}"
            mem = wait_full(dve, o)
            v = mem[:, 0:18 * pairs].rearrange("p (a w) -> p a w", w=18)
            rd = rden[t % 2][:, :].rearrange("p (a h) -> p a h", h=2)
            if t >= 2:
                wait_read(dve, f"{n}.o{t - 2}")
                if a.get("wo"):
                    wait_full(dve, f"{n}.ot{t - 2}")
            nc.vector.reciprocal(rd, v[:, :, 16:18]).then_inc(sem["rden"], 1)
            dve.wait_ge(sem["rden"], at(n, "rden", t + 1))
            ho = heads_out[t % 2][:, :].rearrange("p (a h f) -> p a h f", h=2, f=8)
            num = v[:, :, 0:16].rearrange("p a (h f) -> p a h f", h=2)
            rb = rd.rearrange("p a (h o) -> p a h o", o=1).broadcast_to([P, pairs, 2, 8])
            nc.vector.tensor_tensor(ho, num, rb, ALU.mult).then_inc(read(o), 1)
            if not a.get("wo"):
                wait_read(dve, o)
                nc.vector.tensor_tensor(x_res[:, t, :], x_res[:, t, :], heads_out[t % 2][:, :], ALU.add)\
                  .then_inc(sem[n + ".x"], 1)
                dve.wait_ge(sem[n + ".x"], t + 1)

        def residual_vector(dve, a, t):
            y = f"{a['n']}.y{t}"
            mem = wait_full(dve, y)
            if a.get("bo") and t == 0:
                dve.wait_ge(sem["b_out"], at(a["n"], "b_out", 1))
            nc.vector.tensor_tensor(x_res[:, t, :], mem[:, 0:P], x_res[:, t, :], ALU.add).then_inc(read(y), 1)

        def attention_vector(dve, a):
            nxt = a["next"]
            lag = 3 if a.get("wo") else 1
            if not a.get("spread_early"):
                spread(dve, nc.vector, a, 0, POOL_HEADS, 16, "dve")
            spread(dve, nc.vector, a, 1, POOL_HEADS, 16, "dve")
            for t in range(T + 3):
                if t < T:
                    a.get("softmax", softmax_vector)(dve, a, t)
                if t == 0 and "wv" in a:
                    values_copy(dve, a["n"] + ".v", a["v"], 1)
                if 1 <= t <= T:
                    a.get("normalise", normalise_vector)(dve, a, t - 1)
                if a.get("wo") and t >= 3:
                    residual_vector(dve, a, t - 3)
                if lag <= t < T + lag:
                    residual_ready(a)(dve, t - lag)
                    ln_stats(dve, nxt, t - lag)
                first = T - 2 if a["kind"] in ("plain", "unit") else T
                if t >= first:
                    for u in range(0 if t == first else t - lag - 1, min(t - lag, T)):
                        ln_apply(dve, nxt, u)
                if t + 2 < T:
                    spread(dve, nc.vector, a, t + 2, POOL_HEADS, 16, "dve")
                lead(nxt, "vector", t - T, dve)
                lead(a["n"], "vector", ("step", t), dve)
            for u in range(T + 2 - lag, T):
                ln_apply(dve, nxt, u)

        def exp_scalar(act, a, t, g):
            n = a["n"]
            w = 1024 // a["parts"]
            cols = slice(w * g, w * g + w)
            a["less_done"](act, t, g)
            if a["kind"] == "unit":
                if t >= 2:
                    wait_full(act, f"{n}.t{t - 2}", g)
                mem = wait_full(act, f"{n}.s{t}", g)
                nc.scalar.activation(prob[t % 2][:, cols], mem[:, cols], ACT.Exp, scale=a["scale"]).then_inc(read(f"{n}.s{t}"), 1)
            else:
                nc.scalar.activation(prob[t % 2][:, cols], prob[t % 2][:, cols], ACT.Exp,
                                     scale=1.0 if a["kind"] in ("decay", "bias") else a["scale"]).then_inc(sem["exp"], 1)

        def attention_scalar(act, a):
            n = a["n"]
            for t in range(T + 3):
                if a.get("copy") and t == 0:
                    a["copy"](act, a, 0)
                if a.get("copy") and t + 1 < T:
                    a["copy"](act, a, t + 1)
                if t < T:
                    for g in range(a["parts"]):
                        exp_scalar(act, a, t, g)
                    if t == 0 and "wv" in a:
                        values_copy(act, a["n"] + ".v", a["v"], 0)
                    if t >= 2:
                        wait_full(act, f"{n}.o{t - 2}")
                    for g in range(2):
                        mem = wait_full(act, f"{n}.t{t}", g)
                        nc.scalar.copy(probT[t % 2][:, 512 * g:512 * g + 512], mem[:, 512 * g:512 * g + 512])\
                          .then_inc(read(f"{n}.t{t}"), 1)
                if a.get("wo") and 2 <= t <= T + 1:
                    u = t - 2
                    if u >= 2:
                        wait_full(act, f"{n}.y{u - 2}")
                    mem = wait_full(act, f"{n}.ot{u}")
                    if a.get("bv"):
                        nc.scalar.activation(attnT[u % 2][:, :], mem[:, 0:P], ACT.Identity, bias=W(a["bv"]))\
                          .then_inc(read(f"{n}.ot{u}"), 1)
                    else:
                        nc.scalar.copy(attnT[u % 2][:, :], mem[:, 0:P]).then_inc(read(f"{n}.ot{u}"), 1)
                lead(a["next"], "scalar", t - T, act)
                lead(a["n"], "scalar", ("step", t), act)

        def attention_pool(pool, a, first=0):
            for t in range(first - 2, T):
                if t >= 0 and a["kind"] in ("decay", "bias"):
                    less_pool(pool, a, t)
                if t + 2 < T:
                    spread(pool, nc.gpsimd, a, t + 2, 0, POOL_HEADS, "pool")
                if t == -1 and a.get("bo"):
                    add_bias_pool(pool, a["n"], a["bo"])

        def residual_ready(a):
            if a.get("wo"):
                return lambda eng, t: wait_read(eng, f"{a['n']}.y{t}")
            return lambda eng, t: eng.wait_ge(sem[a["n"] + ".x"], t + 1)

        def attention(n, kind, scale=1.0, heads=16, **more):
            a = dict(n=n, kind=kind, scale=scale, heads=heads, parts=2, next=STAGES[STAGES.index(n) + 1], **more)
            if kind == "plain":
                a["less_done"] = lambda eng, t, g: wait_read(eng, f"{n}.s{t}", g)
            elif kind == "unit":
                a["less_done"] = lambda eng, t, g: None
            elif kind == "topk":
                a["parts"] = 1
                a["less_done"] = lambda eng, t, g: eng.wait_ge(sem["less"], at(n, "less", t + 1))
            else:
                a["less_done"] = lambda eng, t, g: eng.wait_ge(sem["less"], at(n, "less", 2 * t + g + 1))
            if kind == "unit":
                a["prob_ready"] = lambda eng, t, g: wait_read(eng, f"{n}.s{t}", g)
            else:
                a["prob_ready"] = lambda eng, t, g: eng.wait_ge(sem["exp"], at(n, "exp", 2 * t + g + 1))
            return a


        VALUES_SET = 12
        L0A = attention("l0a", "decay", wo="L0_attn_W_o", q=qT, k=kT, v=v_self,
                        before_keys=lambda eng, t: eng.wait_ge(sem["lstm_values"], 2),
                        q_ready=half_ready("l0a.q"), k_ready=half_ready("l0a.k"),
                        v_ready=lambda eng: wait_read(eng, "l0a.v"))
        scr = sb("scratch", [P, 12, 1024])
        kvT, lat_all = scr[:, 0, :], scr[:, 8, :]
        latT = lat_all[0:32]

        def l0a_tensor(pe):
            n = "l0a"
            tiles_T_tensor(pe, n + ".T", xn, "xn", at(n, "xn", 0))
            project_tensor(pe, n + ".kv", [(W("L0_attn_W_k"), xnT), (W("L0_attn_W_v"), xnT)], after=[n + ".T"])
            project_tensor(pe, n + ".q", [(W("L0_attn_W_q"), xnT)])
            project_tensor(pe, n + ".lat", [(W("L0_attn_W_down_kv"), kvT)], rows=32, after=[n + ".kv"])
            pe.wait_ge(sem["latent_padded"], 1)
            project_tensor(pe, n + ".k", [(W_padded("L0_attn_W_up_k"), lat_all)], after=[n + ".lat"])
            values_tensor(pe, n + ".v", W_padded("L0_attn_W_up_v"), lat_all)
            attention_tensor(pe, L0A)

        def blocks_vector(v, name):
            w = v.shape[3] // 2 - 1
            for p0, lo, hi, value in ((0, w, 2 * w, 0.0), (0, 2 * w, 2 * w + 1, 1.0), (0, 2 * w + 1, 2 * w + 2, 0.0),
                                      (64, 0, w, 0.0), (64, 2 * w, 2 * w + 1, 0.0), (64, 2 * w + 1, 2 * w + 2, 1.0)):
                nc.vector.memset(v[p0:p0 + 64, :, :, lo:hi], value).then_inc(sem[name], 1)

        def l0a_vector(dve):
            n = "l0a"
            blocks_vector(v_lstm, "lstm_values_set")
            nc.vector.memset(lstm[:, 3, :], 0.0).then_inc(sem["lstm_values_set"], 1)
            dve.wait_ge(sem["x_loaded"], 16)
            ln_vector(dve, n, lambda eng, t: None)
            weights(dve, "c")
            context_vector(dve)
            copy_half_vector(dve, n + ".T", xnT)
            copy_half_vector(dve, n + ".kv", kvT)
            blocks_vector(v_self, "values_set")
            copy_half_vector(dve, n + ".q", qT)
            mem = wait_full(dve, n + ".lat", 1)
            dve.wait_ge(sem["latent_padded"], 1)
            wait_read(dve, n + ".lat", 0)
            nc.vector.tensor_copy(latT[:, 512:], mem[0:32, 512:]).then_inc(read(n + ".lat"), 1)
            copy_half_vector(dve, n + ".k", kT)
            dve.wait_ge(sem["values_set"], VALUES_SET // 2)
            values_copy(dve, n + ".v", v_self, 1)
            attention_vector(dve, L0A)

        def l0a_scalar(act):
            n = "l0a"
            copy_half_scalar(act, n + ".T", xnT)
            copy_half_scalar(act, n + ".kv", kvT)
            copy_half_scalar(act, n + ".q", qT)
            lstm_values_scalar(act)
            mem = wait_full(act, n + ".lat", 0)
            act.wait_ge(sem["latent_padded"], 1)
            nc.scalar.copy(latT[:, 0:512], mem[0:32, 0:512]).then_inc(read(n + ".lat"), 1)
            copy_half_scalar(act, n + ".k", kT)
            act.wait_ge(sem["values_set"], VALUES_SET // 2)
            values_copy(act, n + ".v", v_self, 0)
            attention_scalar(act, L0A)

        def l0a_pool(pool):
            nc.gpsimd.memset(lat_all, 0.0).then_inc(sem["latent_padded"], 1)
            nc.gpsimd.memset(scr[:, 6:8, :], 0.0).then_inc(sem["gates_padded"], 1)
            ln_pool(pool, "l0a")
            weights(pool, "c")
            attention_pool(pool, L0A)



        links = {}

        def link(eng, name, ins):
            links[name] = links.get(name, 0) + 1
            ins.then_inc(sem[name], 1)
            eng.wait_ge(sem[name], links[name])

        newton_t = sb("newton_t", [P, 256])
        newton_u = sb("newton_u", [P, 256])

        def rsqrt_vector(dve, n, x, y, w):
            t, u = newton_t[:, 0:w], newton_u[:, 0:w]
            U32, I32 = mybir.dt.uint32, mybir.dt.int32
            link(dve, n, nc.vector.tensor_scalar(t.bitcast(U32), x.bitcast(U32), 1, None, ALU.logical_shift_right))
            link(dve, n, nc.vector.tensor_scalar(y.bitcast(I32), t.bitcast(I32), -1.0, float(0x5F3759DF), ALU.mult, ALU.add))
            for _ in range(3):
                link(dve, n, nc.vector.tensor_tensor(t, y, y, ALU.mult))
                link(dve, n, nc.vector.scalar_tensor_tensor(out=u, in0=t, scalar=-0.5, in1=x, op0=ALU.mult, op1=ALU.mult))
                link(dve, n, nc.vector.scalar_tensor_tensor(out=y, in0=u, scalar=1.5, in1=y, op0=ALU.add, op1=ALU.mult))


        ctx_tok = scr[:, 11, :].rearrange("p (t d) -> p t d", t=T)
        ctx_keys = keys[0]
        v_lstm = sb("v_lstm", [P, NSEQ, 4, 34])

        def context_tensor(pe):
            pe.wait_ge(sem["ctx_loaded"], 16)
            mem = fill(pe, "ctx.T", fulls=2, reads=2)
            for t in range(T):
                mm = nc.tensor.transpose(mem[:, t * P:(t + 1) * P], ctx_tok[:, t, :], W("ident"))
                if t % 4 == 3:
                    mm.then_inc(full("ctx.T"), 1)

        def context_vector(dve):
            copy_half_vector(dve, "ctx.T", ctxT)

        def context_scalar(act):
            copy_half_scalar(act, "ctx.T", ctxT)

        def lstm_values_scalar(act):
            act.wait_ge(sem["ctx_keys_loaded"], 32)
            act.wait_ge(sem["lstm_values_set"], 6)
            for h in range(2):
                rows = slice(64 * h, 64 * h + 64)
                src = ctx_keys[rows, :, :].rearrange("p b (a h f) -> p b a h f", h=2, f=16)[:, :, :, h]
                nc.scalar.copy(v_lstm[rows, :, :, 16 * h:16 * h + 16], src).then_inc(sem["lstm_values"], 1)


        gate = scr[0:40, 5, :]
        lstm = scr[0:40, 1:5, :]
        spread_all = [scr[:, 6 + i, :].rearrange("p (h k) -> p h k", h=8) for i in range(2)]
        spread_b = [s[0:8] for s in spread_all]
        tok_gate = sb("tok_gate", [P, T, 40])
        least = sb("least", [P, T, 8])
        lstm_out = xn
        ms = sb("ms", [P, 64])
        rms = sb("rms", [P, 64])
        L0X = attention("l0x", "mlstm", heads=8, t_ring="B", q=xnT, k=ctxT, v=v_lstm,
                        q_ready=half_ready("l0x.T"), k_ready=half_ready("ctx.T"),
                        v_ready=lambda eng: eng.wait_ge(sem["lstm_values"], 2),
                        before_keys=lambda eng, t: wait_full(eng, f"l0a.s{6 + t}"))

        L0X["prob_ready"] = lambda eng, t, g: wait_read(eng, f"l0x.s{t}")

        def first_half_T(n):
            leads[n, "tensor", 0] = [lambda pe: tiles_T_tensor(pe, n + ".T", xn, "xn", at(n, "xn", 0), halves=(0,))]
            leads[n, "scalar", 0] = [lambda act: copy_half_scalar(act, n + ".T", xnT)]

        def second_half_T(pe, n):
            tiles_T_tensor(pe, n + ".T", xn, "xn", at(n, "xn", 0), halves=(1,))

        first_half_T("l0x")

        def l0x_tensor(pe):
            n = "l0x"
            mem = fill(pe, n + ".gate", fulls=2, reads=1)
            parts = ((W("l0x.gate_k"), ctxT), (W("l0x.gate_v"), ctxT), (W("l0x.gate_q"), xnT))
            for i, (w, src) in enumerate(parts):
                if i == 2:
                    second_half_T(pe, n)
                for half in range(2):
                    if i == 2:
                        wait_read(pe, n + ".T", half)
                    s = slice(512 * half, 512 * half + 512)
                    mm = nc.tensor.matmul(mem[0:40, s], w, src[:, s], start=i == 0, stop=i == 2)
                    if i == 2:
                        mm.then_inc(full(n + ".gate"), 1)
            mem = fill(pe, n + ".gateT")
            pe.wait_ge(sem[n + ".gates"], 1)
            for t in range(T):
                mm = nc.tensor.transpose(mem[:, 40 * t:40 * t + 40], lstm[:, 3, t * P:(t + 1) * P], W("ident")[0:40, 0:40])
            mm.then_inc(full(n + ".gateT"), 1)

            def scores(t):
                pe.wait_ge(sem["keys_pool"], at(n, "keys_pool", t + 1))
                pe.wait_ge(sem["keys_dve"], at(n, "keys_dve", t + 1))
                pe.wait_ge(sem[n + ".spread_b"], t + 1)
                pe.wait_ge(sem["gates_padded"], 1)
                mem = fill(pe, f"{n}.s{t}")
                for b in range(2):
                    nc.tensor.matmul(mem[64 * b:64 * b + 64, 0:512], xnT[:, t * P + 64 * b:t * P + 64 * b + 64],
                                     keys[t % 2][:, 0:8, 64 * b:64 * b + 64], start=True, stop=True)
                for b in range(2):
                    mm = nc.tensor.matmul(mem[64 * b:64 * b + 64, 512:1024], W_padded("ones8"),
                                          spread_all[t % 2][:, :, 64 * b:64 * b + 64], start=True, stop=True)
                mm.then_inc(full(f"{n}.s{t}"), 1)

            scores(0)
            for t in range(T + 2):
                if t + 1 < T:
                    scores(t + 1)
                if t >= 2:
                    outputs_tensor(pe, L0X, t - 2)
                if 1 <= t <= T:
                    transposes_tensor(pe, L0X, t - 1, 0)

        def l0x_vector(dve):
            n = "l0x"
            lf, cs, gb, M = (lstm[0:8, i, :] for i in range(4))
            copy_half_vector(dve, n + ".T", xnT)
            blocks_vector(v_ctx, "values_set")
            dve.wait_ge(sem[n + ".softplus"], 3)
            link(dve, "vector_chain", nc.vector.scalar_tensor_tensor(out=lf, in0=gate[32:40, :], scalar=0.0, in1=lstm[32:40, 1, :],
                                                               op0=ALU.min, op1=ALU.subtract))
            link(dve, "vector_chain", nc.vector.tensor_tensor_scan(cs, W("keep"), lf, 0.0, ALU.mult, ALU.add))
            link(dve, "vector_chain", nc.vector.tensor_tensor(gb, gate[0:8, :], cs, ALU.subtract))
            dve.sem_inc(sem[n + ".gb"], 1)
            link(dve, "vector_chain", nc.vector.tensor_tensor_scan(M, W("restart"), gb, MASKED, ALU.add, ALU.max))
            dve.wait_ge(sem["lstm_values_set"], 7)
            nc.vector.tensor_tensor(lstm[32:40, 3, :], M, cs, ALU.add).then_inc(sem[n + ".gates"], 1)
            mem = wait_full(dve, n + ".gateT")
            nc.vector.tensor_copy(tok_gate[:, :, :], mem[:, 0:320].rearrange("p (t g) -> p t g", t=T)).then_inc(read(n + ".gateT"), 1)
            wait_read(dve, n + ".gateT")

            three = lambda x: x.rearrange("p (h k) -> p h k", k=SEQ)

            def weigh(t):
                mem = wait_full(dve, f"{n}.s{t}")
                if t >= 2:
                    wait_read(dve, f"{n}.s{t - 2}")
                    wait_full(dve, f"{n}.t{t - 2}")
                d = three(prob[t % 2][:, 512:1024])
                m = tok_gate[:, t, 0:8].rearrange("p (h o) -> p h o", o=1).broadcast_to([P, 8, SEQ])
                link(dve, "vector_chain", nc.vector.tensor_tensor(d, three(mem[:, 512:1024]), m, ALU.subtract))
                c = W("causal").rearrange("p (o k) -> p o k", o=1).broadcast_to([P, 8, SEQ])
                nc.vector.tensor_tensor(d, d, c, ALU.add).then_inc(sem["less"], 1)

            def combine(t):
                dve.wait_ge(sem[n + ".weight"], t + 1)
                mem = flat[book.record[f"{n}.s{t}"][0]]
                nc.vector.scalar_tensor_tensor(out=prob[t % 2][:, 0:512], in0=mem[:, 0:512], scalar=0.25,
                                               in1=prob[t % 2][:, 512:1024], op0=ALU.mult, op1=ALU.mult)\
                  .then_inc(read(f"{n}.s{t}"), 1)

            def normalise(t):
                mem = wait_full(dve, f"{n}.o{t}")
                v = mem[:, 0:136].rearrange("p (a w) -> p a w", w=34)
                rd = rden[t % 2][:, 0:8].rearrange("p (a h) -> p a h", h=2)
                lt = least[:, t, :].rearrange("p (a h) -> p a h", h=2)
                if t == 0:
                    dve.wait_ge(sem[n + ".least"], 1)
                link(dve, "vector_chain", nc.vector.tensor_scalar(rd, v[:, :, 32:34], -1.0, None, ALU.mult))
                link(dve, "vector_chain", nc.vector.tensor_tensor(rd, rd, v[:, :, 32:34], ALU.max))
                link(dve, "vector_chain", nc.vector.tensor_tensor(rd, rd, lt, ALU.max))
                link(dve, "vector_chain", nc.vector.tensor_scalar(rd, rd, 1e-6, None, ALU.add))
                link(dve, "vector_chain", nc.vector.reciprocal(rd, rd))
                ho = lstm_out[:, t, :].rearrange("p (a h f) -> p a h f", h=2, f=16)
                num = v[:, :, 0:32].rearrange("p a (h f) -> p a h f", h=2)
                rb = rd.rearrange("p a (h o) -> p a h o", o=1).broadcast_to([P, 4, 2, 16])
                nc.vector.tensor_tensor(ho, num, rb, ALU.mult).then_inc(read(f"{n}.o{t}"), 1)

            GROUPS = 8 * T // 2

            def mean_square(half):
                g = slice(GROUPS * half, GROUPS * half + GROUPS)
                dve.wait_ge(sem[n + ".square"], half + 1)
                sq = scr[:, 0, 512 * half:512 * half + 512].rearrange("p (g f) -> p g f", f=16)
                link(dve, "vector_chain", nc.vector.tensor_reduce(ms[:, g], sq, AX, ALU.add))
                nc.vector.tensor_scalar(ms[:, g], ms[:, g], 1.0 / 16, 1e-6, ALU.mult, ALU.add).then_inc(sem[n + ".mean_square"], 1)
                if half == 1:
                    dve.wait_ge(sem[n + ".mean_square"], 2)
                    rsqrt_vector(dve, "vector_chain", ms[:, g], rms[:, g], GROUPS)

            def onto_residual(half):
                if half == 0:
                    dve.wait_ge(sem[n + ".root"], 1)
                four = slice(4 * half, 4 * half + 4)
                lo = lstm_out[:, four, :].rearrange("p t (h f) -> p (t h) f", f=16)
                rb = rms[:, GROUPS * half:GROUPS * half + GROUPS].rearrange("p (g o) -> p g o", o=1).broadcast_to([P, GROUPS, 16])
                link(dve, "vector_chain", nc.vector.tensor_tensor(lo, lo, rb, ALU.mult))
                for t in range(4 * half, 4 * half + 4):
                    nc.vector.tensor_tensor(x_res[:, t, :], x_res[:, t, :], lstm_out[:, t, :], ALU.add).then_inc(sem[n + ".x"], 1)

            spread(dve, nc.vector, L0X, 0, POOL_HEADS, 16, "dve")
            spread(dve, nc.vector, L0X, 1, POOL_HEADS, 16, "dve")
            for t in range(T + 4):
                if 1 <= t <= T:
                    combine(t - 1)
                if 3 <= t <= T + 2:
                    normalise(t - 3)
                if t == T:
                    mean_square(0)
                if t < T:
                    weigh(t)
                if t + 2 < T:
                    spread(dve, nc.vector, L0X, t + 2, POOL_HEADS, 16, "dve")
            onto_residual(0)
            mean_square(1)
            onto_residual(1)

        def l0x_scalar(act):
            n = "l0x"
            mem = wait_full(act, n + ".gate")
            nc.scalar.activation(gate[:, :], mem[0:40, :], ACT.Identity, bias=W("l0x.gate_bias")).then_inc(read(n + ".gate"), 1)
            wait_read(act, n + ".gate")
            for i, (to, src, f, more) in enumerate(((0, gate[32:40, :], ACT.Abs, {}),
                                                    (0, lstm[32:40, 0, :], ACT.Exp, dict(scale=-1.0)),
                                                    (1, lstm[32:40, 0, :], ACT.Ln, dict(bias=1.0)))):
                nc.scalar.activation(lstm[32:40, to, :], src, f, **more).then_inc(sem[n + ".softplus"], 1)
                act.wait_ge(sem[n + ".softplus"], i + 1)
            wait_read(act, n + ".gateT")
            nc.scalar.activation(least[:, :, :], tok_gate[:, :, 32:40], ACT.Exp, scale=-1.0).then_inc(sem[n + ".least"], 1)
            def square(half):
                wait_read(act, f"{n}.o{4 * half + 3}")
                wait_read(act, f"{n}.o{4 * half + 2}")
                nc.scalar.activation(scr[:, 0, 512 * half:512 * half + 512],
                                     lstm_out[:, 4 * half:4 * half + 4, :].rearrange("p t d -> p (t d)"), ACT.Square)\
                  .then_inc(sem[n + ".square"], 1)

            for t in range(T + 2):
                if t == T:
                    square(0)
                if t < T:
                    act.wait_ge(sem["less"], at(n, "less", t + 1))
                    nc.scalar.activation(prob[t % 2][:, 512:1024], prob[t % 2][:, 512:1024], ACT.Exp)\
                       .then_inc(sem[n + ".weight"], 1)
                if t >= 2:
                    u = t - 2
                    if u >= 2:
                        wait_full(act, f"{n}.o{u - 2}")
                    mem = wait_full(act, f"{n}.t{u}")
                    nc.scalar.copy(probT[u % 2][:, 0:512], mem[:, 0:512]).then_inc(read(f"{n}.t{u}"), 1)
            square(1)

        def l0x_pool(pool):
            n = "l0x"
            ln_pool(pool, n)
            for t in range(T):
                spread(pool, nc.gpsimd, L0X, t, 0, POOL_HEADS, "pool")
                if t == 0:
                    pool.wait_ge(sem[n + ".gb"], 1)
                    pool.wait_ge(sem["gates_padded"], 1)
                if t >= 2:
                    wait_full(pool, f"{n}.s{t - 2}")
                b = lstm[0:8, 2, t * P:(t + 1) * P].rearrange("p (o k) -> p o k", o=1).broadcast_to([8, 8, P])
                e = W("ident")[0:8, 0:8].rearrange("p (h o) -> p h o", o=1).broadcast_to([8, 8, P])
                nc.gpsimd.tensor_tensor(spread_b[t % 2][:, :, :], b, e, ALU.mult).then_inc(sem[n + ".spread_b"], 1)
            pool.wait_ge(sem[n + ".mean_square"], 1)
            nc.gpsimd.tensor_tensor(rms[:, 0:4 * T], ms[:, 0:4 * T], minus_half[:, 0:1].broadcast_to([P, 4 * T]), ALU.pow)\
              .then_inc(sem[n + ".root"], 1)



        NE, M = 8, 64
        contT, r1T = scr[0:M, 0, :], scr[0:M, 1, :]
        spike = [scr[:, 2, :], scr[:, 3, :]]
        hidden = [scr[:, 4, :], scr[:, 5, :]]
        gate_rep = [scr[:, 6, :], scr[:, 7, :]]
        gated, moe = scr[:, 8, :], scr[:, 9, :]
        gT = scr[0:NE, 10, :]
        cont_all, r1_all, g_all = scr[:, 0, :], scr[:, 1, :], scr[:, 10, :]
        logit = sb("logit", [P, T, NE])
        pick = sb("pick", [P, T, NE])
        best = sb("best", [P, T, 1])
        tie = prob[0][:, :].rearrange("p (w t e f) -> p w t e f", w=2, t=T, e=NE)

        def tok_bias(name, tiles=T):
            return W(name).rearrange("p (o d) -> p o d", o=1).broadcast_to([P, tiles, W(name).shape[1]])

        def l0f_tensor(pe):
            n = "l0f"
            tiles_T_tensor(pe, n + ".T", xn, "xn", at(n, "xn", 0))
            for c in range(2):
                project_tensor(pe, f"{n}.enc{c}", [(W("L0_ffn_enc_W")[:, 128 * c:128 * c + 128], xnT)], after=[n + ".T"])
            project_tensor(pe, n + ".cont", [(W(f"l0f.s2c{c}"), spike[c]) for c in range(2)], rows=M,
                           after=[n + ".enc0", n + ".enc1"])
            pe.wait_ge(sem[n + ".padded"], 3)
            project_tensor(pe, n + ".r1", [(W_padded("L0_ffn_rW1"), cont_all)], rows=M, after=[n + ".cont"])
            for e in range(2):
                project_tensor(pe, f"{n}.h{e}", [(W_padded(f"l0f.We1_{e}"), cont_all)])
            wait_read(pe, n + ".r1")
            mem = fill(pe, n + ".logit")
            for t in range(T):
                mm = nc.tensor.matmul(mem[:, NE * t:NE * t + NE], r1_all[:, t * P:(t + 1) * P], W_padded("L0_ffn_rW2"),
                                      start=True, stop=True)
            mm.then_inc(full(n + ".logit"), 1)

            def outputs(p):
                mem = fill(pe, f"{n}.eo{p}")
                for half in range(2):
                    for e in range(2):
                        mm = nc.tensor.matmul(mem[64 * e:64 * e + 64, 512 * half:512 * half + 512], W(f"l0f.We2_{2 * p + e}"),
                                              hidden[e][:, 512 * half:512 * half + 512], start=True, stop=True)
                mm.then_inc(full(f"{n}.eo{p}"), 1)

            for p in range(NE // 2):
                if p:
                    for e in (2 * p, 2 * p + 1):
                        project_tensor(pe, f"{n}.h{e}", [(W_padded(f"l0f.We1_{e}"), cont_all)])
                if p == 0:
                    wait_read(pe, n + ".h0")
                    wait_read(pe, n + ".h1")
                    outputs(p)
                    pe.wait_ge(sem[n + ".gates"], 1)
                    mem = fill(pe, n + ".gT")
                    for t in range(T):
                        mm = nc.tensor.transpose(mem[0:NE, t * P:(t + 1) * P], pick[:, t, :], W("ident"))
                    mm.then_inc(full(n + ".gT"), 1)
                    wait_read(pe, n + ".gT")
                project_tensor(pe, f"{n}.rep{p}", [(W_padded(f"l0f.pair{p}"), g_all)])
                if p:
                    wait_read(pe, f"{n}.h{2 * p}")
                    wait_read(pe, f"{n}.h{2 * p + 1}")
                    outputs(p)
            pe.wait_ge(sem[n + ".moe"], 4)
            for c in range(2):
                project_tensor(pe, f"{n}.c2s{c}", [(W("l0f.c2s2")[:, 128 * c:128 * c + 128], moe)])
            mem = fill(pe, n + ".dec", fulls=2, reads=2)
            for t in range(T):
                if t % 4 == 0:
                    wait_read(pe, n + ".c2s0", t // 4)
                    wait_read(pe, n + ".c2s1", t // 4)
                for c in range(2):
                    mm = nc.tensor.matmul(mem[:, t * P:(t + 1) * P], spike[c][:, t * P:(t + 1) * P], W(f"l0f.dec{c}"),
                                          start=c == 0, stop=c == 1)
                if t % 4 == 3:
                    mm.then_inc(full(n + ".dec"), 1)

        def l0f_scalar(act):
            n = "l0f"
            copy_half_scalar(act, n + ".T", xnT)
            act.wait_ge(sem[n + ".padded"], 3)
            for c in range(2):
                for half in range(2):
                    mem = wait_full(act, f"{n}.enc{c}", half)
                    s = slice(512 * half, 512 * half + 512)
                    nc.scalar.activation(spike[c][:, s], mem[:, s], ACT.Sigmoid, bias=W("l0f.enc_b")[:, c:c + 1])\
                      .then_inc(read(f"{n}.enc{c}"), 1)
            mem = wait_full(act, n + ".cont", 0)
            nc.scalar.activation(contT[:, 0:512], mem[0:M, 0:512], ACT.Identity, bias=W("l0f.s2c_b")).then_inc(read(n + ".cont"), 1)
            for half in range(2):
                mem = wait_full(act, n + ".r1", half)
                s = slice(512 * half, 512 * half + 512)
                nc.scalar.activation(r1T[:, s], mem[0:M, s], ACT.Tanh, bias=W("l0f.rb1")).then_inc(read(n + ".r1"), 1)

            def hidden_relu(e):
                mem = wait_full(act, f"{n}.h{e}", 0)
                if e >= 2:
                    wait_full(act, f"{n}.eo{e // 2 - 1}")
                nc.scalar.activation(hidden[e % 2][:, 0:512], mem[:, 0:512], ACT.Relu, bias=W("l0f.be1")[:, e:e + 1])\
                  .then_inc(read(f"{n}.h{e}"), 1)

            hidden_relu(0)
            hidden_relu(1)
            act.wait_ge(sem["less"], at(n, "less", 1))
            nc.scalar.activation(logit[:, :, :], logit[:, :, :], ACT.Exp).then_inc(sem["exp"], 1)
            for p in range(NE // 2):
                if p:
                    hidden_relu(2 * p)
                    hidden_relu(2 * p + 1)
                if p == 0:
                    mem = wait_full(act, n + ".gT")
                    nc.scalar.copy(gT, mem[0:NE, :]).then_inc(read(n + ".gT"), 1)
                if p >= 2:
                    wait_read(act, f"{n}.eo{p - 2}")
                for half in range(2):
                    mem = wait_full(act, f"{n}.rep{p}", half)
                    s = slice(512 * half, 512 * half + 512)
                    nc.scalar.copy(gate_rep[p % 2][:, s], mem[:, s]).then_inc(read(f"{n}.rep{p}"), 1)
            for c in range(2):
                for half in range(2):
                    mem = wait_full(act, f"{n}.c2s{c}", half)
                    s = slice(512 * half, 512 * half + 512)
                    nc.scalar.activation(spike[c][:, s], mem[:, s], ACT.Sigmoid, bias=W("l0f.c2s_b")[:, c:c + 1])\
                      .then_inc(read(f"{n}.c2s{c}"), 1)
            for half in range(2):
                wait_read(act, n + ".dec", half)
                s = slice(4 * half, 4 * half + 4)
                nc.scalar.activation(xn[:, s, :], xn[:, s, :], ACT.Sigmoid).then_inc(sem[n + ".decoded"], 1)

        def l0f_vector(dve):
            n = "l0f"
            ch = "vector_chain"
            ln_vector(dve, n, residual_ready(L0X))
            copy_half_vector(dve, n + ".T", xnT)
            dve.wait_ge(sem[n + ".padded"], 3)
            mem = wait_full(dve, n + ".cont", 1)
            wait_read(dve, n + ".cont", 0)
            nc.vector.tensor_scalar(contT[:, 512:], mem[0:M, 512:], W("l0f.s2c_b"), None, ALU.add).then_inc(read(n + ".cont"), 1)

            def hidden_relu(e):
                mem = wait_full(dve, f"{n}.h{e}", 1)
                if e >= 2:
                    wait_full(dve, f"{n}.eo{e // 2 - 1}")
                nc.vector.tensor_scalar(hidden[e % 2][:, 512:], mem[:, 512:], W("l0f.be1")[:, e:e + 1], 0.0, ALU.add, ALU.max)\
                  .then_inc(read(f"{n}.h{e}"), 1)

            hidden_relu(0)
            hidden_relu(1)
            mem = wait_full(dve, n + ".logit")
            nc.vector.tensor_tensor(logit[:, :, :], mem[:, 0:T * NE].rearrange("p (t e) -> p t e", e=NE), tok_bias("l0f.rb2"),
                                    ALU.add).then_inc(read(n + ".logit"), 1)
            wait_read(dve, n + ".logit")
            mine = logit[:, :, :].rearrange("p t (e o) -> p t e o", o=1).broadcast_to([P, T, NE, NE])
            other = logit[:, :, :].rearrange("p t (o e) -> p t o e", o=1).broadcast_to([P, T, NE, NE])
            link(dve, ch, nc.vector.tensor_tensor(tie[:, 0], other, mine, ALU.is_gt))
            link(dve, ch, nc.vector.tensor_tensor(tie[:, 1], other, mine, ALU.is_equal))
            first = W("before").rearrange("p (o e f) -> p o e f", o=1, e=NE).broadcast_to([P, T, NE, NE])
            link(dve, ch, nc.vector.tensor_tensor(tie[:, 1], tie[:, 1], first, ALU.mult))
            link(dve, ch, nc.vector.tensor_tensor(tie[:, 0], tie[:, 0], tie[:, 1], ALU.add))
            link(dve, ch, nc.vector.tensor_reduce(pick[:, :, :], tie[:, 0], AX, ALU.add))
            link(dve, ch, nc.vector.tensor_reduce(best[:, :, 0], logit[:, :, :], AX, ALU.max))
            nc.vector.tensor_tensor(logit[:, :, :], logit[:, :, :], best[:, :, :].broadcast_to([P, T, NE]), ALU.subtract)\
              .then_inc(sem["less"], 1)
            dve.wait_ge(sem["exp"], at(n, "exp", 1))
            link(dve, ch, nc.vector.scalar_tensor_tensor(out=pick[:, :, :], in0=pick[:, :, :], scalar=2.0, in1=logit[:, :, :],
                                                         op0=ALU.is_lt, op1=ALU.mult))
            link(dve, ch, nc.vector.tensor_reduce(best[:, :, 0], pick[:, :, :], AX, ALU.add))
            link(dve, ch, nc.vector.reciprocal(best[:, :, :], best[:, :, :]))
            nc.vector.tensor_tensor(pick[:, :, :], pick[:, :, :], best[:, :, :].broadcast_to([P, T, NE]), ALU.mult)\
              .then_inc(sem[n + ".gates"], 1)
            for p in range(NE // 2):
                if p:
                    hidden_relu(2 * p)
                    hidden_relu(2 * p + 1)
                mem = wait_full(dve, f"{n}.eo{p}")
                wait_read(dve, f"{n}.rep{p}")
                if p >= 2:
                    dve.wait_ge(sem[n + ".moe"], p)
                to = moe if p == 0 else gated
                if p:
                    dve.wait_ge(sem[n + ".moe"], p)
                nc.vector.scalar_tensor_tensor(out=to, in0=mem, scalar=W("l0f.be2")[:, p:p + 1], in1=gate_rep[p % 2],
                                               op0=ALU.add, op1=ALU.mult).then_inc(read(f"{n}.eo{p}"), 1)
                wait_read(dve, f"{n}.eo{p}")
                if p:
                    nc.vector.tensor_tensor(moe, moe, gated, ALU.add).then_inc(sem[n + ".moe"], 1)
                else:
                    dve.sem_inc(sem[n + ".moe"], 1)
            for half in range(2):
                mem = wait_full(dve, n + ".dec", half)
                nc.vector.tensor_tensor(xn[:, 4 * half:4 * half + 4, :],
                                        mem[:, 512 * half:512 * half + 512].rearrange("p (t d) -> p t d", d=D),
                                        tok_bias("l0f.dec_b", 4), ALU.add).then_inc(read(n + ".dec"), 1)
            gain = W("l0f.ln_g")
            for t in range(T + 2):
                if t < T:
                    dve.wait_ge(sem[n + ".decoded"], t // 4 + 1)
                    ln_stats(dve, n, t, xn, T)
                    dve.wait_ge(sem["moments"], at(n, "moments", T + t + 1))
                    nc.vector.scalar_tensor_tensor(out=xn[:, t, :], in0=xn[:, t, :], scalar=mv[:, t, 0:1], in1=gain,
                                                   op0=ALU.subtract, op1=ALU.mult).then_inc(sem[n + ".centred"], 1)
                if t >= 2:
                    u = t - 2
                    dve.wait_ge(sem[n + ".centred"], u + 1)
                    dve.wait_ge(sem["rstd"], at(n, "rstd", (T + u) // 2 + 1))
                    if u == 0:
                        dve.wait_ge(sem["b_out"], at(n, "b_out", 1))
                    nc.vector.scalar_tensor_tensor(out=x_res[:, u, :], in0=xn[:, u, :], scalar=rstd[:, u:u + 1],
                                                   in1=x_res[:, u, :], op0=ALU.mult, op1=ALU.add).then_inc(sem[n + ".x"], 1)

        def l0f_pool(pool):
            ln_pool(pool, "l0f")
            pool.wait_ge(sem["l0x.x"], T)
            for rows in (cont_all, r1_all, g_all):
                nc.gpsimd.memset(rows, 0.0).then_inc(sem["l0f.padded"], 1)
            add_bias_pool(pool, "l0f", "l0f.ln_b")
            ln_pool(pool, "l0f", T)

        L0F_READY = lambda eng, t: eng.wait_ge(sem["l0f.x"], t + 1)


        mixes = ("w", "a", "k", "v", "r", "g")
        diff = scr[:, 0, :]
        mixed = [scr[:, 1, :], scr[:, 2, :]]
        lin = {m: scr[:, 3 + i, :] for i, m in enumerate(("w", "a", "k", "r", "g"))}
        upd, state = scr[:, 8, :], scr[:, 9, :]
        group = sb("group", [P, 2, 128])

        def l1a_tensor(pe):
            n = "l1a"
            tiles_T_tensor(pe, n + ".T", xn, "xn", at(n, "xn", 0))
            for i, m in enumerate(mixes):
                pe.wait_ge(sem[n + ".mix"], i + 1)
                project_tensor(pe, f"{n}.{m}", [(W("L1_attn_W_" + m), mixed[i % 2])])
            project_tensor(pe, "l1x.k", [(W("L1_xattn_Wk"), ctxT)])
            values_tensor(pe, "l1x.v", W("L1_xattn_Wv"), ctxT)
            pe.wait_ge(sem[n + ".mixed"], 1)
            mem = fill(pe, n + ".mT")
            for t in range(T):
                mm = nc.tensor.transpose(mem[:, t * P:(t + 1) * P], state[:, t * P:(t + 1) * P], W("ident"))
            mm.then_inc(full(n + ".mT"), 1)
            mem = fill(pe, n + ".nT", fulls=1, reads=1)
            pe.wait_ge(sem[n + ".normed"], 1)
            for t in range(T):
                mm = nc.tensor.transpose(mem[:, t * P:(t + 1) * P], xn[:, t, :], W("ident"))
            mm.then_inc(full(n + ".nT"), 1)
            mem = fill(pe, n + ".y", reads=T)
            pe.wait_ge(sem[n + ".gated"], 1)
            for t in range(T):
                mm = nc.tensor.matmul(mem[:, t * P:(t + 1) * P], upd[:, t * P:(t + 1) * P], W("L1_attn_W_out"), start=True, stop=True)
            mm.then_inc(full(n + ".y"), 1)

        def l1a_scalar(act):
            n = "l1a"
            copy_half_scalar(act, n + ".T", xnT)
            for i, m in enumerate(mixes):
                if m == "v":
                    continue
                for half in range(2):
                    mem = wait_full(act, f"{n}.{m}", half)
                    s = slice(512 * half, 512 * half + 512)
                    nc.scalar.activation(lin[m][:, s], mem[:, s], ACT.Tanh if m == "k" else ACT.Sigmoid,
                                         scale=-1.0 if m == "w" else 1.0).then_inc(read(f"{n}.{m}"), 1)
            relu_half(act, "l1x.k", kcT, 0)
            act.wait_ge(sem["values_set"], VALUES_SET)
            values_copy(act, "l1x.v", v_ctx, 0, relu=True)
            act.wait_ge(sem[n + ".centred"], 1)
            nc.scalar.activation(scr[:, 1, :], xn[:, :, :].rearrange("p t d -> p (t d)"), ACT.Square).then_inc(sem[n + ".square"], 1)

        def l1a_vector(dve):
            n = "l1a"
            ch = "vector_chain"
            ln_vector(dve, n, L0F_READY)
            copy_half_vector(dve, n + ".T", xnT)
            wait_read(dve, n + ".T")
            seq = lambda x: x.rearrange("p (b s) -> p b s", s=SEQ)
            nc.vector.tensor_tensor(seq(diff)[:, :, 1:], seq(xnT[:, :])[:, :, :SEQ - 1], seq(xnT[:, :])[:, :, 1:], ALU.subtract)\
              .then_inc(sem[n + ".diff"], 1)
            nc.vector.tensor_scalar(seq(diff)[:, :, 0:1], seq(xnT[:, :])[:, :, 0:1], -1.0, None, ALU.mult).then_inc(sem[n + ".diff"], 1)
            dve.wait_ge(sem[n + ".diff"], 2)

            def mix(i):
                if i >= 2:
                    wait_full(dve, f"{n}.{mixes[i - 2]}")
                nc.vector.scalar_tensor_tensor(out=mixed[i % 2], in0=diff, scalar=W("l1a.x_" + mixes[i]), in1=xnT[:, :],
                                               op0=ALU.mult, op1=ALU.add).then_inc(sem[n + ".mix"], 1)

            for i in range(6):
                mix(i)
                if i == 5:
                    wait_read(dve, n + ".w")
                    link(dve, ch, nc.vector.memset(seq(lin["w"])[:, :, 0:1], 0.0))
                    wait_read(dve, n + ".a")
                    wait_read(dve, n + ".k")
                    link(dve, ch, nc.vector.tensor_tensor(upd, lin["a"], lin["k"], ALU.mult))
                    mem = wait_full(dve, n + ".v")
                    nc.vector.tensor_tensor(upd, mem, upd, ALU.mult).then_inc(read(n + ".v"), 2)
            wait_read(dve, n + ".v")
            link(dve, ch, nc.vector.tensor_tensor_scan(state, lin["w"], upd, 0.0, ALU.mult, ALU.add))
            wait_read(dve, n + ".r")
            nc.vector.tensor_tensor(state, state, lin["r"], ALU.mult).then_inc(sem[n + ".mixed"], 1)
            relu_half(dve, "l1x.k", kcT, 1)
            dve.wait_ge(sem["values_set"], VALUES_SET)
            values_copy(dve, "l1x.v", v_ctx, 1, relu=True)
            mem = wait_full(dve, n + ".mT")
            groups = lambda x: x.rearrange("p (g f) -> p g f", f=8)
            flat_xn = xn[:, :, :].rearrange("p t d -> p (t d)")
            link(dve, ch, nc.vector.tensor_reduce(group[:, 0, :], groups(mem), AX, ALU.add))
            link(dve, ch, nc.vector.tensor_scalar(group[:, 0, :], group[:, 0, :], 1 / 8, None, ALU.mult))
            gb = lambda x: x.rearrange("p (g o) -> p g o", o=1).broadcast_to([P, 128, 8])
            nc.vector.tensor_tensor(groups(flat_xn), groups(mem), gb(group[:, 0, :]), ALU.subtract).then_inc(read(n + ".mT"), 1)
            wait_read(dve, n + ".mT")
            dve.sem_inc(sem[n + ".centred"], 1)
            dve.wait_ge(sem[n + ".square"], 1)
            link(dve, ch, nc.vector.tensor_reduce(group[:, 1, :], groups(scr[:, 1, :]), AX, ALU.add))
            link(dve, ch, nc.vector.tensor_scalar(group[:, 1, :], group[:, 1, :], 1 / 8, 0.00064, ALU.mult, ALU.add))
            rsqrt_vector(dve, ch, group[:, 1, :], group[:, 0, :], 128)
            nc.vector.tensor_tensor(groups(flat_xn), groups(flat_xn), gb(group[:, 0, :]), ALU.mult).then_inc(sem[n + ".normed"], 1)
            mem = wait_full(dve, n + ".nT")
            nc.vector.tensor_scalar(upd, mem, W("l1a.gn_w"), W("l1a.gn_b"), ALU.mult, ALU.add).then_inc(read(n + ".nT"), 1)
            wait_read(dve, n + ".nT")
            wait_read(dve, n + ".g")
            nc.vector.tensor_tensor(upd, upd, lin["g"], ALU.mult).then_inc(sem[n + ".gated"], 1)
            dve.wait_ge(sem["b_out"], at(n, "b_out", 1))
            mem = wait_full(dve, n + ".y")
            for t in range(T):
                nc.vector.tensor_tensor(x_res[:, t, :], mem[:, t * P:(t + 1) * P], x_res[:, t, :], ALU.add).then_inc(read(n + ".y"), 1)

        def add_bias_pool(pool, n, name):
            pool.wait_ge(sem["xn"], at(n, "xn", T))
            nc.gpsimd.tensor_tensor(x_res[:, :, :], x_res[:, :, :], tok_bias(name), ALU.add).then_inc(sem["b_out"], 1)

        def l1a_pool(pool):
            ln_pool(pool, "l1a")
            add_bias_pool(pool, "l1a", "l1a.b_out")

        def product_ready(name):
            return lambda eng, t: eng.wait_ge(sem["read." + book.record[name][0]], book.record[name][3] - T + t + 1)

        table_out = sb("table_out", [P, 3])

        def load_table(act, use, function):
            nc.scalar.activation(table_out[:, use:use + 1], W("ident")[:, 0:1], function)


        L1X = attention("l1x", "plain", scale=8 ** -0.5, q=qT, k=kcT, v=v_ctx,
                        q_ready=half_ready("l1x.q"), k_ready=half_ready("l1x.k"),
                        v_ready=lambda eng: wait_read(eng, "l1x.v"), before_keys=lambda eng, t: wait_full(eng, f"l0x.s{6 + t}"))

        def l1x_tensor(pe):
            n = "l1x"
            tiles_T_tensor(pe, n + ".T", xn, "xn", at(n, "xn", 0))
            project_tensor(pe, n + ".q", [(W("L1_xattn_Wq"), xnT)], after=[n + ".T"])
            attention_tensor(pe, L1X)

        def relu_half(eng, name, dst, half):
            mem = wait_full(eng, name, half)
            s = slice(512 * half, 512 * half + 512)
            if half == 0:
                nc.scalar.activation(dst[:, s], mem[:, s], ACT.Relu).then_inc(read(name), 1)
            else:
                wait_read(eng, name, 0)
                nc.vector.tensor_scalar(dst[:, s], mem[:, s], 0.0, None, ALU.max).then_inc(read(name), 1)

        def l1x_vector(dve):
            n = "l1x"
            ln_vector(dve, n, product_ready("l1a.y"))
            copy_half_vector(dve, n + ".T", xnT)
            relu_half(dve, n + ".q", qT, 1)
            attention_vector(dve, L1X)

        def l1x_scalar(act):
            n = "l1x"
            load_table(act, 0, ACT.Exp)
            copy_half_scalar(act, n + ".T", xnT)
            relu_half(act, n + ".q", qT, 0)
            attention_scalar(act, L1X)

        def l1x_pool(pool):
            ln_pool(pool, "l1x")
            attention_pool(pool, L1X)


        wide = [scr[:, i, :] for i in range(4)]
        mem_v, cur, spikes = scr[:, 4, :], scr[:, 5, :], scr[:, 6, :]
        lif_a = scr[:, 7, :]

        first_half_T("l1f")

        def l1f_tensor(pe):
            n = "l1f"
            second_half_T(pe, n)
            for c in range(4):
                project_tensor(pe, f"{n}.h{c}", [(W("L1_ffn_W_fc")[:, 128 * c:128 * c + 128], xnT)], after=[n + ".T"])
            mem = fill(pe, n + ".y", fulls=2, reads=2)
            for t in range(T):
                for c in range(4):
                    if t % 4 == 0:
                        pe.wait_ge(sem[n + ".square"], 4 * (t // 4) + c + 1)
                    mm = nc.tensor.matmul(mem[:, t * P:(t + 1) * P], wide[c][:, t * P:(t + 1) * P], W(f"l1f.proj{c}"),
                                          start=c == 0, stop=c == 3)
                if t % 4 == 3:
                    mm.then_inc(full(n + ".y"), 1)

        def l1f_scalar(act):
            n = "l1f"
            for c in range(4):
                for half in range(2):
                    mem = wait_full(act, f"{n}.h{c}", half)
                    s = slice(512 * half, 512 * half + 512)
                    nc.scalar.activation(wide[c][:, s], mem[:, s], ACT.Relu).then_inc(read(f"{n}.h{c}"), 1)

        def l1f_vector(dve):
            n = "l1f"
            ch = "vector_chain"
            copy_half_vector(dve, n + ".T", xnT)
            for half in range(2):
                for c in range(4):
                    s = slice(512 * half, 512 * half + 512)
                    wait_read(dve, f"{n}.h{c}")
                    nc.vector.tensor_tensor(wide[c][:, s], wide[c][:, s], wide[c][:, s], ALU.mult).then_inc(sem[n + ".square"], 1)
            def lif_start(half):
                s = slice(512 * half, 512 * half + 512)
                mem = wait_full(dve, n + ".y", half)
                nc.vector.tensor_copy(cur[:, s], mem[:, s]).then_inc(read(n + ".y"), 1)
                wait_read(dve, n + ".y", half)
                nc.vector.tensor_scalar(spikes[:, s], cur[:, s], 1.0, None, ALU.is_gt).then_inc(sem[f"lif{half}"], 1)

            def lif(half, step, part):
                s = slice(512 * half, 512 * half + 512)
                v = mem_v[:, s] if step else cur[:, s]
                dve.wait_ge(sem[f"lif{half}"], 1 + 3 * step + part)
                if part == 0:
                    instr = nc.vector.scalar_tensor_tensor(out=lif_a[:, s], in0=v, scalar=0.9, in1=cur[:, s], op0=ALU.mult, op1=ALU.add)
                elif part == 1:
                    instr = nc.vector.scalar_tensor_tensor(out=mem_v[:, s], in0=v, scalar=1.0, in1=lif_a[:, s], op0=ALU.is_gt,
                                                           op1=ALU.subtract, reverse1=True)
                else:
                    instr = nc.vector.scalar_tensor_tensor(out=spikes[:, s], in0=mem_v[:, s], scalar=1.0, in1=spikes[:, s],
                                                           op0=ALU.is_gt, op1=ALU.add)
                instr.then_inc(sem[f"lif{half}"], 1)

            LIF_STEPS = 4
            lif_start(0)
            for part in range(3):
                lif(0, 0, part)
            lif_start(1)
            for step in range(LIF_STEPS):
                for part in range(3):
                    lif(1, step, part)
                    if step + 1 < LIF_STEPS:
                        lif(0, step + 1, part)
            sp = spikes.rearrange("p (t d) -> p t d", t=T)
            for t in range(T):
                if t % 4 == 0:
                    dve.wait_ge(sem[f"lif{t // 4}"], 1 + 3 * LIF_STEPS)
                nc.vector.scalar_tensor_tensor(out=x_res[:, t, :], in0=sp[:, t, :], scalar=0.2, in1=x_res[:, t, :],
                                               op0=ALU.mult, op1=ALU.add).then_inc(sem[n + ".x"], 1)

        def l1f_pool(pool):
            ln_pool(pool, "l1f")

        L1F_READY = lambda eng, t: eng.wait_ge(sem["l1f.x"], t + 1)



        def bias_half(eng, name, dst, half, bias):
            mem = wait_full(eng, name, half)
            s = slice(512 * half, 512 * half + 512)
            if half == 0:
                nc.scalar.activation(dst[:, s], mem[:, s], ACT.Identity, bias=W(bias)).then_inc(read(name), 1)
            else:
                wait_read(eng, name, 0)
                nc.vector.tensor_scalar(dst[:, s], mem[:, s], W(bias), None, ALU.add).then_inc(read(name), 1)

        rope_qk = scr[:, 0:2, :].rearrange("p a (b c) -> p (a b) c", c=256)
        rope_tmp = scr[:, 2:4, :].rearrange("p a (b c) -> p (a b) c", c=256)
        rope_sq = scr[:, 4:6, :].rearrange("p a b -> p (a b)")
        norm_qk = sb("norm_qk", [P, 2, 256])
        L2A = attention("l2a", "unit", bo=True, scale=8 ** -0.5, q=qT, k=kT, v=v_self, wo="L2_attn_Wo",
                        q_ready=lambda eng, half: wait_read(eng, f"l2a.q{half}"), k_ready=lambda eng, half: wait_read(eng, f"l2a.k{half}"),
                        v_ready=lambda eng: wait_read(eng, "l2a.v"), before_keys=lambda eng, t: wait_full(eng, f"l1x.s{6 + t}"))
        L2A["softmax"] = lambda dve, a, t: None

        raw_qk = scr[:, 6:8, :].rearrange("p a (b c) -> p (a b) c", c=512)
        rope_heads = lambda x: x.rearrange("p t (h f) -> p t h f", f=8)
        rope_table = lambda name: W(name).rearrange("p (a o f) -> p a o f", a=1, o=1).broadcast_to([P, 2, 32, 8])

        def unit_T_tensor(pe, half):
            pe.wait_ge(sem["l2a.unit"], half + 1)
            for part, c in (("k", 1), ("q", 0)):
                mem = fill(pe, f"l2a.{part}{half}", "B")
                for t in range(4):
                    mm = nc.tensor.transpose(mem[:, t * P:(t + 1) * P], rope_qk[:, 4 * half + t, 128 * c:128 * c + 128], W("ident"))
                mm.then_inc(full(f"l2a.{part}{half}"), 1)

        def unit_copy_scalar(act, half):
            mem = wait_full(act, f"l2a.k{half}")
            nc.scalar.copy(kT[:, 512 * half:512 * half + 512], mem).then_inc(read(f"l2a.k{half}"), 1)

        def unit_copy_vector(dve, half):
            mem = wait_full(dve, f"l2a.q{half}")
            nc.vector.tensor_copy(qT[:, 512 * half:512 * half + 512], mem).then_inc(read(f"l2a.q{half}"), 1)

        def unit_vector(dve, half):
            ch = "vector_chain"
            g, rows = slice(128 * half, 128 * half + 128), slice(4 * half, 4 * half + 4)
            dve.wait_ge(sem["l2a.square"], 2 * half + 2)
            sq = rope_sq[:, 1024 * half:1024 * half + 1024].rearrange("p (g f) -> p g f", f=8)
            link(dve, ch, nc.vector.tensor_reduce(norm_qk[:, 0, g], sq, AX, ALU.add))
            link(dve, ch, nc.vector.tensor_scalar(norm_qk[:, 0, g], norm_qk[:, 0, g], 1e-6, None, ALU.add))
            rsqrt_vector(dve, ch, norm_qk[:, 0, g], norm_qk[:, 1, g], 128)
            dve.wait_ge(sem["l2a.rotated"], 2 * half + 2)
            qk = rope_qk[:, rows, :].rearrange("p t (h f) -> p (t h) f", f=8)
            rb = norm_qk[:, 1, g].rearrange("p (g o) -> p g o", o=1).broadcast_to([P, 128, 8])
            nc.vector.tensor_tensor(qk, qk, rb, ALU.mult).then_inc(sem["l2a.unit"], 1)

        leads["l2a", "vector", ("step", 0)] = [lambda dve: unit_vector(dve, 1)]
        leads["l2a", "tensor", ("step", 1)] = [lambda pe: unit_T_tensor(pe, 1)]
        leads["l2a", "scalar", ("step", 1)] = [lambda act: unit_copy_scalar(act, 1)]
        leads["l2a", "vector", ("step", 1)] = [lambda dve: unit_copy_vector(dve, 1)]

        def l2a_tensor(pe):
            n = "l2a"
            tiles_T_tensor(pe, n + ".T", xn, "xn", at(n, "xn", 0))
            for pair in range(T // 2):
                wait_read(pe, n + ".T", pair // 2)
                mem = fill(pe, f"{n}.qk{pair}", reads=1 if pair < 2 else 2)
                for i in range(2):
                    t = 2 * pair + i
                    mm = nc.tensor.matmul(mem[:, 512 * i:512 * i + 512], xnT[:, t * P:(t + 1) * P], W("l2a.qk_rot"), start=True, stop=True)
                mm.then_inc(full(f"{n}.qk{pair}"), 1)
            values_tensor(pe, n + ".v", W("l2a.Wv"), xnT)
            unit_T_tensor(pe, 0)
            attention_tensor(pe, L2A)

        def l2a_vector(dve):
            n = "l2a"
            ln_vector(dve, n, L1F_READY)
            copy_half_vector(dve, n + ".T", xnT)
            for pair in range(2):
                mem = wait_full(dve, f"{n}.qk{pair}").rearrange("p (t c) -> p t c", t=2)
                dve.wait_ge(sem[n + ".square"], pair + 1)
                s = slice(2 * pair, 2 * pair + 2)
                nc.vector.tensor_tensor(rope_heads(rope_qk[:, s, :]), rope_heads(mem[:, :, 0:256]), rope_table("cos8"), ALU.mult)\
                  .then_inc(sem[n + ".cos"], 1)
                nc.vector.tensor_tensor(rope_heads(rope_tmp[:, s, :]), rope_heads(mem[:, :, 256:512]), rope_table("sin8"), ALU.mult)\
                  .then_inc(read(f"{n}.qk{pair}"), 1)
            unit_vector(dve, 0)
            unit_copy_vector(dve, 0)
            values_copy(dve, n + ".v", v_self, 1)
            attention_vector(dve, L2A)

        def l2a_scalar(act):
            n = "l2a"
            copy_half_scalar(act, n + ".T", xnT)
            for pair in range(T // 2):
                mem = wait_full(act, f"{n}.qk{pair}").rearrange("p (t c) -> p t c", t=2)
                sq = rope_sq[:, 512 * pair:512 * pair + 512].rearrange("p (t c) -> p t c", t=2)
                nc.scalar.activation(sq, mem[:, :, 0:256], ACT.Square).then_inc(sem[n + ".square"], 1)
                if pair >= 2:
                    for i in range(2):
                        nc.scalar.copy(raw_qk[:, 2 * (pair - 2) + i, :], mem[:, i, :]).then_inc(read(f"{n}.qk{pair}"), 1)
            values_copy(act, n + ".v", v_self, 0)
            unit_copy_scalar(act, 0)
            attention_scalar(act, L2A)

        def l2a_pool(pool):
            n = "l2a"
            ln_pool(pool, n)
            for pair in range(T // 2):
                s = slice(2 * pair, 2 * pair + 2)
                wait_read(pool, f"{n}.qk{pair}")
                if pair < 2:
                    pool.wait_ge(sem[n + ".cos"], pair + 1)
                else:
                    raw = raw_qk[:, 2 * (pair - 2):2 * (pair - 2) + 2, :]
                    link(pool, "pool_chain", nc.gpsimd.tensor_tensor(rope_heads(rope_qk[:, s, :]), rope_heads(raw[:, :, 0:256]),
                                                                     rope_table("cos8"), ALU.mult))
                    link(pool, "pool_chain", nc.gpsimd.tensor_tensor(rope_heads(rope_tmp[:, s, :]), rope_heads(raw[:, :, 256:512]),
                                                                     rope_table("sin8"), ALU.mult))
                nc.gpsimd.tensor_tensor(rope_qk[:, s, :], rope_qk[:, s, :], rope_tmp[:, s, :], ALU.add).then_inc(sem[n + ".rotated"], 1)
                if pair == 2:
                    spread(pool, nc.gpsimd, L2A, 0, 0, POOL_HEADS, "pool")
                    spread(pool, nc.gpsimd, L2A, 1, 0, POOL_HEADS, "pool")
            for t in range(2, T):
                spread(pool, nc.gpsimd, L2A, t, 0, POOL_HEADS, "pool")
                if t == 3:
                    add_bias_pool(pool, n, "l2a.bo")


        def half_T_tensor(pe, n, half):
            mem = fill(pe, f"{n}.T{half}", "B")
            for t in range(4 * half, 4 * half + 4):
                pe.wait_ge(sem["xn"], at(n, "xn", t + 1))
                mm = nc.tensor.transpose(mem[:, (t % 4) * P:(t % 4 + 1) * P], xn[:, t, :], W("ident"))
            mm.then_inc(full(f"{n}.T{half}"), 1)

        def half_T_scalar(act, n, half):
            mem = wait_full(act, f"{n}.T{half}")
            nc.scalar.copy(xnT[:, 512 * half:512 * half + 512], mem).then_inc(read(f"{n}.T{half}"), 1)

        def half_q_tensor(pe, n, half, wq):
            wait_read(pe, f"{n}.T{half}")
            mem = fill(pe, f"{n}.q{half}", "B")
            nc.tensor.matmul(mem, W(wq), xnT[:, 512 * half:512 * half + 512], start=True, stop=True).then_inc(full(f"{n}.q{half}"), 1)

        def half_q_scalar(act, n, half, bq):
            mem = wait_full(act, f"{n}.q{half}")
            nc.scalar.activation(qT[:, 512 * half:512 * half + 512], mem, ACT.Identity, bias=W(bq)).then_inc(read(f"{n}.q{half}"), 1)

        def context_lead(a, wq, wk, wv, bq, bk):
            n = a["n"]
            leads[n, "tensor", 0] = [lambda pe: project_tensor(pe, n + ".k", [(W(wk), ctxT)]),
                                     lambda pe: half_T_tensor(pe, n, 0)]
            leads[n, "scalar", 0] = [lambda act: bias_half(act, n + ".k", a["k"], 0, bk),
                                     lambda act: half_T_scalar(act, n, 0)]
            leads[n, "vector", 0] = [lambda dve: bias_half(dve, n + ".k", a["k"], 1, bk)]
            leads[n, "tensor", 1] = [lambda pe: values_tensor(pe, n + ".v", W(wv), ctxT)]
            leads[n, "scalar", 1] = [lambda act: values_copy(act, n + ".v", a["v"], 0)]
            leads[n, "vector", 1] = [lambda dve: values_copy(dve, n + ".v", a["v"], 1)]
            a["spread_early"] = True
            leads[n, "vector", 1].append(lambda dve: spread(dve, nc.vector, a, 0, POOL_HEADS, 16, "dve"))
            leads[n, "tensor", 2] = [lambda pe: half_q_tensor(pe, n, 0, wq)]
            leads[n, "scalar", 2] = [lambda act: half_q_scalar(act, n, 0, bq)]
            leads[n, "tensor", ("step", 0)] = [lambda pe: half_T_tensor(pe, n, 1)]
            leads[n, "scalar", ("step", 0)] = [lambda act: half_T_scalar(act, n, 1)]
            leads[n, "tensor", ("step", 1)] = [lambda pe: half_q_tensor(pe, n, 1, wq)]
            leads[n, "scalar", ("step", 1)] = [lambda act: half_q_scalar(act, n, 1, bq)]

        def biased_pool(pool, a, bo):
            n = a["n"]
            a["bo"] = bo
            if a["k"] is kcT:
                ln_pool(pool, n, tiles=(0, T - 2))
                spread(pool, nc.gpsimd, a, 0, 0, POOL_HEADS, "pool")
                ln_pool(pool, n, tiles=(T - 2, T))
                attention_pool(pool, a, first=1)
            else:
                ln_pool(pool, n)
                attention_pool(pool, a)

        def biased_attention(n, kind, cross, last, pre, wo, bv):
            return attention(n, kind, scale=8 ** -0.5, q=qT, k=kcT if cross else kT, v=v_ctx if cross else v_self, wo=wo, bv=bv,
                             bo=True, q_ready=(lambda eng, half: wait_read(eng, f"{n}.q{half}")) if cross else half_ready(n + ".q"),
                             k_ready=half_ready(n + ".k"),
                             v_ready=lambda eng: wait_read(eng, n + ".v"),
                             before_keys=lambda eng, t: wait_full(eng, f"{last}.s{6 + t}"))


        L2X = biased_attention("l2x", "topk", True, "l2a", "L2_xattn", "l2x.Wo", "l2x.bv")
        L2X["prob_ready"] = lambda eng, t, g: eng.wait_ge(sem["l2x.chosen"], t + 1)
        FOUND = -3.0e38
        rest = [scr[:, 8, :], scr[:, 9, :]]
        best8 = [sb(f"best8_{i}", [P, 16, 8]) for i in range(2)]
        ROUNDS = 4

        def topk_vector(dve, a, t):
            n = a["n"]
            wait_read(dve, f"{n}.s{t}")
            pr = prob[t % 2][:, :].rearrange("p (h k) -> p h k", k=SEQ)
            left = rest[t % 2].rearrange("p (h k) -> p h k", k=SEQ)
            for r in range(ROUNDS):
                src = left if r else pr
                b8 = best8[r % 2]
                for h in range(16):
                    if r and h % 8 == 0:
                        dve.wait_ge(sem[n + ".struck"], 16 * (ROUNDS * t + r - 1) + h + 8)
                    nc.vector.max(b8[:, h, :], src[:, h, :]).then_inc(sem[n + ".best"], 1)
                if r == 0 and t >= 2:
                    dve.wait_ge(sem["less"], at(n, "less", t - 1))
                    dve.wait_ge(sem[n + ".chosen"], t - 1)
                for h in range(16):
                    if h % 8 == 0:
                        dve.wait_ge(sem[n + ".best"], 16 * (ROUNDS * t + r) + h + 8)
                    nc.vector.match_replace(out=left[:, h, :], in_to_replace=b8[:, h, :], in_values=src[:, h, :], imm_value=FOUND)\
                      .then_inc(sem[n + ".struck"], 1)
                if r == 0:
                    nc.vector.tensor_copy(top[t % 2][:, :], b8[:, :, 0]).then_inc(sem["top"], 1)
            if t == T - 1:
                weigh(dve, nc.vector, a, t)

        def weigh(eng, ops, a, t):
            n, chain = a["n"], "vector_chain" if t == T - 1 else "pool_chain"
            eng.wait_ge(sem[n + ".struck"], 16 * ROUNDS * (t + 1))
            eng.wait_ge(sem["top"], at(n, "top", t + 1))
            if t == T - 1:
                eng.wait_ge(sem["less"], at(n, "less", t))
                eng.wait_ge(sem[n + ".chosen"], t)
            pr = prob[t % 2][:, :].rearrange("p (h k) -> p h k", k=SEQ)
            tb = top[t % 2][:, :].rearrange("p (h o) -> p h o", o=1).broadcast_to([P, 16, SEQ])
            ops.tensor_tensor(pr, pr, tb, ALU.subtract).then_inc(sem["less"], 1)
            link(eng, chain, ops.tensor_scalar(rest[t % 2], rest[t % 2], -2.0e38, None, ALU.is_le))
            eng.wait_ge(sem["exp"], at(n, "exp", t + 1))
            ops.tensor_tensor(prob[t % 2][:, :], rest[t % 2], prob[t % 2][:, :], ALU.mult).then_inc(sem[n + ".chosen"], 1)

        L2X["softmax"] = topk_vector

        def topk_copy_scalar(act, a, t):
            n = a["n"]
            if t >= 2:
                wait_full(act, f"{n}.t{t - 2}")
            mem = wait_full(act, f"{n}.s{t}")
            nc.scalar.copy(prob[t % 2][:, :], mem).then_inc(read(f"{n}.s{t}"), 1)

        L2X["copy"] = topk_copy_scalar


        share = sb("share", [P, 2])
        thresh = sb("thresh", [P, 2, 2])
        tern = scr[:, 10, 0:512]
        tern2 = scr[:, 10, 512:1024]
        TERNARY = ("l2f.up", "l2f.down")

        def ternary_scalar(act):
            for i, w in enumerate(TERNARY):
                if i:
                    act.wait_ge(sem["tern.sum"], 1)
                nc.scalar.activation(tern, W(w), ACT.Abs, accum_out=share[:, i:i + 1]).then_inc(sem["tern.sum"], 1)

        def ternary_tensor(pe):
            pe.wait_ge(sem["tern.sum"], 2)
            mem = fill(pe, "tern.mean", "B")
            nc.tensor.matmul(mem[:, 0:2], W("ones128"), share[:, :], start=True, stop=True).then_inc(full("tern.mean"), 1)

        def ternary_vector(dve):
            mem = wait_full(dve, "tern.mean")
            half_mean = 0.5 / (512 * 128)
            link(dve, "vector_chain", nc.vector.tensor_scalar(thresh[:, :, 0], mem[:, 0:2], half_mean, None, ALU.mult))
            nc.vector.tensor_scalar(thresh[:, :, 1], mem[:, 0:2], -half_mean, None, ALU.mult).then_inc(read("tern.mean"), 1)

        def ternary_pool(pool):
            wait_read(pool, "tern.mean")
            pool.wait_ge(sem["tern.sum"], 2)
            for i, name in enumerate(TERNARY):
                w = W(name)
                link(pool, "pool_chain", nc.gpsimd.tensor_scalar(tern, w, thresh[:, i, 0:1], None, ALU.is_gt))
                link(pool, "pool_chain", nc.gpsimd.tensor_scalar(tern2, w, thresh[:, i, 1:2], None, ALU.is_lt))
                link(pool, "pool_chain", nc.gpsimd.tensor_tensor(tern, tern, tern2, ALU.subtract))
                link(pool, "pool_chain", nc.gpsimd.tensor_tensor(tern, tern, w, ALU.subtract))
                link(pool, "pool_chain", nc.gpsimd.tensor_tensor(w, w, tern, ALU.add))

        context_lead(L2X, "l2x.Wq", "l2x.Wk", "l2x.Wv", "l2x.bq", "l2x.bk")

        def l2x_tensor(pe):
            ternary_tensor(pe)
            attention_tensor(pe, L2X)

        def l2x_vector(dve):
            ternary_vector(dve)
            attention_vector(dve, L2X)

        def l2x_scalar(act):
            ternary_scalar(act)
            attention_scalar(act, L2X)

        def l2x_pool(pool):
            ln_pool(pool, "l2x", tiles=(0, T - 2))
            spread(pool, nc.gpsimd, L2X, 0, 0, POOL_HEADS, "pool")
            ln_pool(pool, "l2x", tiles=(T - 2, T))
            spread(pool, nc.gpsimd, L2X, 1, 0, POOL_HEADS, "pool")
            add_bias_pool(pool, "l2x", "l2x.bo")
            ternary_pool(pool)
            for t in range(T - 1):
                weigh(pool, nc.gpsimd, L2X, t)
                if t + 2 < T:
                    spread(pool, nc.gpsimd, L2X, t + 2, 0, POOL_HEADS, "pool")


        hid = scr[:, 0:4, :].rearrange("p a (b c) -> p (a b) c", c=512)
        hidT = scr[:, 4:8, :].rearrange("p a b -> p (a b)").rearrange("p (t c k) -> p t c k", t=T, c=4)
        junk = scr[:, 8, 0:512]
        row = sb("row", [P, 4, T])

        def square_tiles(act, tiles):
            for t in range(*tiles):
                act.wait_ge(sem["xn"], at("l2f", "xn", t + 1))
                nc.scalar.activation(scr[:, 10, t * P:(t + 1) * P], xn[:, t, :], ACT.Square, accum_out=row[:, 0, t:t + 1])\
                  .then_inc(sem["l2f.square"], 1)

        first_half_T("l2f")
        leads["l2f", "scalar", 0].append(lambda act: square_tiles(act, (0, 4)))

        def l2f_tensor(pe):
            n = "l2f"
            second_half_T(pe, n)
            for pair in range(T // 2):
                wait_read(pe, n + ".T", pair // 2)
                mem = fill(pe, f"{n}.up{pair}", reads=2)
                for i in range(2):
                    t = 2 * pair + i
                    mm = nc.tensor.matmul(mem[:, 512 * i:512 * i + 512], xnT[:, t * P:(t + 1) * P], W("l2f.up"), start=True, stop=True)
                mm.then_inc(full(f"{n}.up{pair}"), 1)
            for pair in range(T // 2):
                wait_read(pe, f"{n}.up{pair}")
                mem = fill(pe, f"{n}.hT{pair}", fulls=2, reads=2)
                for i in range(2):
                    for c in range(4):
                        at = 512 * i + 128 * c
                        mm = nc.tensor.transpose(mem[:, at:at + 128], hid[:, 2 * pair + i, 128 * c:128 * c + 128], W("ident"))
                    mm.then_inc(full(f"{n}.hT{pair}"), 1)
            for half in range(2):
                for pair in (2 * half, 2 * half + 1):
                    wait_read(pe, f"{n}.hT{pair}")
                mem = fill(pe, f"{n}.y{half}", "B", reads=4)
                for t in range(4 * half, 4 * half + 4):
                    for c in range(4):
                        mm = nc.tensor.matmul(mem[:, (t % 4) * P:(t % 4 + 1) * P], hidT[:, t, c, :], W("l2f.down")[:, 128 * c:128 * c + 128],
                                              start=c == 0, stop=c == 3)
                mm.then_inc(full(f"{n}.y{half}"), 1)

        def l2f_scalar(act):
            n = "l2f"
            load_table(act, 2, ACT.Gelu)
            square_tiles(act, (4, T))
            act.wait_ge(sem[n + ".rms"], 1)
            for t in range(T):
                mem = wait_full(act, f"{n}.up{t // 2}")
                nc.scalar.activation(hid[:, t, :], mem[:, 512 * (t % 2):512 * (t % 2) + 512], ACT.Gelu, scale=row[:, 1, t:t + 1])\
                  .then_inc(read(f"{n}.up{t // 2}"), 1)
            for t in range(T):
                wait_read(act, f"{n}.up{t // 2}")
                if t:
                    act.wait_ge(sem[n + ".ss"], t)
                nc.scalar.activation(junk, hid[:, t, :], ACT.Square, accum_out=row[:, 2, t:t + 1]).then_inc(sem[n + ".ss"], 1)
                if t % 2:
                    pair = t // 2
                    mem = wait_full(act, f"{n}.hT{pair}", 0)
                    nc.scalar.copy(hidT[:, 2 * pair, :, :].rearrange("p c k -> p (c k)"), mem[:, 0:512]).then_inc(read(f"{n}.hT{pair}"), 1)

        def l2f_vector(dve):
            n = "l2f"
            ch = "vector_chain"
            copy_half_vector(dve, n + ".T", xnT)
            dve.wait_ge(sem[n + ".root"], 1)
            nc.vector.reciprocal(row[:, 1, :], row[:, 1, :]).then_inc(sem[n + ".rms"], 1)
            for pair in range(T // 2):
                mem = wait_full(dve, f"{n}.hT{pair}", 1)
                nc.vector.tensor_copy(hidT[:, 2 * pair + 1, :, :].rearrange("p c k -> p (c k)"), mem[:, 512:1024])\
                  .then_inc(read(f"{n}.hT{pair}"), 1)
            weights(dve, "3")
            c = W("causal").rearrange("p (o k) -> p o k", o=1).broadcast_to([P, 16, SEQ])
            link(dve, ch, nc.vector.tensor_tensor(rel_bias.rearrange("p (h k) -> p h k", k=SEQ),
                                                            W("l3a.rel").rearrange("p (h k) -> p h k", k=SEQ), c, ALU.add))
            dve.wait_ge(sem[n + ".root"], 2)
            link(dve, ch, nc.vector.reciprocal(row[:, 3, :], row[:, 3, :]))
            for t in range(T):
                mem = wait_full(dve, f"{n}.y{t // 4}")
                nc.vector.scalar_tensor_tensor(out=x_res[:, t, :], in0=mem[:, (t % 4) * P:(t % 4 + 1) * P], scalar=row[:, 3, t:t + 1],
                                               in1=x_res[:, t, :], op0=ALU.mult, op1=ALU.add).then_inc(read(f"{n}.y{t // 4}"), 1)

        def l2f_pool(pool):
            n = "l2f"
            ln_pool(pool, n)
            for i, (squares, width) in enumerate(((".square", D), (".ss", 512))):
                out = row[:, 2 * i + 1, :]
                pool.wait_ge(sem[n + squares], T)
                link(pool, "pool_chain", nc.gpsimd.tensor_tensor(out, row[:, 2 * i, :], plus_half[:, 0:1].broadcast_to([P, T]), ALU.pow))
                nc.gpsimd.tensor_scalar(out, out, width ** -0.5, 1e-8, ALU.mult, ALU.add).then_inc(sem[n + ".root"], 1)

        L2F_READY = lambda eng, t: wait_read(eng, f"l2f.y{t // 4}")


        L3A = biased_attention("l3a", "bias", False, "l2x", "L3_attn", "l3a.WO", "l3a.bV")
        L3X = biased_attention("l3x", "plain", True, "l3a", "L3_xattn", "l3x.Wo", "l3x.bv")
        L3A["wv"] = W("l3a.WV")
        rel_bias = scr[:, 11, :]

        def l3a_tensor(pe):
            tiles_T_tensor(pe, "l3a.T", xn, "xn", at("l3a", "xn", 0))
            project_tensor(pe, "l3a.k", [(W("l3a.WK"), xnT)], after=["l3a.T"])
            project_tensor(pe, "l3a.q", [(W("l3a.WQ"), xnT)])
            attention_tensor(pe, L3A)

        def l3a_vector(dve):
            ln_vector(dve, "l3a", L2F_READY)
            copy_half_vector(dve, "l3a.T", xnT)
            bias_half(dve, "l3a.k", kT, 1, "l3a.bK")
            bias_half(dve, "l3a.q", qT, 1, "l3a.bQ")
            attention_vector(dve, L3A)

        def l3a_scalar(act):
            load_table(act, 1, ACT.Exp)
            copy_half_scalar(act, "l3a.T", xnT)
            bias_half(act, "l3a.k", kT, 0, "l3a.bK")
            bias_half(act, "l3a.q", qT, 0, "l3a.bQ")
            attention_scalar(act, L3A)

        def l3a_pool(pool):
            biased_pool(pool, L3A, "l3a.bO")

        context_lead(L3X, "l3x.Wq", "l3x.Wk", "l3x.Wv", "l3x.bq", "l3x.bk")

        def l3x_tensor(pe):
            attention_tensor(pe, L3X)

        def l3x_vector(dve):
            attention_vector(dve, L3X)

        def l3x_scalar(act):
            attention_scalar(act, L3X)

        def l3x_pool(pool):
            biased_pool(pool, L3X, "l3x.bo")
            for j in range(2):
                nc.gpsimd.memset(keys4[j][:, :, :, :, :], 0.0).then_inc(sem["zeros_set"], 1)
            nc.gpsimd.memset(v4[0][:, :, :, :], 0.0).then_inc(sem["zeros_set"], 1)


        z = xn
        half_shifted = kcT[:, :].rearrange("p (t d) -> p t d", t=T)
        turned = [scr[:, j, :] for j in (0, 1, 11)]
        square4 = [scr[:, j, :] for j in (2, 3)]
        crossed = [scr[:, j, :] for j in (4, 5)]
        keys4 = [scr[:, j, :].rearrange("p (a b h k) -> p a b h k", a=4, b=2, h=2) for j in (6, 7)]
        qT4 = [scr[:, 8, 512 * j:512 * j + 512].rearrange("p (a k) -> p a k", a=4) for j in (0, 1)]
        out4 = [scr[:, 9, 512 * j:512 * j + 512] for j in (0, 1)]
        outT4 = [scr[:, 10, 512 * j:512 * j + 512] for j in (0, 1)]
        v4 = [v.rearrange("p b a w -> p (b a w)")[:, 0:1040].rearrange("p (b a w) -> p b a w", b=2, a=4) for v in (v_self, v_ctx)]
        gelu4, mlp4 = (k.rearrange("p h k -> p (h k)")[:, 0:1536].rearrange("p (c k) -> p c k", c=3) for k in keys)
        mlpT = ctxT
        len_sq = sb("len_sq", [P, T, 16])
        len_inv = sb("len_inv", [P, T, 16])
        HIDDEN_ROWS = (128, 128, 85)
        LAYERS = ("l3g", "l3h")

        SECOND_LAYER, MLP_START, HALF_LAG = 16, 11, 4

        def run_steps(attention, mlp):
            for u in range(SECOND_LAYER + MLP_START + HALF_LAG + 4):
                for i in range(2):
                    for lag, piece in attention[i]:
                        if 0 <= u - SECOND_LAYER * i - lag < T:
                            piece(u - SECOND_LAYER * i - lag)
                for i in range(2):
                    for half in range(2):
                        k = u - SECOND_LAYER * i - MLP_START - HALF_LAG * half
                        if 0 <= k < len(mlp[i]):
                            mlp[i][k](half)

        def inner_T_tensor(pe, m, half):
            mem = fill(pe, f"{m}.T{half}", "B")
            for t in range(4 * half, 4 * half + 4):
                if m == "l3g":
                    pe.wait_ge(sem["xn"], at("l3f", "xn", t + 1))
                else:
                    wait_read(pe, f"l3g.mlp{half}", t % 4)
                c = slice((t % 4) * P, (t % 4 + 1) * P)
                nc.tensor.transpose(mem[0:64, c], z[:, t, 0:64], W("ident"))
                mm = nc.tensor.matmul(mem[64:128, c], z[:, t, 64:128], W("l3f.shift"), start=True, stop=True)
            mm.then_inc(full(f"{m}.T{half}"), 1)

        def inner_T_scalar(act, m, half):
            mem = wait_full(act, f"{m}.T{half}")
            nc.scalar.copy(xnT[:, 512 * half:512 * half + 512], mem).then_inc(read(f"{m}.T{half}"), 1)

        def inner_attention_tensor(pe, m, i):
            wqkv = W(f"l3f.wqkv{i}")

            def queries_keys(t):
                wait_read(pe, f"{m}.T{t // 4}")
                mem = fill(pe, f"{m}.qk{t}")
                for c in range(2):
                    mm = nc.tensor.matmul(mem[:, 512 * c:512 * c + 512], xnT[:, t * P:(t + 1) * P],
                                          wqkv[:, 512 * c:512 * c + 512], start=True, stop=True)
                mm.then_inc(full(f"{m}.qk{t}"), 1)

            def turned_T(t):
                pe.wait_ge(sem[m + ".unit"], t + 1)
                mem = fill(pe, f"{m}.qkT{t}", fulls=2, reads=3)
                for c in range(8):
                    mm = nc.tensor.transpose(mem[:, c * P:(c + 1) * P], turned[t % 3][:, c * P:(c + 1) * P], W("ident"))
                    if c % 4 == 3:
                        mm.then_inc(full(f"{m}.qkT{t}"), 1)

            def scores(t):
                wait_read(pe, f"{m}.qkT{t}")
                mem = fill(pe, f"{m}.s{t}", "B")
                for p in range(4):
                    for b in range(2):
                        mm = nc.tensor.matmul(mem[64 * b:64 * b + 64, p * P:(p + 1) * P], qT4[t % 2][:, p, 64 * b:64 * b + 64],
                                              keys4[t % 2][:, p, b, :, :], start=True, stop=True)
                mm.then_inc(full(f"{m}.s{t}"), 1)

            def values(t):
                mem = fill(pe, f"{m}.v{t}", "B", reads=2)
                wv = wqkv[:, 1024:1536].rearrange("p (a h f) -> p h a f", h=2, f=64)
                for b in range(2):
                    for h in range(2):
                        mm = nc.tensor.matmul(mem[64 * h:64 * h + 64, 256 * b:256 * b + 256],
                                              xnT[:, t * P + 64 * b:t * P + 64 * b + 64], wv[:, h], start=True, stop=True)
                mm.then_inc(full(f"{m}.v{t}"), 1)

            def prob_T(t):
                pe.wait_ge(sem["exp"], at(m, "exp", t + 1))
                mem = fill(pe, f"{m}.t{t}", "B")
                for p in range(4):
                    mm = nc.tensor.transpose(mem[:, p * P:(p + 1) * P], prob[t % 2][:, p * P:(p + 1) * P], W("ident"))
                mm.then_inc(full(f"{m}.t{t}"), 1)

            def outputs(t):
                wait_read(pe, f"{m}.t{t}")
                wait_read(pe, f"{m}.v{t}")
                mem = fill(pe, f"{m}.o{t}", reads=2)
                for p in range(4):
                    for b in range(2):
                        at_col = 512 * (p // 2) + 130 * (p % 2)
                        mm = nc.tensor.matmul(mem[64 * b:64 * b + 64, at_col:at_col + 130],
                                              probT[t % 2][:, p * P + 64 * b:p * P + 64 * b + 64], v4[t % 2][:, b, p, :],
                                              start=True, stop=True)
                mm.then_inc(full(f"{m}.o{t}"), 1)

            def outputs_T(t):
                wait_read(pe, f"{m}.o{t}")
                mem = fill(pe, f"{m}.ot{t}", "B")
                for c in range(4):
                    mm = nc.tensor.transpose(mem[:, c * P:(c + 1) * P], out4[t % 2][:, c * P:(c + 1) * P], W("ident"))
                mm.then_inc(full(f"{m}.ot{t}"), 1)

            def project(t):
                wait_read(pe, f"{m}.ot{t}")
                mem = fill(pe, f"{m}.y{t}", "B")
                for c in range(4):
                    mm = nc.tensor.matmul(mem[:, 0:P], outT4[t % 2][:, c * P:(c + 1) * P], W(f"l3f.wo{i}")[:, c * P:(c + 1) * P],
                                          start=c == 0, stop=c == 3)
                mm.then_inc(full(f"{m}.y{t}"), 1)

            return [(0, queries_keys), (7, project), (6, outputs_T), (5, outputs), (4, prob_T),
                                   (3, scores), (4, values), (2, turned_T)]

        def inner_attention_vector(dve, m, i):
            def rotate(t):
                mem = wait_full(dve, f"{m}.qk{t}")
                dve.wait_ge(sem[m + ".square"], t + 1)
                nc.vector.tensor_reduce(len_sq[:, t, :], square4[t % 2].rearrange("p (g f) -> p g f", f=64), AX, ALU.add)\
                  .then_inc(sem[m + ".len"], 1)
                if t >= 3:
                    wait_full(dve, f"{m}.qkT{t - 3}", 1)
                if t >= 2:
                    dve.wait_ge(sem[m + ".unit"], t - 1)
                tab = W(f"l3f.scale{i}").rearrange("p (c a o f) -> p c a o f", c=2, a=2, o=1)
                qk = mem.rearrange("p (a h f) -> p a h f", a=2, f=64)
                c4 = crossed[t % 2].rearrange("p (a h f) -> p a h f", a=2, f=64)
                nc.vector.tensor_tensor(turned[t % 3].rearrange("p (a h f) -> p a h f", a=2, f=64), qk,
                                        tab[:, 0].broadcast_to([P, 2, 8, 64]), ALU.mult).then_inc(sem[m + ".turn"], 1)
                for lo, hi in ((0, 32), (32, 0)):
                    nc.vector.tensor_tensor(c4[:, :, :, lo:lo + 32], qk[:, :, :, hi:hi + 32],
                                            tab[:, 1, :, :, lo:lo + 32].broadcast_to([P, 2, 8, 32]), ALU.mult)\
                      .then_inc(read(f"{m}.qk{t}") if lo else sem[m + ".turn"], 1)

            def softmax(t):
                mem = wait_full(dve, f"{m}.s{t}")
                if t >= 2:
                    wait_full(dve, f"{m}.t{t - 2}")
                    dve.wait_ge(sem["less"], at(m, "less", t - 1))
                pr = prob[t % 2][:, 0:512].rearrange("p (h k) -> p h k", k=SEQ)
                c = W("causal").rearrange("p (o k) -> p o k", o=1).broadcast_to([P, 8, SEQ])
                nc.vector.scalar_tensor_tensor(out=pr, in0=mem.rearrange("p (h k) -> p h k", k=SEQ), scalar=8.0, in1=c,
                                               op0=ALU.mult, op1=ALU.add).then_inc(read(f"{m}.s{t}"), 1)
                wait_read(dve, f"{m}.s{t}")
                nc.vector.tensor_reduce(top[t % 2][:, 0:8], pr, AX, ALU.max).then_inc(sem["top"], 1)
                dve.wait_ge(sem["top"], at(m, "top", t + 1))
                tb = top[t % 2][:, 0:8].rearrange("p (h o) -> p h o", o=1).broadcast_to([P, 8, SEQ])
                nc.vector.tensor_tensor(pr, pr, tb, ALU.subtract).then_inc(sem["less"], 1)

            def normalise(t):
                mem = wait_full(dve, f"{m}.o{t}")
                if t >= 2:
                    wait_full(dve, f"{m}.ot{t - 2}")
                v = mem.rearrange("p (g w) -> p g w", g=2)[:, :, 0:260].rearrange("p g (a w) -> p g a w", w=130)
                rd = rden[t % 2][:, 0:8].rearrange("p (g a h) -> p g a h", g=2, a=2)
                nc.vector.reciprocal(rd, v[:, :, :, 128:130]).then_inc(sem["rden"], 1)
                dve.wait_ge(sem["rden"], at(m, "rden", t + 1))
                for g in range(2):
                    to = out4[t % 2][:, 256 * g:256 * g + 256].rearrange("p (a h f) -> p a h f", h=2, f=64)
                    rb = rd[:, g].rearrange("p a (h o) -> p a h o", o=1).broadcast_to([P, 2, 2, 64])
                    nc.vector.tensor_tensor(to, v[:, g, :, 0:128].rearrange("p a (h f) -> p a h f", h=2), rb, ALU.mult)\
                      .then_inc(read(f"{m}.o{t}"), 1)

            def residual(t):
                mem = wait_full(dve, f"{m}.y{t}")
                nc.vector.tensor_tensor(z[:, t, :], z[:, t, :], mem[:, 0:P], ALU.add).then_inc(read(f"{m}.y{t}"), 1)

            return [(7, residual), (0, rotate), (5, normalise), (3, softmax)]

        def values4_copy(act, m, t):
            mem = wait_full(act, f"{m}.v{t}")
            if t >= 2:
                wait_full(act, f"{m}.o{t - 2}")
            for h in range(2):
                src = mem[64 * h:64 * h + 64, 0:512].rearrange("p (b a f) -> p b a f", b=2, f=64)
                nc.scalar.copy(v4[t % 2][64 * h:64 * h + 64, :, :, 64 * h:64 * h + 64], src).then_inc(read(f"{m}.v{t}"), 1)

        def inner_attention_scalar(act, m, i):
            def squares(t):
                mem = wait_full(act, f"{m}.qk{t}")
                if t >= 2:
                    act.wait_ge(sem[m + ".len"], t - 1)
                nc.scalar.activation(square4[t % 2], mem, ACT.Square).then_inc(sem[m + ".square"], 1)

            def turned_copy(t):
                if t >= 2:
                    wait_full(act, f"{m}.s{t - 2}")
                elif i == 0:
                    act.wait_ge(sem["v4_set"], 4)
                mem = wait_full(act, f"{m}.qkT{t}", 0)
                nc.scalar.copy(qT4[t % 2][:, :, :].rearrange("p a k -> p (a k)"), mem[:, 0:512]).then_inc(read(f"{m}.qkT{t}"), 1)
                wait_full(act, f"{m}.qkT{t}", 1)
                for h in range(2):
                    rows = slice(64 * h, 64 * h + 64)
                    nc.scalar.copy(keys4[t % 2][rows, :, :, h, :], mem[rows, 512:1024].rearrange("p (a b k) -> p a b k", a=4, b=2))\
                      .then_inc(read(f"{m}.qkT{t}"), 1)

            def exponential(t):
                act.wait_ge(sem["less"], at(m, "less", t + 1))
                nc.scalar.activation(prob[t % 2][:, 0:512], prob[t % 2][:, 0:512], ACT.Exp).then_inc(sem["exp"], 1)

            def prob_copy(t):
                if t >= 2:
                    wait_full(act, f"{m}.o{t - 2}")
                mem = wait_full(act, f"{m}.t{t}")
                nc.scalar.copy(probT[t % 2][:, 0:512], mem[:, 0:512]).then_inc(read(f"{m}.t{t}"), 1)

            def outputs_copy(t):
                if t >= 2:
                    wait_full(act, f"{m}.y{t - 2}")
                mem = wait_full(act, f"{m}.ot{t}")
                nc.scalar.copy(outT4[t % 2], mem[:, 0:512]).then_inc(read(f"{m}.ot{t}"), 1)

            return [(0, squares), (6, outputs_copy), (4, prob_copy), (4, lambda t: values4_copy(act, m, t)),
                                   (3, exponential), (2, turned_copy)]

        def inner_attention_pool(pool, m, i):
            def unit(t):
                pool.wait_ge(sem[m + ".len"], t + 1)
                link(pool, "pool_chain", nc.gpsimd.tensor_scalar(len_inv[:, t, :], len_sq[:, t, :], 1e-24, None, ALU.max))
                half = minus_half[:, 0:1].broadcast_to([P, 16])
                link(pool, "pool_chain", nc.gpsimd.tensor_tensor(len_inv[:, t, :], len_inv[:, t, :], half, ALU.pow))
                pool.wait_ge(sem[m + ".turn"], 2 * t + 2)
                wait_read(pool, f"{m}.qk{t}")
                link(pool, "pool_chain", nc.gpsimd.tensor_tensor(turned[t % 3], turned[t % 3], crossed[t % 2], ALU.add))
                r = len_inv[:, t, :].rearrange("p (g o) -> p g o", o=1).broadcast_to([P, 16, 64])
                t3 = turned[t % 3].rearrange("p (g f) -> p g f", f=64)
                nc.gpsimd.tensor_tensor(t3, t3, r, ALU.mult).then_inc(sem[m + ".unit"], 1)

            return [(0, unit)]


        def inner_mlp_tensor(pe, m, i):
            def shift(half):
                for t in range(4 * half, 4 * half + 4):
                    wait_read(pe, f"{m}.y{t}")
                mem = fill(pe, f"{m}.shift{half}", "B")
                nc.tensor.matmul(mem[:, 0:256], W("l3f.shift"), z[:, 4 * half:4 * half + 4, 64:128], start=True, stop=True)\
                  .then_inc(full(f"{m}.shift{half}"), 1)

            def hidden(half, c):
                rows = HIDDEN_ROWS[c]
                for part in ("g", "a"):
                    mem = fill(pe, f"{m}.{part}{c}{half}")
                    lo = P * c + (341 if part == "g" else 0)
                    nc.tensor.matmul(mem[0:rows, 0:512], W(f"l3f.w1_{i}")[:, lo:lo + rows], mlpT[:, 512 * half:512 * half + 512],
                                     start=True, stop=True).then_inc(full(f"{m}.{part}{c}{half}"), 1)

            def first(half):
                mem = fill(pe, f"{m}.hT{half}", "B")
                for t in range(4 * half, 4 * half + 4):
                    pe.wait_ge(sem["xn"], at(m, "xn", t + 1))
                    mm = nc.tensor.transpose(mem[:, (t % 4) * P:(t % 4 + 1) * P], half_shifted[:, t, :], W("ident"))
                mm.then_inc(full(f"{m}.hT{half}"), 1)
                wait_read(pe, f"{m}.hT{half}")
                hidden(half, 0)

            def others(half):
                hidden(half, 1)
                hidden(half, 2)

            def project(half):
                for c in range(3):
                    wait_read(pe, f"{m}.a{c}{half}")
                mem = fill(pe, f"{m}.mlp{half}", "B", reads=4)
                for t in range(4):
                    for c, rows in enumerate(HIDDEN_ROWS):
                        mm = nc.tensor.matmul(mem[:, t * P:(t + 1) * P], mlp4[0:rows, c, t * P:(t + 1) * P],
                                              W(f"l3f.w2_{i}")[0:rows, c * P:(c + 1) * P], start=c == 0, stop=c == 2)
                mm.then_inc(full(f"{m}.mlp{half}"), 1)

            return [shift, first, others, project] + ([lambda half: inner_T_tensor(pe, "l3h", half)] if i == 0 else [])

        def inner_mlp_vector(dve, m, i):
            def normalise(half):
                tiles = range(4 * half, 4 * half + 4)
                dve.wait_ge(sem[m + ".first_half"], half + 1)
                wait_read(dve, f"{m}.shift{half}")
                for t in tiles:
                    ln_stats(dve, m, t, half_shifted)
                for t in tiles:
                    ln_apply(dve, m, t, half_shifted, half_shifted)

            def gated(half, c):
                rows = HIDDEN_ROWS[c]
                mem = wait_full(dve, f"{m}.a{c}{half}")
                wait_read(dve, f"{m}.g{c}{half}")
                nc.vector.scalar_tensor_tensor(out=mlp4[0:rows, c, :], in0=mem[0:rows, 0:512], scalar=W(f"l3f.b1a{i}")[0:rows, c:c + 1],
                                               in1=gelu4[0:rows, c, :], op0=ALU.add, op1=ALU.mult).then_inc(read(f"{m}.a{c}{half}"), 1)

            def others(half):
                gated(half, 1)
                gated(half, 2)

            def residual(half):
                dve.wait_ge(sem[m + ".b2"], half + 1)
                mem = wait_full(dve, f"{m}.mlp{half}")
                for t in range(4 * half, 4 * half + 4):
                    nc.vector.tensor_tensor(z[:, t, :], z[:, t, :], mem[:, (t % 4) * P:(t % 4 + 1) * P], ALU.add)\
                      .then_inc(read(f"{m}.mlp{half}"), 1)
                    if i == 1:
                        wait_read(dve, f"{m}.mlp{half}", t % 4)
                        nc.vector.tensor_tensor(x_res[:, t, :], x_res[:, t, :], z[:, t, :], ALU.add).then_inc(sem["l3f.x"], 1)

            return [normalise, lambda half: gated(half, 0), others, residual]

        def inner_mlp_scalar(act, m, i):
            def shifted(half):
                mem = wait_full(act, f"{m}.shift{half}")
                nc.scalar.copy(half_shifted[:, 4 * half:4 * half + 4, 64:128], mem[:, 0:256].rearrange("p (t d) -> p t d", t=4))\
                  .then_inc(read(f"{m}.shift{half}"), 1)

            def gelu(half, c):
                rows = HIDDEN_ROWS[c]
                mem = wait_full(act, f"{m}.g{c}{half}")
                nc.scalar.activation(gelu4[0:rows, c, :], mem[0:rows, 0:512], ACT.Gelu, bias=W(f"l3f.b1g{i}")[0:rows, c:c + 1])\
                  .then_inc(read(f"{m}.g{c}{half}"), 1)

            def first(half):
                mem = wait_full(act, f"{m}.hT{half}")
                nc.scalar.activation(mlpT[:, 512 * half:512 * half + 512], mem, ACT.Identity, scale=W(f"l3f.ln_g{i}"),
                                     bias=W(f"l3f.ln_b{i}")).then_inc(read(f"{m}.hT{half}"), 1)
                gelu(half, 0)

            def others(half):
                gelu(half, 1)
                gelu(half, 2)

            return [shifted, first, others, lambda half: None] + ([lambda half: inner_T_scalar(act, "l3h", half)] if i == 0 else [])

        def inner_mlp_pool(pool, m, i):
            def normalise(half):
                tiles = slice(4 * half, 4 * half + 4)
                for t in range(4 * half, 4 * half + 4):
                    wait_read(pool, f"{m}.y{t}")
                nc.gpsimd.tensor_copy(half_shifted[:, tiles, 0:64], z[:, tiles, 0:64]).then_inc(sem[m + ".first_half"], 1)
                pool.wait_ge(sem[m + ".first_half"], half + 1)
                ln_pool(pool, m, tiles=(4 * half, 4 * half + 4))
                wait_full(pool, f"{m}.shift{half}")
                nc.gpsimd.tensor_tensor(z[:, tiles, :], z[:, tiles, :], tok_bias(f"l3f.b2_{i}", 4), ALU.add).then_inc(sem[m + ".b2"], 1)

            return [normalise]

        def l3f_tensor(pe):
            for half in range(2):
                inner_T_tensor(pe, "l3g", half)
            pe.wait_ge(sem["v4_set"], 4)
            run_steps([inner_attention_tensor(pe, m, i) for i, m in enumerate(LAYERS)],
                      [inner_mlp_tensor(pe, m, i) for i, m in enumerate(LAYERS)])

        def l3f_vector(dve):
            dve.wait_ge(sem["zeros_set"], 4)
            for j in range(2):
                for h in range(2):
                    nc.vector.memset(v4[j][64 * h:64 * h + 64, :, :, 128 + h:129 + h], 1.0).then_inc(sem["v4_set"], 1)
            dve.wait_ge(sem["v4_set"], 4)
            dve.wait_ge(sem["rope_table"], 2)
            run_steps([inner_attention_vector(dve, m, i) for i, m in enumerate(LAYERS)],
                      [inner_mlp_vector(dve, m, i) for i, m in enumerate(LAYERS)])

        def l3f_scalar(act):
            for half in range(2):
                inner_T_scalar(act, "l3g", half)
            run_steps([inner_attention_scalar(act, m, i) for i, m in enumerate(LAYERS)],
                      [inner_mlp_scalar(act, m, i) for i, m in enumerate(LAYERS)])

        def l3f_pool(pool):
            for i in range(2):
                nc.gpsimd.tensor_tensor(W(f"l3f.scale{i}"), W(f"l3f.scale{i}"), W("l3f.rope"), ALU.mult)\
                  .then_inc(sem["rope_table"], 1)
            ln_pool(pool, "l3f")
            wait_full(pool, f"l3x.o{T - 1}")
            nc.gpsimd.memset(v4[1][:, :, :, :], 0.0).then_inc(sem["zeros_set"], 1)
            run_steps([inner_attention_pool(pool, m, i) for i, m in enumerate(LAYERS)],
                      [inner_mlp_pool(pool, m, i) for i, m in enumerate(LAYERS)])

        stages = [
            ("0a", l0a_tensor, l0a_vector, l0a_scalar, l0a_pool, residual_ready(L0A)),
            ("0x", l0x_tensor, l0x_vector, l0x_scalar, l0x_pool, residual_ready(L0X)),
            ("0f", l0f_tensor, l0f_vector, l0f_scalar, l0f_pool, L0F_READY),
            ("1", l1a_tensor, l1a_vector, l1a_scalar, l1a_pool, product_ready("l1a.y")),
            ("1", l1x_tensor, l1x_vector, l1x_scalar, l1x_pool, residual_ready(L1X)),
            ("1", l1f_tensor, l1f_vector, l1f_scalar, l1f_pool, L1F_READY),
            ("2", l2a_tensor, l2a_vector, l2a_scalar, l2a_pool, residual_ready(L2A)),
            ("2", l2x_tensor, l2x_vector, l2x_scalar, l2x_pool, residual_ready(L2X)),
            ("2", l2f_tensor, l2f_vector, l2f_scalar, l2f_pool, L2F_READY),
            ("3", l3a_tensor, l3a_vector, l3a_scalar, l3a_pool, residual_ready(L3A)),
            ("3", l3x_tensor, l3x_vector, l3x_scalar, l3x_pool, residual_ready(L3X)),
            ("4", l3f_tensor, l3f_vector, l3f_scalar, l3f_pool, lambda eng, t: eng.wait_ge(sem["l3f.x"], t + 1)),
        ]

        block = ctx.enter_context(nc.Block())

        @block.tensor
        def _(pe):
            weights(pe, "c")
            context_tensor(pe)
            for s in stages:
                weights(pe, s[0])
                s[1](pe)

        @block.vector
        def _(dve):
            nc.vector.memset(minus_half[:, :], -0.5).then_inc(sem["powers_set"], 1)
            nc.vector.memset(plus_half[:, :], 0.5).then_inc(sem["powers_set"], 1)
            for s in stages:
                if s[0] != "0a":
                    weights(dve, s[0])
                s[2](dve)

        @block.scalar
        def _(act):
            weights(act, "c")
            context_scalar(act)
            for s in stages:
                weights(act, s[0])
                s[3](act)

        @block.gpsimd
        def _(pool):
            pool.wait_ge(sem["powers_set"], 2)
            for s in stages:
                if s[0] != "0a":
                    weights(pool, s[0])
                s[4](pool)

        @block.sync
        def _(sp):
            sp.dma_start(x_res[:, :, :], dram["x"].rearrange("t p d -> p t d")).then_inc(sem["x_loaded"], 16)
            sp.dma_start(packed["c"][:, :], dram["c"]).then_inc(sem["pack.c"], 16)
            sp.dma_start(ctx_tok, dram["ctx"].rearrange("t p d -> p t d")).then_inc(sem["ctx_loaded"], 16)
            sp.dma_start(packed["0a"][:, :], dram["0a"]).then_inc(sem["pack.0a"], 16)
            for h in range(2):
                sp.dma_start(ctx_keys[64 * h:64 * h + 64, :, :],
                             dram["ctx"].rearrange("t (b k) d -> k (t b) d", b=2)).then_inc(sem["ctx_keys_loaded"], 16)
            for g in packs[2:]:
                if g == "4":
                    for t in range(T):
                        L1F_READY(sp, t)
                sp.dma_start(packed[g][:, :], dram[g]).then_inc(sem["pack." + g], 16)
            for half in range(2):
                tiles = slice(4 * half, 4 * half + 4)
                for t in range(4 * half, 4 * half + 4):
                    stages[-1][5](sp, t)
                sp.dma_start(out[tiles].rearrange("t p d -> p t d"), x_res[:, tiles, :]).then_inc(sem["stored"], 16)
            sp.wait_ge(sem["stored"], 32)



def arrange(inputs):
    import numpy as np

    i = {k: np.asarray(v) for k, v in inputs.items()}
    packs = {}
    where = {}

    def put(pack, name, a):
        a = np.asarray(a)
        assert a.dtype == np.float32, (name, a.dtype)
        cols = packs.setdefault(pack, [])
        at = sum(c.shape[1] for c in cols)
        where[name] = (pack, at, a.shape[0], a.shape[1])
        if a.shape[0] < P:
            a = np.concatenate([a, np.zeros((P - a.shape[0], a.shape[1]), np.float32)], 0)
        cols.append(a)

    pos = np.arange(SEQ)
    feature = np.arange(P)
    put("c", "ident", np.eye(P, dtype=np.float32))
    put("c", "head_mask", (feature[:, None] // 8 == np.arange(16)[None]).astype(np.float32))
    put("c", "head_mask8", (feature[:, None] // 16 == np.arange(8)[None]).astype(np.float32))
    decay = np.exp(-0.01 * np.abs(pos[:, None] - pos[None]).astype(np.float32)) / np.float32(np.sqrt(128))
    put("c", "decay", np.tile(decay.astype(np.float32), (2, 1)))
    put("c", "causal", np.tile(np.where(pos[None] <= pos[:, None], 0, MASKED).astype(np.float32), (2, 1)))
    for w in ("W_k", "W_v", "W_q", "W_down_kv", "W_up_k", "W_up_v", "W_o"):
        put("0a", "L0_attn_" + w, i["L0_attn_" + w])
    for part, rows in (("q", slice(0, 128)), ("k", slice(128, 256)), ("v", slice(256, 384))):
        g = np.zeros((P, 40), np.float32)
        g[:, 0:8] = i["L0_xattn_igate_kernel"][rows]
        g[:, 32:40] = i["L0_xattn_fgate_kernel"][rows]
        put("0x", "l0x.gate_" + part, g)
    g = np.zeros((40, 1), np.float32)
    g[0:8, 0], g[32:40, 0] = i["L0_xattn_igate_bias"], i["L0_xattn_fgate_bias"]
    put("0x", "l0x.gate_bias", g)
    put("0x", "ones8", np.ones((8, 64), np.float32))
    start = np.arange(TOK)[None] % SEQ == 0
    put("0x", "keep", np.tile(np.where(start, 0, 1).astype(np.float32), (8, 1)))
    put("0x", "restart", np.tile(np.where(start, 2 * MASKED, 0).astype(np.float32), (8, 1)))

    def column(v):
        return v.reshape(-1, 1)

    def chunks(v):
        return np.ascontiguousarray(v.reshape(-1, P).T)

    def rows(v):
        return np.broadcast_to(v.reshape(1, -1), (P, v.size))

    f = "L0_ffn_"
    put("0f", f + "enc_W", i[f + "enc_W"])
    put("0f", "l0f.enc_b", chunks(i[f + "enc_b"]))
    for c in range(2):
        put("0f", f"l0f.s2c{c}", i[f + "s2c_W"][128 * c:128 * c + 128])
    put("0f", "l0f.s2c_b", column(i[f + "s2c_b"]))
    put("0f", f + "rW1", i[f + "rW1"])
    put("0f", "l0f.rb1", column(i[f + "rb1"]))
    put("0f", f + "rW2", i[f + "rW2"])
    put("0f", "l0f.rb2", rows(i[f + "rb2"]))
    for e in range(8):
        put("0f", f"l0f.We1_{e}", i[f + "We1"][e])
        put("0f", f"l0f.We2_{e}", i[f + "We2"][e])
    put("0f", "l0f.be1", i[f + "be1"].T)
    put("0f", "l0f.be2", i[f + "be2"].reshape(4, P).T)
    for p in range(4):
        put("0f", f"l0f.pair{p}", (np.arange(8)[:, None] == 2 * p + np.arange(P)[None] // 64).astype(np.float32))
    put("0f", "before", rows((np.arange(8)[None] < np.arange(8)[:, None]).astype(np.float32)))
    put("0f", "l0f.c2s2", np.concatenate([i[f + "c2s_W"]] * 2, 0))
    put("0f", "l0f.c2s_b", chunks(i[f + "c2s_b"]))
    for c in range(2):
        put("0f", f"l0f.dec{c}", i[f + "dec_W"][128 * c:128 * c + 128])
    for b in ("dec_b", "ln_g", "ln_b"):
        put("0f", "l0f." + b, rows(i[f + b]))

    for m in ("r", "w", "k", "v", "a", "g", "out"):
        put("1", "L1_attn_W_" + m, i["L1_attn_W_" + m].T)
    for m in ("r", "w", "k", "v", "a", "g"):
        put("1", "l1a.x_" + m, column(i["L1_attn_x_" + m]))
    put("1", "l1a.gn_w", column(i["L1_attn_gn_w"]))
    put("1", "l1a.gn_b", column(i["L1_attn_gn_b"]))
    put("1", "l1a.b_out", rows(i["L1_attn_b_out"]))
    for m in ("Wq", "Wk", "Wv"):
        put("1", "L1_xattn_" + m, i["L1_xattn_" + m].T)
    put("1", "L1_ffn_W_fc", i["L1_ffn_W_fc"].T)
    for c in range(4):
        put("1", f"l1f.proj{c}", i["L1_ffn_W_proj"].T[128 * c:128 * c + 128])

    angle = pos[:, None].astype(np.float32) * (1.0 / 10000.0 ** (np.arange(4, dtype=np.float32) / 4))[None]
    put("2", "cos8", np.tile(np.cos(angle).astype(np.float32), (2, 2)))
    put("2", "sin8", np.tile(np.concatenate([-np.sin(angle), np.sin(angle)], 1).astype(np.float32), (2, 1)))
    w = i["L2_attn_Wqkv"]
    swapped = np.arange(256).reshape(32, 2, 4)[:, ::-1].reshape(-1)
    put("2", "l2a.qk_rot", np.concatenate([w[:, 0:256], w[:, swapped]], 1))
    put("2", "l2a.Wv", w[:, 256:384])
    put("2", "L2_attn_Wo", i["L2_attn_Wo"])
    put("2", "l2a.bo", rows(i["L2_attn_bo"]))
    for m in ("Wq", "Wk", "Wv", "Wo"):
        put("2", "l2x." + m, i["L2_xattn_" + m].T)
    for m in ("bq", "bk", "bv"):
        put("2", "l2x." + m, column(i["L2_xattn_" + m]))
    put("2", "l2x.bo", rows(i["L2_xattn_bo"]))
    put("2", "l2f.up", i["L2_ffn_w_up"].T)
    put("2", "l2f.down", np.concatenate([i["L2_ffn_w_down"].T[128 * c:128 * c + 128] for c in range(4)], 1))
    put("2", "ones128", np.ones((P, P), np.float32))

    for m in ("WQ", "WK", "WV", "WO"):
        put("3", "l3a." + m, i["L3_attn_" + m].T)
    for m in ("bQ", "bK", "bV"):
        put("3", "l3a." + m, column(i["L3_attn_" + m]))
    put("3", "l3a.bO", rows(i["L3_attn_bO"]))
    rel = i["L3_attn_rel_pos_table"][pos[:, None] - pos[None] + 255]
    rel = rel.transpose(0, 2, 1).reshape(SEQ, -1)
    put("3", "l3a.rel", np.concatenate([rel, rel], 0))
    for m in ("Wq", "Wk", "Wv", "Wo"):
        put("3", "l3x." + m, i["L3_xattn_" + m])
    for m in ("bq", "bk", "bv"):
        put("3", "l3x." + m, column(i["L3_xattn_" + m]))
    put("3", "l3x.bo", rows(i["L3_xattn_bo"]))

    put("4", "l3f.shift", ((feature[:, None] == feature[None] - 1) & (feature[None] % SEQ != 0)).astype(np.float32))
    f = "L3_ffn_"
    half = np.arange(0, 64, 2, dtype=np.float32)
    at = np.arange(SEQ, dtype=np.float32)
    angle = at[:, None] * (1.0 / 10000.0 ** (half / 64))[None]
    power = (at - SEQ // 2) / 32.0
    grow = ((half + 0.4 * 64) / (1.4 * 64))[None] ** power[:, None]
    twice = lambda a: np.concatenate([a, a], 1)
    cos, grow, sin = twice(np.cos(angle)), twice(grow), np.concatenate([-np.sin(angle), np.sin(angle)], 1)
    rope = np.concatenate([cos * grow, cos / grow, sin * grow, sin / grow], 1).astype(np.float32)
    put("4", "l3f.rope", np.tile(rope, (2, 1)))
    other = (np.arange(64) + 32) % 64
    for l in range(2):
        qs, ks = i[f + "q_scale"][l].reshape(-1), i[f + "k_scale"][l].reshape(-1)
        put("4", f"l3f.scale{l}", np.broadcast_to(np.concatenate([qs, ks, qs[other], ks[other]])[None], (P, 256)))
        put("4", f"l3f.wqkv{l}", i[f + "wqkv"][l])
        put("4", f"l3f.wo{l}", np.concatenate([i[f + "wo"][l][128 * c:128 * c + 128] for c in range(4)], 1))
        put("4", f"l3f.ln_g{l}", column(i[f + "ln_g"][l]))
        put("4", f"l3f.ln_b{l}", column(i[f + "ln_b"][l]))
        put("4", f"l3f.w1_{l}", i[f + "w1"][l])

        def padded(v):
            v = v.reshape(341, -1)
            v = np.concatenate([v, np.zeros((384 - 341, v.shape[1]), np.float32)], 0)
            return np.concatenate([v[128 * c:128 * c + 128] for c in range(3)], 1)

        put("4", f"l3f.b1a{l}", padded(i[f + "b1"][l][:341]))
        put("4", f"l3f.b1g{l}", padded(i[f + "b1"][l][341:]))
        put("4", f"l3f.w2_{l}", padded(i[f + "w2"][l]))
        put("4", f"l3f.b2_{l}", rows(i[f + "b2"][l]))
    arrays = {g: np.concatenate(c, 1) for g, c in packs.items()}
    arrays["x"] = i["x"].reshape(T, P, D)
    arrays["ctx"] = i["ctx_1024"].reshape(T, P, D)
    return arrays, where


def kernel(**inputs):
    import numpy as np
    import concourse.bacc as bacc
    from concourse.bass_utils import run_bass_kernel_spmd

    arrays, where = arrange(inputs)
    nc = bacc.Bacc("TRN2", target_bir_lowering=False, num_devices=1)
    dram = {g: nc.dram_tensor("in_" + g, a.shape, F32, kind="ExternalInput").ap() for g, a in arrays.items()}
    out = nc.dram_tensor("out", (T, P, D), F32, kind="ExternalOutput").ap()
    build(nc, dram, where, out)
    r = run_bass_kernel_spmd(nc, [{"in_" + g: a for g, a in arrays.items()}], core_ids=[0])
    return np.asarray(r.results[0]["out"]).reshape(NSEQ, SEQ, D)
```
